# Optimizing a Trainium2 kernel written in Bass

```python
import numpy as np
import jax
import jax.numpy as jnp

def _softmax(x, axis=-1):
    return jax.nn.softmax(x, axis=axis)

def _gelu(x):
    return jax.nn.gelu(x, approximate=True)

def _silu(x):
    return jax.nn.silu(x)

def _sigmoid(x):
    return jax.nn.sigmoid(x)

def _layernorm(x, axis=-1, eps=1e-05):
    m = jnp.mean(x, axis=axis, keepdims=True)
    v = jnp.var(x, axis=axis, keepdims=True)
    return (x - m) / jnp.sqrt(v + eps)

def _scatter_add(tgt, idx, src, axis=0):
    return tgt.at[idx].add(src)

def _segment_sum(src, seg, n):
    return jax.ops.segment_sum(src, seg, n)
kernel_name = 'mk_xattn_ffn_d4_seqx_r8_4d9dc2'

def setup_inputs(seed: int=0):
    np.random.seed(seed)
    _w = jnp.asarray

    def _rec_inputs():
        import jax
        import jax.numpy as jnp
        _rk = jax.random.key(seed)
        x = -0.0005207 + 1.001 * jax.random.normal(jax.random.fold_in(_rk, 1), (32, 128, 128), jnp.float32)
        _lenS = 128 - jax.random.randint(jax.random.fold_in(_rk, 7), (32,), 0, max(1, 128 // 4) + 1, jnp.int32)
        _lenS2 = 77 - jax.random.randint(jax.random.fold_in(_rk, 8), (32,), 0, max(1, 77 // 4) + 1, jnp.int32)
        _ctx_1024P = jax.random.normal(jax.random.fold_in(_rk, 12), (32, 16, 128), jnp.float32)
        _ctx_1024c = jax.random.dirichlet(jax.random.fold_in(_rk, 512), 0.3 * jnp.ones((16,), jnp.float32), (32, 77))
        _ctx_1024t = jnp.einsum('bsk,bkd->bsd', _ctx_1024c, _ctx_1024P)
        _ctx_1024t = _ctx_1024t * jax.lax.rsqrt(jnp.mean(jnp.square(_ctx_1024t)) + 1e-12) * 0.953939
        ctx_1024 = 0.00191187 + 0.999416 * (_ctx_1024t + 0.3 * jax.random.normal(jax.random.fold_in(_rk, 612), (32, 77, 128), jnp.float32))
        _validS = jnp.arange(128)[None, :] < _lenS[:, None]
        _validS2 = jnp.arange(77)[None, :] < _lenS2[:, None]
        _causal = jnp.tril(jnp.ones((128, 128), dtype=bool))
        mask_BxS_ff1 = jnp.where(jnp.ones((32, 128), dtype=bool), 1.0, 0.0).astype(jnp.float32)
        mask_BxS2_ik0 = jnp.where(jnp.broadcast_to(_validS2[:, :], (32, 77)), 0, 1).astype(jnp.int32)
        mask_BxS2_if0 = jnp.where(jnp.ones((32, 77), dtype=bool), 0, 1).astype(jnp.int32)
        return (x, ctx_1024, mask_BxS_ff1, mask_BxS2_ik0, mask_BxS2_if0)
    x, ctx_1024, mask_BxS_ff1, mask_BxS2_ik0, mask_BxS2_if0 = _rec_inputs()

    def _L0_xattn_setup():
        import jax, jax.numpy as jnp
        import numpy as np
        B, F, T, D = (8, 32, 32, 128)
        NEG = -1e+30
        key = jax.random.key(seed)
        ks = jax.random.split(key, 10)
        s = 1.0 / np.sqrt(D)
        return {'features': jax.random.normal(ks[0], (B, F, D), jnp.float32), 'masks': jnp.ones((B, F), jnp.float32), 'textual_features': jax.random.normal(ks[1], (B, T, D), jnp.float32), 'q_masks': jax.random.randint(ks[2], (B, T), 0, 2, jnp.int32), 'Ws': jax.random.normal(ks[3], (D, D), jnp.float32) * s, 'W': jax.random.normal(ks[4], (D, D), jnp.float32) * s, 'w': jax.random.normal(ks[5], (D, 1), jnp.float32) * s, 'b': jax.random.normal(ks[6], (1, D), jnp.float32) * s, 'Wcw': jax.random.normal(ks[7], (1, D), jnp.float32) * s, 'bcw': jnp.zeros((1,), jnp.float32), 'Wcb': jax.random.normal(ks[8], (1, D), jnp.float32) * s, 'bcb': jnp.zeros((1,), jnp.float32)}
    _L0_xattn_all = _L0_xattn_setup()
    _L0_xattn_in = {k: v for k, v in _L0_xattn_all.items() if k in ('Ws', 'W', 'w', 'b', 'Wcw', 'bcw', 'Wcb', 'bcb')}
    del _L0_xattn_all

    def _L0_ffn_setup():
        import jax, jax.numpy as jnp
        import numpy as np
        DIM = 128
        DEPTH = 6
        HEADS = 16
        DIM_HEAD = 64
        WINDOW = 32
        INNER = HEADS * DIM_HEAD
        DIM_INNER = int(DIM * 4 * 2 / 3)
        QK_SCALE = 8.0

        def shift_tokens(t):
            a, s = jnp.split(t, 2, -1)
            s = jnp.pad(s, ((0, 0), (1, 0), (0, 0)))[:, :-1]
            return jnp.concatenate([a, s], -1)

        def l2norm(t):
            return t / jnp.maximum(jnp.linalg.norm(t, axis=-1, keepdims=True), 1e-12)

        def rotate_half(x):
            x1, x2 = jnp.split(x, 2, -1)
            return jnp.concatenate([-x2, x1], -1)

        def rotary_tables(n):
            half = jnp.arange(0, DIM_HEAD, 2, dtype=jnp.float32)
            inv_freq = 1.0 / 10000.0 ** (half / DIM_HEAD)
            t = jnp.arange(n, dtype=jnp.float32)
            freqs = t[:, None] * inv_freq[None, :]
            freqs = jnp.concatenate([freqs, freqs], -1)
            base_scale = (half + 0.4 * DIM_HEAD) / (1.4 * DIM_HEAD)
            power = (t - n // 2) / (WINDOW // 2)
            scale = base_scale[None, :] ** power[:, None]
            scale = jnp.concatenate([scale, scale], -1)
            return (freqs, scale)

        def local_attention(q, k, v):
            b, h, n, d = q.shape
            w = WINDOW
            nw = n // w
            bq = q.reshape(b, h, nw, w, d)
            bk = k.reshape(b, h, nw, w, d)
            bv = v.reshape(b, h, nw, w, d)

            def look(t):
                p = jnp.pad(t, ((0, 0), (0, 0), (1, 0), (0, 0), (0, 0)))
                return jnp.concatenate([p[:, :, :nw], p[:, :, 1:]], axis=3)
            bk2, bv2 = (look(bk), look(bv))
            seq = jnp.arange(n).reshape(nw, w)
            seq_p = jnp.pad(seq, ((1, 0), (0, 0)), constant_values=-1)
            jt = jnp.concatenate([seq_p[:nw], seq_p[1:]], axis=1)
            it = seq[:, :, None]
            jb = jt[:, None, :]
            mask = (it < jb) | (it > jb + w) | (jb == -1)
            sim = jnp.einsum('bhwie,bhwje->bhwij', bq, bk2) * QK_SCALE
            sim = jnp.where(mask, -jnp.finfo(sim.dtype).max, sim)
            attn = jax.nn.softmax(sim, -1)
            out = jnp.einsum('bhwij,bhwje->bhwie', attn, bv2)
            return out.reshape(b, h, n, d)

        def attn_layer(x, Wqkv, qs, ksc, Wo):
            b, n, _ = x.shape
            qkv = x @ Wqkv
            q, k, v = jnp.split(qkv, 3, -1)
            sh = lambda t: t.reshape(b, n, HEADS, DIM_HEAD).transpose(0, 2, 1, 3)
            q, k, v = (sh(q), sh(k), sh(v))
            q = l2norm(q) * qs
            k = l2norm(k) * ksc
            freqs, scale = rotary_tables(n)
            cos, sin = (jnp.cos(freqs), jnp.sin(freqs))
            q = q * cos * scale + rotate_half(q) * sin * scale
            inv = 1.0 / scale
            k = k * cos * inv + rotate_half(k) * sin * inv
            out = local_attention(q, k, v)
            out = out.transpose(0, 2, 1, 3).reshape(b, n, INNER)
            return out @ Wo

        def ffn_layer(x, g, bln, W1, b1, W2, b2):
            mu = x.mean(-1, keepdims=True)
            var = ((x - mu) ** 2).mean(-1, keepdims=True)
            xn = (x - mu) / jnp.sqrt(var + 1e-05) * g + bln
            hg = xn @ W1 + b1
            a, gate = jnp.split(hg, 2, -1)
            return a * jax.nn.gelu(gate, approximate=False) @ W2 + b2
        key = jax.random.key(seed)
        ks = jax.random.split(key, 8)
        B, N = (2, 256)
        init = lambda k, shape: jax.random.normal(k, shape, jnp.float32) * 0.02
        return {'x': jax.random.normal(ks[0], (B, N, DIM), jnp.float32), 'Wqkv': init(ks[1], (DEPTH, DIM, 3 * INNER)), 'q_scale': jnp.ones((DEPTH, DIM_HEAD), jnp.float32), 'k_scale': jnp.ones((DEPTH, DIM_HEAD), jnp.float32), 'Wo': init(ks[2], (DEPTH, INNER, DIM)), 'ln_g': jnp.ones((DEPTH, DIM), jnp.float32), 'ln_b': jnp.zeros((DEPTH, DIM), jnp.float32), 'W1': init(ks[3], (DEPTH, DIM, 2 * DIM_INNER)), 'b1': jnp.zeros((DEPTH, 2 * DIM_INNER), jnp.float32), 'W2': init(ks[4], (DEPTH, DIM_INNER, DIM)), 'b2': jnp.zeros((DEPTH, DIM), jnp.float32)}
    _L0_ffn_all = _L0_ffn_setup()
    _L0_ffn_in = {k: v for k, v in _L0_ffn_all.items() if k in ('Wqkv', 'q_scale', 'k_scale', 'Wo', 'ln_g', 'ln_b', 'W1', 'b1', 'W2', 'b2')}
    del _L0_ffn_all

    def _L1_xattn_setup():
        import jax, jax.numpy as jnp
        import numpy as np
        D_MODEL = 128
        N_HEADS = 16
        key = jax.random.key(seed)
        ks = jax.random.split(key, 11)
        B, L, S, D = (2, 256, 256, D_MODEL)
        s = 1.0 / np.sqrt(D)
        return {'Q': jax.random.normal(ks[0], (B, L, D), jnp.float32), 'K': jax.random.normal(ks[1], (B, S, D), jnp.float32), 'V': jax.random.normal(ks[2], (B, S, D), jnp.float32), 'Wq': jax.random.normal(ks[3], (D, D), jnp.float32) * s, 'bq': jnp.zeros((D,), jnp.float32), 'Wk': jax.random.normal(ks[4], (D, D), jnp.float32) * s, 'bk': jnp.zeros((D,), jnp.float32), 'Wv': jax.random.normal(ks[5], (D, D), jnp.float32) * s, 'bv': jnp.zeros((D,), jnp.float32), 'We': jax.random.normal(ks[6], (D, D), jnp.float32) * s, 'be': jnp.zeros((D,), jnp.float32)}
    _L1_xattn_all = _L1_xattn_setup()
    _L1_xattn_in = {k: v for k, v in _L1_xattn_all.items() if k in ('Wq', 'bq', 'Wk', 'bk', 'Wv', 'bv', 'We', 'be')}
    del _L1_xattn_all

    def _L1_ffn_setup():
        import jax, jax.numpy as jnp
        import numpy as np
        FEATURES = 128
        D_IN = 128

        def fp8_gemm_optimized(x, input_scale, kernel, kernel_scale):
            s_in = input_scale[0]
            s_k = kernel_scale[0]
            x_q = (x.astype(jnp.float32) / s_in).astype(jnp.float8_e4m3fn)
            k_q = (kernel.astype(jnp.float32) / s_k).astype(jnp.float8_e4m3fn)
            y = jnp.dot(x_q.astype(jnp.float32), k_q.astype(jnp.float32), preferred_element_type=jnp.float32)
            return y * (s_in * s_k)
        key = jax.random.key(seed)
        kx, kk, kb = jax.random.split(key, 3)
        x = jax.random.normal(kx, (4, 1024, D_IN), dtype=jnp.float32)
        limit = np.sqrt(6.0 / (D_IN + FEATURES)).astype(np.float32)
        kernel = jax.random.uniform(kk, (D_IN, FEATURES), dtype=jnp.float32, minval=-limit, maxval=limit).astype(jnp.bfloat16)
        input_scale = jnp.ones((1,), dtype=jnp.float32)
        kernel_scale = jnp.ones((1,), dtype=jnp.float32)
        bias = jnp.zeros((FEATURES,), dtype=jnp.bfloat16)
        return {'x': x, 'kernel': kernel, 'input_scale': input_scale, 'kernel_scale': kernel_scale, 'bias': bias}
    _L1_ffn_all = _L1_ffn_setup()
    _L1_ffn_in = {k: v for k, v in _L1_ffn_all.items() if k in ('kernel', 'input_scale', 'kernel_scale', 'bias')}
    del _L1_ffn_all

    def _L2_xattn_setup():
        import jax, jax.numpy as jnp
        import numpy as np
        EMB = 128
        NH = 16
        HD = EMB // NH
        key = jax.random.key(seed)
        ks = jax.random.split(key, 11)
        B, S = (4, 256)
        s_in = 1.0 / np.sqrt(EMB)
        return {'q': jax.random.normal(ks[0], (B, S, EMB), jnp.float32), 'k': jax.random.normal(ks[1], (B, S, EMB), jnp.float32), 'v': jax.random.normal(ks[2], (B, S, EMB), jnp.float32), 'Wq': jax.random.normal(ks[3], (EMB, NH * HD), jnp.float32) * s_in, 'bq': jnp.zeros((NH * HD,), jnp.float32), 'Wk': jax.random.normal(ks[4], (EMB, HD), jnp.float32) * s_in, 'bk': jnp.zeros((HD,), jnp.float32), 'Wv': jax.random.normal(ks[5], (EMB, HD), jnp.float32) * s_in, 'bv': jnp.zeros((HD,), jnp.float32), 'Wo': jax.random.normal(ks[6], (NH * HD, EMB), jnp.float32) * s_in, 'bo': jnp.zeros((EMB,), jnp.float32)}
    _L2_xattn_all = _L2_xattn_setup()
    _L2_xattn_in = {k: v for k, v in _L2_xattn_all.items() if k in ('Wq', 'bq', 'Wk', 'bk', 'Wv', 'bv', 'Wo', 'bo')}
    del _L2_xattn_all

    def _L2_ffn_setup():
        import jax, jax.numpy as jnp
        import numpy as np
        B, T, D, DFF, E = (4, 256, 128, 512, 8)
        key = jax.random.key(seed)
        ks = jax.random.split(key, 4)
        s_in = 1.0 / np.sqrt(D)
        s_ff = 1.0 / np.sqrt(DFF)
        return {'x': jax.random.normal(ks[0], (B, T, D), dtype=jnp.float32), 'gate_W': jax.random.normal(ks[1], (D, E), dtype=jnp.float32) * s_in, 'gate_b': jnp.zeros((E,), dtype=jnp.float32), 'W1': jax.random.normal(ks[2], (E, D, DFF), dtype=jnp.float32) * s_in, 'b1': jnp.zeros((E, DFF), dtype=jnp.float32), 'W2': jax.random.normal(ks[3], (E, DFF, D), dtype=jnp.float32) * s_ff, 'b2': jnp.zeros((E, D), dtype=jnp.float32)}
    _L2_ffn_all = _L2_ffn_setup()
    _L2_ffn_in = {k: v for k, v in _L2_ffn_all.items() if k in ('gate_W', 'gate_b', 'W1', 'b1', 'W2', 'b2')}
    del _L2_ffn_all

    def _L3_xattn_setup():
        import jax, jax.numpy as jnp
        import numpy as np
        import math
        B, M, D, H, NK = (4, 256, 128, 16, 5)
        HD = D // H

        def _gather_pad0(x, idx):
            Bx, Hx, W, hd = x.shape
            valid = (idx >= 0) & (idx < W)
            idxc = jnp.clip(idx, 0, W - 1).reshape(Bx, Hx, -1)
            g = jnp.take_along_axis(x, idxc[..., None], axis=2)
            g = g.reshape(idx.shape + (hd,))
            return g * valid[..., None].astype(x.dtype)
        key = jax.random.key(seed)
        ks = jax.random.split(key, 9)
        w = lambda k, shape: jax.random.normal(k, shape, jnp.float32) * 0.02
        return {'k': jax.random.normal(ks[0], (B, M, D), jnp.float32), 'v': jax.random.normal(ks[1], (B, M, D), jnp.float32), 'q': jax.random.normal(ks[2], (B, M, D), jnp.float32), 'mask': jnp.zeros((B, M), jnp.int32), 'Wk': w(ks[3], (D, D)), 'bk': jnp.zeros((D,), jnp.float32), 'Wv': w(ks[4], (D, D)), 'bv': jnp.zeros((D,), jnp.float32), 'Wq': w(ks[5], (D, D)), 'bq': jnp.zeros((D,), jnp.float32), 'Woff': w(ks[6], (H * NK, D)), 'boff': jnp.zeros((H * NK,), jnp.float32), 'Wo': w(ks[7], (D, D)), 'bo': jnp.zeros((D,), jnp.float32)}
    _L3_xattn_all = _L3_xattn_setup()
    _L3_xattn_in = {k: v for k, v in _L3_xattn_all.items() if k in ('Wk', 'bk', 'Wv', 'bv', 'Wq', 'bq', 'Woff', 'boff', 'Wo', 'bo')}
    del _L3_xattn_all

    def _L3_ffn_setup():
        import jax, jax.numpy as jnp
        import numpy as np
        TOP_K = 2
        key = jax.random.key(seed)
        ks = jax.random.split(key, 6)
        B, S, D, BN, E = (32, 256, 128, 64, 8)
        return {'x': jax.random.normal(ks[0], (B, S, D), dtype=jnp.float32), 'gate_w': jax.random.normal(ks[1], (E, D), dtype=jnp.float32) * 0.02, 'down_w': jax.random.normal(ks[2], (E, BN, D), dtype=jnp.float32) * 0.02, 'down_b': jax.random.normal(ks[3], (E, BN), dtype=jnp.float32) * 0.02, 'up_w': jax.random.normal(ks[4], (E, D, BN), dtype=jnp.float32) * 0.02, 'up_b': jax.random.normal(ks[5], (E, D), dtype=jnp.float32) * 0.02}
    _L3_ffn_all = _L3_ffn_setup()
    _L3_ffn_in = {k: v for k, v in _L3_ffn_all.items() if k in ('gate_w', 'down_w', 'down_b', 'up_w', 'up_b')}
    del _L3_ffn_all
    return {'x': x, 'ctx_1024': ctx_1024, 'mask_BxS_ff1': mask_BxS_ff1, 'mask_BxS2_ik0': mask_BxS2_ik0, 'mask_BxS2_if0': mask_BxS2_if0, 'L0_xattn_Ws': _L0_xattn_in['Ws'], 'L0_xattn_W': _L0_xattn_in['W'], 'L0_xattn_w': _L0_xattn_in['w'], 'L0_xattn_b': _L0_xattn_in['b'], 'L0_xattn_Wcw': _L0_xattn_in['Wcw'], 'L0_xattn_bcw': _L0_xattn_in['bcw'], 'L0_xattn_Wcb': _L0_xattn_in['Wcb'], 'L0_xattn_bcb': _L0_xattn_in['bcb'], 'L0_ffn_Wqkv': _L0_ffn_in['Wqkv'], 'L0_ffn_q_scale': _L0_ffn_in['q_scale'], 'L0_ffn_k_scale': _L0_ffn_in['k_scale'], 'L0_ffn_Wo': _L0_ffn_in['Wo'], 'L0_ffn_ln_g': _L0_ffn_in['ln_g'], 'L0_ffn_ln_b': _L0_ffn_in['ln_b'], 'L0_ffn_W1': _L0_ffn_in['W1'], 'L0_ffn_b1': _L0_ffn_in['b1'], 'L0_ffn_W2': _L0_ffn_in['W2'], 'L0_ffn_b2': _L0_ffn_in['b2'], 'L1_xattn_Wq': _L1_xattn_in['Wq'], 'L1_xattn_bq': _L1_xattn_in['bq'], 'L1_xattn_Wk': _L1_xattn_in['Wk'], 'L1_xattn_bk': _L1_xattn_in['bk'], 'L1_xattn_Wv': _L1_xattn_in['Wv'], 'L1_xattn_bv': _L1_xattn_in['bv'], 'L1_xattn_We': _L1_xattn_in['We'], 'L1_xattn_be': _L1_xattn_in['be'], 'L1_ffn_kernel': _L1_ffn_in['kernel'], 'L1_ffn_input_scale': _L1_ffn_in['input_scale'], 'L1_ffn_kernel_scale': _L1_ffn_in['kernel_scale'], 'L1_ffn_bias': _L1_ffn_in['bias'], 'L2_xattn_Wq': _L2_xattn_in['Wq'], 'L2_xattn_bq': _L2_xattn_in['bq'], 'L2_xattn_Wk': _L2_xattn_in['Wk'], 'L2_xattn_bk': _L2_xattn_in['bk'], 'L2_xattn_Wv': _L2_xattn_in['Wv'], 'L2_xattn_bv': _L2_xattn_in['bv'], 'L2_xattn_Wo': _L2_xattn_in['Wo'], 'L2_xattn_bo': _L2_xattn_in['bo'], 'L2_ffn_gate_W': _L2_ffn_in['gate_W'], 'L2_ffn_gate_b': _L2_ffn_in['gate_b'], 'L2_ffn_W1': _L2_ffn_in['W1'], 'L2_ffn_b1': _L2_ffn_in['b1'], 'L2_ffn_W2': _L2_ffn_in['W2'], 'L2_ffn_b2': _L2_ffn_in['b2'], 'L3_xattn_Wk': _L3_xattn_in['Wk'], 'L3_xattn_bk': _L3_xattn_in['bk'], 'L3_xattn_Wv': _L3_xattn_in['Wv'], 'L3_xattn_bv': _L3_xattn_in['bv'], 'L3_xattn_Wq': _L3_xattn_in['Wq'], 'L3_xattn_bq': _L3_xattn_in['bq'], 'L3_xattn_Woff': _L3_xattn_in['Woff'], 'L3_xattn_boff': _L3_xattn_in['boff'], 'L3_xattn_Wo': _L3_xattn_in['Wo'], 'L3_xattn_bo': _L3_xattn_in['bo'], 'L3_ffn_gate_w': _L3_ffn_in['gate_w'], 'L3_ffn_down_w': _L3_ffn_in['down_w'], 'L3_ffn_down_b': _L3_ffn_in['down_b'], 'L3_ffn_up_w': _L3_ffn_in['up_w'], 'L3_ffn_up_b': _L3_ffn_in['up_b']}

def reference(x, ctx_1024, mask_BxS_ff1, mask_BxS2_ik0, mask_BxS2_if0, L0_xattn_Ws, L0_xattn_W, L0_xattn_w, L0_xattn_b, L0_xattn_Wcw, L0_xattn_bcw, L0_xattn_Wcb, L0_xattn_bcb, L0_ffn_Wqkv, L0_ffn_q_scale, L0_ffn_k_scale, L0_ffn_Wo, L0_ffn_ln_g, L0_ffn_ln_b, L0_ffn_W1, L0_ffn_b1, L0_ffn_W2, L0_ffn_b2, L1_xattn_Wq, L1_xattn_bq, L1_xattn_Wk, L1_xattn_bk, L1_xattn_Wv, L1_xattn_bv, L1_xattn_We, L1_xattn_be, L1_ffn_kernel, L1_ffn_input_scale, L1_ffn_kernel_scale, L1_ffn_bias, L2_xattn_Wq, L2_xattn_bq, L2_xattn_Wk, L2_xattn_bk, L2_xattn_Wv, L2_xattn_bv, L2_xattn_Wo, L2_xattn_bo, L2_ffn_gate_W, L2_ffn_gate_b, L2_ffn_W1, L2_ffn_b1, L2_ffn_W2, L2_ffn_b2, L3_xattn_Wk, L3_xattn_bk, L3_xattn_Wv, L3_xattn_bv, L3_xattn_Wq, L3_xattn_bq, L3_xattn_Woff, L3_xattn_boff, L3_xattn_Wo, L3_xattn_bo, L3_ffn_gate_w, L3_ffn_down_w, L3_ffn_down_b, L3_ffn_up_w, L3_ffn_up_b):
    import jax
    import jax.numpy as jnp

    def _L0_xattn_ref(features, masks, textual_features, q_masks, Ws, W, w, b, Wcw, bcw, Wcb, bcb):
        import jax, jax.numpy as jnp
        import numpy as np
        B, F, T, D = (8, 32, 32, 128)
        NEG = -1e+30
        txt_proj = jnp.einsum('btd,de->bte', textual_features, Ws)
        feat_proj = jnp.einsum('bfd,de->bfe', features, W)
        h = jnp.tanh(txt_proj[:, None, :, :] + feat_proj[:, :, None, :] + b[None, None, :, :][..., 0, :])
        rho = jnp.einsum('bftd,d->bft', h, w[:, 0])
        qm = q_masks.astype(jnp.float32)
        rho = rho + (1.0 - qm)[:, None, :] * NEG
        att = jax.nn.softmax(rho, axis=-1)
        txt_h = jnp.einsum('bft,btd->bfd', att, textual_features)
        w_s = jnp.tanh(jnp.einsum('bfd,od->bfo', txt_h, Wcw) + bcw)
        b_s = jnp.tanh(jnp.einsum('bfd,od->bfo', txt_h, Wcb) + bcb)
        return w_s * features + b_s

    def _L0_ffn_ref(x, Wqkv, q_scale, k_scale, Wo, ln_g, ln_b, W1, b1, W2, b2):
        import jax, jax.numpy as jnp
        import numpy as np
        DIM = 128
        DEPTH = 6
        HEADS = 16
        DIM_HEAD = 64
        WINDOW = 32
        INNER = HEADS * DIM_HEAD
        DIM_INNER = int(DIM * 4 * 2 / 3)
        QK_SCALE = 8.0

        def shift_tokens(t):
            a, s = jnp.split(t, 2, -1)
            s = jnp.pad(s, ((0, 0), (1, 0), (0, 0)))[:, :-1]
            return jnp.concatenate([a, s], -1)

        def l2norm(t):
            return t / jnp.maximum(jnp.linalg.norm(t, axis=-1, keepdims=True), 1e-12)

        def rotate_half(x):
            x1, x2 = jnp.split(x, 2, -1)
            return jnp.concatenate([-x2, x1], -1)

        def rotary_tables(n):
            half = jnp.arange(0, DIM_HEAD, 2, dtype=jnp.float32)
            inv_freq = 1.0 / 10000.0 ** (half / DIM_HEAD)
            t = jnp.arange(n, dtype=jnp.float32)
            freqs = t[:, None] * inv_freq[None, :]
            freqs = jnp.concatenate([freqs, freqs], -1)
            base_scale = (half + 0.4 * DIM_HEAD) / (1.4 * DIM_HEAD)
            power = (t - n // 2) / (WINDOW // 2)
            scale = base_scale[None, :] ** power[:, None]
            scale = jnp.concatenate([scale, scale], -1)
            return (freqs, scale)

        def local_attention(q, k, v):
            b, h, n, d = q.shape
            w = WINDOW
            nw = n // w
            bq = q.reshape(b, h, nw, w, d)
            bk = k.reshape(b, h, nw, w, d)
            bv = v.reshape(b, h, nw, w, d)

            def look(t):
                p = jnp.pad(t, ((0, 0), (0, 0), (1, 0), (0, 0), (0, 0)))
                return jnp.concatenate([p[:, :, :nw], p[:, :, 1:]], axis=3)
            bk2, bv2 = (look(bk), look(bv))
            seq = jnp.arange(n).reshape(nw, w)
            seq_p = jnp.pad(seq, ((1, 0), (0, 0)), constant_values=-1)
            jt = jnp.concatenate([seq_p[:nw], seq_p[1:]], axis=1)
            it = seq[:, :, None]
            jb = jt[:, None, :]
            mask = (it < jb) | (it > jb + w) | (jb == -1)
            sim = jnp.einsum('bhwie,bhwje->bhwij', bq, bk2) * QK_SCALE
            sim = jnp.where(mask, -jnp.finfo(sim.dtype).max, sim)
            attn = jax.nn.softmax(sim, -1)
            out = jnp.einsum('bhwij,bhwje->bhwie', attn, bv2)
            return out.reshape(b, h, n, d)

        def attn_layer(x, Wqkv, qs, ksc, Wo):
            b, n, _ = x.shape
            qkv = x @ Wqkv
            q, k, v = jnp.split(qkv, 3, -1)
            sh = lambda t: t.reshape(b, n, HEADS, DIM_HEAD).transpose(0, 2, 1, 3)
            q, k, v = (sh(q), sh(k), sh(v))
            q = l2norm(q) * qs
            k = l2norm(k) * ksc
            freqs, scale = rotary_tables(n)
            cos, sin = (jnp.cos(freqs), jnp.sin(freqs))
            q = q * cos * scale + rotate_half(q) * sin * scale
            inv = 1.0 / scale
            k = k * cos * inv + rotate_half(k) * sin * inv
            out = local_attention(q, k, v)
            out = out.transpose(0, 2, 1, 3).reshape(b, n, INNER)
            return out @ Wo

        def ffn_layer(x, g, bln, W1, b1, W2, b2):
            mu = x.mean(-1, keepdims=True)
            var = ((x - mu) ** 2).mean(-1, keepdims=True)
            xn = (x - mu) / jnp.sqrt(var + 1e-05) * g + bln
            hg = xn @ W1 + b1
            a, gate = jnp.split(hg, 2, -1)
            return a * jax.nn.gelu(gate, approximate=False) @ W2 + b2
        for i in range(DEPTH):
            x = attn_layer(shift_tokens(x), Wqkv[i], q_scale[i], k_scale[i], Wo[i]) + x
            x = ffn_layer(shift_tokens(x), ln_g[i], ln_b[i], W1[i], b1[i], W2[i], b2[i]) + x
        return x

    def _L1_xattn_ref(Q, K, V, Wq, bq, Wk, bk, Wv, bv, We, be):
        import jax, jax.numpy as jnp
        import numpy as np
        D_MODEL = 128
        N_HEADS = 16
        B, L, D = Q.shape
        S = K.shape[1]
        H = N_HEADS
        E = D // H
        q = (Q @ Wq + bq).reshape(B, L, H, E)
        k = (K @ Wk + bk).reshape(B, S, H, E)
        v = (V @ Wv + bv).reshape(B, S, H, E)
        scale = 1.0 / np.sqrt(E)
        scores = jnp.einsum('blhe,bshe->bhls', q, k)
        A = jax.nn.softmax(scale * scores, axis=-1)
        out = jnp.einsum('bhls,bshd->blhd', A, v).reshape(B, L, H * E)
        return out @ We + be

    def _L1_ffn_ref(x, kernel, input_scale, kernel_scale, bias):
        import jax, jax.numpy as jnp
        import numpy as np
        FEATURES = 128
        D_IN = 128

        def fp8_gemm_optimized(x, input_scale, kernel, kernel_scale):
            s_in = input_scale[0]
            s_k = kernel_scale[0]
            x_q = (x.astype(jnp.float32) / s_in).astype(jnp.float8_e4m3fn)
            k_q = (kernel.astype(jnp.float32) / s_k).astype(jnp.float8_e4m3fn)
            y = jnp.dot(x_q.astype(jnp.float32), k_q.astype(jnp.float32), preferred_element_type=jnp.float32)
            return y * (s_in * s_k)
        dtype = jnp.bfloat16
        x = x.astype(dtype)
        orig_shape = x.shape
        x2 = x.reshape(-1, x.shape[-1])
        y = fp8_gemm_optimized(x2, input_scale, kernel, kernel_scale)
        y = y.astype(dtype) + bias
        return y.reshape(orig_shape[:-1] + (FEATURES,))

    def _L2_xattn_ref(q, k, v, Wq, bq, Wk, bk, Wv, bv, Wo, bo):
        import jax, jax.numpy as jnp
        import numpy as np
        EMB = 128
        NH = 16
        HD = EMB // NH
        B, S, _ = q.shape
        scale = HD ** (-0.5)
        Q = (q @ Wq + bq).reshape(B, S, NH, HD).transpose(0, 2, 1, 3)
        K = k @ Wk + bk
        V = v @ Wv + bv
        scores = jnp.einsum('bhqd,bkd->bhqk', Q, K) * scale
        attn = jax.nn.softmax(scores, axis=-1)
        out = jnp.einsum('bhqk,bkd->bhqd', attn, V)
        out = out.transpose(0, 2, 1, 3).reshape(B, S, NH * HD)
        return out @ Wo + bo

    def _L2_ffn_ref(x, gate_W, gate_b, W1, b1, W2, b2):
        import jax, jax.numpy as jnp
        import numpy as np
        B, T, D, DFF, E = (4, 256, 128, 512, 8)
        b, t, d = x.shape
        num_experts = gate_W.shape[-1]
        logits = jnp.einsum('btd,de->bte', x, gate_W) + gate_b
        top1 = jnp.argmax(logits, axis=-1).reshape(-1)
        flat_x = x.reshape(b * t, d)
        out = jnp.zeros_like(flat_x)
        for e in range(num_experts):
            mask = (top1 == e).astype(x.dtype)[:, None]
            h = jax.nn.gelu(flat_x * mask @ W1[e] + b1[e], approximate=False)
            out = out + (h @ W2[e] + b2[e]) * mask
        return out.reshape(b, t, d)

    def _L3_xattn_ref(k, v, q, mask, Wk, bk, Wv, bv, Wq, bq, Woff, boff, Wo, bo):
        import jax, jax.numpy as jnp
        import numpy as np
        import math
        B, M, D, H, NK = (4, 256, 128, 16, 5)
        HD = D // H

        def _gather_pad0(x, idx):
            Bx, Hx, W, hd = x.shape
            valid = (idx >= 0) & (idx < W)
            idxc = jnp.clip(idx, 0, W - 1).reshape(Bx, Hx, -1)
            g = jnp.take_along_axis(x, idxc[..., None], axis=2)
            g = g.reshape(idx.shape + (hd,))
            return g * valid[..., None].astype(x.dtype)
        Bq, Q, _ = q.shape
        key_len = k.shape[1]
        K = jnp.einsum('bmd,ed->bme', k, Wk) + bk
        V = jnp.einsum('bmd,ed->bme', v, Wv) + bv
        Qp = jnp.einsum('bqd,ed->bqe', q, Wq) + bq
        off = jnp.einsum('bqd,ed->bqe', Qp, Woff) + boff
        off = off.reshape(Bq, Q, H, NK).transpose(0, 2, 1, 3)
        Kh = K.reshape(Bq, key_len, H, HD).transpose(0, 2, 1, 3)
        Vh = V.reshape(Bq, key_len, H, HD).transpose(0, 2, 1, 3)
        Qh = Qp.reshape(Bq, Q, H, HD).transpose(0, 2, 1, 3)
        loc = jnp.arange(Q, dtype=jnp.float32)[:, None]
        left = -NK // 2
        ref = jnp.arange(left, NK + left, dtype=jnp.float32)
        sign_lens = (1 - mask).sum(-1).astype(jnp.float32) - 1.0
        loc_x = jnp.mod(ref + off + loc, sign_lens[:, None, None, None])
        xg = loc_x / (key_len - 1) * 2.0 - 1.0
        ix = ((xg + 1.0) * key_len - 1.0) / 2.0
        x0 = jnp.floor(ix)
        dx = ix - x0
        i0 = x0.astype(jnp.int32)
        i1 = i0 + 1
        w0 = (1.0 - dx)[..., None]
        w1 = dx[..., None]
        sk = 0.5 * (w0 * _gather_pad0(Kh, i0) + w1 * _gather_pad0(Kh, i1))
        sv = 0.5 * (w0 * _gather_pad0(Vh, i0) + w1 * _gather_pad0(Vh, i1))
        scores = jnp.einsum('bhqd,bhqkd->bhqk', Qh / math.sqrt(HD), sk)
        attn = jax.nn.softmax(scores, axis=-1)
        ctx = jnp.einsum('bhqk,bhqkd->bhqd', attn, sv)
        ctx = ctx.transpose(0, 2, 1, 3).reshape(Bq, Q, H * HD)
        return jnp.einsum('bqd,ed->bqe', ctx, Wo) + bo

    def _L3_ffn_ref(x, gate_w, down_w, down_b, up_w, up_b):
        import jax, jax.numpy as jnp
        import numpy as np
        TOP_K = 2
        pooled = x.mean(axis=1)
        gate = jax.nn.softmax(pooled @ gate_w.T, axis=-1)
        top_w, top_i = jax.lax.top_k(gate, TOP_K)
        top_w = top_w / (top_w.sum(axis=-1, keepdims=True) + 1e-08)
        Wd = down_w[top_i]
        bd = down_b[top_i]
        Wu = up_w[top_i]
        bu = up_b[top_i]
        h = jax.nn.gelu(jnp.einsum('bsd,bkcd->bksc', x, Wd) + bd[:, :, None, :], approximate=False)
        h = h * top_w[:, :, None, None]
        out = jnp.einsum('bksc,bkdc->bsd', h, Wu)
        out = out + (top_w[:, :, None] * bu).sum(axis=1)[:, None, :]
        return out
    x = x + _L0_xattn_ref(_layernorm(x, axis=-1), mask_BxS_ff1, ctx_1024, mask_BxS2_ik0, L0_xattn_Ws, L0_xattn_W, L0_xattn_w, L0_xattn_b, L0_xattn_Wcw, L0_xattn_bcw, L0_xattn_Wcb, L0_xattn_bcb)
    x = x + _L0_ffn_ref(_layernorm(x, axis=-1), L0_ffn_Wqkv, L0_ffn_q_scale, L0_ffn_k_scale, L0_ffn_Wo, L0_ffn_ln_g, L0_ffn_ln_b, L0_ffn_W1, L0_ffn_b1, L0_ffn_W2, L0_ffn_b2)
    x = x + _L1_xattn_ref(_layernorm(x, axis=-1), ctx_1024, ctx_1024, L1_xattn_Wq, L1_xattn_bq, L1_xattn_Wk, L1_xattn_bk, L1_xattn_Wv, L1_xattn_bv, L1_xattn_We, L1_xattn_be)
    x = x + _L1_ffn_ref(_layernorm(x, axis=-1), L1_ffn_kernel, L1_ffn_input_scale, L1_ffn_kernel_scale, L1_ffn_bias)
    x = x + _L2_xattn_ref(_layernorm(x, axis=-1), ctx_1024, ctx_1024, L2_xattn_Wq, L2_xattn_bq, L2_xattn_Wk, L2_xattn_bk, L2_xattn_Wv, L2_xattn_bv, L2_xattn_Wo, L2_xattn_bo)
    x = x + _L2_ffn_ref(_layernorm(x, axis=-1), L2_ffn_gate_W, L2_ffn_gate_b, L2_ffn_W1, L2_ffn_b1, L2_ffn_W2, L2_ffn_b2)
    x = x + _L3_xattn_ref(ctx_1024, ctx_1024, _layernorm(x, axis=-1), mask_BxS2_if0, L3_xattn_Wk, L3_xattn_bk, L3_xattn_Wv, L3_xattn_bv, L3_xattn_Wq, L3_xattn_bq, L3_xattn_Woff, L3_xattn_boff, L3_xattn_Wo, L3_xattn_bo)
    x = x + _L3_ffn_ref(_layernorm(x, axis=-1), L3_ffn_gate_w, L3_ffn_down_w, L3_ffn_down_b, L3_ffn_up_w, L3_ffn_up_b)
    return x

_drawn_inputs = setup_inputs


def setup_inputs(seed=0):
    import zlib

    import numpy as np

    out = dict(_drawn_inputs(seed))
    spreads = {'L0_ffn_q_scale': (1.0, 0.2),
     'L0_ffn_k_scale': (1.0, 0.2),
     'L0_ffn_ln_g': (1.0, 0.2),
     'L0_ffn_ln_b': (0.0, 0.331),
     'L0_ffn_b1': (0.0, 0.1),
     'L0_ffn_b2': (0.0, 0.1),
     'L1_xattn_bq': (0.0, 0.1),
     'L1_xattn_bk': (0.0, 0.8),
     'L1_xattn_bv': (0.0, 0.1),
     'L1_xattn_be': (0.0, 0.1),
     'L1_ffn_bias': (0.0, 0.1),
     'L2_xattn_bq': (0.0, 0.1),
     'L2_xattn_bk': (0.0, 0.8),
     'L2_xattn_bv': (0.0, 0.1),
     'L2_xattn_bo': (0.0, 0.1),
     'L2_ffn_gate_b': (0.0, 0.1),
     'L2_ffn_b1': (0.0, 0.311),
     'L2_ffn_b2': (0.0, 0.1),
     'L3_xattn_bk': (0.0, 0.8),
     'L3_xattn_bv': (0.0, 0.8),
     'L3_xattn_bq': (0.0, 0.8),
     'L3_xattn_boff': (0.0, 0.8),
     'L3_xattn_bo': (0.0, 0.1)}
    factors = {'L0_xattn_b': 3.927,
     'L3_xattn_Wk': 8.0,
     'L3_xattn_Wv': 8.0,
     'L3_xattn_Wq': 8.0,
     'L3_xattn_Woff': 8.0,
     'L3_xattn_Wo': 7.496,
     'L3_ffn_gate_w': 7.862,
     'L3_ffn_down_w': 8.0,
     'L3_ffn_down_b': 8.0,
     'L3_ffn_up_w': 8.0,
     'L3_ffn_up_b': 8.0}
    for name, (base, spread) in spreads.items():
        noise = np.random.default_rng([zlib.crc32(name.encode()), seed]).standard_normal(out[name].shape)
        drawn = base * np.exp(spread * noise) if base else spread * noise
        out[name] = jnp.asarray(drawn.astype(out[name].dtype))
    for name, factor in factors.items():
        out[name] = (out[name] * factor).astype(out[name].dtype)
    return out
```

```python
from contextlib import ExitStack

import concourse.bass as bass
from concourse import mybir

ALU = mybir.AluOpType
ACT = mybir.ActivationFunctionType
AX = mybir.AxisListType
F32 = mybir.dt.float32
BF16 = mybir.dt.bfloat16
FP8 = mybir.dt.float8e4
I32 = mybir.dt.int32

B, S, D, S2 = 32, 128, 128, 77
LANES = 4
ITERS = B // LANES
WIDE = 2
GB = 4
ROUNDS = B // GB // WIDE
DEPTH, HEADS, DH = 6, 16, 64
INNER = HEADS * DH
HG = 8
WINDOW = 32
FF = int(D * 4 * 2 / 3)
FFC = [(0, 128), (128, 128), (256, FF - 256)]
XH, XD = 16, 8
NK = 5
DFF, E = 512, 8
BN = 64
NEG = -1e30
EPS = 1e-5
MAGIC = 1.5 * 2.0 ** 23
PHASES = (1, 2, 3, 4, 5, 6, 7, 8)


class Buffers:

    def __init__(self, nc, ctx, phase):
        self.nc, self.ctx, self.phase, self.held = nc, ctx, phase, []
        ctx.callback(self.free_sems)

    def free_sems(self):
        if self.held:
            self.nc.all_engine_barrier()
            self.nc.clear_and_free_semaphores(self.held)
            self.nc.all_engine_barrier()

    def sb(self, name, shape, dt=F32):
        return self.ctx.enter_context(self.nc.sbuf_tensor(f"{self.phase}_{name}", list(shape), dt))

    def lanes(self, name, shape, dt=F32, n=LANES):
        return [self.sb(f"{name}{i}", shape, dt) for i in range(n)]

    def sem(self, name):
        self.held.append(self.nc.alloc_semaphore(f"{self.phase}_{name}"))
        return self.held[-1]

    def sems(self, name, n=LANES):
        return [self.sem(f"{name}{i}") for i in range(n)]


def bc(ap, axis, n):
    shape = list(ap.shape)
    shape.insert(axis, n)
    return ap.unsqueeze(axis).to_broadcast(shape)


def cols(t, b, n=1):
    return t[:, bass.ds(b, n), :].rearrange("p b d -> p (b d)")


def setup_phase(nc, a, k, ps):
    with ExitStack() as ctx:
        m = Buffers(nc, ctx, "setup")
        s_load, s_zero, s_shape, s_x = m.sem("loaded"), m.sem("zeroed"), m.sem("shaped"), m.sem("x_loaded")
        s_turn, s_evac, s_int, s_col = m.sem("turned"), m.sem("turn_copied"), m.sem("mask_float"), m.sem("wide_column")
        raw = {n: m.sb(f"raw_{n}", [128, 128]) for n in ("Wk", "Wv", "Wq", "Wo", "Woff", "gate")}
        raw_b1 = m.sb("raw_b1", [E * DFF // 128, 128])
        raw_down = m.sb("raw_down", [128, 4, 128])
        raw_up = m.sb("raw_up", [128, E, BN])
        qmask = m.sb("qmask", [128, B * S2], I32)
        fmask = m.sb("fmask", [128, B * S2], I32)
        fmaskf = m.sb("fmaskf", [128, B, S2])
        iota_i = m.sb("iota_i", [128, S2], I32)
        pos_i = m.sb("pos_i", [128, 1], I32)
        col = m.sb("col", [128, 3])
        turns = [(raw[n][:, :], k[f"T_{n}"][:, :], 128) for n in ("Wk", "Wv", "Wq", "Wo")]
        turns += [(raw["Woff"][0:XH * NK, :], k["T_Woff"][:, :], XH * NK), (raw["gate"][0:E, :], k["T_gate"][:, :], E)]
        turns.append((raw_b1[:, :], k["T_b1"][:, :], E * DFF // 128))
        turns += [(raw_down[:, c, :], k["T_down"][:, c, :], 128) for c in range(4)]
        turns += [(raw_up[:, 2 * c:2 * c + 2, :].rearrange("p e n -> p (e n)"), k["T_up"][:, c, :], 128) for c in range(4)]

        loads = [(k["x"][:, :, :], a["x"].rearrange("b s d -> s b d"))]
        for n in ("Wk", "Wv", "Wq", "Wo"):
            loads.append((raw[n][:, :], a[f"L3_xattn_{n}"]))
        loads.append((raw["Woff"][0:XH * NK, :], a["L3_xattn_Woff"]))
        loads.append((raw["gate"][0:E, :], a["L3_ffn_gate_w"]))
        loads.append((raw_b1[:, :], a["L2_ffn_b1"].rearrange("e (c n) -> (e c) n", n=128)))
        loads.append((k["gateW"][:, :], a["L2_ffn_gate_W"]))
        loads.append((raw_down[:, :, :], a["L3_ffn_down_w"].rearrange("(c e) n d -> (e n) c d", c=4)))
        loads.append((raw_up[:, :, :], a["L3_ffn_up_w"].rearrange("e d n -> d e n")))
        loads.append((qmask[:, :], a["mask_BxS2_ik0"].rearrange("b s -> (b s)").partition_broadcast(128)))
        loads.append((fmask[:, :], a["mask_BxS2_if0"].rearrange("b s -> (b s)").partition_broadcast(128)))
        loads += [(col[:, 0:1], a["L0_xattn_w"]),
                  (col[:, 1:2], a["L0_xattn_Wcw"].rearrange("o d -> d o")),
                  (col[:, 2:3], a["L0_xattn_Wcb"].rearrange("o d -> d o"))]
        for n, src in (("L0_W", "L0_xattn_W"), ("L0_Ws", "L0_xattn_Ws"), ("L1_Wq", "L1_xattn_Wq"), ("L1_Wk", "L1_xattn_Wk"),
                       ("L1_Wv", "L1_xattn_Wv"), ("L1_We", "L1_xattn_We"), ("L2_Wq", "L2_xattn_Wq"), ("L2_Wo", "L2_xattn_Wo")):
            loads.append((k[n][:, :], a[src]))
        for n in ("Wk", "Wv"):
            for h in range(XH):
                loads.append((k[f"L2_{n}"][:, h * XD:(h + 1) * XD], a[f"L2_xattn_{n}"]))
        for h in range(XH):
            loads.append((k["c_L2_bk"][h * XD:(h + 1) * XD, :], a["L2_xattn_bk"].rearrange("(d o) -> d o", o=1)))
            loads.append((k["r_L2_bv"][:, h * XD:(h + 1) * XD], a["L2_xattn_bv"].partition_broadcast(128)))
        for n, src in (("c_L1_bq", "L1_xattn_bq"), ("c_L1_bk", "L1_xattn_bk"), ("c_L2_bq", "L2_xattn_bq"),
                       ("c_L3_bq", "L3_xattn_bq"), ("c_L3_bk", "L3_xattn_bk")):
            loads.append((k[n][:, :], a[src].rearrange("(d o) -> d o", o=1)))
        loads.append((k["c_L0_b"][:, :], a["L0_xattn_b"].rearrange("o d -> d o")))
        for n, src in (("r_L1_bv", "L1_xattn_bv"), ("r_L1_bo", "L1_xattn_be"), ("r_L2_bo", "L2_xattn_bo"),
                       ("r_L3_bv", "L3_xattn_bv"), ("r_L3_bo", "L3_xattn_bo"), ("r_L3_boff", "L3_xattn_boff"),
                       ("r_bcw", "L0_xattn_bcw"), ("r_bcb", "L0_xattn_bcb"), ("r_gateb", "L2_ffn_gate_b"),
                       ("r_sin", "L1_ffn_input_scale"), ("r_sk", "L1_ffn_kernel_scale"), ("r_fbias", "L1_ffn_bias")):
            loads.append((k[n][:, :], a[src].partition_broadcast(128)))
        loads.append((k["fkernel"][:, :], a["L1_ffn_kernel"]))
        loads.append((k["cosS"][:, :, :], a["rope_cos"]))
        loads.append((k["sinS"][:, :, :], a["rope_sin"]))
        for c in range(4):
            loads.append((k["c_down_b"][:, c:c + 1], a["L3_ffn_down_b"][2 * c:2 * c + 2, :].rearrange("e (n o) -> (e n) o", o=1)))

        with nc.Block() as block:
            @block.sync
            def _(sp):
                sp.wait_ge(s_zero, 16)
                for b in range(GB):
                    sp.dma_start(k["up_b"][E * b:E * b + E, b, :], a["L3_ffn_up_b"]).then_inc(s_load, 16)
                    sp.dma_start(k["b2blk"][32 * b:32 * b + E, b, :], a["L2_ffn_b2"]).then_inc(s_load, 16)
                for dst, src in loads:
                    sp.dma_start(dst, src).then_inc(s_load, 16)
                sp.wait_ge(s_load, 16 * (len(loads) + 2 * GB))

            n_loads = 16 * (len(loads) + 2 * GB)

            @block.gpsimd
            def _(pool):
                pool.memset(k["ident"][:, :], 0.0).then_inc(s_zero, 1)
                pool.memset(k["identb"][:, :], 0.0).then_inc(s_zero, 1)
                pool.memset(k["shift"][:, :], 0.0).then_inc(s_zero, 1)
                pool.memset(k["band"][:, :, :], 0.0).then_inc(s_zero, 1)
                pool.memset(k["headmask"][:, :], 1.0).then_inc(s_zero, 1)
                pool.memset(k["ones"][:, :], 1.0).then_inc(s_zero, 1)
                pool.memset(k["minus_half"][:, :], -0.5).then_inc(s_zero, 1)
                pool.memset(k["eps"][:, :], EPS).then_inc(s_zero, 1)
                pool.memset(k["huge"][:, :], 1e12).then_inc(s_zero, 1)
                pool.memset(k["eight"][:, :], 8.0).then_inc(s_zero, 1)
                pool.memset(k["wpad"][:, :], 0.0).then_inc(s_zero, 1)
                pool.memset(k["up_b"][:, :, :], 0.0).then_inc(s_zero, 1)
                pool.memset(k["b2blk"][:, :, :], 0.0).then_inc(s_zero, 1)
                pool.memset(k["lower"][:, :, :], 1.0).then_inc(s_zero, 1)
                pool.iota(iota_i[:, :], pattern=[[1, S2]], base=0, channel_multiplier=0).then_inc(s_zero, 1)
                pool.iota(pos_i[:, :], pattern=[[0, 1]], base=0, channel_multiplier=1).then_inc(s_zero, 1)
                pool.wait_ge(s_zero, 16)
                for n in ("ident", "identb"):
                    pool.affine_select(out=k[n][:, :], in_=k[n][:, :], compare_op=ALU.not_equal, fill=1.0, base=0,
                                       pattern=[[-1, 128]], channel_multiplier=1).then_inc(s_shape, 1)
                pool.affine_select(out=k["shift"][:, :], in_=k["shift"][:, :], compare_op=ALU.not_equal, fill=1.0,
                                   base=-1, pattern=[[1, 128]], channel_multiplier=-1).then_inc(s_shape, 1)
                pool.affine_select(out=k["band"][:, :, :], in_=k["band"][:, :, :], compare_op=ALU.is_ge, fill=NEG,
                                   base=0, pattern=[[0, 4], [-1, 128]], channel_multiplier=1).then_inc(s_shape, 1)
                pool.affine_select(out=k["headmask"][:, :], in_=k["headmask"][:, :], compare_op=ALU.is_ge, fill=0.0,
                                   base=0, pattern=[[-XD, XH]], channel_multiplier=1).then_inc(s_shape, 1)
                pool.affine_select(out=k["lower"][:, :, :], in_=k["lower"][:, :, :], compare_op=ALU.is_gt, fill=0.0,
                                   base=0, pattern=[[1, E], [-1, E]], channel_multiplier=0).then_inc(s_shape, 1)
                pool.wait_ge(s_shape, 6)
                pool.affine_select(out=k["band"][:, :, :], in_=k["band"][:, :, :], compare_op=ALU.is_ge, fill=NEG,
                                   base=WINDOW, pattern=[[0, 4], [1, 128]], channel_multiplier=-1).then_inc(s_shape, 1)
                pool.affine_select(out=k["headmask"][:, :], in_=k["headmask"][:, :], compare_op=ALU.is_ge, fill=0.0,
                                   base=XD - 1, pattern=[[XD, XH]], channel_multiplier=-1).then_inc(s_shape, 1)

            @block.tensor
            def _(pe):
                pe.wait_ge(s_load, n_loads)
                pe.wait_ge(s_shape, 8)
                for j, (src, _, n) in enumerate(turns):
                    if j >= 8:
                        pe.wait_ge(s_evac, j - 7)
                    nc.tensor.transpose(ps[:, j % 8, 0:n], src, k["ident"][0:n, 0:n]).then_inc(s_turn, 1)

            @block.scalar
            def _(act):
                for j, (_, dst, n) in enumerate(turns):
                    act.wait_ge(s_turn, j + 1)
                    nc.scalar.copy(dst, ps[:, j % 8, 0:n]).then_inc(s_evac, 1)

            @block.vector
            def _(dve):
                dve.wait_ge(s_load, n_loads)
                dve.wait_ge(s_zero, 16)
                nc.vector.tensor_copy(k["iota"][:, :], iota_i[:, :])
                nc.vector.tensor_copy(k["pos"][:, :], pos_i[:, :])
                nc.vector.tensor_copy(k["wpad"][:, 31:32], col[:, 0:1])
                nc.vector.tensor_scalar(k["Wcw"][:, :], k["ones"][:, :], col[:, 1:2], None, ALU.mult)
                nc.vector.tensor_scalar(k["Wcb"][:, :], k["ones"][:, :], col[:, 2:3], None, ALU.mult)
                nc.vector.tensor_scalar(k["negm"][:, :, :].rearrange("p b s -> p (b s)"), qmask[:, :], -1.0, 1.0,
                                        ALU.mult, ALU.add).then_inc(s_int, 1)
                nc.vector.tensor_scalar(fmaskf[:, :, :].rearrange("p b s -> p (b s)"), fmask[:, :], -1.0, 1.0,
                                        ALU.mult, ALU.add).then_inc(s_int, 1)
                for n in range(NK):
                    nc.vector.tensor_scalar(k["boffpos"][:, :].rearrange("p (h n) -> p h n", n=NK)[:, :, n],
                                            k["r_L3_boff"][:, :].rearrange("p (h n) -> p h n", n=NK)[:, :, n],
                                            float(-NK // 2 + n), None, ALU.add).then_inc(s_col, 1)
                dve.wait_ge(s_int, 2)
                nc.vector.tensor_scalar(k["negm"][:, :, :], k["negm"][:, :, :], NEG, None, ALU.mult)
                nc.vector.tensor_reduce(k["span"][:, :], fmaskf[:, :, :], AX.X, ALU.add).then_inc(s_int, 1)
                dve.wait_ge(s_col, NK)
                dve.wait_ge(s_int, 3)
                nc.vector.tensor_scalar(k["span"][:, :], k["span"][:, :], -1.0, None, ALU.add).then_inc(s_int, 1)
                nc.vector.tensor_tensor(k["sscale"][:, :], k["r_sin"][:, :], k["r_sk"][:, :], ALU.mult)
                dve.wait_ge(s_int, 4)
                nc.vector.tensor_scalar(k["sgn"][:, :], k["span"][:, :], 0.0, 2.0, ALU.is_ge, ALU.mult).then_inc(s_int, 1)
                dve.wait_ge(s_int, 5)
                nc.vector.tensor_scalar(k["sgn"][:, :], k["sgn"][:, :], -1.0, None, ALU.add).then_inc(s_int, 1)
                dve.wait_ge(s_int, 6)
                nc.vector.tensor_tensor(k["span"][:, :], k["span"][:, :], k["sgn"][:, :], ALU.mult).then_inc(s_int, 1)
                dve.wait_ge(s_int, 7)
                nc.vector.reciprocal(k["rspan"][:, :], k["span"][:, :])


def additive_attention(nc, a, k, ps):
    CF = 16
    NCH = S // CF
    RING = 4
    with ExitStack() as ctx:
        m = Buffers(nc, ctx, "p1")
        stat, mv, ve, rstd = m.lanes("stat", [128, 6]), m.lanes("mv", [128, 2]), m.lanes("ve", [128, 1]), m.lanes("rstd", [128, 1])
        xn, xnT = m.lanes("xn", [128, 128]), m.lanes("xnT", [128, 128])
        ctl, ctxT = m.lanes("ctl", [S2, 128]), m.lanes("ctxT", [128, S2])
        featT, proj = m.lanes("featT", [128, 128]), m.lanes("proj", [128, 3, S2])
        ring = m.lanes("ring", [128, 4, 4, S2], n=RING)
        sc, pr, tw = m.lanes("sc", [128, S2]), m.lanes("pr", [128, S2]), m.lanes("tw", [128, 2, S2])
        nm, den, rd, z, g = (m.lanes(n, [128, w]) for n, w in (("nm", 1), ("den", 1), ("rd", 1), ("z", 2), ("g", 2)))
        upd = m.lanes("upd", [128, 128])
        passed = m.sem("passed")
        ctx_loaded, ctx_free = m.sems("ctx_loaded"), m.sems("ctx_free")
        stats, moments, var_eps, rstd_ready, xn_ready = (m.sems(n) for n in ("stats", "moments", "var_eps", "rstd", "xn"))
        turned, turn_copied, projected, proj_copied = (m.sems(n) for n in ("turned", "turn_copied", "projected", "proj_copied"))
        summed, tanhed, dotted = m.sem("summed"), m.sem("tanhed"), m.sem("dotted")
        rho_ready = m.sems("rho_ready")
        masked, maxed, expd, weighted, gathered, scaled, gates, updated, x_done = (
            m.sems(n) for n in ("masked", "maxed", "expd", "weighted", "gathered", "scaled", "gates", "updated", "x_done"))
        ctxT_kept = m.sem("ctxT_kept")

        with nc.Block() as block:
            @block.sync
            def _(sp):
                with sp.Fori(0, ITERS) as i:
                    u1 = sp.snap(i + 1)
                    for l in range(LANES):
                        sp.wait_ge(ctx_free[l], u1)
                        sp.dma_start(ctl[l][:, :], a["ctx_1024"][bass.ds(i * LANES + l, 1), :, :].rearrange("b s d -> (b s) d")
                                     ).then_inc(ctx_loaded[l], 16)

            @block.tensor
            def _(pe):
                with pe.Fori(0, ITERS) as i:
                    u1 = pe.snap(i + 1)
                    u16 = pe.snap(i * 16 + 16)
                    for l in range(LANES):
                        pe.wait_ge(masked[l], u1)
                        pe.wait_ge(xn_ready[l], u1)
                        pe.wait_ge(ctx_loaded[l], u16)
                        nc.tensor.transpose(ps[:, 2 * l, 0:128], xn[l][:, :], k["ident"][:, :])
                        nc.tensor.transpose(ps[:, 2 * l, 128:128 + S2], ctl[l][:, :], k["ident"][0:S2, 0:S2]
                                            ).then_inc(turned[l], 1)
                    for l in range(LANES):
                        pe.wait_ge(turn_copied[l], u1)
                        nc.tensor.matmul(ps[:, 2 * l, 0:128], k["L0_W"][:, :], xnT[l][:, :], start=True, stop=True)
                        for j, w in enumerate(("L0_Ws", "Wcw", "Wcb")):
                            last = nc.tensor.matmul(ps[:, 2 * l, 128 + j * S2:128 + (j + 1) * S2], k[w][:, :], ctxT[l][:, :],
                                                    start=True, stop=True)
                        last.then_inc(projected[l], 1)
                    for l in range(LANES):
                        for c in range(NCH):
                            pe.wait_ge(tanhed, i * (LANES * NCH) + (l * NCH + c + 1))
                            for kk in range(4):
                                for q in range(4):
                                    row = 4 * c + kk
                                    last = nc.tensor.matmul(ps[32 * q:32 * q + 32, 2 * l + 1, 0:S2],
                                                            k["wpad"][:, 31 - row:63 - row], ring[c % RING][:, q, kk, :],
                                                            start=(row == 0), stop=(row == 31))
                            if c == NCH - 1:
                                last.then_inc(rho_ready[l], 1)
                                pe.wait_ge(rho_ready[l], u1)
                                pe.sem_inc(dotted, 1)
                            else:
                                last.then_inc(dotted, 1)

            @block.vector
            def _(dve):
                for l in range(LANES):
                    dve.sem_inc(masked[l], 1)
                    dve.sem_inc(ctx_free[l], 1)
                dve.sem_inc(dotted, RING)
                with dve.Fori(0, ITERS) as i:
                    u1, u2 = dve.snap(i + 1), dve.snap(i + 2)
                    for l in range(LANES):
                        nc.vector.bn_stats(stat[l][:, :], cols(k["x"], i * LANES + l)).then_inc(stats[l], 1)
                    dve.wait_ge(stats[LANES - 1], u1)
                    dve.sem_inc(passed, 1)
                    for l in range(LANES):
                        nc.vector.bn_aggr(mv[l][:, :], stat[l][:, :]).then_inc(moments[l], 1)
                    for l in range(LANES):
                        dve.wait_ge(rstd_ready[l], u1)
                        nc.vector.tensor_scalar(xn[l][:, :], cols(k["x"], i * LANES + l), mv[l][:, 0:1], rstd[l][:, 0:1],
                                                ALU.subtract, ALU.mult).then_inc(xn_ready[l], 1)
                    for l in range(LANES):
                        dve.wait_ge(proj_copied[l], u1)
                        for c in range(NCH):
                            dve.wait_ge(dotted, i * (LANES * NCH) + (l * NCH + c + 1))
                            feats = featT[l][:, :].rearrange("p (q c k) -> p q c k", q=4, c=NCH)[:, :, c, :]
                            for q in range(4):
                                last = nc.vector.tensor_tensor(ring[c % RING][:, q, :, :], bc(feats[:, q, :], 2, S2),
                                                               bc(proj[l][:, 0, :], 1, 4), ALU.add)
                            last.then_inc(summed, 1)
                    for l in range(LANES):
                        dve.wait_ge(rho_ready[l], u1)
                        nc.vector.tensor_tensor(sc[l][:, :], ps[:, 2 * l + 1, 0:S2], cols(k["negm"], i * LANES + l),
                                                ALU.add).then_inc(masked[l], 1)
                    for l in range(LANES):
                        dve.wait_ge(masked[l], u2)
                        nc.vector.tensor_reduce(nm[l][:, :], sc[l][:, :], AX.X, ALU.max, negate=True).then_inc(maxed[l], 1)
                    for l in range(LANES):
                        dve.wait_ge(expd[l], u1)
                        nc.vector.tensor_tensor(tw[l][:, :, :], bc(pr[l][:, :], 1, 2), proj[l][:, 1:3, :],
                                                ALU.mult).then_inc(weighted[l], 1)
                        nc.vector.reciprocal(rd[l][:, :], den[l][:, :]).then_inc(weighted[l], 1)
                    w2 = dve.snap(i * 2 + 2)
                    for l in range(LANES):
                        dve.wait_ge(weighted[l], w2)
                        nc.vector.tensor_reduce(z[l][:, :], tw[l][:, :, :], AX.X, ALU.add).then_inc(gathered[l], 1)
                    for l in range(LANES):
                        dve.wait_ge(gathered[l], u1)
                        nc.vector.tensor_scalar(z[l][:, :], z[l][:, :], rd[l][:, 0:1], None, ALU.mult).then_inc(scaled[l], 1)
                    for l in range(LANES):
                        dve.wait_ge(gates[l], u1)
                        nc.vector.tensor_scalar(upd[l][:, :], xn[l][:, :], g[l][:, 0:1], g[l][:, 1:2], ALU.mult, ALU.add
                                                ).then_inc(updated[l], 1)
                    for l in range(LANES):
                        dve.wait_ge(updated[l], u1)
                        nc.vector.tensor_tensor(cols(k["x"], i * LANES + l), cols(k["x"], i * LANES + l), upd[l][:, :],
                                                ALU.add).then_inc(x_done[l], 1)

            @block.scalar
            def _(act):
                with act.Fori(0, ITERS) as i:
                    u1 = act.snap(i + 1)
                    for l in range(LANES):
                        act.wait_ge(turned[l], u1)
                        nc.scalar.copy(xnT[l][:, :], ps[:, 2 * l, 0:128])
                        nc.scalar.copy(cols(k["ctxT"], i * LANES + l), ps[:, 2 * l, 128:128 + S2])
                        nc.scalar.copy(ctxT[l][:, :], ps[:, 2 * l, 128:128 + S2]).then_inc(turn_copied[l], 1)
                        act.sem_inc(ctx_free[l], 1)
                    for l in range(LANES):
                        act.wait_ge(projected[l], u1)
                        nc.scalar.activation(featT[l][:, :], ps[:, 2 * l, 0:128], ACT.Identity, bias=k["c_L0_b"][:, 0:1])
                        nc.scalar.copy(proj[l][:, :, :].rearrange("p j s -> p (j s)"), ps[:, 2 * l, 128:128 + 3 * S2]
                                       ).then_inc(proj_copied[l], 1)
                    for l in range(LANES):
                        for c in range(NCH):
                            act.wait_ge(summed, i * (LANES * NCH) + (l * NCH + c + 1))
                            h = ring[c % RING][:, :, :, :].rearrange("p q k s -> p (q k s)")
                            nc.scalar.activation(h, h, ACT.Tanh).then_inc(tanhed, 1)
                    for l in range(LANES):
                        act.wait_ge(maxed[l], u1)
                        nc.scalar.activation(pr[l][:, :], sc[l][:, :], ACT.Exp, bias=nm[l][:, 0:1],
                                             accum_out=den[l][:, 0:1]).then_inc(expd[l], 1)
                    for l in range(LANES):
                        act.wait_ge(scaled[l], u1)
                        nc.scalar.activation(g[l][:, 0:1], z[l][:, 0:1], ACT.Tanh, bias=k["r_bcw"][:, 0:1])
                        nc.scalar.activation(g[l][:, 1:2], z[l][:, 1:2], ACT.Tanh, bias=k["r_bcb"][:, 0:1]).then_inc(gates[l], 1)

            @block.gpsimd
            def _(pool):
                with pool.Fori(0, ITERS) as i:
                    u1 = pool.snap(i + 1)
                    for l in range(LANES):
                        pool.wait_ge(moments[l], u1)
                        nc.gpsimd.tensor_tensor(ve[l][:, :], mv[l][:, 1:2], k["eps"][:, 0:1], ALU.add).then_inc(var_eps[l], 1)
                        pool.wait_ge(var_eps[l], u1)
                        nc.gpsimd.tensor_tensor(rstd[l][:, :], ve[l][:, :], k["minus_half"][:, 0:1], ALU.pow
                                                ).then_inc(rstd_ready[l], 1)


def normalise_all(nc, k, ps):
    with ExitStack() as ctx:
        m = Buffers(nc, ctx, "p2n")
        stat, mv, ve, rstd = m.sb("stat", [128, B, 6]), m.sb("mv", [128, B, 2]), m.sb("ve", [128, B]), m.sb("rstd", [128, B])
        passed = m.sem("passed")
        stats, moments, var_eps, rstd_ready = (m.sem(n) for n in ("stats", "moments", "var_eps", "rstd"))
        with nc.Block() as block:
            @block.vector
            def _(dve):
                for b in range(B):
                    nc.vector.bn_stats(stat[:, b, :], k["x"][:, b, :]).then_inc(stats, 1)
                dve.wait_ge(stats, B)
                dve.sem_inc(passed, 1)
                for b in range(B):
                    nc.vector.bn_aggr(mv[:, b, :], stat[:, b, :]).then_inc(moments, 1)
                dve.wait_ge(rstd_ready, 1)
                for b in range(B):
                    nc.vector.tensor_scalar(k["z"][:, b, :], k["x"][:, b, :], mv[:, b, 0:1], rstd[:, b:b + 1],
                                            ALU.subtract, ALU.mult)

            @block.gpsimd
            def _(pool):
                pool.wait_ge(moments, B)
                nc.gpsimd.tensor_tensor(ve[:, :], mv[:, :, 1], k["eps"][:, 0:1].to_broadcast([128, B]), ALU.add).then_inc(var_eps, 1)
                pool.wait_ge(var_eps, 1)
                nc.gpsimd.tensor_tensor(rstd[:, :], ve[:, :], k["minus_half"][:, 0:1].to_broadcast([128, B]), ALU.pow
                                        ).then_inc(rstd_ready, 1)


A_STEPS = 13
B_STEPS = 13


def attention_layer(eng, layer, project, attend):
    G = ((0, 1), (2, 3))

    def numbers(i):
        it = layer * ITERS + i
        return i, eng.snap(it + 1), (eng.snap(it * 2 + 1), eng.snap(it * 2 + 2))

    def slot(projecting, attending):
        for t in range(max(A_STEPS, B_STEPS)):
            if attending and t < B_STEPS:
                attend(t, *attending)
            if projecting and t < A_STEPS:
                project(t, *projecting)

    def turn(n, following):
        slot((G[1], 0, n), (G[0], 0, n))
        slot((G[0], 1, n), (G[1], 0, n))
        slot((G[1], 1, n), (G[0], 1, n))
        slot((G[0], 0, following) if following else None, (G[1], 1, n))

    slot((G[0], 0, numbers(0)), None)
    with eng.Fori(0, ITERS - 1) as i:
        turn(numbers(i), numbers(i + 1))
    turn(numbers(ITERS - 1), None)


def local_transformer(nc, a, k, ps):
    QK = 2 * HG
    with ExitStack() as ctx:
        m = Buffers(nc, ctx, "p2")
        wqkv, wo = m.sb("wqkv", [128, 3, 2, HG * DH]), m.sb("wo", [128, HG, D])
        w1, w2 = m.sb("w1", [128, 2 * FF]), m.sb("w2", [128, 3, D])
        b1, gcol, bcol, b2 = m.sb("b1", [128, 2, 3]), m.sb("gcol", [128, 1]), m.sb("bcol", [128, 1]), m.sb("b2", [128, D])
        qks, tabA, tabB = m.sb("qks", [128, 2, DH]), m.sb("tabA", [128, 2, DH]), m.sb("tabB", [128, 2, DH])
        zl, zT = m.lanes("zl", [128, 128]), m.lanes("zT", [128, 128])
        sq = m.lanes("sq", [128, QK, DH])
        ropeB = sq
        qn = m.lanes("qn", [128, 2, HG, DH])
        probs = [t[:, :, :, :].rearrange("p a h d -> p (a h d)").rearrange("p (r j n) -> p r j n", r=2, j=4) for t in qn]
        rope = m.lanes("rope", [128, 2, HG, DH])
        oh = [t[:, 0, :, :] for t in rope]
        qkT = m.lanes("qkT", [128, 2, 4, 128])
        vx = m.lanes("vx", [128, HEADS, DH + 1])
        oT = m.lanes("oT", [128, HG, 128])
        ss, rn, rn1 = m.lanes("ss", [128, QK]), m.lanes("rn", [128, QK]), m.lanes("rn1", [128, QK])
        nm, rd = m.lanes("nm", [128, HG]), m.lanes("rd", [128, HG])

        attn_loaded, attn_free, ffn_loaded, ffn_free = (m.sem(n) for n in ("attn_loaded", "attn_free", "ffn_loaded", "ffn_free"))
        passed = m.sem("passed")
        tabs_half, tabs_ready = m.sem("tabs_half"), m.sem("tabs_ready")
        (zl_ready, zT_ps, zT_ready, v_ps, v_ready, qk_ps, sq_ready, ss_ready, ss_floored, rn_ready, qn_ready, ropeB_ready,
         ropeA_ready, rope_ready, qkT_ps, qkT_ready, s_ps, max_ready, sub_ready, p_ready, pT_ps, pT_ready, pv_ps, rd_ready,
         o_ready, oT_ps, oT_ready, y_ps, z_done) = (
            m.sems(n) for n in ("zl", "zT_ps", "zT", "v_ps", "v", "qk_ps", "sq", "ss", "ss_floored", "rn", "qn", "ropeB", "ropeA",
                                "rope", "qkT_ps", "qkT", "s_ps", "max", "sub", "p", "pT_ps", "pT", "pv_ps", "rd", "o",
                                "oT_ps", "oT", "y_ps", "z_done"))
        fz = [t[:, :, :, :].rearrange("p a h d -> p (a h d)")[:, 0:512].rearrange("p (b d) -> p b d", b=GB) for t in qn[0:WIDE]]
        fxn = [t[:, :, :, :].rearrange("p a h d -> p (a h d)")[:, 512:1024].rearrange("p (b d) -> p b d", b=GB) for t in qn[0:WIDE]]
        fsecond = [t[:, :, :].rearrange("p a d -> p (a d)")[:, 0:256].rearrange("p (b d) -> p b d", b=GB) for t in sq[0:WIDE]]
        fxT = [t[:, :, :, :].rearrange("p a h d -> p (a h d)")[:, 0:512] for t in qkT[0:WIDE]]
        fg = [t[:, :, :, :].rearrange("p a h d -> p (a h d)")[:, 0:512] for t in rope[0:WIDE]]
        fh = [[t[:, :, :].rearrange("p a d -> p (a d)")[:, 0:512] for t in (oT[l], oT[l + 2], sq[l + 2])] for l in range(WIDE)]
        fzb = [t[:, :, :, :].rearrange("p a h d -> p (a h d)")[:, 512:1024].rearrange("p (b d) -> p b d", b=GB) for t in rope[0:WIDE]]
        fst, fmv, fve, frs = (m.lanes(n, s, n=WIDE) for n, s in (("fst", [128, GB, 6]), ("fmv", [128, GB, 2]), ("fve", [128, GB]),
                                                                 ("frs", [128, GB])))
        (f_split, f_shift_ps, f_shifted, f_stats, f_moments, f_eps, f_rs, f_xn, f_xT_ps, f_xT, f_y_ps, f_zb, f_done) = (
            m.sems(n, WIDE) for n in ("f_split", "f_shift_ps", "f_shifted", "f_stats", "f_moments", "f_eps", "f_rs", "f_xn",
                                      "f_xT_ps", "f_xT", "f_y_ps", "f_zb", "f_done"))
        f_ag_ps, f_gelu, f_h = m.sems("f_ag_ps", WIDE), m.sems("f_gelu", WIDE), m.sems("f_h", WIDE)

        N_ATTN, N_FFN = 6, 4 + 3 + 6 - 2
        z = k["z"]

        with nc.Block() as block:
            @block.sync
            def _(sp):
                with sp.Fori(0, DEPTH) as layer:
                    n1 = sp.snap(layer + 1)
                    row = lambda t: a[f"L0_ffn_{t}"][bass.ds(layer, 1)]
                    sp.wait_ge(attn_free, n1)
                    for j in range(3):
                        sp.dma_start(wqkv[:, j, :, :], row("Wqkv").rearrange("o d (j h n) -> (o d) j h n", j=3, h=2)[:, j, :, :]
                                     ).then_inc(attn_loaded, 16)
                    sp.dma_start(wo[:, :, :], row("Wo").rearrange("o (c p) n -> p (o c) n", p=128)).then_inc(attn_loaded, 16)
                    sp.dma_start(qks[:, 0, :], row("q_scale").rearrange("o d -> (o d)").partition_broadcast(128)).then_inc(attn_loaded, 16)
                    sp.dma_start(qks[:, 1, :], row("k_scale").rearrange("o d -> (o d)").partition_broadcast(128)).then_inc(attn_loaded, 16)
                    sp.wait_ge(ffn_free, n1)
                    sp.dma_start(w1[:, :], row("W1").rearrange("o d n -> (o d) n")).then_inc(ffn_loaded, 16)
                    sp.dma_start(w2[:, 0:2, :], row("W2")[:, 0:256, :].rearrange("o (c p) n -> p (o c) n", p=128)).then_inc(ffn_loaded, 16)
                    sp.dma_start(w2[0:FF - 256, 2, :], row("W2")[:, 256:FF, :].rearrange("o p n -> (o p) n")).then_inc(ffn_loaded, 16)
                    for c, (f0, fn) in enumerate(FFC):
                        for half in range(2):
                            sp.dma_start(b1[0:fn, half, c:c + 1],
                                         row("b1")[:, half * FF + f0:half * FF + f0 + fn].rearrange("o d -> d o")).then_inc(ffn_loaded, 16)
                    sp.dma_start(gcol[:, :], row("ln_g").rearrange("o d -> d o")).then_inc(ffn_loaded, 16)
                    sp.dma_start(bcol[:, :], row("ln_b").rearrange("o d -> d o")).then_inc(ffn_loaded, 16)
                    sp.dma_start(b2[:, :], row("b2").rearrange("o d -> (o d)").partition_broadcast(128)).then_inc(ffn_loaded, 16)

            N_FFN_LOADS = 12

            @block.tensor
            def _(pe):
                def project(t, lanes, h, n):
                    i, u1, v = n
                    for l in lanes:
                        if t == 0 and h == 0:
                            pe.wait_ge(z_done[l], u1)
                            pe.wait_ge(zl_ready[l], u1)
                            nc.tensor.transpose(ps[:, 2 * l, 0:128], zl[l][:, :], k["ident"][:, :]).then_inc(zT_ps[l], 1)
                        if t == 2 and h == 0:
                            pe.wait_ge(zT_ready[l], u1)
                            for j in range(2):
                                last = nc.tensor.matmul(ps[:, 2 * l + j, :], zT[l][:, :], wqkv[:, 2, j, :], start=True, stop=True)
                            last.then_inc(v_ps[l], 1)
                        if t == 4:
                            if h == 0:
                                pe.wait_ge(v_ready[l], u1)
                            else:
                                pe.wait_ge(oT_ready[l], v[0])
                            for j in range(2):
                                last = nc.tensor.matmul(ps[:, 2 * l + j, :], zT[l][:, :], wqkv[:, j, h, :], start=True, stop=True)
                            last.then_inc(qk_ps[l], 1)
                        if t == 11:
                            pe.wait_ge(rope_ready[l], v[h])
                            for j in range(2):
                                for c in range(4):
                                    last = nc.tensor.transpose(ps[:, 2 * l + j, c * 128:(c + 1) * 128],
                                                               rope[l][:, j, 2 * c:2 * c + 2, :].rearrange("p h d -> p (h d)"),
                                                               k["ident"][:, :])
                            last.then_inc(qkT_ps[l], 1)

                def attend(t, lanes, h, n):
                    i, u1, v = n
                    for l in lanes:
                        if t == 0:
                            pe.wait_ge(qkT_ready[l], v[h])
                            for r in range(2):
                                nc.tensor.matmul(ps[:, 2 * l + r, :], k["identb"][:, :], k["band"][:, :, :].rearrange("p j n -> p (j n)"),
                                                 start=True, stop=False)
                            for c in range(4):
                                for r in range(2):
                                    last = nc.tensor.matmul(ps[:, 2 * l + r, c * 128:(c + 1) * 128],
                                                            qkT[l][DH * r:DH * r + DH, 0, c, :], qkT[l][DH * r:DH * r + DH, 1, c, :],
                                                            start=False, stop=(c == 3))
                            last.then_inc(s_ps[l], 1)
                        if t == 4:
                            pe.wait_ge(p_ready[l], v[h])
                            for r in range(2):
                                for c in range(4):
                                    last = nc.tensor.transpose(ps[:, 2 * l + r, c * 128:(c + 1) * 128], probs[l][:, r, c, :],
                                                               k["ident"][:, :])
                            last.then_inc(pT_ps[l], 1)
                        if t == 6:
                            pe.wait_ge(pT_ready[l], v[h])
                            for r in range(2):
                                for c in range(4):
                                    last = nc.tensor.matmul(ps[:, 2 * l + r, c * (DH + 1):(c + 1) * (DH + 1)], qkT[l][:, r, c, :],
                                                            vx[l][:, h * HG + 2 * c + r, :], start=True, stop=True)
                            last.then_inc(pv_ps[l], 1)
                        if t == 9:
                            pe.wait_ge(o_ready[l], v[h])
                            for c in range(4):
                                last = nc.tensor.transpose(ps[:, 2 * l, c * 128:(c + 1) * 128],
                                                           oh[l][:, 2 * c:2 * c + 2, :].rearrange("p h d -> p (h d)"), k["ident"][:, :])
                            last.then_inc(oT_ps[l], 1)
                        if t == 11 and h == 1:
                            pe.wait_ge(oT_ready[l], v[1])
                            for c in range(HG):
                                last = nc.tensor.matmul(ps[:, 2 * l, 0:128], oT[l][:, c, :], wo[:, c, :], start=(c == 0), stop=(c == HG - 1))
                            last.then_inc(y_ps[l], 1)

                def ffn(it):
                    u1, w1_, w2_, w3 = pe.snap(it + 1), pe.snap(it * 3 + 1), pe.snap(it * 3 + 2), pe.snap(it * 3 + 3)
                    w = [w1_, w2_, w3]
                    for l in range(WIDE):
                        pe.wait_ge(f_split[l], u1)
                        pe.wait_ge(f_done[l], u1)
                        nc.tensor.matmul(ps[:, 4 * l, 0:256], k["shift"][:, :], fsecond[l], start=True, stop=True).then_inc(f_shift_ps[l], 1)
                    for l in range(WIDE):
                        pe.wait_ge(f_xn[l], u1)
                        for b in range(GB):
                            last = nc.tensor.transpose(ps[:, 4 * l + 1, b * 128:(b + 1) * 128], fxn[l][:, b, :], k["ident"][:, :])
                        last.then_inc(f_xT_ps[l], 1)
                    for c, (f0, fn) in enumerate(FFC):
                        for l in range(WIDE):
                            if c == 0:
                                pe.wait_ge(f_xT[l], u1)
                            if c == 2:
                                pe.wait_ge(f_h[l], w[0])
                            o = 4 * l + 2 * (c % 2)
                            nc.tensor.matmul(ps[0:fn, o, :], w1[:, f0:f0 + fn], fxT[l], start=True, stop=True)
                            nc.tensor.matmul(ps[0:fn, o + 1, :], w1[:, FF + f0:FF + f0 + fn], fxT[l], start=True, stop=True
                                             ).then_inc(f_ag_ps[l], 1)
                    for l in range(WIDE):
                        pe.wait_ge(f_h[l], w[2])
                        for b in range(GB):
                            for c, (f0, fn) in enumerate(FFC):
                                last = nc.tensor.matmul(ps[:, 4 * l + 2, b * 128:(b + 1) * 128], fh[l][c][0:fn, b * 128:(b + 1) * 128],
                                                        w2[0:fn, c, :], start=(c == 0), stop=(c == 2))
                        last.then_inc(f_y_ps[l], 1)

                with pe.Fori(0, DEPTH) as layer:
                    pe.wait_ge(attn_loaded, layer * (16 * N_ATTN) + 16 * N_ATTN)
                    pe.sem_inc(passed, 1)
                    attention_layer(pe, layer, project, attend)
                    for l in range(LANES):
                        pe.wait_ge(y_ps[l], layer * ITERS + ITERS)
                    pe.sem_inc(attn_free, 1)
                    pe.wait_ge(ffn_loaded, layer * (16 * N_FFN_LOADS) + 16 * N_FFN_LOADS)
                    pe.sem_inc(passed, 1)
                    with pe.Fori(0, ROUNDS) as i:
                        ffn(layer * ROUNDS + i)

            @block.vector
            def _(dve):
                for l in range(LANES):
                    nc.vector.memset(vx[l][:, :, DH:DH + 1], 1.0)
                    nc.vector.memset(zT[l][64:128, 0:1], 0.0).then_inc(z_done[l], 1)
                for l in range(WIDE):
                    dve.sem_inc(f_done[l], 1)

                def project(t, lanes, h, n):
                    i, u1, v = n
                    for l in lanes:
                        if t == 6:
                            dve.wait_ge(sq_ready[l], v[h])
                            nc.vector.tensor_reduce(ss[l][:, :], sq[l][:, :, :], AX.X, ALU.add).then_inc(ss_ready[l], 1)
                        if t == 8:
                            dve.wait_ge(rn_ready[l], v[h])
                            nc.vector.tensor_tensor(qn[l][:, :, :, :].rearrange("p a h d -> p (a h) d"),
                                                    ps[:, 2 * l:2 * l + 2, :].rearrange("p a (h d) -> p (a h) d", d=DH),
                                                    bc(rn[l][:, :], 2, DH), ALU.mult).then_inc(qn_ready[l], 1)
                        if t == 9:
                            dve.wait_ge(qn_ready[l], v[h])
                            nc.vector.tensor_tensor(rope[l][:, :, :, :], qn[l][:, :, :, :], bc(tabA[:, :, :], 2, HG), ALU.mult
                                                    ).then_inc(ropeA_ready[l], 1)
                        if t == 10:
                            dve.wait_ge(ropeA_ready[l], v[h])
                            dve.wait_ge(ropeB_ready[l], v[h])
                            flat = rope[l][:, :, :, :].rearrange("p a h d -> p (a h d)")
                            nc.vector.tensor_tensor(flat, flat, ropeB[l][:, :, :].rearrange("p h d -> p (h d)"), ALU.add
                                                    ).then_inc(rope_ready[l], 1)

                def attend(t, lanes, h, n):
                    i, u1, v = n
                    for l in lanes:
                        s = ps[:, 2 * l:2 * l + 2, :].rearrange("p r (j n) -> p (r j) n", n=128)
                        pv = ps[:, 2 * l:2 * l + 2, 0:4 * (DH + 1)].rearrange("p r (j d) -> p r j d", d=DH + 1)
                        if t == 1:
                            dve.wait_ge(s_ps[l], v[h])
                            nc.vector.tensor_reduce(nm[l][:, :], s, AX.X, ALU.max).then_inc(max_ready[l], 1)
                        if t == 2:
                            dve.wait_ge(max_ready[l], v[h])
                            nc.vector.tensor_tensor(probs[l].rearrange("p r j n -> p (r j) n"), s, bc(nm[l][:, :], 2, 128), ALU.subtract
                                                    ).then_inc(sub_ready[l], 1)
                        if t == 7:
                            dve.wait_ge(pv_ps[l], v[h])
                            nc.vector.reciprocal(rd[l][:, :].rearrange("p (r j) -> p r j", r=2), pv[:, :, :, DH]).then_inc(rd_ready[l], 1)
                        if t == 8:
                            dve.wait_ge(rd_ready[l], v[h])
                            nc.vector.tensor_tensor(oh[l].rearrange("p (j r) d -> p r j d", r=2), pv[:, :, :, 0:DH],
                                                    bc(rd[l][:, :].rearrange("p (r j) -> p r j", r=2), 3, DH), ALU.mult
                                                    ).then_inc(o_ready[l], 1)
                        if t == 12 and h == 1:
                            dve.wait_ge(y_ps[l], u1)
                            zb = cols(z, i * LANES + l)
                            nc.vector.tensor_tensor(zb, zb, ps[:, 2 * l, 0:128], ALU.add).then_inc(z_done[l], 1)

                def ffn(layer, i):
                    it = layer * ROUNDS + i
                    u1, u4 = dve.snap(it + 1), dve.snap(it * 4 + 4)
                    w = [dve.snap(it * 3 + 1), dve.snap(it * 3 + 2), dve.snap(it * 3 + 3)]
                    for l in range(WIDE):
                        dve.wait_ge(f_shifted[l], u1)
                        for b in range(GB):
                            nc.vector.bn_stats(fst[l][:, b, :], fz[l][:, b, :]).then_inc(f_stats[l], 1)
                    for l in range(WIDE):
                        dve.wait_ge(f_stats[l], u4)
                        dve.sem_inc(passed, 1)
                        for b in range(GB):
                            last = nc.vector.bn_aggr(fmv[l][:, b, :], fst[l][:, b, :])
                        last.then_inc(f_moments[l], 1)
                    for l in range(WIDE):
                        dve.wait_ge(f_rs[l], u1)
                        for b in range(GB):
                            last = nc.vector.tensor_scalar(fxn[l][:, b, :], fz[l][:, b, :], fmv[l][:, b, 0:1], frs[l][:, b:b + 1],
                                                           ALU.subtract, ALU.mult)
                        last.then_inc(f_xn[l], 1)
                    for c, (f0, fn) in enumerate(FFC):
                        for l in range(WIDE):
                            dve.wait_ge(f_gelu[l], w[c])
                            nc.vector.scalar_tensor_tensor(out=fh[l][c][0:fn, :], in0=ps[0:fn, 4 * l + 2 * (c % 2), :],
                                                           scalar=b1[0:fn, 0, c:c + 1], in1=fg[l][0:fn, :], op0=ALU.add, op1=ALU.mult
                                                           ).then_inc(f_h[l], 1)
                    for l in range(WIDE):
                        dve.wait_ge(f_y_ps[l], u1)
                        dve.wait_ge(f_zb[l], u1)
                        nc.vector.tensor_tensor(cols(z, (i * WIDE + l) * GB, GB), fzb[l].rearrange("p b d -> p (b d)"),
                                                ps[:, 4 * l + 2, :], ALU.add).then_inc(f_done[l], 1)

                with dve.Fori(0, DEPTH) as layer:
                    dve.wait_ge(tabs_ready, layer * 2 + 2)
                    for l in range(WIDE):
                        dve.wait_ge(f_done[l], layer * ROUNDS + 1)
                    dve.sem_inc(passed, 1)
                    attention_layer(dve, layer, project, attend)
                    for l in range(LANES):
                        dve.wait_ge(z_done[l], layer * ITERS + (ITERS + 1))
                    dve.wait_ge(ffn_loaded, layer * (16 * N_FFN_LOADS) + 16 * N_FFN_LOADS)
                    dve.sem_inc(passed, 1)
                    with dve.Fori(0, ROUNDS) as i:
                        ffn(layer, i)
                    for l in range(WIDE):
                        dve.wait_ge(f_done[l], layer * ROUNDS + (ROUNDS + 1))
                    dve.sem_inc(ffn_free, 1)
                for b in range(0, B, GB):
                    nc.vector.tensor_tensor(k["x"][:, b:b + GB, :], k["x"][:, b:b + GB, :], z[:, b:b + GB, :], ALU.add)

            @block.scalar
            def _(act):
                def project(t, lanes, h, n):
                    i, u1, v = n
                    for l in lanes:
                        if t == 0 and h == 0:
                            nc.scalar.copy(zl[l][:, :], cols(z, i * LANES + l)).then_inc(zl_ready[l], 1)
                        if t == 1 and h == 0:
                            act.wait_ge(zT_ps[l], u1)
                            nc.scalar.copy(zT[l][0:64, :], ps[0:64, 2 * l, 0:128])
                            nc.scalar.copy(zT[l][64:128, 1:128], ps[64:128, 2 * l, 0:127]).then_inc(zT_ready[l], 1)
                        if t == 3 and h == 0:
                            act.wait_ge(v_ps[l], u1)
                            nc.scalar.copy(vx[l][:, :, 0:DH], ps[:, 2 * l:2 * l + 2, :].rearrange("p a (h d) -> p (a h) d", d=DH)
                                           ).then_inc(v_ready[l], 1)
                        if t == 5:
                            act.wait_ge(qk_ps[l], v[h])
                            nc.scalar.activation(sq[l][:, :, :].rearrange("p h d -> p (h d)"),
                                                 ps[:, 2 * l:2 * l + 2, :].rearrange("p a n -> p (a n)"), ACT.Square).then_inc(sq_ready[l], 1)
                        if t == 12:
                            act.wait_ge(qkT_ps[l], v[h])
                            nc.scalar.copy(qkT[l][:, :, :, :].rearrange("p a c n -> p (a c n)"),
                                           ps[:, 2 * l:2 * l + 2, :].rearrange("p a n -> p (a n)")).then_inc(qkT_ready[l], 1)

                def attend(t, lanes, h, n):
                    i, u1, v = n
                    for l in lanes:
                        if t == 3:
                            act.wait_ge(sub_ready[l], v[h])
                            pf = probs[l].rearrange("p r j n -> p (r j n)")
                            nc.scalar.activation(pf, pf, ACT.Exp).then_inc(p_ready[l], 1)
                        if t == 5:
                            act.wait_ge(pT_ps[l], v[h])
                            nc.scalar.copy(qkT[l][:, :, :, :].rearrange("p a c n -> p (a c n)"),
                                           ps[:, 2 * l:2 * l + 2, :].rearrange("p a n -> p (a n)")).then_inc(pT_ready[l], 1)
                        if t == 10:
                            act.wait_ge(oT_ps[l], v[h])
                            nc.scalar.copy(oT[l][:, 4 * h:4 * h + 4, :].rearrange("p c n -> p (c n)"), ps[:, 2 * l, :]
                                           ).then_inc(oT_ready[l], 1)

                def ffn(layer, i):
                    it = layer * ROUNDS + i
                    u1 = act.snap(it + 1)
                    w = [act.snap(it * 3 + 1), act.snap(it * 3 + 2), act.snap(it * 3 + 3)]
                    for l in range(WIDE):
                        act.wait_ge(f_done[l], u1)
                        zb = z[:, bass.ds((i * WIDE + l) * GB, GB), :]
                        nc.scalar.copy(fz[l][:, :, 0:64], zb[:, :, 0:64])
                        nc.scalar.copy(fsecond[l], zb[:, :, 64:128]).then_inc(f_split[l], 1)
                    for l in range(WIDE):
                        act.wait_ge(f_shift_ps[l], u1)
                        nc.scalar.copy(fz[l][:, :, 64:128], ps[:, 4 * l, 0:256].rearrange("p (b d) -> p b d", b=GB)).then_inc(f_shifted[l], 1)
                    for l in range(WIDE):
                        act.wait_ge(f_xT_ps[l], u1)
                        nc.scalar.activation(fxT[l], ps[:, 4 * l + 1, :], ACT.Identity, scale=gcol[:, 0:1], bias=bcol[:, 0:1]
                                             ).then_inc(f_xT[l], 1)
                    for c, (f0, fn) in enumerate(FFC):
                        for l in range(WIDE):
                            act.wait_ge(f_ag_ps[l], w[c])
                            if c > 0:
                                act.wait_ge(f_h[l], w[c - 1])
                            nc.scalar.activation(fg[l][0:fn, :], ps[0:fn, 4 * l + 2 * (c % 2) + 1, :], ACT.Gelu,
                                                 bias=b1[0:fn, 1, c:c + 1]).then_inc(f_gelu[l], 1)

                with act.Fori(0, DEPTH) as layer:
                    for l in range(LANES):
                        act.wait_ge(z_done[l], layer * ITERS + 1)
                    for l in range(WIDE):
                        act.wait_ge(f_done[l], layer * ROUNDS + 1)
                    attention_layer(act, layer, project, attend)
                    for l in range(LANES):
                        act.wait_ge(z_done[l], layer * ITERS + (ITERS + 1))
                    act.wait_ge(ffn_loaded, layer * (16 * N_FFN_LOADS) + 16 * N_FFN_LOADS)
                    with act.Fori(0, ROUNDS) as i:
                        ffn(layer, i)

            @block.gpsimd
            def _(pool):
                pool.sem_inc(attn_free, 1)
                pool.sem_inc(ffn_free, 1)
                H2 = DH // 2

                def project(t, lanes, h, n):
                    i, u1, v = n
                    for l in lanes:
                        if t == 7:
                            pool.wait_ge(ss_ready[l], v[h])
                            pool.sem_inc(passed, 1)
                            nc.gpsimd.tensor_scalar(rn1[l][:, :], ss[l][:, :], 1e-24, None, ALU.max).then_inc(ss_floored[l], 1)
                            pool.wait_ge(ss_floored[l], v[h])
                            nc.gpsimd.tensor_tensor(rn[l][:, :], rn1[l][:, :], k["minus_half"][:, :], ALU.pow).then_inc(rn_ready[l], 1)
                        if t == 9:
                            pool.wait_ge(qn_ready[l], v[h])
                            out = ropeB[l][:, :, :].rearrange("p (a h) d -> p a h d", a=2)
                            for half in range(2):
                                last = nc.gpsimd.tensor_tensor(out[:, :, :, half * H2:(half + 1) * H2],
                                                               qn[l][:, :, :, (1 - half) * H2:(2 - half) * H2],
                                                               bc(tabB[:, :, half * H2:(half + 1) * H2], 2, HG), ALU.mult)
                            last.then_inc(ropeB_ready[l], 1)

                def attend(t, lanes, h, n):
                    pass

                def ffn(layer, i):
                    it = layer * ROUNDS + i
                    u1 = pool.snap(it + 1)
                    for l in range(WIDE):
                        pool.wait_ge(f_moments[l], u1)
                        nc.gpsimd.tensor_tensor(fve[l][:, :], fmv[l][:, :, 1], k["eps"][:, 0:GB], ALU.add).then_inc(f_eps[l], 1)
                    for l in range(WIDE):
                        pool.wait_ge(f_eps[l], u1)
                        nc.gpsimd.tensor_tensor(frs[l][:, :], fve[l][:, :], k["minus_half"][:, 0:GB], ALU.pow).then_inc(f_rs[l], 1)
                    for l in range(WIDE):
                        pool.wait_ge(f_xT[l], u1)
                        nc.gpsimd.tensor_tensor(fzb[l], z[:, bass.ds((i * WIDE + l) * GB, GB), :], bc(b2[:, :], 1, GB), ALU.add
                                                ).then_inc(f_zb[l], 1)

                with pool.Fori(0, DEPTH) as layer:
                    pool.wait_ge(attn_loaded, layer * (16 * N_ATTN) + 16 * N_ATTN)
                    for l in range(LANES):
                        pool.wait_ge(z_done[l], layer * ITERS + 1)
                    for l in range(WIDE):
                        pool.wait_ge(f_done[l], layer * ROUNDS + 1)
                    nc.gpsimd.tensor_tensor(qks[:, 0, :], qks[:, 0, :], k["eight"][:, :], ALU.mult).then_inc(tabs_half, 1)
                    pool.wait_ge(tabs_half, layer + 1)
                    nc.gpsimd.tensor_tensor(tabA[:, :, :], qks[:, :, :], k["cosS"][:, :, :], ALU.mult).then_inc(tabs_ready, 1)
                    for half in range(2):
                        last = nc.gpsimd.tensor_tensor(tabB[:, :, half * H2:(half + 1) * H2], qks[:, :, (1 - half) * H2:(2 - half) * H2],
                                                       k["sinS"][:, :, half * H2:(half + 1) * H2], ALU.mult)
                    last.then_inc(tabs_ready, 1)
                    pool.wait_ge(tabs_ready, layer * 2 + 2)
                    pool.sem_inc(passed, 1)
                    attention_layer(pool, layer, project, attend)
                    pool.wait_ge(ffn_loaded, layer * (16 * N_FFN_LOADS) + 16 * N_FFN_LOADS)
                    for l in range(LANES):
                        pool.wait_ge(z_done[l], layer * ITERS + (ITERS + 1))
                    pool.sem_inc(passed, 1)
                    with pool.Fori(0, ROUNDS) as i:
                        ffn(layer, i)


def cross_attention(nc, a, k, ps, kind, w):
    C2 = 4
    scale = float(XD) ** -0.5 * (0.5 if kind == "sampled" else 1.0)
    with ExitStack() as ctx:
        m = Buffers(nc, ctx, w["phase"])
        passed = m.sem("passed")
        stat, mv, ve, rstd = m.lanes("stat", [128, 6]), m.lanes("mv", [128, 2]), m.lanes("ve", [128, 1]), m.lanes("rstd", [128, 1])
        xn, xnT, ctxT = m.lanes("xn", [128, 128]), m.lanes("xnT", [128, 128]), m.lanes("ctxT", [128, S2])
        qT, kT = m.lanes("qT", [128, 128]), m.lanes("kT", [128, S2])
        vx = m.lanes("vx", [S2, XH, XD + 1])
        kbd = m.lanes("kbd", [128, XH, S2])
        probs, pT = m.lanes("probs", [128, HG, S2]), m.lanes("pT", [S2, HG, 128])
        nm, rd = m.lanes("nm", [128, HG]), m.lanes("rd", [128, HG])
        o, oT, yb = m.lanes("o", [128, XH, XD]), m.lanes("oT", [128, 128]), m.lanes("yb", [128, 128])
        (stats, moments, var_eps, rstd_ready, xn_ready, xT_ps, xT_ready, qkv_ps, q_ready, kbd_ready, v_ready, s_ps,
         p_ready, pT_ps, pT_ready, pv_ps, o_ready, oT_ps, oT_ready, y_ps, yb_ready, x_done,
         k_ready) = (
            m.sems(n) for n in ("stats", "moments", "var_eps", "rstd", "xn", "xT_ps", "xT", "qkv_ps", "q", "kbd", "v", "s_ps",
                                "p", "pT_ps", "pT", "pv_ps", "o", "oT_ps", "oT", "y_ps", "yb", "x_done", "k"))
        sampled = kind == "sampled"
        if not sampled:
            max_ready, sub_ready, rd_ready = m.sems("max"), m.sems("sub"), m.sems("rd")
        if sampled:
            HN = XH * NK
            loc, quo, rnd, rem, low, high, ix = (m.lanes(n, [128, HN]) for n in ("loc", "quo", "rnd", "rem", "low", "high", "ix"))
            hat, prod = m.lanes("hat", [128, C2 * NK, S2]), m.lanes("prod", [128, C2 * NK, S2])
            sc, sc2, at = (m.lanes(n, [128, C2, NK]) for n in ("sc", "sc2", "at"))
            smx, ssum, srd = (m.lanes(n, [128, C2]) for n in ("smx", "ssum", "srd"))
            sp_l, rsp_l, sgn_l = (m.lanes(n, [128, 1]) for n in ("sp_l", "rsp_l", "sgn_l"))
            (off_ps, span_ready, chain, dist, bumped, hat_ready, prod_ready, sc_ready, soft, weighted, c_half) = (
                m.sems(n) for n in ("off_ps", "span", "chain", "dist", "bumped", "hat", "prod", "sc", "soft", "weighted", "c_half"))

        with nc.Block() as block:
            @block.tensor
            def _(pe):
                with pe.Fori(0, ITERS) as i:
                    u1 = pe.snap(i + 1)
                    v = [pe.snap(i * 2 + 1), pe.snap(i * 2 + 2)]
                    for l in range(LANES):
                        pe.wait_ge(x_done[l], u1)
                        pe.wait_ge(xn_ready[l], u1)
                        nc.tensor.transpose(ps[:, 2 * l, 0:128], xn[l][:, :], k["ident"][:, :]).then_inc(xT_ps[l], 1)
                    for l in range(LANES):
                        pe.wait_ge(xT_ready[l], u1)
                        nc.tensor.matmul(ps[:, 2 * l, 0:128], w["Wq"][:, :], xnT[l][:, :], start=True, stop=True)
                        nc.tensor.matmul(ps[:, 2 * l, 128:128 + S2], w["Wk"][:, :], ctxT[l][:, :], start=True, stop=True)
                        nc.tensor.matmul(ps[0:S2, 2 * l + 1, 0:128], ctxT[l][:, :], w["Wv"][:, :], start=True, stop=True
                                         ).then_inc(qkv_ps[l], 1)
                    if sampled:
                        for l in range(LANES):
                            pe.wait_ge(q_ready[l], u1)
                            pe.wait_ge(k_ready[l], u1)
                            nc.tensor.matmul(ps[:, 2 * l, 0:XH * NK], qT[l][:, :], k["T_Woff"][:, :], start=True, stop=True
                                             ).then_inc(off_ps[l], 1)
                    for h in range(2):
                        for l in range(LANES):
                            if h == 0:
                                pe.wait_ge(q_ready[l], u1)
                                pe.wait_ge(v_ready[l], u1)
                                pe.wait_ge(kbd_ready[l], u1)
                                if sampled:
                                    pe.wait_ge(span_ready[l], u1)
                            else:
                                pe.wait_ge(o_ready[l], v[0])
                            for j in range(2):
                                h0 = h * HG + j * C2
                                last = nc.tensor.matmul(ps[:, 2 * l + j, 0:C2 * S2], qT[l][:, :],
                                                        kbd[l][:, h0:h0 + C2, :].rearrange("p h s -> p (h s)"), start=True, stop=True)
                            last.then_inc(s_ps[l], 1)
                        for l in range(LANES):
                            pe.wait_ge(p_ready[l], v[h])
                            for j in range(HG):
                                last = nc.tensor.transpose(ps[0:S2, 2 * l + j // 4, (j % 4) * 128:(j % 4 + 1) * 128], probs[l][:, j, :],
                                                           k["ident"][:, :])
                            last.then_inc(pT_ps[l], 1)
                        for l in range(LANES):
                            pe.wait_ge(pT_ready[l], v[h])
                            for j in range(HG):
                                last = nc.tensor.matmul(ps[:, 2 * l, j * (XD + 1):(j + 1) * (XD + 1)], pT[l][:, j, :],
                                                        vx[l][:, h * HG + j, :], start=True, stop=True)
                            last.then_inc(pv_ps[l], 1)
                    for l in range(LANES):
                        pe.wait_ge(o_ready[l], v[1])
                        nc.tensor.transpose(ps[:, 2 * l, 0:128], o[l][:, :, :].rearrange("p h d -> p (h d)"), k["ident"][:, :]
                                            ).then_inc(oT_ps[l], 1)
                    for l in range(LANES):
                        pe.wait_ge(oT_ready[l], u1)
                        nc.tensor.matmul(ps[:, 2 * l, 0:128], oT[l][:, :], w["Wo"][:, :], start=True, stop=True).then_inc(y_ps[l], 1)

            @block.vector
            def _(dve):
                for l in range(LANES):
                    nc.vector.memset(vx[l][:, :, XD:XD + 1], 1.0).then_inc(x_done[l], 1)
                with dve.Fori(0, ITERS) as i:
                    u1 = dve.snap(i + 1)
                    v = [dve.snap(i * 2 + 1), dve.snap(i * 2 + 2)]
                    for l in range(LANES):
                        nc.vector.bn_stats(stat[l][:, :], cols(k["x"], i * LANES + l)).then_inc(stats[l], 1)
                    dve.wait_ge(stats[LANES - 1], u1)
                    dve.sem_inc(passed, 1)
                    for l in range(LANES):
                        nc.vector.bn_aggr(mv[l][:, :], stat[l][:, :]).then_inc(moments[l], 1)
                    for l in range(LANES):
                        dve.wait_ge(rstd_ready[l], u1)
                        nc.vector.tensor_scalar(xn[l][:, :], cols(k["x"], i * LANES + l), mv[l][:, 0:1], rstd[l][:, 0:1],
                                                ALU.subtract, ALU.mult).then_inc(xn_ready[l], 1)
                    for l in range(LANES):
                        dve.wait_ge(qkv_ps[l], u1)
                        nc.vector.tensor_scalar(kT[l][:, :], ps[:, 2 * l, 128:128 + S2], w["bk"][:, 0:1], scale, ALU.add, ALU.mult
                                                ).then_inc(k_ready[l], 1)
                        nc.vector.tensor_scalar(qT[l][:, :], ps[:, 2 * l, 0:128], w["bq"][:, 0:1], None, ALU.add).then_inc(q_ready[l], 1)
                        nc.vector.tensor_tensor(vx[l][:, :, 0:XD], ps[0:S2, 2 * l + 1, 0:128].rearrange("p (h d) -> p h d", d=XD),
                                                w["bv"][0:S2, :].rearrange("p (h d) -> p h d", d=XD), ALU.add).then_inc(v_ready[l], 1)
                    if sampled:
                        for l in range(LANES):
                            nc.vector.tensor_copy(sp_l[l][:, :], k["span"][:, bass.ds(i * LANES + l, 1)])
                            nc.vector.tensor_copy(rsp_l[l][:, :], k["rspan"][:, bass.ds(i * LANES + l, 1)])
                            nc.vector.tensor_copy(sgn_l[l][:, :], k["sgn"][:, bass.ds(i * LANES + l, 1)])
                            dve.wait_ge(off_ps[l], u1)
                            nc.vector.tensor_tensor(loc[l][:, :], ps[:, 2 * l, 0:HN], k["boffpos"][:, :], ALU.add).then_inc(span_ready[l], 1)
                        c = [dve.snap(i * 11 + j + 1) for j in range(11)]
                        for l in range(LANES):
                            dve.wait_ge(span_ready[l], u1)
                            nc.vector.tensor_scalar(loc[l][:, :], loc[l][:, :], k["pos"][:, 0:1], sgn_l[l][:, 0:1], ALU.add, ALU.mult
                                                    ).then_inc(chain[l], 1)
                        for l in range(LANES):
                            dve.wait_ge(chain[l], c[0])
                            nc.vector.tensor_scalar(quo[l][:, :], loc[l][:, :], rsp_l[l][:, 0:1], None, ALU.mult).then_inc(chain[l], 1)
                        for l in range(LANES):
                            dve.wait_ge(chain[l], c[1])
                            nc.vector.tensor_scalar(rnd[l][:, :], quo[l][:, :], MAGIC, MAGIC, ALU.add, ALU.subtract).then_inc(chain[l], 1)
                        for l in range(LANES):
                            dve.wait_ge(chain[l], c[2])
                            nc.vector.tensor_scalar(rnd[l][:, :], rnd[l][:, :], sp_l[l][:, 0:1], None, ALU.mult).then_inc(chain[l], 1)
                        for l in range(LANES):
                            dve.wait_ge(chain[l], c[3])
                            nc.vector.tensor_tensor(rem[l][:, :], loc[l][:, :], rnd[l][:, :], ALU.subtract).then_inc(chain[l], 1)
                        for l in range(LANES):
                            dve.wait_ge(chain[l], c[4])
                            nc.vector.tensor_scalar(low[l][:, :], rem[l][:, :], 0.0, sp_l[l][:, 0:1], ALU.is_lt, ALU.mult).then_inc(chain[l], 1)
                        for l in range(LANES):
                            dve.wait_ge(chain[l], c[5])
                            nc.vector.tensor_tensor(rem[l][:, :], rem[l][:, :], low[l][:, :], ALU.add).then_inc(chain[l], 1)
                        for l in range(LANES):
                            dve.wait_ge(chain[l], c[6])
                            nc.vector.tensor_scalar(low[l][:, :], rem[l][:, :], sp_l[l][:, 0:1], sp_l[l][:, 0:1], ALU.is_ge, ALU.mult
                                                    ).then_inc(chain[l], 1)
                        for l in range(LANES):
                            dve.wait_ge(chain[l], c[7])
                            nc.vector.tensor_tensor(rem[l][:, :], rem[l][:, :], low[l][:, :], ALU.subtract).then_inc(chain[l], 1)
                        for l in range(LANES):
                            dve.wait_ge(chain[l], c[8])
                            nc.vector.tensor_scalar(high[l][:, :], rem[l][:, :], sgn_l[l][:, 0:1], S2 / (S2 - 1.0), ALU.mult, ALU.mult
                                                    ).then_inc(chain[l], 1)
                        for l in range(LANES):
                            dve.wait_ge(chain[l], c[9])
                            nc.vector.tensor_scalar(ix[l][:, :], high[l][:, :], -0.5, None, ALU.add).then_inc(chain[l], 1)
                    for h in range(2):
                        if not sampled:
                            for l in range(LANES):
                                dve.wait_ge(s_ps[l], v[h])
                                s = ps[:, 2 * l:2 * l + 2, 0:C2 * S2].rearrange("p j (h s) -> p j h s", s=S2)
                                nc.vector.tensor_reduce(nm[l][:, :].rearrange("p (j h) -> p j h", j=2), s, AX.X, ALU.max).then_inc(max_ready[l], 1)
                            for l in range(LANES):
                                dve.wait_ge(max_ready[l], v[h])
                                s = ps[:, 2 * l:2 * l + 2, 0:C2 * S2].rearrange("p j (h s) -> p j h s", s=S2)
                                nc.vector.tensor_tensor(probs[l][:, :, :].rearrange("p (j h) s -> p j h s", j=2), s,
                                                        bc(nm[l][:, :].rearrange("p (j h) -> p j h", j=2), 3, S2), ALU.subtract
                                                        ).then_inc(sub_ready[l], 1)
                        else:
                            for c2 in range(2):
                                n = dve.snap(i * 4 + (2 * h + c2 + 1))
                                t = [dve.snap(i * 24 + (6 * (2 * h + c2) + j + 1)) for j in range(6)]
                                h0 = (h * HG + c2 * C2) * NK
                                for l in range(LANES):
                                    if h == 0 and c2 == 0:
                                        dve.wait_ge(chain[l], c[10])
                                    nc.vector.tensor_tensor(hat[l][:, :, :], bc(ix[l][:, h0:h0 + C2 * NK], 2, S2),
                                                            bc(k["iota"][:, :], 1, C2 * NK), ALU.subtract).then_inc(dist[l], 1)
                                for l in range(LANES):
                                    if c2 == 0:
                                        dve.wait_ge(s_ps[l], v[h])
                                    dve.wait_ge(hat_ready[l], n)
                                    nc.vector.tensor_tensor(prod[l][:, :, :].rearrange("p (h n) s -> p h n s", n=NK),
                                                            hat[l][:, :, :].rearrange("p (h n) s -> p h n s", n=NK),
                                                            bc(ps[:, 2 * l + c2, 0:C2 * S2].rearrange("p (h s) -> p h s", s=S2), 2, NK),
                                                            ALU.mult).then_inc(prod_ready[l], 1)
                                for l in range(LANES):
                                    dve.wait_ge(prod_ready[l], n)
                                    nc.vector.tensor_reduce(sc[l][:, :, :].rearrange("p h n -> p (h n)"), prod[l][:, :, :], AX.X, ALU.add
                                                            ).then_inc(sc_ready[l], 1)
                                for l in range(LANES):
                                    dve.wait_ge(sc_ready[l], n)
                                    nc.vector.tensor_reduce(smx[l][:, :], sc[l][:, :, :], AX.X, ALU.max).then_inc(soft[l], 1)
                                for l in range(LANES):
                                    dve.wait_ge(soft[l], t[0])
                                    nc.vector.tensor_tensor(sc2[l][:, :, :], sc[l][:, :, :], bc(smx[l][:, :], 2, NK), ALU.subtract
                                                            ).then_inc(soft[l], 1)
                                for l in range(LANES):
                                    dve.wait_ge(soft[l], t[2])
                                    nc.vector.tensor_reduce(ssum[l][:, :], sc2[l][:, :, :], AX.X, ALU.add).then_inc(soft[l], 1)
                                for l in range(LANES):
                                    dve.wait_ge(soft[l], t[3])
                                    nc.vector.reciprocal(srd[l][:, :], ssum[l][:, :]).then_inc(soft[l], 1)
                                for l in range(LANES):
                                    dve.wait_ge(soft[l], t[4])
                                    nc.vector.tensor_tensor(at[l][:, :, :], sc2[l][:, :, :], bc(srd[l][:, :], 2, NK), ALU.mult
                                                            ).then_inc(soft[l], 1)
                                for l in range(LANES):
                                    dve.wait_ge(weighted[l], n)
                                    nc.vector.tensor_reduce(probs[l][:, c2 * C2:(c2 + 1) * C2, :],
                                                            prod[l][:, :, :].rearrange("p (h n) s -> p h s n", n=NK), AX.X, ALU.add
                                                            ).then_inc(p_ready[l] if c2 else c_half[l], 1)
                        for l in range(LANES):
                            dve.wait_ge(pv_ps[l], v[h])
                            pv = ps[:, 2 * l, 0:HG * (XD + 1)].rearrange("p (h d) -> p h d", d=XD + 1)
                            if sampled:
                                nc.vector.tensor_scalar(o[l][:, h * HG:(h + 1) * HG, :], pv[:, :, 0:XD], 0.5, None, ALU.mult
                                                        ).then_inc(o_ready[l], 1)
                            else:
                                nc.vector.reciprocal(rd[l][:, :], pv[:, :, XD]).then_inc(rd_ready[l], 1)
                        if not sampled:
                            for l in range(LANES):
                                dve.wait_ge(rd_ready[l], v[h])
                                pv = ps[:, 2 * l, 0:HG * (XD + 1)].rearrange("p (h d) -> p h d", d=XD + 1)
                                nc.vector.tensor_tensor(o[l][:, h * HG:(h + 1) * HG, :], pv[:, :, 0:XD], bc(rd[l][:, :], 2, XD), ALU.mult
                                                        ).then_inc(o_ready[l], 1)
                    for l in range(LANES):
                        dve.wait_ge(y_ps[l], u1)
                        nc.vector.tensor_tensor(yb[l][:, :], ps[:, 2 * l, 0:128], w["bo"][:, :], ALU.add).then_inc(yb_ready[l], 1)
                    for l in range(LANES):
                        dve.wait_ge(yb_ready[l], u1)
                        xb = cols(k["x"], i * LANES + l)
                        nc.vector.tensor_tensor(xb, xb, yb[l][:, :], ALU.add).then_inc(x_done[l], 1)

            @block.scalar
            def _(act):
                with act.Fori(0, ITERS) as i:
                    u1 = act.snap(i + 1)
                    v = [act.snap(i * 2 + 1), act.snap(i * 2 + 2)]
                    for l in range(LANES):
                        act.wait_ge(xT_ps[l], u1)
                        nc.scalar.copy(xnT[l][:, :], ps[:, 2 * l, 0:128])
                        nc.scalar.copy(ctxT[l][:, :], cols(k["ctxT"], i * LANES + l)).then_inc(xT_ready[l], 1)
                    for h in range(2):
                        if sampled:
                            for c2 in range(2):
                                n = act.snap(i * 4 + (2 * h + c2 + 1))
                                t = {1: act.snap(i * 24 + (6 * (2 * h + c2) + 2))}
                                for l in range(LANES):
                                    act.wait_ge(dist[l], n)
                                    f = hat[l][:, :, :].rearrange("p n s -> p (n s)")
                                    nc.scalar.activation(f, f, ACT.Abs).then_inc(bumped[l], 1)
                                for l in range(LANES):
                                    act.wait_ge(bumped[l], n)
                                    f = hat[l][:, :, :].rearrange("p n s -> p (n s)")
                                    nc.scalar.activation(f, f, ACT.Relu, bias=1.0, scale=-1.0).then_inc(hat_ready[l], 1)
                                for l in range(LANES):
                                    act.wait_ge(soft[l], t[1])
                                    f = sc2[l][:, :, :].rearrange("p h n -> p (h n)")
                                    nc.scalar.activation(f, f, ACT.Exp).then_inc(soft[l], 1)
                        else:
                            for l in range(LANES):
                                act.wait_ge(sub_ready[l], v[h])
                                f = probs[l][:, :, :].rearrange("p h s -> p (h s)")
                                nc.scalar.activation(f, f, ACT.Exp).then_inc(p_ready[l], 1)
                        for l in range(LANES):
                            act.wait_ge(pT_ps[l], v[h])
                            nc.scalar.copy(pT[l][:, :, :].rearrange("p h n -> p (h n)"),
                                           ps[0:S2, 2 * l:2 * l + 2, :].rearrange("p a n -> p (a n)")).then_inc(pT_ready[l], 1)
                    for l in range(LANES):
                        act.wait_ge(oT_ps[l], u1)
                        nc.scalar.copy(oT[l][:, :], ps[:, 2 * l, 0:128]).then_inc(oT_ready[l], 1)

            @block.gpsimd
            def _(pool):
                with pool.Fori(0, ITERS) as i:
                    u1 = pool.snap(i + 1)
                    for l in range(LANES):
                        pool.wait_ge(moments[l], u1)
                        nc.gpsimd.tensor_tensor(ve[l][:, :], mv[l][:, 1:2], k["eps"][:, 0:1], ALU.add).then_inc(var_eps[l], 1)
                    for l in range(LANES):
                        pool.wait_ge(var_eps[l], u1)
                        nc.gpsimd.tensor_tensor(rstd[l][:, :], ve[l][:, :], k["minus_half"][:, 0:1], ALU.pow).then_inc(rstd_ready[l], 1)
                    for l in range(LANES):
                        pool.wait_ge(k_ready[l], u1)
                        nc.gpsimd.tensor_tensor(kbd[l][:, :, :], bc(kT[l][:, :], 1, XH), bc(k["headmask"][:, :], 2, S2), ALU.mult
                                                ).then_inc(kbd_ready[l], 1)
                    if sampled:
                        for h in range(2):
                            for c2 in range(2):
                                n = pool.snap(i * 4 + (2 * h + c2 + 1))
                                t = {5: pool.snap(i * 24 + (6 * (2 * h + c2) + 6))}
                                for l in range(LANES):
                                    pool.wait_ge(soft[l], t[5])
                                    nc.gpsimd.tensor_tensor(prod[l][:, :, :], hat[l][:, :, :],
                                                            bc(at[l][:, :, :].rearrange("p h n -> p (h n)"), 2, S2), ALU.mult
                                                            ).then_inc(weighted[l], 1)


def norm_front(nc, m, k):
    f = {"stat": m.lanes("stat", [128, GB, 6], n=WIDE), "mv": m.lanes("mv", [128, GB, 2], n=WIDE),
         "ve": m.lanes("ve", [128, GB], n=WIDE), "rs": m.lanes("rs", [128, GB], n=WIDE)}
    for n in ("stats", "moments", "eps", "rstd", "xn_ready"):
        f[n] = m.sems(n, WIDE)
    return f


def norm_vector(nc, dve, k, f, xn, i, passed):
    u1, u4 = dve.snap(i + 1), dve.snap(i * GB + GB)
    for l in range(WIDE):
        for b in range(GB):
            nc.vector.bn_stats(f["stat"][l][:, b, :], cols(k["x"], (i * WIDE + l) * GB + b)).then_inc(f["stats"][l], 1)
    for l in range(WIDE):
        dve.wait_ge(f["stats"][l], u4)
        dve.sem_inc(passed, 1)
        for b in range(GB):
            last = nc.vector.bn_aggr(f["mv"][l][:, b, :], f["stat"][l][:, b, :])
        last.then_inc(f["moments"][l], 1)
    for l in range(WIDE):
        dve.wait_ge(f["rstd"][l], u1)
        for b in range(GB):
            last = nc.vector.tensor_scalar(xn[l][:, b, :], cols(k["x"], (i * WIDE + l) * GB + b), f["mv"][l][:, b, 0:1],
                                           f["rs"][l][:, b:b + 1], ALU.subtract, ALU.mult)
        last.then_inc(f["xn_ready"][l], 1)


def norm_pool(nc, pool, k, f, i):
    u1 = pool.snap(i + 1)
    for l in range(WIDE):
        pool.wait_ge(f["moments"][l], u1)
        nc.gpsimd.tensor_tensor(f["ve"][l][:, :], f["mv"][l][:, :, 1], k["eps"][:, 0:GB], ALU.add).then_inc(f["eps"][l], 1)
    for l in range(WIDE):
        pool.wait_ge(f["eps"][l], u1)
        nc.gpsimd.tensor_tensor(f["rs"][l][:, :], f["ve"][l][:, :], k["minus_half"][:, 0:GB], ALU.pow).then_inc(f["rstd"][l], 1)


Q_STEPS = 10


def quantise(nc, dve, src, rscale, t, step, count, passed):
    u, v, lo, hi, big, ok, sq = t
    nc.vector.tensor_scalar(u, src, rscale, None, ALU.mult).then_inc(step, 1)
    dve.wait_ge(step, count(1))
    dve.sem_inc(passed, 1)
    nc.vector.tensor_scalar(lo, u, 240.0, -240.0, ALU.min, ALU.max, saturate=False)
    nc.vector.tensor_scalar(v, u, 0.5, 240.0, ALU.mult, ALU.min).then_inc(step, 1)
    nc.vector.tensor_tensor(sq, u, u, ALU.mult).then_inc(step, 1)
    dve.wait_ge(step, count(3))
    nc.vector.tensor_scalar(big, sq, 240.0 ** 2, None, ALU.is_gt)
    nc.vector.tensor_scalar(ok, sq, 464.0 ** 2, None, ALU.is_le).then_inc(step, 1)
    nc.vector.tensor_scalar(hi, v, -240.0, None, ALU.max, saturate=False).then_inc(step, 1)
    dve.wait_ge(step, count(5))
    dve.sem_inc(passed, 1)
    nc.vector.scalar_tensor_tensor(out=v, in0=hi, scalar=2.0, in1=lo, op0=ALU.mult, op1=ALU.subtract).then_inc(step, 1)
    nc.vector.reciprocal(sq, ok).then_inc(step, 1)
    dve.wait_ge(step, count(7))
    nc.vector.tensor_tensor(v, v, big, ALU.mult).then_inc(step, 1)
    nc.vector.tensor_tensor(ok, ok, sq, ALU.mult).then_inc(step, 1)
    dve.wait_ge(step, count(9))
    dve.sem_inc(passed, 1)
    nc.vector.tensor_tensor(u, v, lo, ALU.add).then_inc(step, 1)
    dve.wait_ge(step, count(10))


def quantised_dense(nc, a, k, ps):
    with ExitStack() as ctx:
        m = Buffers(nc, ctx, "p4")
        passed = m.sem("passed")
        f = norm_front(nc, m, k)
        xn = m.lanes("xn", [128, GB, D], BF16, n=WIDE)
        tmp = [(m.sb(f"u{l}", [128, 512]), m.sb(f"v{l}", [128, 512]), m.sb(f"lo{l}", [128, 512], FP8), m.sb(f"hi{l}", [128, 512], FP8),
                m.sb(f"big{l}", [128, 512]), m.sb(f"ok{l}", [128, 512]), m.sb(f"sq{l}", [128, 512])) for l in range(WIDE)]
        xq = m.lanes("xq", [128, 512], BF16, n=WIDE)
        xqT = m.lanes("xqT", [128, 512], BF16, n=WIDE)
        kq = m.sb("kq", [128, 128], BF16)
        rin, rk = m.sb("rin", [128, 1]), m.sb("rk", [128, 1])
        y, y2 = m.lanes("y", [128, 512], BF16, n=WIDE), m.lanes("y2", [128, 512], BF16, n=WIDE)
        kstep, k_ready = m.sem("kstep"), m.sem("k_ready")
        step, q_ready, qT_ps, qT_ready, y_ps, y_ready, yb_ready, x_done = (
            m.sems(n, WIDE) for n in ("step", "q", "qT_ps", "qT", "y_ps", "y", "yb", "x_done"))
        turned = [ps[:, 4 * l, 0:256].bitcast(BF16) for l in range(WIDE)]

        with nc.Block() as block:
            @block.vector
            def _(dve):
                for l in range(WIDE):
                    dve.sem_inc(x_done[l], 1)
                nc.vector.reciprocal(rin[:, :], k["r_sin"][:, :])
                nc.vector.reciprocal(rk[:, :], k["r_sk"][:, :]).then_inc(k_ready, 1)
                dve.wait_ge(k_ready, 1)
                quantise(nc, dve, k["fkernel"][:, :], rk[:, 0:1], [t[:, 0:128] for t in tmp[0]], kstep, lambda n: n, passed)
                nc.vector.tensor_tensor(kq[:, :], tmp[0][0][:, 0:128], tmp[0][5][:, 0:128], ALU.mult).then_inc(k_ready, 1)
                dve.wait_ge(k_ready, 2)
                with dve.Fori(0, ROUNDS) as i:
                    u1 = dve.snap(i + 1)
                    norm_vector(nc, dve, k, f, xn, i, passed)
                    for l in range(WIDE):
                        dve.wait_ge(f["xn_ready"][l], u1)
                        quantise(nc, dve, xn[l][:, :, :].rearrange("p b d -> p (b d)"), rin[:, 0:1], [t[:, :] for t in tmp[l]],
                                 step[l], lambda n: i * Q_STEPS + n, passed)
                        nc.vector.tensor_tensor(xq[l][:, :], tmp[l][0][:, :], tmp[l][5][:, :], ALU.mult).then_inc(q_ready[l], 1)
                    for l in range(WIDE):
                        dve.wait_ge(y_ps[l], u1)
                        nc.vector.tensor_scalar(y[l][:, :], ps[:, 4 * l + 1, :], k["sscale"][:, 0:1], None, ALU.mult).then_inc(y_ready[l], 1)
                    for l in range(WIDE):
                        dve.wait_ge(y_ready[l], u1)
                        nc.vector.tensor_tensor(y2[l][:, :].rearrange("p (b d) -> p b d", b=GB),
                                                y[l][:, :].rearrange("p (b d) -> p b d", b=GB), bc(k["r_fbias"][:, :], 1, GB), ALU.add
                                                ).then_inc(yb_ready[l], 1)
                    for l in range(WIDE):
                        dve.wait_ge(yb_ready[l], u1)
                        xb = cols(k["x"], (i * WIDE + l) * GB, GB)
                        nc.vector.tensor_tensor(xb, xb, y2[l][:, :], ALU.add).then_inc(x_done[l], 1)

            @block.gpsimd
            def _(pool):
                with pool.Fori(0, ROUNDS) as i:
                    norm_pool(nc, pool, k, f, i)

            @block.tensor
            def _(pe):
                pe.wait_ge(k_ready, 2)
                pe.sem_inc(passed, 1)
                with pe.Fori(0, ROUNDS) as i:
                    u1 = pe.snap(i + 1)
                    for l in range(WIDE):
                        pe.wait_ge(x_done[l], u1)
                        pe.wait_ge(q_ready[l], u1)
                        for b in range(GB):
                            last = nc.tensor.transpose(turned[l][:, b * 128:(b + 1) * 128], xq[l][:, b * 128:(b + 1) * 128], k["identb"][:, :])
                        last.then_inc(qT_ps[l], 1)
                    for l in range(WIDE):
                        pe.wait_ge(qT_ready[l], u1)
                        for b in range(GB):
                            last = nc.tensor.matmul(ps[:, 4 * l + 1, b * 128:(b + 1) * 128], xqT[l][:, b * 128:(b + 1) * 128], kq[:, :],
                                                    start=True, stop=True)
                        last.then_inc(y_ps[l], 1)

            @block.scalar
            def _(act):
                with act.Fori(0, ROUNDS) as i:
                    u1 = act.snap(i + 1)
                    for l in range(WIDE):
                        act.wait_ge(qT_ps[l], u1)
                        nc.scalar.copy(xqT[l][:, :], turned[l]).then_inc(qT_ready[l], 1)


def mixture_top1(nc, a, k, ps):
    NC = DFF // 128
    with ExitStack() as ctx:
        m = Buffers(nc, ctx, "p6")
        passed = m.sem("passed")
        f = norm_front(nc, m, k)
        xn, xT = m.lanes("xn", [128, GB, D], n=WIDE), m.lanes("xT", [128, 512], n=WIDE)
        lg, top, hit, before = (m.lanes(n, s, n=WIDE) for n, s in (("lg", [128, GB, E]), ("top", [128, GB]), ("hit", [128, GB, E]),
                                                                   ("before", [128, GB, E])))
        prior = m.lanes("prior", [128, GB, E, E], n=WIDE)
        sel, selT = m.lanes("sel", [128, GB, 32], n=WIDE), m.lanes("selT", [128, 128], n=WIDE)
        acc, pick = m.lanes("acc", [128, GB, D], n=WIDE), m.lanes("pick", [128, GB, D], n=WIDE)
        hT = [[m.sb(f"hT{l}_{c}", [128, 512]) for c in range(NC)] for l in range(WIDE)]
        (xT_ps, xT_ready, lg_ps, route, sel_ready, selT_ps, selT_ready, b_ps, acc_ready, h_ps, gelu_ready, y_ps, picked, x_done) = (
            m.sems(n, WIDE) for n in ("xT_ps", "xT", "lg_ps", "route", "sel", "selT_ps", "selT", "b_ps", "acc", "h_ps", "gelu",
                                      "y_ps", "picked", "x_done"))

        with nc.Block() as block:
            @block.vector
            def _(dve):
                for l in range(WIDE):
                    nc.vector.memset(sel[l][:, :, :], 0.0).then_inc(x_done[l], 1)
                    dve.sem_inc(picked[l], 2)
                    dve.wait_ge(x_done[l], 1)
                with dve.Fori(0, ROUNDS) as i:
                    u1 = dve.snap(i + 1)
                    norm_vector(nc, dve, k, f, xn, i, passed)
                    r = [dve.snap(i * 5 + j + 1) for j in range(5)]
                    for l in range(WIDE):
                        dve.wait_ge(lg_ps[l], u1)
                        nc.vector.tensor_tensor(lg[l][:, :, :], ps[:, 4 * l + 1, 0:GB * E].rearrange("p (b e) -> p b e", b=GB),
                                                bc(k["r_gateb"][:, :], 1, GB), ALU.add).then_inc(route[l], 1)
                    for l in range(WIDE):
                        dve.wait_ge(route[l], r[0])
                        nc.vector.tensor_reduce(top[l][:, :], lg[l][:, :, :], AX.X, ALU.max).then_inc(route[l], 1)
                    for l in range(WIDE):
                        dve.wait_ge(route[l], r[1])
                        nc.vector.tensor_tensor(hit[l][:, :, :], lg[l][:, :, :], bc(top[l][:, :], 2, E), ALU.is_equal).then_inc(route[l], 1)
                    for l in range(WIDE):
                        dve.wait_ge(route[l], r[2])
                        nc.vector.tensor_tensor(prior[l][:, :, :, :], bc(hit[l][:, :, :], 2, E), bc(k["lower"][:, :, :], 1, GB), ALU.mult
                                                ).then_inc(route[l], 1)
                    for l in range(WIDE):
                        dve.wait_ge(route[l], r[3])
                        nc.vector.tensor_reduce(before[l][:, :, :], prior[l][:, :, :, :], AX.X, ALU.add).then_inc(route[l], 1)
                    for l in range(WIDE):
                        dve.wait_ge(route[l], r[4])
                        nc.vector.scalar_tensor_tensor(out=sel[l][:, :, 0:E], in0=before[l][:, :, :], scalar=0.5, in1=hit[l][:, :, :],
                                                       op0=ALU.is_lt, op1=ALU.mult).then_inc(sel_ready[l], 1)
                    for l in range(WIDE):
                        dve.wait_ge(b_ps[l], u1)
                        dve.wait_ge(sel_ready[l], u1)
                        nc.vector.tensor_tensor(acc[l][:, :, :].rearrange("p b d -> p (b d)"), ps[:, 4 * l + 2, :],
                                                cols(k["x"], (i * WIDE + l) * GB, GB), ALU.add).then_inc(acc_ready[l], 1)
                    for e in range(E):
                        w = dve.snap(i * E + (e + 1))
                        w3 = dve.snap(i * E + (e + 3))
                        for l in range(WIDE):
                            dve.wait_ge(acc_ready[l], w)
                            dve.wait_ge(y_ps[l], w)
                            nc.vector.tensor_tensor(pick[l][:, :, :], ps[:, 4 * l + 2 + e % 2, :].rearrange("p (b d) -> p b d", b=GB),
                                                    bc(sel[l][:, :, e], 2, D), ALU.mult).then_inc(picked[l], 1)
                        for l in range(WIDE):
                            dve.wait_ge(picked[l], w3)
                            if e < E - 1:
                                nc.vector.tensor_tensor(acc[l][:, :, :], acc[l][:, :, :], pick[l][:, :, :], ALU.add).then_inc(acc_ready[l], 1)
                            else:
                                nc.vector.tensor_tensor(cols(k["x"], (i * WIDE + l) * GB, GB), acc[l][:, :, :].rearrange("p b d -> p (b d)"),
                                                        pick[l][:, :, :].rearrange("p b d -> p (b d)"), ALU.add).then_inc(x_done[l], 1)

            @block.gpsimd
            def _(pool):
                with pool.Fori(0, ROUNDS) as i:
                    norm_pool(nc, pool, k, f, i)

            @block.tensor
            def _(pe):
                pe.wait_ge(k["moe_loaded"], 32)
                pe.sem_inc(passed, 1)
                with pe.Fori(0, ROUNDS) as i:
                    u1 = pe.snap(i + 1)
                    for l in range(WIDE):
                        pe.wait_ge(x_done[l], u1)
                        pe.wait_ge(f["xn_ready"][l], u1)
                        for b in range(GB):
                            last = nc.tensor.transpose(ps[:, 4 * l, b * 128:(b + 1) * 128], xn[l][:, b, :], k["ident"][:, :])
                        last.then_inc(xT_ps[l], 1)
                    for l in range(WIDE):
                        pe.wait_ge(xT_ready[l], u1)
                        for b in range(GB):
                            last = nc.tensor.matmul(ps[:, 4 * l + 1, b * E:(b + 1) * E], xT[l][:, b * 128:(b + 1) * 128], k["gateW"][:, :],
                                                    start=True, stop=True)
                        last.then_inc(lg_ps[l], 1)
                    for l in range(WIDE):
                        pe.wait_ge(sel_ready[l], u1)
                        nc.tensor.transpose(ps[:, 4 * l + 1, 0:128], sel[l][:, :, :].rearrange("p b e -> p (b e)"), k["ident"][:, :]
                                            ).then_inc(selT_ps[l], 1)
                    for l in range(WIDE):
                        pe.wait_ge(selT_ready[l], u1)
                        nc.tensor.matmul(ps[:, 4 * l + 2, :], selT[l][:, :], k["b2blk"][:, :, :].rearrange("p b d -> p (b d)"),
                                         start=True, stop=True).then_inc(b_ps[l], 1)

                    def outputs(e):
                        g4 = pe.snap(i * (E * NC) + (e * NC + NC))
                        w = pe.snap(i * E + (e + 1))
                        for l in range(WIDE):
                            pe.wait_ge(gelu_ready[l], g4)
                            pe.wait_ge(picked[l], w)
                            if e == 0:
                                pe.wait_ge(acc_ready[l], w)
                            for b in range(GB):
                                for c in range(NC):
                                    last = nc.tensor.matmul(ps[:, 4 * l + 2 + e % 2, b * 128:(b + 1) * 128],
                                                            hT[l][c][:, b * 128:(b + 1) * 128], k["moe_w2"][:, e, c, :],
                                                            start=(c == 0), stop=(c == NC - 1))
                            last.then_inc(y_ps[l], 1)

                    for e in range(E):
                        for c in range(NC):
                            for l in range(WIDE):
                                if e * NC + c >= 2:
                                    pe.wait_ge(gelu_ready[l], i * (E * NC) + (e * NC + c - 1))
                                elif c == 1:
                                    pe.wait_ge(selT_ready[l], u1)
                                nc.tensor.matmul(ps[:, 4 * l + c % 2, :], k["moe_w1"][:, e, c * 128:(c + 1) * 128], xT[l][:, :],
                                                 start=True, stop=True).then_inc(h_ps[l], 1)
                        outputs(e)

            @block.scalar
            def _(act):
                with act.Fori(0, ROUNDS) as i:
                    u1 = act.snap(i + 1)
                    for l in range(WIDE):
                        act.wait_ge(xT_ps[l], u1)
                        nc.scalar.copy(xT[l][:, :], ps[:, 4 * l, :]).then_inc(xT_ready[l], 1)
                    for l in range(WIDE):
                        act.wait_ge(selT_ps[l], u1)
                        nc.scalar.copy(selT[l][:, :], ps[:, 4 * l + 1, 0:128]).then_inc(selT_ready[l], 1)
                    for e in range(E):
                        for c in range(NC):
                            for l in range(WIDE):
                                if e and c == 0:
                                    act.wait_ge(y_ps[l], i * E + e)
                                act.wait_ge(h_ps[l], i * (E * NC) + (e * NC + c + 1))
                                nc.scalar.activation(hT[l][c][:, :], ps[:, 4 * l + c % 2, :], ACT.Gelu,
                                                     bias=k["T_b1"][:, e * NC + c:e * NC + c + 1]).then_inc(gelu_ready[l], 1)


def adapters_top2(nc, a, k, ps):
    NC = E * BN // 128
    with ExitStack() as ctx:
        m = Buffers(nc, ctx, "p8")
        passed = m.sem("passed")
        f = norm_front(nc, m, k)
        L = lambda n, s: m.lanes(n, s, n=WIDE)
        xn, xT, pooled, gp = L("xn", [128, GB, D]), L("xT", [128, GB, 128]), L("pooled", [128, GB]), L("gp", [128, GB, E])
        lg, lg2, top, gate, tot, rtot = L("lg", [128, GB, E]), L("lg2", [128, GB, E]), L("top", [128, GB]), L("gate", [128, GB, E]), L("tot", [128, GB]), L("rtot", [128, GB])
        above, same, rank, kept = L("above", [128, GB, E, E]), L("same", [128, GB, E, E]), L("rank", [128, GB, E]), L("kept", [128, GB, E])
        tw, twT, twcol = L("tw", [128, GB, E]), L("twT", [GB * E, 128]), L("twcol", [128, NC, GB])
        h = [[m.sb(f"h{l}_{c}", [128, 512]) for c in range(NC)] for l in range(WIDE)]
        hs = [[m.sb(f"hs{l}_{c}", [128, 512]) for c in range(NC)] for l in range(WIDE)]
        xT_ps, xT_ready, gp_ready, lg_ps, route, exp_ready, tw_ready, twT_ps, twT_ready, h_ps, h_ready, hs_ready, y_ps, x_done = (
            m.sems(n, WIDE) for n in ("xT_ps", "xT", "gp", "lg_ps", "route", "exp", "tw", "twT_ps", "twT", "h_ps", "h", "hs", "y_ps",
                                      "x_done"))
        N_ROUTE = 16

        with nc.Block() as block:
            @block.vector
            def _(dve):
                for l in range(WIDE):
                    dve.sem_inc(x_done[l], 1)
                with dve.Fori(0, ROUNDS) as i:
                    u1 = dve.snap(i + 1)
                    norm_vector(nc, dve, k, f, xn, i, passed)
                    r = [dve.snap(i * N_ROUTE + j) if j else None for j in range(N_ROUTE + 1)]

                    def each(after, emit):
                        for l in range(WIDE):
                            dve.wait_ge(route[l], r[after])
                            emit(l).then_inc(route[l], 1)

                    for l in range(WIDE):
                        dve.wait_ge(xT_ready[l], u1)
                        nc.vector.tensor_reduce(pooled[l][:, :], xT[l][:, :, :], AX.X, ALU.add).then_inc(route[l], 1)
                    for l in range(WIDE):
                        dve.wait_ge(route[l], r[1])
                        nc.vector.tensor_tensor(gp[l][:, :, :], bc(k["T_gate"][:, :], 1, GB), bc(pooled[l][:, :], 2, E), ALU.mult
                                                ).then_inc(gp_ready[l], 1)
                    for l in range(WIDE):
                        dve.wait_ge(lg_ps[l], u1)
                        nc.vector.tensor_scalar(lg[l][:, :, :].rearrange("p b e -> p (b e)"), ps[:, 4 * l + 1, 0:GB * E], 1.0 / S, None,
                                                ALU.mult).then_inc(route[l], 1)
                    each(2, lambda l: nc.vector.tensor_reduce(top[l][:, :], lg[l][:, :, :], AX.X, ALU.max))
                    each(3, lambda l: nc.vector.tensor_tensor(lg2[l][:, :, :], lg[l][:, :, :], bc(top[l][:, :], 2, E), ALU.subtract))
                    for l in range(WIDE):
                        dve.wait_ge(exp_ready[l], u1)
                        nc.vector.tensor_reduce(tot[l][:, :], lg2[l][:, :, :], AX.X, ALU.add).then_inc(route[l], 1)
                    each(5, lambda l: nc.vector.reciprocal(rtot[l][:, :], tot[l][:, :]))
                    each(6, lambda l: nc.vector.tensor_tensor(gate[l][:, :, :], lg2[l][:, :, :], bc(rtot[l][:, :], 2, E), ALU.mult))
                    each(7, lambda l: nc.vector.tensor_tensor(above[l][:, :, :, :], bc(gate[l][:, :, :], 2, E), bc(gate[l][:, :, :], 3, E), ALU.is_gt))
                    each(7, lambda l: nc.vector.tensor_tensor(same[l][:, :, :, :], bc(gate[l][:, :, :], 2, E), bc(gate[l][:, :, :], 3, E), ALU.is_equal))
                    each(9, lambda l: nc.vector.tensor_tensor(same[l][:, :, :, :], same[l][:, :, :, :], bc(k["lower"][:, :, :], 1, GB), ALU.mult))
                    each(10, lambda l: nc.vector.tensor_tensor(above[l][:, :, :, :], above[l][:, :, :, :], same[l][:, :, :, :], ALU.add))
                    each(11, lambda l: nc.vector.tensor_reduce(rank[l][:, :, :], above[l][:, :, :, :], AX.X, ALU.add))
                    each(12, lambda l: nc.vector.scalar_tensor_tensor(out=kept[l][:, :, :], in0=rank[l][:, :, :], scalar=1.5,
                                                                      in1=gate[l][:, :, :], op0=ALU.is_lt, op1=ALU.mult))
                    each(13, lambda l: nc.vector.tensor_reduce(tot[l][:, :], kept[l][:, :, :], AX.X, ALU.add))
                    each(14, lambda l: nc.vector.tensor_scalar(tot[l][:, :], tot[l][:, :], 1e-8, None, ALU.add))
                    each(15, lambda l: nc.vector.reciprocal(rtot[l][:, :], tot[l][:, :]))
                    for l in range(WIDE):
                        dve.wait_ge(route[l], r[16])
                        nc.vector.tensor_tensor(tw[l][:, :, :], kept[l][:, :, :], bc(rtot[l][:, :], 2, E), ALU.mult).then_inc(tw_ready[l], 1)
                    for l in range(WIDE):
                        dve.wait_ge(tw_ready[l], i * 2 + 1)
                        for half in range(2):
                            v = tw[l][64 * half:64 * half + 64, :, :].rearrange("p b (c e) -> p c b e", e=2)[:, :, :, half]
                            last = nc.vector.tensor_copy(twcol[l][64 * half:64 * half + 64, :, :], v)
                        last.then_inc(tw_ready[l], 1)
                    for c in range(NC):
                        for l in range(WIDE):
                            if c == 0:
                                dve.wait_ge(tw_ready[l], i * 2 + 2)
                            dve.wait_ge(h_ready[l], i * NC + (c + 1))
                            nc.vector.tensor_tensor(hs[l][c][:, :].rearrange("p (b s) -> p b s", b=GB), h[l][c][:, :].rearrange("p (b s) -> p b s", b=GB),
                                                    bc(twcol[l][:, c, :], 2, 128), ALU.mult).then_inc(hs_ready[l], 1)
                    for l in range(WIDE):
                        dve.wait_ge(y_ps[l], u1)
                        xb = cols(k["x"], (i * WIDE + l) * GB, GB)
                        nc.vector.tensor_tensor(xb, xb, ps[:, 4 * l + 2, :], ALU.add).then_inc(x_done[l], 1)

            @block.gpsimd
            def _(pool):
                with pool.Fori(0, ROUNDS) as i:
                    norm_pool(nc, pool, k, f, i)

            @block.tensor
            def _(pe):
                with pe.Fori(0, ROUNDS) as i:
                    u1 = pe.snap(i + 1)
                    for l in range(WIDE):
                        pe.wait_ge(x_done[l], u1)
                        pe.wait_ge(f["xn_ready"][l], u1)
                        for b in range(GB):
                            last = nc.tensor.transpose(ps[:, 4 * l, b * 128:(b + 1) * 128], xn[l][:, b, :], k["ident"][:, :])
                        last.then_inc(xT_ps[l], 1)
                    for c in range(NC):
                        for l in range(WIDE):
                            pe.wait_ge(xT_ready[l], u1)
                            if c >= 2:
                                pe.wait_ge(h_ready[l], i * NC + (c - 1))
                            nc.tensor.matmul(ps[:, 4 * l + 3 * (c % 2), :], k["T_down"][:, c, :], xT[l][:, :, :].rearrange("p b s -> p (b s)"),
                                             start=True, stop=True).then_inc(h_ps[l], 1)
                    for l in range(WIDE):
                        pe.wait_ge(gp_ready[l], u1)
                        nc.tensor.matmul(ps[:, 4 * l + 1, 0:GB * E], k["ones"][:, :], gp[l][:, :, :].rearrange("p b e -> p (b e)"),
                                         start=True, stop=True).then_inc(lg_ps[l], 1)
                    for l in range(WIDE):
                        pe.wait_ge(tw_ready[l], i * 2 + 1)
                        nc.tensor.transpose(ps[0:GB * E, 4 * l + 1, 0:128], tw[l][:, :, :].rearrange("p b e -> p (b e)"), k["ident"][:, :]
                                            ).then_inc(twT_ps[l], 1)
                    for l in range(WIDE):
                        pe.wait_ge(twT_ready[l], u1)
                        pe.wait_ge(hs_ready[l], i * NC + NC)
                        nc.tensor.matmul(ps[:, 4 * l + 2, :], twT[l][:, :], k["up_b"][:, :, :].rearrange("p b d -> p (b d)"), start=True, stop=False)
                        for b in range(GB):
                            for c in range(NC):
                                last = nc.tensor.matmul(ps[:, 4 * l + 2, b * 128:(b + 1) * 128], hs[l][c][:, b * 128:(b + 1) * 128],
                                                        k["T_up"][:, c, :], start=False, stop=(b == GB - 1 and c == NC - 1))
                        last.then_inc(y_ps[l], 1)

            @block.scalar
            def _(act):
                with act.Fori(0, ROUNDS) as i:
                    u1 = act.snap(i + 1)
                    for l in range(WIDE):
                        act.wait_ge(xT_ps[l], u1)
                        nc.scalar.copy(xT[l][:, :, :].rearrange("p b s -> p (b s)"), ps[:, 4 * l, :]).then_inc(xT_ready[l], 1)
                    for c in range(NC):
                        for l in range(WIDE):
                            act.wait_ge(h_ps[l], i * NC + (c + 1))
                            nc.scalar.activation(h[l][c][:, :], ps[:, 4 * l + 3 * (c % 2), :], ACT.Gelu, bias=k["c_down_b"][:, c:c + 1]
                                                 ).then_inc(h_ready[l], 1)
                    for l in range(WIDE):
                        act.wait_ge(route[l], i * N_ROUTE + 4)
                        v = lg2[l][:, :, :].rearrange("p b e -> p (b e)")
                        nc.scalar.activation(v, v, ACT.Exp).then_inc(exp_ready[l], 1)
                    for l in range(WIDE):
                        act.wait_ge(twT_ps[l], u1)
                        nc.scalar.copy(twT[l][:, :], ps[0:GB * E, 4 * l + 1, 0:128]).then_inc(twT_ready[l], 1)



def build(nc, a, out):
    with ExitStack() as ctx:
        m = Buffers(nc, ctx, "k")
        k = {}
        for n, shape in (("x", [128, B, D]), ("ctxT", [128, B, S2]), ("negm", [128, B, S2]), ("ident", [128, 128]),
                         ("shift", [128, 128]), ("headmask", [128, XH]), ("ones", [128, 128]), ("minus_half", [128, 16]), ("eps", [128, 16]), ("huge", [128, 16]), ("eight", [128, DH]),
                         ("wpad", [128, 63]), ("up_b", [GB * E, GB, D]), ("b2blk", [128, GB, D]), ("T_b1", [128, E * DFF // 128]), ("gateW", [128, E]), ("lower", [128, E, E]),
                         ("iota", [128, S2]), ("pos", [128, 1]), ("Wcw", [128, 128]), ("Wcb", [128, 128]),
                         ("boffpos", [128, XH * NK]), ("span", [128, B]), ("rspan", [128, B]), ("sgn", [128, B]),
                         ("sscale", [128, 1]), ("T_Woff", [128, XH * NK]), ("T_gate", [128, E]), ("T_down", [128, 4, 128]),
                         ("T_up", [128, 4, 128]), ("T_Wk", [128, 128]), ("T_Wv", [128, 128]), ("T_Wq", [128, 128]),
                         ("T_Wo", [128, 128]), ("L0_W", [128, 128]), ("L0_Ws", [128, 128]), ("L1_Wq", [128, 128]),
                         ("L1_Wk", [128, 128]), ("L1_Wv", [128, 128]), ("L1_We", [128, 128]), ("L2_Wq", [128, 128]),
                         ("L2_Wk", [128, 128]), ("L2_Wv", [128, 128]), ("L2_Wo", [128, 128]),
                         ("c_L1_bq", [128, 1]), ("c_L1_bk", [128, 1]), ("c_L2_bq", [128, 1]), ("c_L2_bk", [128, 1]),
                         ("c_L3_bq", [128, 1]), ("c_L3_bk", [128, 1]), ("c_L0_b", [128, 1]), ("c_down_b", [128, 4]),
                         ("r_L1_bv", [128, D]), ("r_L1_bo", [128, D]), ("r_L2_bv", [128, D]), ("r_L2_bo", [128, D]),
                         ("r_L3_bv", [128, D]), ("r_L3_bo", [128, D]), ("r_L3_boff", [128, XH * NK]), ("r_bcw", [128, 1]),
                         ("r_bcb", [128, 1]), ("r_gateb", [128, E]), ("r_sin", [128, 1]), ("r_sk", [128, 1]),
                         ("cosS", [128, 2, DH]), ("sinS", [128, 2, DH])):
            k[n] = m.sb(n, shape)
        k["identb"] = m.sb("identb", [128, 128], BF16)
        k["band"] = m.sb("band", [128, 4, 128], BF16)
        k["fkernel"] = m.sb("fkernel", [128, 128], BF16)
        k["r_fbias"] = m.sb("r_fbias", [128, 128], BF16)
        ps = ctx.enter_context(nc.psum_tensor("ps", [128, 8, 512], F32))
        setup_phase(nc, a, k, ps)
        if 1 in PHASES:
            additive_attention(nc, a, k, ps)
        if 2 in PHASES:
            with ExitStack() as p2:
                k["z"] = p2.enter_context(nc.sbuf_tensor("k_z", [128, B, D], F32))
                normalise_all(nc, k, ps)
                local_transformer(nc, a, k, ps)
        if 3 in PHASES:
            cross_attention(nc, a, k, ps, "dense", {"phase": "p3", "Wq": k["L1_Wq"], "Wk": k["L1_Wk"], "Wv": k["L1_Wv"], "Wo": k["L1_We"],
                                                    "bq": k["c_L1_bq"], "bk": k["c_L1_bk"], "bv": k["r_L1_bv"], "bo": k["r_L1_bo"]})
        with ExitStack() as moe:
            k["moe_w1"] = moe.enter_context(nc.sbuf_tensor("k_moe_w1", [128, E, DFF], F32))
            k["moe_w2"] = moe.enter_context(nc.sbuf_tensor("k_moe_w2", [128, E, DFF // 128, D], F32))
            k["moe_loaded"] = m.sem("moe_loaded")
            if 6 in PHASES:
                with nc.Block() as block:
                    @block.sync
                    def _(sp):
                        sp.dma_start(k["moe_w1"][:, :, :], a["L2_ffn_W1"].rearrange("e d n -> d e n")).then_inc(k["moe_loaded"], 16)
                        sp.dma_start(k["moe_w2"][:, :, :, :].rearrange("p e c n -> p (e c) n"),
                                     a["L2_ffn_W2"].rearrange("e (c p) n -> p (e c) n", p=128)).then_inc(k["moe_loaded"], 16)
            if 4 in PHASES:
                quantised_dense(nc, a, k, ps)
            if 5 in PHASES:
                cross_attention(nc, a, k, ps, "dense", {"phase": "p5", "Wq": k["L2_Wq"], "Wk": k["L2_Wk"], "Wv": k["L2_Wv"],
                                                        "Wo": k["L2_Wo"], "bq": k["c_L2_bq"], "bk": k["c_L2_bk"],
                                                        "bv": k["r_L2_bv"], "bo": k["r_L2_bo"]})
            if 6 in PHASES:
                mixture_top1(nc, a, k, ps)
        if 7 in PHASES:
            cross_attention(nc, a, k, ps, "sampled", {"phase": "p7", "Wq": k["T_Wq"], "Wk": k["T_Wk"], "Wv": k["T_Wv"], "Wo": k["T_Wo"],
                                                      "bq": k["c_L3_bq"], "bk": k["c_L3_bk"], "bv": k["r_L3_bv"], "bo": k["r_L3_bo"]})
        if 8 in PHASES:
            adapters_top2(nc, a, k, ps)
        stored = m.sem("stored")
        with nc.Block() as block:
            @block.sync
            def _(sp):
                sp.dma_start(out.rearrange("b s d -> s b d"), k["x"][:, :, :]).then_inc(stored, 16)
                sp.wait_ge(stored, 16)


def rope_tables(np):
    half = np.arange(0, DH, 2, dtype=np.float32)
    inv_freq = (np.float32(1.0) / np.float32(10000.0) ** (half / np.float32(DH))).astype(np.float32)
    t = np.arange(S, dtype=np.float32)
    freqs = (t[:, None] * inv_freq[None, :]).astype(np.float32)
    base = ((half + np.float32(0.4 * DH)) / np.float32(1.4 * DH)).astype(np.float32)
    scale = base[None, :] ** ((t - S // 2) / np.float32(WINDOW // 2))[:, None]
    cos, sin = np.cos(freqs), np.sin(freqs)
    c = np.stack([np.concatenate([cos * f, cos * f], -1) for f in (scale, 1.0 / scale)], 1)
    s = np.stack([np.concatenate([-sin * f, sin * f], -1) for f in (scale, 1.0 / scale)], 1)
    return c.astype(np.float32), s.astype(np.float32)


_OUTS = [((B, S, D), 'float32')]


def kernel(**inputs):
    import numpy as _np
    import concourse.bacc as _bacc
    from concourse import mybir as _mybir
    from concourse.bass_utils import run_bass_kernel_spmd as _run

    nc = _bacc.Bacc("TRN2", target_bir_lowering=False, num_devices=1)
    arrays, args = {}, {}
    cos, sin = rope_tables(_np)
    named = dict(inputs)
    del named["mask_BxS_ff1"]
    named["rope_cos"] = cos
    named["rope_sin"] = sin
    for name, value in named.items():
        v = _np.ascontiguousarray(value)
        arrays[f"in_{name}_dram"] = v
        args[name] = nc.dram_tensor(f"in_{name}_dram", v.shape, _mybir.dt.from_np(v.dtype), kind="ExternalInput").ap()
    shape, dtype = _OUTS[0]
    out = nc.dram_tensor("out_0_dram", shape, _mybir.dt.from_np(_np.dtype(dtype)), kind="ExternalOutput").ap()
    build(nc, args, out)
    r = _run(nc, [arrays], core_ids=[0])
    return r.results[0]["out_0_dram"]
```

```python
from contextlib import ExitStack

import concourse.bass as bass
from concourse import mybir

ALU = mybir.AluOpType
ACT = mybir.ActivationFunctionType
AX = mybir.AxisListType
F32 = mybir.dt.float32
BF16 = mybir.dt.bfloat16
FP8 = mybir.dt.float8e4
I32 = mybir.dt.int32

B, S, D, S2 = 32, 128, 128, 77
LANES = 4
ITERS = B // LANES
WIDE = 2
GB = 4
ROUNDS = B // GB // WIDE
DEPTH, HEADS, DH = 6, 16, 64
INNER = HEADS * DH
HG = 8
WINDOW = 32
FF = int(D * 4 * 2 / 3)
FFC = [(0, 128), (128, 128), (256, FF - 256)]
XH, XD = 16, 8
NK = 5
DFF, E = 512, 8
BN = 64
NEG = -1e30
EPS = 1e-5
MAGIC = 1.5 * 2.0 ** 23
PHASES = (1, 2, 3, 4, 5, 6, 7, 8)


class Buffers:

    def __init__(self, nc, ctx, phase):
        self.nc, self.ctx, self.phase, self.held = nc, ctx, phase, []
        ctx.callback(self.free_sems)

    def free_sems(self):
        if self.held:
            self.nc.all_engine_barrier()
            self.nc.clear_and_free_semaphores(self.held)
            self.nc.all_engine_barrier()

    def sb(self, name, shape, dt=F32):
        return self.ctx.enter_context(self.nc.sbuf_tensor(f"{self.phase}_{name}", list(shape), dt))

    def lanes(self, name, shape, dt=F32, n=LANES):
        return [self.sb(f"{name}{i}", shape, dt) for i in range(n)]

    def sem(self, name):
        self.held.append(self.nc.alloc_semaphore(f"{self.phase}_{name}"))
        return self.held[-1]

    def sems(self, name, n=LANES):
        return [self.sem(f"{name}{i}") for i in range(n)]


def bc(ap, axis, n):
    shape = list(ap.shape)
    shape.insert(axis, n)
    return ap.unsqueeze(axis).to_broadcast(shape)


def cols(t, b, n=1):
    return t[:, bass.ds(b, n), :].rearrange("p b d -> p (b d)")


def setup_phase(nc, a, k, ps):
    with ExitStack() as ctx:
        m = Buffers(nc, ctx, "setup")
        s_load, s_zero, s_shape, s_x = m.sem("loaded"), m.sem("zeroed"), m.sem("shaped"), m.sem("x_loaded")
        s_turn, s_evac, s_int, s_col = m.sem("turned"), m.sem("turn_copied"), m.sem("mask_float"), m.sem("wide_column")
        raw = {n: m.sb(f"raw_{n}", [128, 128]) for n in ("Wk", "Wv", "Wq", "Wo", "Woff", "gate")}
        raw_b1 = m.sb("raw_b1", [E * DFF // 128, 128])
        raw_down = m.sb("raw_down", [128, 4, 128])
        raw_up = m.sb("raw_up", [128, E, BN])
        qmask = m.sb("qmask", [128, B * S2], I32)
        fmask = m.sb("fmask", [128, B * S2], I32)
        fmaskf = m.sb("fmaskf", [128, B, S2])
        iota_i = m.sb("iota_i", [128, S2], I32)
        pos_i = m.sb("pos_i", [128, 1], I32)
        col = m.sb("col", [128, 3])
        turns = [(raw[n][:, :], k[f"T_{n}"][:, :], 128) for n in ("Wk", "Wv", "Wq", "Wo")]
        turns += [(raw["Woff"][0:XH * NK, :], k["T_Woff"][:, :], XH * NK), (raw["gate"][0:E, :], k["T_gate"][:, :], E)]
        turns.append((raw_b1[:, :], k["T_b1"][:, :], E * DFF // 128))
        turns += [(raw_down[:, c, :], k["T_down"][:, c, :], 128) for c in range(4)]
        turns += [(raw_up[:, 2 * c:2 * c + 2, :].rearrange("p e n -> p (e n)"), k["T_up"][:, c, :], 128) for c in range(4)]

        loads = [(k["x"][:, :, :], a["x"].rearrange("b s d -> s b d"))]
        for n in ("Wk", "Wv", "Wq", "Wo"):
            loads.append((raw[n][:, :], a[f"L3_xattn_{n}"]))
        loads.append((raw["Woff"][0:XH * NK, :], a["L3_xattn_Woff"]))
        loads.append((raw["gate"][0:E, :], a["L3_ffn_gate_w"]))
        loads.append((raw_b1[:, :], a["L2_ffn_b1"].rearrange("e (c n) -> (e c) n", n=128)))
        loads.append((k["gateW"][:, :], a["L2_ffn_gate_W"]))
        loads.append((raw_down[:, :, :], a["L3_ffn_down_w"].rearrange("(c e) n d -> (e n) c d", c=4)))
        loads.append((raw_up[:, :, :], a["L3_ffn_up_w"].rearrange("e d n -> d e n")))
        loads.append((qmask[:, :], a["mask_BxS2_ik0"].rearrange("b s -> (b s)").partition_broadcast(128)))
        loads.append((fmask[:, :], a["mask_BxS2_if0"].rearrange("b s -> (b s)").partition_broadcast(128)))
        loads += [(col[:, 0:1], a["L0_xattn_w"]),
                  (col[:, 1:2], a["L0_xattn_Wcw"].rearrange("o d -> d o")),
                  (col[:, 2:3], a["L0_xattn_Wcb"].rearrange("o d -> d o"))]
        for n, src in (("L0_W", "L0_xattn_W"), ("L0_Ws", "L0_xattn_Ws"), ("L1_Wq", "L1_xattn_Wq"), ("L1_Wk", "L1_xattn_Wk"),
                       ("L1_Wv", "L1_xattn_Wv"), ("L1_We", "L1_xattn_We"), ("L2_Wq", "L2_xattn_Wq"), ("L2_Wo", "L2_xattn_Wo")):
            loads.append((k[n][:, :], a[src]))
        for n in ("Wk", "Wv"):
            for h in range(XH):
                loads.append((k[f"L2_{n}"][:, h * XD:(h + 1) * XD], a[f"L2_xattn_{n}"]))
        for h in range(XH):
            loads.append((k["c_L2_bk"][h * XD:(h + 1) * XD, :], a["L2_xattn_bk"].rearrange("(d o) -> d o", o=1)))
            loads.append((k["r_L2_bv"][:, h * XD:(h + 1) * XD], a["L2_xattn_bv"].partition_broadcast(128)))
        for n, src in (("c_L1_bq", "L1_xattn_bq"), ("c_L1_bk", "L1_xattn_bk"), ("c_L2_bq", "L2_xattn_bq"),
                       ("c_L3_bq", "L3_xattn_bq"), ("c_L3_bk", "L3_xattn_bk")):
            loads.append((k[n][:, :], a[src].rearrange("(d o) -> d o", o=1)))
        loads.append((k["c_L0_b"][:, :], a["L0_xattn_b"].rearrange("o d -> d o")))
        for n, src in (("r_L1_bv", "L1_xattn_bv"), ("r_L1_bo", "L1_xattn_be"), ("r_L2_bo", "L2_xattn_bo"),
                       ("r_L3_bv", "L3_xattn_bv"), ("r_L3_bo", "L3_xattn_bo"), ("r_L3_boff", "L3_xattn_boff"),
                       ("r_bcw", "L0_xattn_bcw"), ("r_bcb", "L0_xattn_bcb"), ("r_gateb", "L2_ffn_gate_b"),
                       ("r_sin", "L1_ffn_input_scale"), ("r_sk", "L1_ffn_kernel_scale"), ("r_fbias", "L1_ffn_bias")):
            loads.append((k[n][:, :], a[src].partition_broadcast(128)))
        loads.append((k["fkernel"][:, :], a["L1_ffn_kernel"]))
        loads.append((k["cosS"][:, :, :], a["rope_cos"]))
        loads.append((k["sinS"][:, :, :], a["rope_sin"]))
        for c in range(4):
            loads.append((k["c_down_b"][:, c:c + 1], a["L3_ffn_down_b"][2 * c:2 * c + 2, :].rearrange("e (n o) -> (e n) o", o=1)))

        with nc.Block() as block:
            @block.sync
            def _(sp):
                sp.wait_ge(s_zero, 16)
                for b in range(GB):
                    sp.dma_start(k["up_b"][E * b:E * b + E, b, :], a["L3_ffn_up_b"]).then_inc(s_load, 16)
                    sp.dma_start(k["b2blk"][32 * b:32 * b + E, b, :], a["L2_ffn_b2"]).then_inc(s_load, 16)
                for dst, src in loads:
                    sp.dma_start(dst, src).then_inc(s_load, 16)
                sp.wait_ge(s_load, 16 * (len(loads) + 2 * GB))

            n_loads = 16 * (len(loads) + 2 * GB)

            @block.gpsimd
            def _(pool):
                pool.memset(k["ident"][:, :], 0.0).then_inc(s_zero, 1)
                pool.memset(k["identb"][:, :], 0.0).then_inc(s_zero, 1)
                pool.memset(k["shift"][:, :], 0.0).then_inc(s_zero, 1)
                pool.memset(k["band"][:, :, :], 0.0).then_inc(s_zero, 1)
                pool.memset(k["headmask"][:, :], 1.0).then_inc(s_zero, 1)
                pool.memset(k["ones"][:, :], 1.0).then_inc(s_zero, 1)
                pool.memset(k["minus_half"][:, :], -0.5).then_inc(s_zero, 1)
                pool.memset(k["eps"][:, :], EPS).then_inc(s_zero, 1)
                pool.memset(k["huge"][:, :], 1e12).then_inc(s_zero, 1)
                pool.memset(k["eight"][:, :], 8.0).then_inc(s_zero, 1)
                pool.memset(k["wpad"][:, :], 0.0).then_inc(s_zero, 1)
                pool.memset(k["up_b"][:, :, :], 0.0).then_inc(s_zero, 1)
                pool.memset(k["b2blk"][:, :, :], 0.0).then_inc(s_zero, 1)
                pool.memset(k["lower"][:, :, :], 1.0).then_inc(s_zero, 1)
                pool.iota(iota_i[:, :], pattern=[[1, S2]], base=0, channel_multiplier=0).then_inc(s_zero, 1)
                pool.iota(pos_i[:, :], pattern=[[0, 1]], base=0, channel_multiplier=1).then_inc(s_zero, 1)
                pool.wait_ge(s_zero, 16)
                for n in ("ident", "identb"):
                    pool.affine_select(out=k[n][:, :], in_=k[n][:, :], compare_op=ALU.not_equal, fill=1.0, base=0,
                                       pattern=[[-1, 128]], channel_multiplier=1).then_inc(s_shape, 1)
                pool.affine_select(out=k["shift"][:, :], in_=k["shift"][:, :], compare_op=ALU.not_equal, fill=1.0,
                                   base=-1, pattern=[[1, 128]], channel_multiplier=-1).then_inc(s_shape, 1)
                pool.affine_select(out=k["band"][:, :, :], in_=k["band"][:, :, :], compare_op=ALU.is_ge, fill=NEG,
                                   base=0, pattern=[[0, 4], [-1, 128]], channel_multiplier=1).then_inc(s_shape, 1)
                pool.affine_select(out=k["headmask"][:, :], in_=k["headmask"][:, :], compare_op=ALU.is_ge, fill=0.0,
                                   base=0, pattern=[[-XD, XH]], channel_multiplier=1).then_inc(s_shape, 1)
                pool.affine_select(out=k["lower"][:, :, :], in_=k["lower"][:, :, :], compare_op=ALU.is_gt, fill=0.0,
                                   base=0, pattern=[[1, E], [-1, E]], channel_multiplier=0).then_inc(s_shape, 1)
                pool.wait_ge(s_shape, 6)
                pool.affine_select(out=k["band"][:, :, :], in_=k["band"][:, :, :], compare_op=ALU.is_ge, fill=NEG,
                                   base=WINDOW, pattern=[[0, 4], [1, 128]], channel_multiplier=-1).then_inc(s_shape, 1)
                pool.affine_select(out=k["headmask"][:, :], in_=k["headmask"][:, :], compare_op=ALU.is_ge, fill=0.0,
                                   base=XD - 1, pattern=[[XD, XH]], channel_multiplier=-1).then_inc(s_shape, 1)

            @block.tensor
            def _(pe):
                pe.wait_ge(s_load, n_loads)
                pe.wait_ge(s_shape, 8)
                for j, (src, _, n) in enumerate(turns):
                    if j >= 8:
                        pe.wait_ge(s_evac, j - 7)
                    nc.tensor.transpose(ps[:, j % 8, 0:n], src, k["ident"][0:n, 0:n]).then_inc(s_turn, 1)

            @block.scalar
            def _(act):
                for j, (_, dst, n) in enumerate(turns):
                    act.wait_ge(s_turn, j + 1)
                    nc.scalar.copy(dst, ps[:, j % 8, 0:n]).then_inc(s_evac, 1)

            @block.vector
            def _(dve):
                dve.wait_ge(s_load, n_loads)
                dve.wait_ge(s_zero, 16)
                nc.vector.tensor_copy(k["iota"][:, :], iota_i[:, :])
                nc.vector.tensor_copy(k["pos"][:, :], pos_i[:, :])
                nc.vector.tensor_copy(k["wpad"][:, 31:32], col[:, 0:1])
                nc.vector.tensor_scalar(k["Wcw"][:, :], k["ones"][:, :], col[:, 1:2], None, ALU.mult)
                nc.vector.tensor_scalar(k["Wcb"][:, :], k["ones"][:, :], col[:, 2:3], None, ALU.mult)
                nc.vector.tensor_scalar(k["negm"][:, :, :].rearrange("p b s -> p (b s)"), qmask[:, :], -1.0, 1.0,
                                        ALU.mult, ALU.add).then_inc(s_int, 1)
                nc.vector.tensor_scalar(fmaskf[:, :, :].rearrange("p b s -> p (b s)"), fmask[:, :], -1.0, 1.0,
                                        ALU.mult, ALU.add).then_inc(s_int, 1)
                for n in range(NK):
                    nc.vector.tensor_scalar(k["boffpos"][:, :].rearrange("p (h n) -> p h n", n=NK)[:, :, n],
                                            k["r_L3_boff"][:, :].rearrange("p (h n) -> p h n", n=NK)[:, :, n],
                                            float(-NK // 2 + n), None, ALU.add).then_inc(s_col, 1)
                dve.wait_ge(s_int, 2)
                nc.vector.tensor_scalar(k["negm"][:, :, :], k["negm"][:, :, :], NEG, None, ALU.mult)
                nc.vector.tensor_reduce(k["span"][:, :], fmaskf[:, :, :], AX.X, ALU.add).then_inc(s_int, 1)
                dve.wait_ge(s_col, NK)
                dve.wait_ge(s_int, 3)
                nc.vector.tensor_scalar(k["span"][:, :], k["span"][:, :], -1.0, None, ALU.add).then_inc(s_int, 1)
                nc.vector.tensor_tensor(k["sscale"][:, :], k["r_sin"][:, :], k["r_sk"][:, :], ALU.mult)
                dve.wait_ge(s_int, 4)
                nc.vector.tensor_scalar(k["sgn"][:, :], k["span"][:, :], 0.0, 2.0, ALU.is_ge, ALU.mult).then_inc(s_int, 1)
                dve.wait_ge(s_int, 5)
                nc.vector.tensor_scalar(k["sgn"][:, :], k["sgn"][:, :], -1.0, None, ALU.add).then_inc(s_int, 1)
                dve.wait_ge(s_int, 6)
                nc.vector.tensor_tensor(k["span"][:, :], k["span"][:, :], k["sgn"][:, :], ALU.mult).then_inc(s_int, 1)
                dve.wait_ge(s_int, 7)
                nc.vector.reciprocal(k["rspan"][:, :], k["span"][:, :])


def additive_attention(nc, a, k, ps):
    CF = 16
    NCH = S // CF
    RING = 4
    with ExitStack() as ctx:
        m = Buffers(nc, ctx, "p1")
        stat, mv, ve, rstd = m.lanes("stat", [128, 6]), m.lanes("mv", [128, 2]), m.lanes("ve", [128, 1]), m.lanes("rstd", [128, 1])
        xn, xnT = m.lanes("xn", [128, 128]), m.lanes("xnT", [128, 128])
        ctl, ctxT = m.lanes("ctl", [S2, 128]), m.lanes("ctxT", [128, S2])
        featT, proj = m.lanes("featT", [128, 128]), m.lanes("proj", [128, 3, S2])
        ring = m.lanes("ring", [128, 4, 4, S2], n=RING)
        sc, pr, tw = m.lanes("sc", [128, S2]), m.lanes("pr", [128, S2]), m.lanes("tw", [128, 2, S2])
        nm, den, rd, z, g = (m.lanes(n, [128, w]) for n, w in (("nm", 1), ("den", 1), ("rd", 1), ("z", 2), ("g", 2)))
        upd = m.lanes("upd", [128, 128])
        passed = m.sem("passed")
        ctx_loaded, ctx_free = m.sems("ctx_loaded"), m.sems("ctx_free")
        stats, moments, var_eps, rstd_ready, xn_ready = (m.sems(n) for n in ("stats", "moments", "var_eps", "rstd", "xn"))
        turned, turn_copied, projected, proj_copied = (m.sems(n) for n in ("turned", "turn_copied", "projected", "proj_copied"))
        summed, tanhed, dotted = m.sem("summed"), m.sem("tanhed"), m.sem("dotted")
        rho_ready = m.sems("rho_ready")
        masked, maxed, expd, weighted, gathered, scaled, gates, updated, x_done = (
            m.sems(n) for n in ("masked", "maxed", "expd", "weighted", "gathered", "scaled", "gates", "updated", "x_done"))
        ctxT_kept = m.sem("ctxT_kept")

        with nc.Block() as block:
            @block.sync
            def _(sp):
                with sp.Fori(0, ITERS) as i:
                    u1 = sp.snap(i + 1)
                    for l in range(LANES):
                        sp.wait_ge(ctx_free[l], u1)
                        sp.dma_start(ctl[l][:, :], a["ctx_1024"][bass.ds(i * LANES + l, 1), :, :].rearrange("b s d -> (b s) d")
                                     ).then_inc(ctx_loaded[l], 16)

            @block.tensor
            def _(pe):
                with pe.Fori(0, ITERS) as i:
                    u1 = pe.snap(i + 1)
                    u16 = pe.snap(i * 16 + 16)
                    for l in range(LANES):
                        pe.wait_ge(masked[l], u1)
                        pe.wait_ge(xn_ready[l], u1)
                        pe.wait_ge(ctx_loaded[l], u16)
                        nc.tensor.transpose(ps[:, 2 * l, 0:128], xn[l][:, :], k["ident"][:, :])
                        nc.tensor.transpose(ps[:, 2 * l, 128:128 + S2], ctl[l][:, :], k["ident"][0:S2, 0:S2]
                                            ).then_inc(turned[l], 1)
                    for l in range(LANES):
                        pe.wait_ge(turn_copied[l], u1)
                        nc.tensor.matmul(ps[:, 2 * l, 0:128], k["L0_W"][:, :], xnT[l][:, :], start=True, stop=True)
                        for j, w in enumerate(("L0_Ws", "Wcw", "Wcb")):
                            last = nc.tensor.matmul(ps[:, 2 * l, 128 + j * S2:128 + (j + 1) * S2], k[w][:, :], ctxT[l][:, :],
                                                    start=True, stop=True)
                        last.then_inc(projected[l], 1)
                    for l in range(LANES):
                        for c in range(NCH):
                            pe.wait_ge(tanhed, i * (LANES * NCH) + (l * NCH + c + 1))
                            for kk in range(4):
                                for q in range(4):
                                    row = 4 * c + kk
                                    last = nc.tensor.matmul(ps[32 * q:32 * q + 32, 2 * l + 1, 0:S2],
                                                            k["wpad"][:, 31 - row:63 - row], ring[c % RING][:, q, kk, :],
                                                            start=(row == 0), stop=(row == 31))
                            if c == NCH - 1:
                                last.then_inc(rho_ready[l], 1)
                                pe.wait_ge(rho_ready[l], u1)
                                pe.sem_inc(dotted, 1)
                            else:
                                last.then_inc(dotted, 1)

            @block.vector
            def _(dve):
                for l in range(LANES):
                    dve.sem_inc(masked[l], 1)
                    dve.sem_inc(ctx_free[l], 1)
                dve.sem_inc(dotted, RING)
                with dve.Fori(0, ITERS) as i:
                    u1, u2 = dve.snap(i + 1), dve.snap(i + 2)
                    for l in range(LANES):
                        nc.vector.bn_stats(stat[l][:, :], cols(k["x"], i * LANES + l)).then_inc(stats[l], 1)
                    dve.wait_ge(stats[LANES - 1], u1)
                    dve.sem_inc(passed, 1)
                    for l in range(LANES):
                        nc.vector.bn_aggr(mv[l][:, :], stat[l][:, :]).then_inc(moments[l], 1)
                    for l in range(LANES):
                        dve.wait_ge(rstd_ready[l], u1)
                        nc.vector.tensor_scalar(xn[l][:, :], cols(k["x"], i * LANES + l), mv[l][:, 0:1], rstd[l][:, 0:1],
                                                ALU.subtract, ALU.mult).then_inc(xn_ready[l], 1)
                    for l in range(LANES):
                        dve.wait_ge(proj_copied[l], u1)
                        for c in range(NCH):
                            dve.wait_ge(dotted, i * (LANES * NCH) + (l * NCH + c + 1))
                            feats = featT[l][:, :].rearrange("p (q c k) -> p q c k", q=4, c=NCH)[:, :, c, :]
                            for q in range(4):
                                last = nc.vector.tensor_tensor(ring[c % RING][:, q, :, :], bc(feats[:, q, :], 2, S2),
                                                               bc(proj[l][:, 0, :], 1, 4), ALU.add)
                            last.then_inc(summed, 1)
                    for l in range(LANES):
                        dve.wait_ge(rho_ready[l], u1)
                        nc.vector.tensor_tensor(sc[l][:, :], ps[:, 2 * l + 1, 0:S2], cols(k["negm"], i * LANES + l),
                                                ALU.add).then_inc(masked[l], 1)
                    for l in range(LANES):
                        dve.wait_ge(masked[l], u2)
                        nc.vector.tensor_reduce(nm[l][:, :], sc[l][:, :], AX.X, ALU.max, negate=True).then_inc(maxed[l], 1)
                    for l in range(LANES):
                        dve.wait_ge(expd[l], u1)
                        nc.vector.tensor_tensor(tw[l][:, :, :], bc(pr[l][:, :], 1, 2), proj[l][:, 1:3, :],
                                                ALU.mult).then_inc(weighted[l], 1)
                        nc.vector.reciprocal(rd[l][:, :], den[l][:, :]).then_inc(weighted[l], 1)
                    w2 = dve.snap(i * 2 + 2)
                    for l in range(LANES):
                        dve.wait_ge(weighted[l], w2)
                        nc.vector.tensor_reduce(z[l][:, :], tw[l][:, :, :], AX.X, ALU.add).then_inc(gathered[l], 1)
                    for l in range(LANES):
                        dve.wait_ge(gathered[l], u1)
                        nc.vector.tensor_scalar(z[l][:, :], z[l][:, :], rd[l][:, 0:1], None, ALU.mult).then_inc(scaled[l], 1)
                    for l in range(LANES):
                        dve.wait_ge(gates[l], u1)
                        nc.vector.tensor_scalar(upd[l][:, :], xn[l][:, :], g[l][:, 0:1], g[l][:, 1:2], ALU.mult, ALU.add
                                                ).then_inc(updated[l], 1)
                    for l in range(LANES):
                        dve.wait_ge(updated[l], u1)
                        nc.vector.tensor_tensor(cols(k["x"], i * LANES + l), cols(k["x"], i * LANES + l), upd[l][:, :],
                                                ALU.add).then_inc(x_done[l], 1)

            @block.scalar
            def _(act):
                with act.Fori(0, ITERS) as i:
                    u1 = act.snap(i + 1)
                    for l in range(LANES):
                        act.wait_ge(turned[l], u1)
                        nc.scalar.copy(xnT[l][:, :], ps[:, 2 * l, 0:128])
                        nc.scalar.copy(cols(k["ctxT"], i * LANES + l), ps[:, 2 * l, 128:128 + S2])
                        nc.scalar.copy(ctxT[l][:, :], ps[:, 2 * l, 128:128 + S2]).then_inc(turn_copied[l], 1)
                        act.sem_inc(ctx_free[l], 1)
                    for l in range(LANES):
                        act.wait_ge(projected[l], u1)
                        nc.scalar.activation(featT[l][:, :], ps[:, 2 * l, 0:128], ACT.Identity, bias=k["c_L0_b"][:, 0:1])
                        nc.scalar.copy(proj[l][:, :, :].rearrange("p j s -> p (j s)"), ps[:, 2 * l, 128:128 + 3 * S2]
                                       ).then_inc(proj_copied[l], 1)
                    for l in range(LANES):
                        for c in range(NCH):
                            act.wait_ge(summed, i * (LANES * NCH) + (l * NCH + c + 1))
                            h = ring[c % RING][:, :, :, :].rearrange("p q k s -> p (q k s)")
                            nc.scalar.activation(h, h, ACT.Tanh).then_inc(tanhed, 1)
                    for l in range(LANES):
                        act.wait_ge(maxed[l], u1)
                        nc.scalar.activation(pr[l][:, :], sc[l][:, :], ACT.Exp, bias=nm[l][:, 0:1],
                                             accum_out=den[l][:, 0:1]).then_inc(expd[l], 1)
                    for l in range(LANES):
                        act.wait_ge(scaled[l], u1)
                        nc.scalar.activation(g[l][:, 0:1], z[l][:, 0:1], ACT.Tanh, bias=k["r_bcw"][:, 0:1])
                        nc.scalar.activation(g[l][:, 1:2], z[l][:, 1:2], ACT.Tanh, bias=k["r_bcb"][:, 0:1]).then_inc(gates[l], 1)

            @block.gpsimd
            def _(pool):
                with pool.Fori(0, ITERS) as i:
                    u1 = pool.snap(i + 1)
                    for l in range(LANES):
                        pool.wait_ge(moments[l], u1)
                        nc.gpsimd.tensor_tensor(ve[l][:, :], mv[l][:, 1:2], k["eps"][:, 0:1], ALU.add).then_inc(var_eps[l], 1)
                        pool.wait_ge(var_eps[l], u1)
                        nc.gpsimd.tensor_tensor(rstd[l][:, :], ve[l][:, :], k["minus_half"][:, 0:1], ALU.pow
                                                ).then_inc(rstd_ready[l], 1)


def normalise_all(nc, k, ps):
    with ExitStack() as ctx:
        m = Buffers(nc, ctx, "p2n")
        stat, mv, ve, rstd = m.sb("stat", [128, B, 6]), m.sb("mv", [128, B, 2]), m.sb("ve", [128, B]), m.sb("rstd", [128, B])
        passed = m.sem("passed")
        stats, moments, var_eps, rstd_ready = (m.sem(n) for n in ("stats", "moments", "var_eps", "rstd"))
        with nc.Block() as block:
            @block.vector
            def _(dve):
                for b in range(B):
                    nc.vector.bn_stats(stat[:, b, :], k["x"][:, b, :]).then_inc(stats, 1)
                dve.wait_ge(stats, B)
                dve.sem_inc(passed, 1)
                for b in range(B):
                    nc.vector.bn_aggr(mv[:, b, :], stat[:, b, :]).then_inc(moments, 1)
                dve.wait_ge(rstd_ready, 1)
                for b in range(B):
                    nc.vector.tensor_scalar(k["z"][:, b, :], k["x"][:, b, :], mv[:, b, 0:1], rstd[:, b:b + 1],
                                            ALU.subtract, ALU.mult)

            @block.gpsimd
            def _(pool):
                pool.wait_ge(moments, B)
                nc.gpsimd.tensor_tensor(ve[:, :], mv[:, :, 1], k["eps"][:, 0:1].to_broadcast([128, B]), ALU.add).then_inc(var_eps, 1)
                pool.wait_ge(var_eps, 1)
                nc.gpsimd.tensor_tensor(rstd[:, :], ve[:, :], k["minus_half"][:, 0:1].to_broadcast([128, B]), ALU.pow
                                        ).then_inc(rstd_ready, 1)


def attention_layer(eng, layer, prefetch, slot):
    G = ((0, 1), (2, 3))

    def numbers(i):
        it = layer * ITERS + i
        return i, eng.snap(it + 1), (eng.snap(it * 2 + 1), eng.snap(it * 2 + 2))

    def turn(n, following):
        slot((G[1], 0, n), (G[0], 0, n, None))
        slot((G[0], 1, n), (G[1], 0, n, None))
        slot((G[1], 1, n), (G[0], 1, n, following))
        slot((G[0], 0, following) if following else None, (G[1], 1, n, following))

    first = numbers(0)
    for l in range(LANES):
        prefetch(l, first)
    slot((G[0], 0, first), None)
    with eng.Fori(0, ITERS - 1) as i:
        turn(numbers(i), numbers(i + 1))
    turn(numbers(ITERS - 1), None)


def local_transformer(nc, a, k, ps):
    QK = 2 * HG
    with ExitStack() as ctx:
        m = Buffers(nc, ctx, "p2")
        wqkv, wo = m.sb("wqkv", [128, 3, 2, HG * DH]), m.sb("wo", [128, HG, D])
        w1, w2 = m.sb("w1", [128, 2 * FF]), m.sb("w2", [128, 3, D])
        b1, gcol, bcol, b2 = m.sb("b1", [128, 2, 3]), m.sb("gcol", [128, 1]), m.sb("bcol", [128, 1]), m.sb("b2", [128, D])
        qks, tabA, tabB = m.sb("qks", [128, 2, DH]), m.sb("tabA", [128, 2, DH]), m.sb("tabB", [128, 2, DH])
        zl, zT = m.lanes("zl", [128, 128]), m.lanes("zT", [128, 128])
        sq = m.lanes("sq", [128, QK, DH])
        ropeB = sq
        qn = m.lanes("qn", [128, 2, HG, DH])
        probs = [t[:, :, :, :].rearrange("p a h d -> p (a h d)").rearrange("p (r j n) -> p r j n", r=2, j=4) for t in qn]
        rope = m.lanes("rope", [128, 2, HG, DH])
        oh = [t[:, 0, :, :] for t in rope]
        qkT = m.lanes("qkT", [128, 2, 4, 128])
        vx = m.lanes("vx", [128, HEADS, DH + 1])
        oT = m.lanes("oT", [128, HG, 128])
        ss, rn, rn1 = m.lanes("ss", [128, QK]), m.lanes("rn", [128, QK]), m.lanes("rn1", [128, QK])
        nm, rd = m.lanes("nm", [128, HG]), m.lanes("rd", [128, HG])

        attn_loaded, attn_free, ffn_loaded, ffn_free = (m.sem(n) for n in ("attn_loaded", "attn_free", "ffn_loaded", "ffn_free"))
        passed = m.sem("passed")
        tabs_half, tabs_ready = m.sem("tabs_half"), m.sem("tabs_ready")
        (zl_ready, zT_ps, zT_ready, v_ps, v_ready, qk_ps, sq_ready, ss_ready, ss_floored, rn_ready, qn_ready, ropeB_ready,
         ropeA_ready, rope_ready, qkT_ps, qkT_ready, s_ps, max_ready, sub_ready, p_ready, pT_ps, pT_ready, pv_ps, rd_ready,
         o_ready, oT_ps, oT_ready, y_ps, z_done) = (
            m.sems(n) for n in ("zl", "zT_ps", "zT", "v_ps", "v", "qk_ps", "sq", "ss", "ss_floored", "rn", "qn", "ropeB", "ropeA",
                                "rope", "qkT_ps", "qkT", "s_ps", "max", "sub", "p", "pT_ps", "pT", "pv_ps", "rd", "o",
                                "oT_ps", "oT", "y_ps", "z_done"))
        fz = [t[:, :, :, :].rearrange("p a h d -> p (a h d)")[:, 0:512].rearrange("p (b d) -> p b d", b=GB) for t in qn[0:WIDE]]
        fxn = [t[:, :, :, :].rearrange("p a h d -> p (a h d)")[:, 512:1024].rearrange("p (b d) -> p b d", b=GB) for t in qn[0:WIDE]]
        fsecond = [t[:, :, :].rearrange("p a d -> p (a d)")[:, 0:256].rearrange("p (b d) -> p b d", b=GB) for t in sq[0:WIDE]]
        fxT = [t[:, :, :, :].rearrange("p a h d -> p (a h d)")[:, 0:512] for t in qkT[0:WIDE]]
        fg = [t[:, :, :, :].rearrange("p a h d -> p (a h d)")[:, 0:512] for t in rope[0:WIDE]]
        fh = [[t[:, :, :].rearrange("p a d -> p (a d)")[:, 0:512] for t in (oT[l], oT[l + 2], sq[l + 2])] for l in range(WIDE)]
        fzb = [t[:, :, :, :].rearrange("p a h d -> p (a h d)")[:, 512:1024].rearrange("p (b d) -> p b d", b=GB) for t in rope[0:WIDE]]
        fst, fmv, fve, frs = (m.lanes(n, s, n=WIDE) for n, s in (("fst", [128, GB, 6]), ("fmv", [128, GB, 2]), ("fve", [128, GB]),
                                                                 ("frs", [128, GB])))
        (f_split, f_shift_ps, f_shifted, f_stats, f_moments, f_eps, f_rs, f_xn, f_xT_ps, f_xT, f_y_ps, f_zb, f_done) = (
            m.sems(n, WIDE) for n in ("f_split", "f_shift_ps", "f_shifted", "f_stats", "f_moments", "f_eps", "f_rs", "f_xn",
                                      "f_xT_ps", "f_xT", "f_y_ps", "f_zb", "f_done"))
        f_ag_ps, f_gelu, f_h = m.sems("f_ag_ps", WIDE), m.sems("f_gelu", WIDE), m.sems("f_h", WIDE)

        N_ATTN, N_FFN = 6, 4 + 3 + 6 - 2
        z = k["z"]

        with nc.Block() as block:
            @block.sync
            def _(sp):
                with sp.Fori(0, DEPTH) as layer:
                    n1 = sp.snap(layer + 1)
                    row = lambda t: a[f"L0_ffn_{t}"][bass.ds(layer, 1)]
                    sp.wait_ge(attn_free, n1)
                    for j in range(3):
                        sp.dma_start(wqkv[:, j, :, :], row("Wqkv").rearrange("o d (j h n) -> (o d) j h n", j=3, h=2)[:, j, :, :]
                                     ).then_inc(attn_loaded, 16)
                    sp.dma_start(wo[:, :, :], row("Wo").rearrange("o (c p) n -> p (o c) n", p=128)).then_inc(attn_loaded, 16)
                    sp.dma_start(qks[:, 0, :], row("q_scale").rearrange("o d -> (o d)").partition_broadcast(128)).then_inc(attn_loaded, 16)
                    sp.dma_start(qks[:, 1, :], row("k_scale").rearrange("o d -> (o d)").partition_broadcast(128)).then_inc(attn_loaded, 16)
                    sp.wait_ge(ffn_free, n1)
                    sp.dma_start(w1[:, :], row("W1").rearrange("o d n -> (o d) n")).then_inc(ffn_loaded, 16)
                    sp.dma_start(w2[:, 0:2, :], row("W2")[:, 0:256, :].rearrange("o (c p) n -> p (o c) n", p=128)).then_inc(ffn_loaded, 16)
                    sp.dma_start(w2[0:FF - 256, 2, :], row("W2")[:, 256:FF, :].rearrange("o p n -> (o p) n")).then_inc(ffn_loaded, 16)
                    for c, (f0, fn) in enumerate(FFC):
                        for half in range(2):
                            sp.dma_start(b1[0:fn, half, c:c + 1],
                                         row("b1")[:, half * FF + f0:half * FF + f0 + fn].rearrange("o d -> d o")).then_inc(ffn_loaded, 16)
                    sp.dma_start(gcol[:, :], row("ln_g").rearrange("o d -> d o")).then_inc(ffn_loaded, 16)
                    sp.dma_start(bcol[:, :], row("ln_b").rearrange("o d -> d o")).then_inc(ffn_loaded, 16)
                    sp.dma_start(b2[:, :], row("b2").rearrange("o d -> (o d)").partition_broadcast(128)).then_inc(ffn_loaded, 16)

            N_FFN_LOADS = 12

            @block.tensor
            def _(pe):
                def zT_turn(l, n):
                    pe.wait_ge(zl_ready[l], n[1])
                    nc.tensor.transpose(ps[:, 2 * l + 1, 0:128], zl[l][:, :], k["ident"][:, :]).then_inc(zT_ps[l], 1)

                def values(l, n, j):
                    if j == 0:
                        pe.wait_ge(zT_ready[l], n[1])
                    else:
                        pe.wait_ge(v_ready[l], n[2][0])
                    nc.tensor.matmul(ps[:, 2 * l + 1, :], zT[l][:, :], wqkv[:, 2, j, :], start=True, stop=True).then_inc(v_ps[l], 1)

                def prefetch(l, n):
                    zT_turn(l, n)
                    for j in range(2):
                        values(l, n, j)

                def queries_keys(l, h, n):
                    if h == 0:
                        pe.wait_ge(z_done[l], n[1])
                        pe.wait_ge(v_ready[l], n[2][1])
                    else:
                        pe.wait_ge(oT_ready[l], n[2][0])
                    for j in range(2):
                        last = nc.tensor.matmul(ps[:, 2 * l + j, :], zT[l][:, :], wqkv[:, j, h, :], start=True, stop=True)
                    last.then_inc(qk_ps[l], 1)

                def qkT_turn(l, h, n):
                    pe.wait_ge(rope_ready[l], n[2][h])
                    for j in range(2):
                        for c in range(4):
                            last = nc.tensor.transpose(ps[:, 2 * l + j, c * 128:(c + 1) * 128],
                                                       rope[l][:, j, 2 * c:2 * c + 2, :].rearrange("p h d -> p (h d)"), k["ident"][:, :])
                    last.then_inc(qkT_ps[l], 1)

                def scores(l, h, n):
                    pe.wait_ge(qkT_ready[l], n[2][h])
                    for r in range(2):
                        nc.tensor.matmul(ps[:, 2 * l + r, :], k["identb"][:, :], k["band"][:, :, :].rearrange("p j n -> p (j n)"),
                                         start=True, stop=False)
                    for c in range(4):
                        for r in range(2):
                            last = nc.tensor.matmul(ps[:, 2 * l + r, c * 128:(c + 1) * 128],
                                                    qkT[l][DH * r:DH * r + DH, 0, c, :], qkT[l][DH * r:DH * r + DH, 1, c, :],
                                                    start=False, stop=(c == 3))
                    last.then_inc(s_ps[l], 1)

                def probs_turn(l, h, n):
                    pe.wait_ge(p_ready[l], n[2][h])
                    for r in range(2):
                        for c in range(4):
                            last = nc.tensor.transpose(ps[:, 2 * l + r, c * 128:(c + 1) * 128], probs[l][:, r, c, :], k["ident"][:, :])
                    last.then_inc(pT_ps[l], 1)

                def values_sum(l, h, n):
                    pe.wait_ge(pT_ready[l], n[2][h])
                    for r in range(2):
                        for c in range(4):
                            last = nc.tensor.matmul(ps[:, 2 * l + r, c * (DH + 1):(c + 1) * (DH + 1)], qkT[l][:, r, c, :],
                                                    vx[l][:, h * HG + 2 * c + r, :], start=True, stop=True)
                    last.then_inc(pv_ps[l], 1)

                def out_turn(l, h, n):
                    pe.wait_ge(o_ready[l], n[2][h])
                    for c in range(4):
                        last = nc.tensor.transpose(ps[:, 2 * l, c * 128:(c + 1) * 128],
                                                   oh[l][:, 2 * c:2 * c + 2, :].rearrange("p h d -> p (h d)"), k["ident"][:, :])
                    last.then_inc(oT_ps[l], 1)

                def out_project(l, n):
                    pe.wait_ge(oT_ready[l], n[2][1])
                    for c in range(HG):
                        last = nc.tensor.matmul(ps[:, 2 * l, 0:128], oT[l][:, c, :], wo[:, c, :], start=(c == 0), stop=(c == HG - 1))
                    last.then_inc(y_ps[l], 1)

                def slot(P, A):
                    (p0, p1), ph, pn = P or ((0, 0), 0, None)
                    (a0, a1), ah, an, following = A or ((0, 0), 0, None, None)
                    ends = ah == 1
                    following = following if ends else None
                    if P:
                        queries_keys(p0, ph, pn)
                    if A:
                        scores(a0, ah, an)
                    if P:
                        queries_keys(p1, ph, pn)
                    if A:
                        scores(a1, ah, an)
                        probs_turn(a0, ah, an)
                        values_sum(a0, ah, an)
                        probs_turn(a1, ah, an)
                        out_turn(a0, ah, an)
                    if following:
                        zT_turn(a0, following)
                    if A:
                        values_sum(a1, ah, an)
                    if ends:
                        out_project(a0, an)
                    if P:
                        qkT_turn(p0, ph, pn)
                    if A:
                        out_turn(a1, ah, an)
                    if following:
                        values(a0, following, 0)
                        zT_turn(a1, following)
                    if ends:
                        out_project(a1, an)
                    if following:
                        values(a0, following, 1)
                        values(a1, following, 0)
                    if P:
                        qkT_turn(p1, ph, pn)
                    if following:
                        values(a1, following, 1)

                def ffn(it):
                    u1, w1_, w2_, w3 = pe.snap(it + 1), pe.snap(it * 3 + 1), pe.snap(it * 3 + 2), pe.snap(it * 3 + 3)
                    w = [w1_, w2_, w3]
                    for l in range(WIDE):
                        pe.wait_ge(f_split[l], u1)
                        pe.wait_ge(f_done[l], u1)
                        nc.tensor.matmul(ps[:, 4 * l, 0:256], k["shift"][:, :], fsecond[l], start=True, stop=True).then_inc(f_shift_ps[l], 1)
                    for l in range(WIDE):
                        pe.wait_ge(f_xn[l], u1)
                        for b in range(GB):
                            last = nc.tensor.transpose(ps[:, 4 * l + 1, b * 128:(b + 1) * 128], fxn[l][:, b, :], k["ident"][:, :])
                        last.then_inc(f_xT_ps[l], 1)
                    for c, (f0, fn) in enumerate(FFC):
                        for l in range(WIDE):
                            if c == 0:
                                pe.wait_ge(f_xT[l], u1)
                            if c == 2:
                                pe.wait_ge(f_h[l], w[0])
                            o = 4 * l + 2 * (c % 2)
                            nc.tensor.matmul(ps[0:fn, o, :], w1[:, f0:f0 + fn], fxT[l], start=True, stop=True)
                            nc.tensor.matmul(ps[0:fn, o + 1, :], w1[:, FF + f0:FF + f0 + fn], fxT[l], start=True, stop=True
                                             ).then_inc(f_ag_ps[l], 1)
                    for l in range(WIDE):
                        pe.wait_ge(f_h[l], w[2])
                        for b in range(GB):
                            for c, (f0, fn) in enumerate(FFC):
                                last = nc.tensor.matmul(ps[:, 4 * l + 2, b * 128:(b + 1) * 128], fh[l][c][0:fn, b * 128:(b + 1) * 128],
                                                        w2[0:fn, c, :], start=(c == 0), stop=(c == 2))
                        last.then_inc(f_y_ps[l], 1)

                with pe.Fori(0, DEPTH) as layer:
                    pe.wait_ge(attn_loaded, layer * (16 * N_ATTN) + 16 * N_ATTN)
                    pe.sem_inc(passed, 1)
                    attention_layer(pe, layer, prefetch, slot)
                    for l in range(LANES):
                        pe.wait_ge(y_ps[l], layer * ITERS + ITERS)
                    pe.sem_inc(attn_free, 1)
                    pe.wait_ge(ffn_loaded, layer * (16 * N_FFN_LOADS) + 16 * N_FFN_LOADS)
                    pe.sem_inc(passed, 1)
                    with pe.Fori(0, ROUNDS) as i:
                        ffn(layer * ROUNDS + i)

            @block.vector
            def _(dve):
                for l in range(LANES):
                    nc.vector.memset(vx[l][:, :, DH:DH + 1], 1.0)
                    nc.vector.memset(zT[l][64:128, 0:1], 0.0).then_inc(z_done[l], 1)
                for l in range(WIDE):
                    dve.sem_inc(f_done[l], 1)

                def prefetch(l, n):
                    pass

                def norms(l, h, n):
                    dve.wait_ge(sq_ready[l], n[2][h])
                    nc.vector.tensor_reduce(ss[l][:, :], sq[l][:, :, :], AX.X, ALU.add).then_inc(ss_ready[l], 1)

                def normalise(l, h, n):
                    dve.wait_ge(rn_ready[l], n[2][h])
                    nc.vector.tensor_tensor(qn[l][:, :, :, :].rearrange("p a h d -> p (a h) d"),
                                            ps[:, 2 * l:2 * l + 2, :].rearrange("p a (h d) -> p (a h) d", d=DH),
                                            bc(rn[l][:, :], 2, DH), ALU.mult).then_inc(qn_ready[l], 1)

                def rotate(l, h, n):
                    dve.wait_ge(qn_ready[l], n[2][h])
                    nc.vector.tensor_tensor(rope[l][:, :, :, :], qn[l][:, :, :, :], bc(tabA[:, :, :], 2, HG), ALU.mult
                                            ).then_inc(ropeA_ready[l], 1)

                def rotate_sum(l, h, n):
                    dve.wait_ge(ropeA_ready[l], n[2][h])
                    dve.wait_ge(ropeB_ready[l], n[2][h])
                    flat = rope[l][:, :, :, :].rearrange("p a h d -> p (a h d)")
                    nc.vector.tensor_tensor(flat, flat, ropeB[l][:, :, :].rearrange("p h d -> p (h d)"), ALU.add
                                            ).then_inc(rope_ready[l], 1)

                def largest(l, h, n):
                    dve.wait_ge(s_ps[l], n[2][h])
                    nc.vector.tensor_reduce(nm[l][:, :], ps[:, 2 * l:2 * l + 2, :].rearrange("p r (j n) -> p (r j) n", n=128),
                                            AX.X, ALU.max).then_inc(max_ready[l], 1)

                def less_largest(l, h, n):
                    dve.wait_ge(max_ready[l], n[2][h])
                    nc.vector.tensor_tensor(probs[l].rearrange("p r j n -> p (r j) n"),
                                            ps[:, 2 * l:2 * l + 2, :].rearrange("p r (j n) -> p (r j) n", n=128),
                                            bc(nm[l][:, :], 2, 128), ALU.subtract).then_inc(sub_ready[l], 1)

                def inverse_sums(l, h, n):
                    dve.wait_ge(pv_ps[l], n[2][h])
                    pv = ps[:, 2 * l:2 * l + 2, 0:4 * (DH + 1)].rearrange("p r (j d) -> p r j d", d=DH + 1)
                    nc.vector.reciprocal(rd[l][:, :].rearrange("p (r j) -> p r j", r=2), pv[:, :, :, DH]).then_inc(rd_ready[l], 1)

                def outputs(l, h, n):
                    dve.wait_ge(rd_ready[l], n[2][h])
                    pv = ps[:, 2 * l:2 * l + 2, 0:4 * (DH + 1)].rearrange("p r (j d) -> p r j d", d=DH + 1)
                    nc.vector.tensor_tensor(oh[l].rearrange("p (j r) d -> p r j d", r=2), pv[:, :, :, 0:DH],
                                            bc(rd[l][:, :].rearrange("p (r j) -> p r j", r=2), 3, DH), ALU.mult
                                            ).then_inc(o_ready[l], 1)

                def add_to_stream(l, n):
                    dve.wait_ge(y_ps[l], n[1])
                    zb = cols(z, n[0] * LANES + l)
                    nc.vector.tensor_tensor(zb, zb, ps[:, 2 * l, 0:128], ALU.add).then_inc(z_done[l], 1)

                def slot(P, A):
                    (p0, p1), ph, pn = P or ((0, 0), 0, None)
                    (a0, a1), ah, an, following = A or ((0, 0), 0, None, None)
                    ends = ah == 1
                    following = following if ends else None
                    if P:
                        norms(p0, ph, pn)
                    if A:
                        largest(a0, ah, an)
                        less_largest(a0, ah, an)
                    if P:
                        norms(p1, ph, pn)
                    if A:
                        largest(a1, ah, an)
                        less_largest(a1, ah, an)
                    if P:
                        normalise(p0, ph, pn)
                    if A:
                        inverse_sums(a0, ah, an)
                        outputs(a0, ah, an)
                    if P:
                        rotate(p0, ph, pn)
                        normalise(p1, ph, pn)
                        rotate_sum(p0, ph, pn)
                    if A:
                        inverse_sums(a1, ah, an)
                    if P:
                        rotate(p1, ph, pn)
                    if A:
                        outputs(a1, ah, an)
                    if P:
                        rotate_sum(p1, ph, pn)
                    if ends:
                        add_to_stream(a1, an)
                        add_to_stream(a0, an)

                def ffn(layer, i):
                    it = layer * ROUNDS + i
                    u1, u4 = dve.snap(it + 1), dve.snap(it * 4 + 4)
                    w = [dve.snap(it * 3 + 1), dve.snap(it * 3 + 2), dve.snap(it * 3 + 3)]
                    for l in range(WIDE):
                        dve.wait_ge(f_shifted[l], u1)
                        for b in range(GB):
                            nc.vector.bn_stats(fst[l][:, b, :], fz[l][:, b, :]).then_inc(f_stats[l], 1)
                    for l in range(WIDE):
                        dve.wait_ge(f_stats[l], u4)
                        dve.sem_inc(passed, 1)
                        for b in range(GB):
                            last = nc.vector.bn_aggr(fmv[l][:, b, :], fst[l][:, b, :])
                        last.then_inc(f_moments[l], 1)
                    for l in range(WIDE):
                        dve.wait_ge(f_rs[l], u1)
                        for b in range(GB):
                            last = nc.vector.tensor_scalar(fxn[l][:, b, :], fz[l][:, b, :], fmv[l][:, b, 0:1], frs[l][:, b:b + 1],
                                                           ALU.subtract, ALU.mult)
                        last.then_inc(f_xn[l], 1)
                    for c, (f0, fn) in enumerate(FFC):
                        for l in range(WIDE):
                            dve.wait_ge(f_gelu[l], w[c])
                            nc.vector.scalar_tensor_tensor(out=fh[l][c][0:fn, :], in0=ps[0:fn, 4 * l + 2 * (c % 2), :],
                                                           scalar=b1[0:fn, 0, c:c + 1], in1=fg[l][0:fn, :], op0=ALU.add, op1=ALU.mult
                                                           ).then_inc(f_h[l], 1)
                    for l in range(WIDE):
                        dve.wait_ge(f_y_ps[l], u1)
                        dve.wait_ge(f_zb[l], u1)
                        nc.vector.tensor_tensor(cols(z, (i * WIDE + l) * GB, GB), fzb[l].rearrange("p b d -> p (b d)"),
                                                ps[:, 4 * l + 2, :], ALU.add).then_inc(f_done[l], 1)

                with dve.Fori(0, DEPTH) as layer:
                    dve.wait_ge(tabs_ready, layer * 2 + 2)
                    for l in range(WIDE):
                        dve.wait_ge(f_done[l], layer * ROUNDS + 1)
                    dve.sem_inc(passed, 1)
                    attention_layer(dve, layer, prefetch, slot)
                    for l in range(LANES):
                        dve.wait_ge(z_done[l], layer * ITERS + (ITERS + 1))
                    dve.wait_ge(ffn_loaded, layer * (16 * N_FFN_LOADS) + 16 * N_FFN_LOADS)
                    dve.sem_inc(passed, 1)
                    with dve.Fori(0, ROUNDS) as i:
                        ffn(layer, i)
                    for l in range(WIDE):
                        dve.wait_ge(f_done[l], layer * ROUNDS + (ROUNDS + 1))
                    dve.sem_inc(ffn_free, 1)
                for b in range(0, B, GB):
                    nc.vector.tensor_tensor(k["x"][:, b:b + GB, :], k["x"][:, b:b + GB, :], z[:, b:b + GB, :], ALU.add)

            @block.scalar
            def _(act):
                def z_lane(l, n):
                    nc.scalar.copy(zl[l][:, :], cols(z, n[0] * LANES + l)).then_inc(zl_ready[l], 1)

                def zT_copy(l, n):
                    act.wait_ge(zT_ps[l], n[1])
                    nc.scalar.copy(zT[l][0:64, :], ps[0:64, 2 * l + 1, 0:128])
                    nc.scalar.copy(zT[l][64:128, 1:128], ps[64:128, 2 * l + 1, 0:127]).then_inc(zT_ready[l], 1)

                def values_copy(l, n, j):
                    act.wait_ge(v_ps[l], n[2][j])
                    nc.scalar.copy(vx[l][:, HG * j:HG * j + HG, 0:DH], ps[:, 2 * l + 1, :].rearrange("p (h d) -> p h d", d=DH)
                                   ).then_inc(v_ready[l], 1)

                def prefetch(l, n):
                    z_lane(l, n)
                    zT_copy(l, n)
                    for j in range(2):
                        values_copy(l, n, j)

                def squares(l, h, n):
                    act.wait_ge(qk_ps[l], n[2][h])
                    nc.scalar.activation(sq[l][:, :, :].rearrange("p h d -> p (h d)"),
                                         ps[:, 2 * l:2 * l + 2, :].rearrange("p a n -> p (a n)"), ACT.Square).then_inc(sq_ready[l], 1)

                def qkT_copy(l, h, n):
                    act.wait_ge(qkT_ps[l], n[2][h])
                    nc.scalar.copy(qkT[l][:, :, :, :].rearrange("p a c n -> p (a c n)"),
                                   ps[:, 2 * l:2 * l + 2, :].rearrange("p a n -> p (a n)")).then_inc(qkT_ready[l], 1)

                def exponent(l, h, n):
                    act.wait_ge(sub_ready[l], n[2][h])
                    pf = probs[l].rearrange("p r j n -> p (r j n)")
                    nc.scalar.activation(pf, pf, ACT.Exp).then_inc(p_ready[l], 1)

                def pT_copy(l, h, n):
                    act.wait_ge(pT_ps[l], n[2][h])
                    nc.scalar.copy(qkT[l][:, :, :, :].rearrange("p a c n -> p (a c n)"),
                                   ps[:, 2 * l:2 * l + 2, :].rearrange("p a n -> p (a n)")).then_inc(pT_ready[l], 1)

                def oT_copy(l, h, n):
                    act.wait_ge(oT_ps[l], n[2][h])
                    nc.scalar.copy(oT[l][:, 4 * h:4 * h + 4, :].rearrange("p c n -> p (c n)"), ps[:, 2 * l, :]).then_inc(oT_ready[l], 1)

                def slot(P, A):
                    (p0, p1), ph, pn = P or ((0, 0), 0, None)
                    (a0, a1), ah, an, following = A or ((0, 0), 0, None, None)
                    ends = ah == 1
                    following = following if ends else None
                    if P:
                        squares(p0, ph, pn)
                        squares(p1, ph, pn)
                    if A:
                        exponent(a0, ah, an)
                        pT_copy(a0, ah, an)
                    if following:
                        z_lane(a0, following)
                    if A:
                        exponent(a1, ah, an)
                        pT_copy(a1, ah, an)
                    if following:
                        z_lane(a1, following)
                        zT_copy(a0, following)
                    if A:
                        oT_copy(a0, ah, an)
                        oT_copy(a1, ah, an)
                    if following:
                        values_copy(a0, following, 0)
                    if P:
                        qkT_copy(p0, ph, pn)
                    if following:
                        zT_copy(a1, following)
                        values_copy(a0, following, 1)
                        values_copy(a1, following, 0)
                        values_copy(a1, following, 1)
                    if P:
                        qkT_copy(p1, ph, pn)

                def ffn(layer, i):
                    it = layer * ROUNDS + i
                    u1 = act.snap(it + 1)
                    w = [act.snap(it * 3 + 1), act.snap(it * 3 + 2), act.snap(it * 3 + 3)]
                    for l in range(WIDE):
                        act.wait_ge(f_done[l], u1)
                        zb = z[:, bass.ds((i * WIDE + l) * GB, GB), :]
                        nc.scalar.copy(fz[l][:, :, 0:64], zb[:, :, 0:64])
                        nc.scalar.copy(fsecond[l], zb[:, :, 64:128]).then_inc(f_split[l], 1)
                    for l in range(WIDE):
                        act.wait_ge(f_shift_ps[l], u1)
                        nc.scalar.copy(fz[l][:, :, 64:128], ps[:, 4 * l, 0:256].rearrange("p (b d) -> p b d", b=GB)).then_inc(f_shifted[l], 1)
                    for l in range(WIDE):
                        act.wait_ge(f_xT_ps[l], u1)
                        nc.scalar.activation(fxT[l], ps[:, 4 * l + 1, :], ACT.Identity, scale=gcol[:, 0:1], bias=bcol[:, 0:1]
                                             ).then_inc(f_xT[l], 1)
                    for c, (f0, fn) in enumerate(FFC):
                        for l in range(WIDE):
                            act.wait_ge(f_ag_ps[l], w[c])
                            if c > 0:
                                act.wait_ge(f_h[l], w[c - 1])
                            nc.scalar.activation(fg[l][0:fn, :], ps[0:fn, 4 * l + 2 * (c % 2) + 1, :], ACT.Gelu,
                                                 bias=b1[0:fn, 1, c:c + 1]).then_inc(f_gelu[l], 1)

                with act.Fori(0, DEPTH) as layer:
                    for l in range(LANES):
                        act.wait_ge(z_done[l], layer * ITERS + 1)
                    for l in range(WIDE):
                        act.wait_ge(f_done[l], layer * ROUNDS + 1)
                    attention_layer(act, layer, prefetch, slot)
                    for l in range(LANES):
                        act.wait_ge(z_done[l], layer * ITERS + (ITERS + 1))
                    act.wait_ge(ffn_loaded, layer * (16 * N_FFN_LOADS) + 16 * N_FFN_LOADS)
                    with act.Fori(0, ROUNDS) as i:
                        ffn(layer, i)

            @block.gpsimd
            def _(pool):
                pool.sem_inc(attn_free, 1)
                pool.sem_inc(ffn_free, 1)
                H2 = DH // 2

                def prefetch(l, n):
                    pass

                def inverse_norms(l, h, n):
                    pool.wait_ge(ss_ready[l], n[2][h])
                    pool.sem_inc(passed, 1)
                    nc.gpsimd.tensor_scalar(rn1[l][:, :], ss[l][:, :], 1e-24, None, ALU.max).then_inc(ss_floored[l], 1)
                    pool.wait_ge(ss_floored[l], n[2][h])
                    nc.gpsimd.tensor_tensor(rn[l][:, :], rn1[l][:, :], k["minus_half"][:, :], ALU.pow).then_inc(rn_ready[l], 1)

                def rotate_partner(l, h, n):
                    pool.wait_ge(qn_ready[l], n[2][h])
                    out = ropeB[l][:, :, :].rearrange("p (a h) d -> p a h d", a=2)
                    for half in range(2):
                        last = nc.gpsimd.tensor_tensor(out[:, :, :, half * H2:(half + 1) * H2],
                                                       qn[l][:, :, :, (1 - half) * H2:(2 - half) * H2],
                                                       bc(tabB[:, :, half * H2:(half + 1) * H2], 2, HG), ALU.mult)
                    last.then_inc(ropeB_ready[l], 1)

                def slot(P, A):
                    (p0, p1), ph, pn = P or ((0, 0), 0, None)
                    (a0, a1), ah, an, following = A or ((0, 0), 0, None, None)
                    ends = ah == 1
                    following = following if ends else None
                    if P:
                        inverse_norms(p0, ph, pn)
                        inverse_norms(p1, ph, pn)
                        rotate_partner(p0, ph, pn)
                        rotate_partner(p1, ph, pn)

                def ffn(layer, i):
                    it = layer * ROUNDS + i
                    u1 = pool.snap(it + 1)
                    for l in range(WIDE):
                        pool.wait_ge(f_moments[l], u1)
                        nc.gpsimd.tensor_tensor(fve[l][:, :], fmv[l][:, :, 1], k["eps"][:, 0:GB], ALU.add).then_inc(f_eps[l], 1)
                    for l in range(WIDE):
                        pool.wait_ge(f_eps[l], u1)
                        nc.gpsimd.tensor_tensor(frs[l][:, :], fve[l][:, :], k["minus_half"][:, 0:GB], ALU.pow).then_inc(f_rs[l], 1)
                    for l in range(WIDE):
                        pool.wait_ge(f_xT[l], u1)
                        nc.gpsimd.tensor_tensor(fzb[l], z[:, bass.ds((i * WIDE + l) * GB, GB), :], bc(b2[:, :], 1, GB), ALU.add
                                                ).then_inc(f_zb[l], 1)

                with pool.Fori(0, DEPTH) as layer:
                    pool.wait_ge(attn_loaded, layer * (16 * N_ATTN) + 16 * N_ATTN)
                    for l in range(LANES):
                        pool.wait_ge(z_done[l], layer * ITERS + 1)
                    for l in range(WIDE):
                        pool.wait_ge(f_done[l], layer * ROUNDS + 1)
                    nc.gpsimd.tensor_tensor(qks[:, 0, :], qks[:, 0, :], k["eight"][:, :], ALU.mult).then_inc(tabs_half, 1)
                    pool.wait_ge(tabs_half, layer + 1)
                    nc.gpsimd.tensor_tensor(tabA[:, :, :], qks[:, :, :], k["cosS"][:, :, :], ALU.mult).then_inc(tabs_ready, 1)
                    for half in range(2):
                        last = nc.gpsimd.tensor_tensor(tabB[:, :, half * H2:(half + 1) * H2], qks[:, :, (1 - half) * H2:(2 - half) * H2],
                                                       k["sinS"][:, :, half * H2:(half + 1) * H2], ALU.mult)
                    last.then_inc(tabs_ready, 1)
                    pool.wait_ge(tabs_ready, layer * 2 + 2)
                    pool.sem_inc(passed, 1)
                    attention_layer(pool, layer, prefetch, slot)
                    pool.wait_ge(ffn_loaded, layer * (16 * N_FFN_LOADS) + 16 * N_FFN_LOADS)
                    for l in range(LANES):
                        pool.wait_ge(z_done[l], layer * ITERS + (ITERS + 1))
                    pool.sem_inc(passed, 1)
                    with pool.Fori(0, ROUNDS) as i:
                        ffn(layer, i)


def cross_attention(nc, a, k, ps, kind, w):
    C2 = 4
    scale = float(XD) ** -0.5 * (0.5 if kind == "sampled" else 1.0)
    with ExitStack() as ctx:
        m = Buffers(nc, ctx, w["phase"])
        passed = m.sem("passed")
        stat, mv, ve, rstd = m.lanes("stat", [128, 6]), m.lanes("mv", [128, 2]), m.lanes("ve", [128, 1]), m.lanes("rstd", [128, 1])
        xn, xnT, ctxT = m.lanes("xn", [128, 128]), m.lanes("xnT", [128, 128]), m.lanes("ctxT", [128, S2])
        qT, kT = m.lanes("qT", [128, 128]), m.lanes("kT", [128, S2])
        vx = m.lanes("vx", [S2, XH, XD + 1])
        kbd = m.lanes("kbd", [128, XH, S2])
        probs, pT = m.lanes("probs", [128, HG, S2]), m.lanes("pT", [S2, HG, 128])
        nm, rd = m.lanes("nm", [128, HG]), m.lanes("rd", [128, HG])
        o, oT, yb = m.lanes("o", [128, XH, XD]), m.lanes("oT", [128, 128]), m.lanes("yb", [128, 128])
        (stats, moments, var_eps, rstd_ready, xn_ready, xT_ps, xT_ready, qkv_ps, q_ready, kbd_ready, v_ready, s_ps,
         p_ready, pT_ps, pT_ready, pv_ps, o_ready, oT_ps, oT_ready, y_ps, yb_ready, x_done,
         k_ready) = (
            m.sems(n) for n in ("stats", "moments", "var_eps", "rstd", "xn", "xT_ps", "xT", "qkv_ps", "q", "kbd", "v", "s_ps",
                                "p", "pT_ps", "pT", "pv_ps", "o", "oT_ps", "oT", "y_ps", "yb", "x_done", "k"))
        sampled = kind == "sampled"
        if not sampled:
            max_ready, sub_ready, rd_ready = m.sems("max"), m.sems("sub"), m.sems("rd")
        if sampled:
            HN = XH * NK
            loc, quo, rnd, rem, low, high, ix = (m.lanes(n, [128, HN]) for n in ("loc", "quo", "rnd", "rem", "low", "high", "ix"))
            hat, prod = m.lanes("hat", [128, C2 * NK, S2]), m.lanes("prod", [128, C2 * NK, S2])
            sc, sc2, at = (m.lanes(n, [128, C2, NK]) for n in ("sc", "sc2", "at"))
            smx, ssum, srd = (m.lanes(n, [128, C2]) for n in ("smx", "ssum", "srd"))
            sp_l, rsp_l, sgn_l = (m.lanes(n, [128, 1]) for n in ("sp_l", "rsp_l", "sgn_l"))
            (off_ps, span_ready, chain, dist, bumped, hat_ready, prod_ready, sc_ready, soft, weighted, c_half) = (
                m.sems(n) for n in ("off_ps", "span", "chain", "dist", "bumped", "hat", "prod", "sc", "soft", "weighted", "c_half"))

        with nc.Block() as block:
            @block.tensor
            def _(pe):
                with pe.Fori(0, ITERS) as i:
                    u1 = pe.snap(i + 1)
                    v = [pe.snap(i * 2 + 1), pe.snap(i * 2 + 2)]
                    for l in range(LANES):
                        pe.wait_ge(x_done[l], u1)
                        pe.wait_ge(xn_ready[l], u1)
                        nc.tensor.transpose(ps[:, 2 * l, 0:128], xn[l][:, :], k["ident"][:, :]).then_inc(xT_ps[l], 1)
                    for l in range(LANES):
                        pe.wait_ge(xT_ready[l], u1)
                        nc.tensor.matmul(ps[:, 2 * l, 0:128], w["Wq"][:, :], xnT[l][:, :], start=True, stop=True)
                        nc.tensor.matmul(ps[:, 2 * l, 128:128 + S2], w["Wk"][:, :], ctxT[l][:, :], start=True, stop=True)
                        nc.tensor.matmul(ps[0:S2, 2 * l + 1, 0:128], ctxT[l][:, :], w["Wv"][:, :], start=True, stop=True
                                         ).then_inc(qkv_ps[l], 1)
                    if sampled:
                        for l in range(LANES):
                            pe.wait_ge(q_ready[l], u1)
                            pe.wait_ge(k_ready[l], u1)
                            nc.tensor.matmul(ps[:, 2 * l, 0:XH * NK], qT[l][:, :], k["T_Woff"][:, :], start=True, stop=True
                                             ).then_inc(off_ps[l], 1)
                    for h in range(2):
                        for l in range(LANES):
                            if h == 0:
                                pe.wait_ge(q_ready[l], u1)
                                pe.wait_ge(v_ready[l], u1)
                                pe.wait_ge(kbd_ready[l], u1)
                                if sampled:
                                    pe.wait_ge(span_ready[l], u1)
                            else:
                                pe.wait_ge(o_ready[l], v[0])
                            for j in range(2):
                                h0 = h * HG + j * C2
                                last = nc.tensor.matmul(ps[:, 2 * l + j, 0:C2 * S2], qT[l][:, :],
                                                        kbd[l][:, h0:h0 + C2, :].rearrange("p h s -> p (h s)"), start=True, stop=True)
                            last.then_inc(s_ps[l], 1)
                        for l in range(LANES):
                            pe.wait_ge(p_ready[l], v[h])
                            for j in range(HG):
                                last = nc.tensor.transpose(ps[0:S2, 2 * l + j // 4, (j % 4) * 128:(j % 4 + 1) * 128], probs[l][:, j, :],
                                                           k["ident"][:, :])
                            last.then_inc(pT_ps[l], 1)
                        for l in range(LANES):
                            pe.wait_ge(pT_ready[l], v[h])
                            for j in range(HG):
                                last = nc.tensor.matmul(ps[:, 2 * l, j * (XD + 1):(j + 1) * (XD + 1)], pT[l][:, j, :],
                                                        vx[l][:, h * HG + j, :], start=True, stop=True)
                            last.then_inc(pv_ps[l], 1)
                    for l in range(LANES):
                        pe.wait_ge(o_ready[l], v[1])
                        nc.tensor.transpose(ps[:, 2 * l, 0:128], o[l][:, :, :].rearrange("p h d -> p (h d)"), k["ident"][:, :]
                                            ).then_inc(oT_ps[l], 1)
                    for l in range(LANES):
                        pe.wait_ge(oT_ready[l], u1)
                        nc.tensor.matmul(ps[:, 2 * l, 0:128], oT[l][:, :], w["Wo"][:, :], start=True, stop=True).then_inc(y_ps[l], 1)

            @block.vector
            def _(dve):
                for l in range(LANES):
                    nc.vector.memset(vx[l][:, :, XD:XD + 1], 1.0).then_inc(x_done[l], 1)
                with dve.Fori(0, ITERS) as i:
                    u1 = dve.snap(i + 1)
                    v = [dve.snap(i * 2 + 1), dve.snap(i * 2 + 2)]
                    for l in range(LANES):
                        nc.vector.bn_stats(stat[l][:, :], cols(k["x"], i * LANES + l)).then_inc(stats[l], 1)
                    dve.wait_ge(stats[LANES - 1], u1)
                    dve.sem_inc(passed, 1)
                    for l in range(LANES):
                        nc.vector.bn_aggr(mv[l][:, :], stat[l][:, :]).then_inc(moments[l], 1)
                    for l in range(LANES):
                        dve.wait_ge(rstd_ready[l], u1)
                        nc.vector.tensor_scalar(xn[l][:, :], cols(k["x"], i * LANES + l), mv[l][:, 0:1], rstd[l][:, 0:1],
                                                ALU.subtract, ALU.mult).then_inc(xn_ready[l], 1)
                    for l in range(LANES):
                        dve.wait_ge(qkv_ps[l], u1)
                        nc.vector.tensor_scalar(kT[l][:, :], ps[:, 2 * l, 128:128 + S2], w["bk"][:, 0:1], scale, ALU.add, ALU.mult
                                                ).then_inc(k_ready[l], 1)
                        nc.vector.tensor_scalar(qT[l][:, :], ps[:, 2 * l, 0:128], w["bq"][:, 0:1], None, ALU.add).then_inc(q_ready[l], 1)
                        nc.vector.tensor_tensor(vx[l][:, :, 0:XD], ps[0:S2, 2 * l + 1, 0:128].rearrange("p (h d) -> p h d", d=XD),
                                                w["bv"][0:S2, :].rearrange("p (h d) -> p h d", d=XD), ALU.add).then_inc(v_ready[l], 1)
                    if sampled:
                        for l in range(LANES):
                            nc.vector.tensor_copy(sp_l[l][:, :], k["span"][:, bass.ds(i * LANES + l, 1)])
                            nc.vector.tensor_copy(rsp_l[l][:, :], k["rspan"][:, bass.ds(i * LANES + l, 1)])
                            nc.vector.tensor_copy(sgn_l[l][:, :], k["sgn"][:, bass.ds(i * LANES + l, 1)])
                            dve.wait_ge(off_ps[l], u1)
                            nc.vector.tensor_tensor(loc[l][:, :], ps[:, 2 * l, 0:HN], k["boffpos"][:, :], ALU.add).then_inc(span_ready[l], 1)
                        c = [dve.snap(i * 11 + j + 1) for j in range(11)]
                        for l in range(LANES):
                            dve.wait_ge(span_ready[l], u1)
                            nc.vector.tensor_scalar(loc[l][:, :], loc[l][:, :], k["pos"][:, 0:1], sgn_l[l][:, 0:1], ALU.add, ALU.mult
                                                    ).then_inc(chain[l], 1)
                        for l in range(LANES):
                            dve.wait_ge(chain[l], c[0])
                            nc.vector.tensor_scalar(quo[l][:, :], loc[l][:, :], rsp_l[l][:, 0:1], None, ALU.mult).then_inc(chain[l], 1)
                        for l in range(LANES):
                            dve.wait_ge(chain[l], c[1])
                            nc.vector.tensor_scalar(rnd[l][:, :], quo[l][:, :], MAGIC, MAGIC, ALU.add, ALU.subtract).then_inc(chain[l], 1)
                        for l in range(LANES):
                            dve.wait_ge(chain[l], c[2])
                            nc.vector.tensor_scalar(rnd[l][:, :], rnd[l][:, :], sp_l[l][:, 0:1], None, ALU.mult).then_inc(chain[l], 1)
                        for l in range(LANES):
                            dve.wait_ge(chain[l], c[3])
                            nc.vector.tensor_tensor(rem[l][:, :], loc[l][:, :], rnd[l][:, :], ALU.subtract).then_inc(chain[l], 1)
                        for l in range(LANES):
                            dve.wait_ge(chain[l], c[4])
                            nc.vector.tensor_scalar(low[l][:, :], rem[l][:, :], 0.0, sp_l[l][:, 0:1], ALU.is_lt, ALU.mult).then_inc(chain[l], 1)
                        for l in range(LANES):
                            dve.wait_ge(chain[l], c[5])
                            nc.vector.tensor_tensor(rem[l][:, :], rem[l][:, :], low[l][:, :], ALU.add).then_inc(chain[l], 1)
                        for l in range(LANES):
                            dve.wait_ge(chain[l], c[6])
                            nc.vector.tensor_scalar(low[l][:, :], rem[l][:, :], sp_l[l][:, 0:1], sp_l[l][:, 0:1], ALU.is_ge, ALU.mult
                                                    ).then_inc(chain[l], 1)
                        for l in range(LANES):
                            dve.wait_ge(chain[l], c[7])
                            nc.vector.tensor_tensor(rem[l][:, :], rem[l][:, :], low[l][:, :], ALU.subtract).then_inc(chain[l], 1)
                        for l in range(LANES):
                            dve.wait_ge(chain[l], c[8])
                            nc.vector.tensor_scalar(high[l][:, :], rem[l][:, :], sgn_l[l][:, 0:1], S2 / (S2 - 1.0), ALU.mult, ALU.mult
                                                    ).then_inc(chain[l], 1)
                        for l in range(LANES):
                            dve.wait_ge(chain[l], c[9])
                            nc.vector.tensor_scalar(ix[l][:, :], high[l][:, :], -0.5, None, ALU.add).then_inc(chain[l], 1)
                    for h in range(2):
                        if not sampled:
                            for l in range(LANES):
                                dve.wait_ge(s_ps[l], v[h])
                                s = ps[:, 2 * l:2 * l + 2, 0:C2 * S2].rearrange("p j (h s) -> p j h s", s=S2)
                                nc.vector.tensor_reduce(nm[l][:, :].rearrange("p (j h) -> p j h", j=2), s, AX.X, ALU.max).then_inc(max_ready[l], 1)
                            for l in range(LANES):
                                dve.wait_ge(max_ready[l], v[h])
                                s = ps[:, 2 * l:2 * l + 2, 0:C2 * S2].rearrange("p j (h s) -> p j h s", s=S2)
                                nc.vector.tensor_tensor(probs[l][:, :, :].rearrange("p (j h) s -> p j h s", j=2), s,
                                                        bc(nm[l][:, :].rearrange("p (j h) -> p j h", j=2), 3, S2), ALU.subtract
                                                        ).then_inc(sub_ready[l], 1)
                        else:
                            for c2 in range(2):
                                n = dve.snap(i * 4 + (2 * h + c2 + 1))
                                t = [dve.snap(i * 24 + (6 * (2 * h + c2) + j + 1)) for j in range(6)]
                                h0 = (h * HG + c2 * C2) * NK
                                for l in range(LANES):
                                    if h == 0 and c2 == 0:
                                        dve.wait_ge(chain[l], c[10])
                                    nc.vector.tensor_tensor(hat[l][:, :, :], bc(ix[l][:, h0:h0 + C2 * NK], 2, S2),
                                                            bc(k["iota"][:, :], 1, C2 * NK), ALU.subtract).then_inc(dist[l], 1)
                                for l in range(LANES):
                                    if c2 == 0:
                                        dve.wait_ge(s_ps[l], v[h])
                                    dve.wait_ge(hat_ready[l], n)
                                    nc.vector.tensor_tensor(prod[l][:, :, :].rearrange("p (h n) s -> p h n s", n=NK),
                                                            hat[l][:, :, :].rearrange("p (h n) s -> p h n s", n=NK),
                                                            bc(ps[:, 2 * l + c2, 0:C2 * S2].rearrange("p (h s) -> p h s", s=S2), 2, NK),
                                                            ALU.mult).then_inc(prod_ready[l], 1)
                                for l in range(LANES):
                                    dve.wait_ge(prod_ready[l], n)
                                    nc.vector.tensor_reduce(sc[l][:, :, :].rearrange("p h n -> p (h n)"), prod[l][:, :, :], AX.X, ALU.add
                                                            ).then_inc(sc_ready[l], 1)
                                for l in range(LANES):
                                    dve.wait_ge(sc_ready[l], n)
                                    nc.vector.tensor_reduce(smx[l][:, :], sc[l][:, :, :], AX.X, ALU.max).then_inc(soft[l], 1)
                                for l in range(LANES):
                                    dve.wait_ge(soft[l], t[0])
                                    nc.vector.tensor_tensor(sc2[l][:, :, :], sc[l][:, :, :], bc(smx[l][:, :], 2, NK), ALU.subtract
                                                            ).then_inc(soft[l], 1)
                                for l in range(LANES):
                                    dve.wait_ge(soft[l], t[2])
                                    nc.vector.tensor_reduce(ssum[l][:, :], sc2[l][:, :, :], AX.X, ALU.add).then_inc(soft[l], 1)
                                for l in range(LANES):
                                    dve.wait_ge(soft[l], t[3])
                                    nc.vector.reciprocal(srd[l][:, :], ssum[l][:, :]).then_inc(soft[l], 1)
                                for l in range(LANES):
                                    dve.wait_ge(soft[l], t[4])
                                    nc.vector.tensor_tensor(at[l][:, :, :], sc2[l][:, :, :], bc(srd[l][:, :], 2, NK), ALU.mult
                                                            ).then_inc(soft[l], 1)
                                for l in range(LANES):
                                    dve.wait_ge(weighted[l], n)
                                    nc.vector.tensor_reduce(probs[l][:, c2 * C2:(c2 + 1) * C2, :],
                                                            prod[l][:, :, :].rearrange("p (h n) s -> p h s n", n=NK), AX.X, ALU.add
                                                            ).then_inc(p_ready[l] if c2 else c_half[l], 1)
                        for l in range(LANES):
                            dve.wait_ge(pv_ps[l], v[h])
                            pv = ps[:, 2 * l, 0:HG * (XD + 1)].rearrange("p (h d) -> p h d", d=XD + 1)
                            if sampled:
                                nc.vector.tensor_scalar(o[l][:, h * HG:(h + 1) * HG, :], pv[:, :, 0:XD], 0.5, None, ALU.mult
                                                        ).then_inc(o_ready[l], 1)
                            else:
                                nc.vector.reciprocal(rd[l][:, :], pv[:, :, XD]).then_inc(rd_ready[l], 1)
                        if not sampled:
                            for l in range(LANES):
                                dve.wait_ge(rd_ready[l], v[h])
                                pv = ps[:, 2 * l, 0:HG * (XD + 1)].rearrange("p (h d) -> p h d", d=XD + 1)
                                nc.vector.tensor_tensor(o[l][:, h * HG:(h + 1) * HG, :], pv[:, :, 0:XD], bc(rd[l][:, :], 2, XD), ALU.mult
                                                        ).then_inc(o_ready[l], 1)
                    for l in range(LANES):
                        dve.wait_ge(y_ps[l], u1)
                        nc.vector.tensor_tensor(yb[l][:, :], ps[:, 2 * l, 0:128], w["bo"][:, :], ALU.add).then_inc(yb_ready[l], 1)
                    for l in range(LANES):
                        dve.wait_ge(yb_ready[l], u1)
                        xb = cols(k["x"], i * LANES + l)
                        nc.vector.tensor_tensor(xb, xb, yb[l][:, :], ALU.add).then_inc(x_done[l], 1)

            @block.scalar
            def _(act):
                with act.Fori(0, ITERS) as i:
                    u1 = act.snap(i + 1)
                    v = [act.snap(i * 2 + 1), act.snap(i * 2 + 2)]
                    for l in range(LANES):
                        act.wait_ge(xT_ps[l], u1)
                        nc.scalar.copy(xnT[l][:, :], ps[:, 2 * l, 0:128])
                        nc.scalar.copy(ctxT[l][:, :], cols(k["ctxT"], i * LANES + l)).then_inc(xT_ready[l], 1)
                    for h in range(2):
                        if sampled:
                            for c2 in range(2):
                                n = act.snap(i * 4 + (2 * h + c2 + 1))
                                t = {1: act.snap(i * 24 + (6 * (2 * h + c2) + 2))}
                                for l in range(LANES):
                                    act.wait_ge(dist[l], n)
                                    f = hat[l][:, :, :].rearrange("p n s -> p (n s)")
                                    nc.scalar.activation(f, f, ACT.Abs).then_inc(bumped[l], 1)
                                for l in range(LANES):
                                    act.wait_ge(bumped[l], n)
                                    f = hat[l][:, :, :].rearrange("p n s -> p (n s)")
                                    nc.scalar.activation(f, f, ACT.Relu, bias=1.0, scale=-1.0).then_inc(hat_ready[l], 1)
                                for l in range(LANES):
                                    act.wait_ge(soft[l], t[1])
                                    f = sc2[l][:, :, :].rearrange("p h n -> p (h n)")
                                    nc.scalar.activation(f, f, ACT.Exp).then_inc(soft[l], 1)
                        else:
                            for l in range(LANES):
                                act.wait_ge(sub_ready[l], v[h])
                                f = probs[l][:, :, :].rearrange("p h s -> p (h s)")
                                nc.scalar.activation(f, f, ACT.Exp).then_inc(p_ready[l], 1)
                        for l in range(LANES):
                            act.wait_ge(pT_ps[l], v[h])
                            nc.scalar.copy(pT[l][:, :, :].rearrange("p h n -> p (h n)"),
                                           ps[0:S2, 2 * l:2 * l + 2, :].rearrange("p a n -> p (a n)")).then_inc(pT_ready[l], 1)
                    for l in range(LANES):
                        act.wait_ge(oT_ps[l], u1)
                        nc.scalar.copy(oT[l][:, :], ps[:, 2 * l, 0:128]).then_inc(oT_ready[l], 1)

            @block.gpsimd
            def _(pool):
                with pool.Fori(0, ITERS) as i:
                    u1 = pool.snap(i + 1)
                    for l in range(LANES):
                        pool.wait_ge(moments[l], u1)
                        nc.gpsimd.tensor_tensor(ve[l][:, :], mv[l][:, 1:2], k["eps"][:, 0:1], ALU.add).then_inc(var_eps[l], 1)
                    for l in range(LANES):
                        pool.wait_ge(var_eps[l], u1)
                        nc.gpsimd.tensor_tensor(rstd[l][:, :], ve[l][:, :], k["minus_half"][:, 0:1], ALU.pow).then_inc(rstd_ready[l], 1)
                    for l in range(LANES):
                        pool.wait_ge(k_ready[l], u1)
                        nc.gpsimd.tensor_tensor(kbd[l][:, :, :], bc(kT[l][:, :], 1, XH), bc(k["headmask"][:, :], 2, S2), ALU.mult
                                                ).then_inc(kbd_ready[l], 1)
                    if sampled:
                        for h in range(2):
                            for c2 in range(2):
                                n = pool.snap(i * 4 + (2 * h + c2 + 1))
                                t = {5: pool.snap(i * 24 + (6 * (2 * h + c2) + 6))}
                                for l in range(LANES):
                                    pool.wait_ge(soft[l], t[5])
                                    nc.gpsimd.tensor_tensor(prod[l][:, :, :], hat[l][:, :, :],
                                                            bc(at[l][:, :, :].rearrange("p h n -> p (h n)"), 2, S2), ALU.mult
                                                            ).then_inc(weighted[l], 1)


def norm_front(nc, m, k):
    f = {"stat": m.lanes("stat", [128, GB, 6], n=WIDE), "mv": m.lanes("mv", [128, GB, 2], n=WIDE),
         "ve": m.lanes("ve", [128, GB], n=WIDE), "rs": m.lanes("rs", [128, GB], n=WIDE)}
    for n in ("stats", "moments", "eps", "rstd", "xn_ready"):
        f[n] = m.sems(n, WIDE)
    return f


def norm_vector(nc, dve, k, f, xn, i, passed):
    u1, u4 = dve.snap(i + 1), dve.snap(i * GB + GB)
    for l in range(WIDE):
        for b in range(GB):
            nc.vector.bn_stats(f["stat"][l][:, b, :], cols(k["x"], (i * WIDE + l) * GB + b)).then_inc(f["stats"][l], 1)
    for l in range(WIDE):
        dve.wait_ge(f["stats"][l], u4)
        dve.sem_inc(passed, 1)
        for b in range(GB):
            last = nc.vector.bn_aggr(f["mv"][l][:, b, :], f["stat"][l][:, b, :])
        last.then_inc(f["moments"][l], 1)
    for l in range(WIDE):
        dve.wait_ge(f["rstd"][l], u1)
        for b in range(GB):
            last = nc.vector.tensor_scalar(xn[l][:, b, :], cols(k["x"], (i * WIDE + l) * GB + b), f["mv"][l][:, b, 0:1],
                                           f["rs"][l][:, b:b + 1], ALU.subtract, ALU.mult)
        last.then_inc(f["xn_ready"][l], 1)


def norm_pool(nc, pool, k, f, i):
    u1 = pool.snap(i + 1)
    for l in range(WIDE):
        pool.wait_ge(f["moments"][l], u1)
        nc.gpsimd.tensor_tensor(f["ve"][l][:, :], f["mv"][l][:, :, 1], k["eps"][:, 0:GB], ALU.add).then_inc(f["eps"][l], 1)
    for l in range(WIDE):
        pool.wait_ge(f["eps"][l], u1)
        nc.gpsimd.tensor_tensor(f["rs"][l][:, :], f["ve"][l][:, :], k["minus_half"][:, 0:GB], ALU.pow).then_inc(f["rstd"][l], 1)


Q_STEPS = 10


def quantise(nc, dve, src, rscale, t, step, count, passed):
    u, v, lo, hi, big, ok, sq = t
    nc.vector.tensor_scalar(u, src, rscale, None, ALU.mult).then_inc(step, 1)
    dve.wait_ge(step, count(1))
    dve.sem_inc(passed, 1)
    nc.vector.tensor_scalar(lo, u, 240.0, -240.0, ALU.min, ALU.max, saturate=False)
    nc.vector.tensor_scalar(v, u, 0.5, 240.0, ALU.mult, ALU.min).then_inc(step, 1)
    nc.vector.tensor_tensor(sq, u, u, ALU.mult).then_inc(step, 1)
    dve.wait_ge(step, count(3))
    nc.vector.tensor_scalar(big, sq, 240.0 ** 2, None, ALU.is_gt)
    nc.vector.tensor_scalar(ok, sq, 464.0 ** 2, None, ALU.is_le).then_inc(step, 1)
    nc.vector.tensor_scalar(hi, v, -240.0, None, ALU.max, saturate=False).then_inc(step, 1)
    dve.wait_ge(step, count(5))
    dve.sem_inc(passed, 1)
    nc.vector.scalar_tensor_tensor(out=v, in0=hi, scalar=2.0, in1=lo, op0=ALU.mult, op1=ALU.subtract).then_inc(step, 1)
    nc.vector.reciprocal(sq, ok).then_inc(step, 1)
    dve.wait_ge(step, count(7))
    nc.vector.tensor_tensor(v, v, big, ALU.mult).then_inc(step, 1)
    nc.vector.tensor_tensor(ok, ok, sq, ALU.mult).then_inc(step, 1)
    dve.wait_ge(step, count(9))
    dve.sem_inc(passed, 1)
    nc.vector.tensor_tensor(u, v, lo, ALU.add).then_inc(step, 1)
    dve.wait_ge(step, count(10))


def quantised_dense(nc, a, k, ps):
    with ExitStack() as ctx:
        m = Buffers(nc, ctx, "p4")
        passed = m.sem("passed")
        f = norm_front(nc, m, k)
        xn = m.lanes("xn", [128, GB, D], BF16, n=WIDE)
        tmp = [(m.sb(f"u{l}", [128, 512]), m.sb(f"v{l}", [128, 512]), m.sb(f"lo{l}", [128, 512], FP8), m.sb(f"hi{l}", [128, 512], FP8),
                m.sb(f"big{l}", [128, 512]), m.sb(f"ok{l}", [128, 512]), m.sb(f"sq{l}", [128, 512])) for l in range(WIDE)]
        xq = m.lanes("xq", [128, 512], BF16, n=WIDE)
        xqT = m.lanes("xqT", [128, 512], BF16, n=WIDE)
        kq = m.sb("kq", [128, 128], BF16)
        rin, rk = m.sb("rin", [128, 1]), m.sb("rk", [128, 1])
        y, y2 = m.lanes("y", [128, 512], BF16, n=WIDE), m.lanes("y2", [128, 512], BF16, n=WIDE)
        kstep, k_ready = m.sem("kstep"), m.sem("k_ready")
        step, q_ready, qT_ps, qT_ready, y_ps, y_ready, yb_ready, x_done = (
            m.sems(n, WIDE) for n in ("step", "q", "qT_ps", "qT", "y_ps", "y", "yb", "x_done"))
        turned = [ps[:, 4 * l, 0:256].bitcast(BF16) for l in range(WIDE)]

        with nc.Block() as block:
            @block.vector
            def _(dve):
                for l in range(WIDE):
                    dve.sem_inc(x_done[l], 1)
                nc.vector.reciprocal(rin[:, :], k["r_sin"][:, :])
                nc.vector.reciprocal(rk[:, :], k["r_sk"][:, :]).then_inc(k_ready, 1)
                dve.wait_ge(k_ready, 1)
                quantise(nc, dve, k["fkernel"][:, :], rk[:, 0:1], [t[:, 0:128] for t in tmp[0]], kstep, lambda n: n, passed)
                nc.vector.tensor_tensor(kq[:, :], tmp[0][0][:, 0:128], tmp[0][5][:, 0:128], ALU.mult).then_inc(k_ready, 1)
                dve.wait_ge(k_ready, 2)
                with dve.Fori(0, ROUNDS) as i:
                    u1 = dve.snap(i + 1)
                    norm_vector(nc, dve, k, f, xn, i, passed)
                    for l in range(WIDE):
                        dve.wait_ge(f["xn_ready"][l], u1)
                        quantise(nc, dve, xn[l][:, :, :].rearrange("p b d -> p (b d)"), rin[:, 0:1], [t[:, :] for t in tmp[l]],
                                 step[l], lambda n: i * Q_STEPS + n, passed)
                        nc.vector.tensor_tensor(xq[l][:, :], tmp[l][0][:, :], tmp[l][5][:, :], ALU.mult).then_inc(q_ready[l], 1)
                    for l in range(WIDE):
                        dve.wait_ge(y_ps[l], u1)
                        nc.vector.tensor_scalar(y[l][:, :], ps[:, 4 * l + 1, :], k["sscale"][:, 0:1], None, ALU.mult).then_inc(y_ready[l], 1)
                    for l in range(WIDE):
                        dve.wait_ge(y_ready[l], u1)
                        nc.vector.tensor_tensor(y2[l][:, :].rearrange("p (b d) -> p b d", b=GB),
                                                y[l][:, :].rearrange("p (b d) -> p b d", b=GB), bc(k["r_fbias"][:, :], 1, GB), ALU.add
                                                ).then_inc(yb_ready[l], 1)
                    for l in range(WIDE):
                        dve.wait_ge(yb_ready[l], u1)
                        xb = cols(k["x"], (i * WIDE + l) * GB, GB)
                        nc.vector.tensor_tensor(xb, xb, y2[l][:, :], ALU.add).then_inc(x_done[l], 1)

            @block.gpsimd
            def _(pool):
                with pool.Fori(0, ROUNDS) as i:
                    norm_pool(nc, pool, k, f, i)

            @block.tensor
            def _(pe):
                pe.wait_ge(k_ready, 2)
                pe.sem_inc(passed, 1)
                with pe.Fori(0, ROUNDS) as i:
                    u1 = pe.snap(i + 1)
                    for l in range(WIDE):
                        pe.wait_ge(x_done[l], u1)
                        pe.wait_ge(q_ready[l], u1)
                        for b in range(GB):
                            last = nc.tensor.transpose(turned[l][:, b * 128:(b + 1) * 128], xq[l][:, b * 128:(b + 1) * 128], k["identb"][:, :])
                        last.then_inc(qT_ps[l], 1)
                    for l in range(WIDE):
                        pe.wait_ge(qT_ready[l], u1)
                        for b in range(GB):
                            last = nc.tensor.matmul(ps[:, 4 * l + 1, b * 128:(b + 1) * 128], xqT[l][:, b * 128:(b + 1) * 128], kq[:, :],
                                                    start=True, stop=True)
                        last.then_inc(y_ps[l], 1)

            @block.scalar
            def _(act):
                with act.Fori(0, ROUNDS) as i:
                    u1 = act.snap(i + 1)
                    for l in range(WIDE):
                        act.wait_ge(qT_ps[l], u1)
                        nc.scalar.copy(xqT[l][:, :], turned[l]).then_inc(qT_ready[l], 1)


def mixture_top1(nc, a, k, ps):
    NC = DFF // 128
    with ExitStack() as ctx:
        m = Buffers(nc, ctx, "p6")
        passed = m.sem("passed")
        f = norm_front(nc, m, k)
        xn, xT = m.lanes("xn", [128, GB, D], n=WIDE), m.lanes("xT", [128, 512], n=WIDE)
        lg, top, hit, before = (m.lanes(n, s, n=WIDE) for n, s in (("lg", [128, GB, E]), ("top", [128, GB]), ("hit", [128, GB, E]),
                                                                   ("before", [128, GB, E])))
        prior = m.lanes("prior", [128, GB, E, E], n=WIDE)
        sel, selT = m.lanes("sel", [128, GB, 32], n=WIDE), m.lanes("selT", [128, 128], n=WIDE)
        acc, pick = m.lanes("acc", [128, GB, D], n=WIDE), m.lanes("pick", [128, GB, D], n=WIDE)
        hT = [[m.sb(f"hT{l}_{c}", [128, 512]) for c in range(NC)] for l in range(WIDE)]
        (xT_ps, xT_ready, lg_ps, route, sel_ready, selT_ps, selT_ready, b_ps, acc_ready, h_ps, gelu_ready, y_ps, picked, x_done) = (
            m.sems(n, WIDE) for n in ("xT_ps", "xT", "lg_ps", "route", "sel", "selT_ps", "selT", "b_ps", "acc", "h_ps", "gelu",
                                      "y_ps", "picked", "x_done"))

        with nc.Block() as block:
            @block.vector
            def _(dve):
                for l in range(WIDE):
                    nc.vector.memset(sel[l][:, :, :], 0.0).then_inc(x_done[l], 1)
                    dve.sem_inc(picked[l], 2)
                    dve.wait_ge(x_done[l], 1)
                with dve.Fori(0, ROUNDS) as i:
                    u1 = dve.snap(i + 1)
                    norm_vector(nc, dve, k, f, xn, i, passed)
                    r = [dve.snap(i * 5 + j + 1) for j in range(5)]
                    for l in range(WIDE):
                        dve.wait_ge(lg_ps[l], u1)
                        nc.vector.tensor_tensor(lg[l][:, :, :], ps[:, 4 * l + 1, 0:GB * E].rearrange("p (b e) -> p b e", b=GB),
                                                bc(k["r_gateb"][:, :], 1, GB), ALU.add).then_inc(route[l], 1)
                    for l in range(WIDE):
                        dve.wait_ge(route[l], r[0])
                        nc.vector.tensor_reduce(top[l][:, :], lg[l][:, :, :], AX.X, ALU.max).then_inc(route[l], 1)
                    for l in range(WIDE):
                        dve.wait_ge(route[l], r[1])
                        nc.vector.tensor_tensor(hit[l][:, :, :], lg[l][:, :, :], bc(top[l][:, :], 2, E), ALU.is_equal).then_inc(route[l], 1)
                    for l in range(WIDE):
                        dve.wait_ge(route[l], r[2])
                        nc.vector.tensor_tensor(prior[l][:, :, :, :], bc(hit[l][:, :, :], 2, E), bc(k["lower"][:, :, :], 1, GB), ALU.mult
                                                ).then_inc(route[l], 1)
                    for l in range(WIDE):
                        dve.wait_ge(route[l], r[3])
                        nc.vector.tensor_reduce(before[l][:, :, :], prior[l][:, :, :, :], AX.X, ALU.add).then_inc(route[l], 1)
                    for l in range(WIDE):
                        dve.wait_ge(route[l], r[4])
                        nc.vector.scalar_tensor_tensor(out=sel[l][:, :, 0:E], in0=before[l][:, :, :], scalar=0.5, in1=hit[l][:, :, :],
                                                       op0=ALU.is_lt, op1=ALU.mult).then_inc(sel_ready[l], 1)
                    for l in range(WIDE):
                        dve.wait_ge(b_ps[l], u1)
                        dve.wait_ge(sel_ready[l], u1)
                        nc.vector.tensor_tensor(acc[l][:, :, :].rearrange("p b d -> p (b d)"), ps[:, 4 * l + 2, :],
                                                cols(k["x"], (i * WIDE + l) * GB, GB), ALU.add).then_inc(acc_ready[l], 1)
                    for e in range(E):
                        w = dve.snap(i * E + (e + 1))
                        w3 = dve.snap(i * E + (e + 3))
                        for l in range(WIDE):
                            dve.wait_ge(acc_ready[l], w)
                            dve.wait_ge(y_ps[l], w)
                            nc.vector.tensor_tensor(pick[l][:, :, :], ps[:, 4 * l + 2 + e % 2, :].rearrange("p (b d) -> p b d", b=GB),
                                                    bc(sel[l][:, :, e], 2, D), ALU.mult).then_inc(picked[l], 1)
                        for l in range(WIDE):
                            dve.wait_ge(picked[l], w3)
                            if e < E - 1:
                                nc.vector.tensor_tensor(acc[l][:, :, :], acc[l][:, :, :], pick[l][:, :, :], ALU.add).then_inc(acc_ready[l], 1)
                            else:
                                nc.vector.tensor_tensor(cols(k["x"], (i * WIDE + l) * GB, GB), acc[l][:, :, :].rearrange("p b d -> p (b d)"),
                                                        pick[l][:, :, :].rearrange("p b d -> p (b d)"), ALU.add).then_inc(x_done[l], 1)

            @block.gpsimd
            def _(pool):
                with pool.Fori(0, ROUNDS) as i:
                    norm_pool(nc, pool, k, f, i)

            @block.tensor
            def _(pe):
                pe.wait_ge(k["moe_loaded"], 32)
                pe.sem_inc(passed, 1)
                with pe.Fori(0, ROUNDS) as i:
                    u1 = pe.snap(i + 1)
                    for l in range(WIDE):
                        pe.wait_ge(x_done[l], u1)
                        pe.wait_ge(f["xn_ready"][l], u1)
                        for b in range(GB):
                            last = nc.tensor.transpose(ps[:, 4 * l, b * 128:(b + 1) * 128], xn[l][:, b, :], k["ident"][:, :])
                        last.then_inc(xT_ps[l], 1)
                    for l in range(WIDE):
                        pe.wait_ge(xT_ready[l], u1)
                        for b in range(GB):
                            last = nc.tensor.matmul(ps[:, 4 * l + 1, b * E:(b + 1) * E], xT[l][:, b * 128:(b + 1) * 128], k["gateW"][:, :],
                                                    start=True, stop=True)
                        last.then_inc(lg_ps[l], 1)
                    for l in range(WIDE):
                        pe.wait_ge(sel_ready[l], u1)
                        nc.tensor.transpose(ps[:, 4 * l + 1, 0:128], sel[l][:, :, :].rearrange("p b e -> p (b e)"), k["ident"][:, :]
                                            ).then_inc(selT_ps[l], 1)
                    for l in range(WIDE):
                        pe.wait_ge(selT_ready[l], u1)
                        nc.tensor.matmul(ps[:, 4 * l + 2, :], selT[l][:, :], k["b2blk"][:, :, :].rearrange("p b d -> p (b d)"),
                                         start=True, stop=True).then_inc(b_ps[l], 1)

                    def outputs(e):
                        g4 = pe.snap(i * (E * NC) + (e * NC + NC))
                        w = pe.snap(i * E + (e + 1))
                        for l in range(WIDE):
                            pe.wait_ge(gelu_ready[l], g4)
                            pe.wait_ge(picked[l], w)
                            if e == 0:
                                pe.wait_ge(acc_ready[l], w)
                            for b in range(GB):
                                for c in range(NC):
                                    last = nc.tensor.matmul(ps[:, 4 * l + 2 + e % 2, b * 128:(b + 1) * 128],
                                                            hT[l][c][:, b * 128:(b + 1) * 128], k["moe_w2"][:, e, c, :],
                                                            start=(c == 0), stop=(c == NC - 1))
                            last.then_inc(y_ps[l], 1)

                    for e in range(E):
                        for c in range(NC):
                            for l in range(WIDE):
                                if e * NC + c >= 2:
                                    pe.wait_ge(gelu_ready[l], i * (E * NC) + (e * NC + c - 1))
                                elif c == 1:
                                    pe.wait_ge(selT_ready[l], u1)
                                nc.tensor.matmul(ps[:, 4 * l + c % 2, :], k["moe_w1"][:, e, c * 128:(c + 1) * 128], xT[l][:, :],
                                                 start=True, stop=True).then_inc(h_ps[l], 1)
                        outputs(e)

            @block.scalar
            def _(act):
                with act.Fori(0, ROUNDS) as i:
                    u1 = act.snap(i + 1)
                    for l in range(WIDE):
                        act.wait_ge(xT_ps[l], u1)
                        nc.scalar.copy(xT[l][:, :], ps[:, 4 * l, :]).then_inc(xT_ready[l], 1)
                    for l in range(WIDE):
                        act.wait_ge(selT_ps[l], u1)
                        nc.scalar.copy(selT[l][:, :], ps[:, 4 * l + 1, 0:128]).then_inc(selT_ready[l], 1)
                    for e in range(E):
                        for c in range(NC):
                            for l in range(WIDE):
                                if e and c == 0:
                                    act.wait_ge(y_ps[l], i * E + e)
                                act.wait_ge(h_ps[l], i * (E * NC) + (e * NC + c + 1))
                                nc.scalar.activation(hT[l][c][:, :], ps[:, 4 * l + c % 2, :], ACT.Gelu,
                                                     bias=k["T_b1"][:, e * NC + c:e * NC + c + 1]).then_inc(gelu_ready[l], 1)


def adapters_top2(nc, a, k, ps):
    NC = E * BN // 128
    with ExitStack() as ctx:
        m = Buffers(nc, ctx, "p8")
        passed = m.sem("passed")
        f = norm_front(nc, m, k)
        L = lambda n, s: m.lanes(n, s, n=WIDE)
        xn, xT, pooled, gp = L("xn", [128, GB, D]), L("xT", [128, GB, 128]), L("pooled", [128, GB]), L("gp", [128, GB, E])
        lg, lg2, top, gate, tot, rtot = L("lg", [128, GB, E]), L("lg2", [128, GB, E]), L("top", [128, GB]), L("gate", [128, GB, E]), L("tot", [128, GB]), L("rtot", [128, GB])
        above, same, rank, kept = L("above", [128, GB, E, E]), L("same", [128, GB, E, E]), L("rank", [128, GB, E]), L("kept", [128, GB, E])
        tw, twT, twcol = L("tw", [128, GB, E]), L("twT", [GB * E, 128]), L("twcol", [128, NC, GB])
        h = [[m.sb(f"h{l}_{c}", [128, 512]) for c in range(NC)] for l in range(WIDE)]
        hs = [[m.sb(f"hs{l}_{c}", [128, 512]) for c in range(NC)] for l in range(WIDE)]
        xT_ps, xT_ready, gp_ready, lg_ps, route, exp_ready, tw_ready, twT_ps, twT_ready, h_ps, h_ready, hs_ready, y_ps, x_done = (
            m.sems(n, WIDE) for n in ("xT_ps", "xT", "gp", "lg_ps", "route", "exp", "tw", "twT_ps", "twT", "h_ps", "h", "hs", "y_ps",
                                      "x_done"))
        N_ROUTE = 16

        with nc.Block() as block:
            @block.vector
            def _(dve):
                for l in range(WIDE):
                    dve.sem_inc(x_done[l], 1)
                with dve.Fori(0, ROUNDS) as i:
                    u1 = dve.snap(i + 1)
                    norm_vector(nc, dve, k, f, xn, i, passed)
                    r = [dve.snap(i * N_ROUTE + j) if j else None for j in range(N_ROUTE + 1)]

                    def each(after, emit):
                        for l in range(WIDE):
                            dve.wait_ge(route[l], r[after])
                            emit(l).then_inc(route[l], 1)

                    for l in range(WIDE):
                        dve.wait_ge(xT_ready[l], u1)
                        nc.vector.tensor_reduce(pooled[l][:, :], xT[l][:, :, :], AX.X, ALU.add).then_inc(route[l], 1)
                    for l in range(WIDE):
                        dve.wait_ge(route[l], r[1])
                        nc.vector.tensor_tensor(gp[l][:, :, :], bc(k["T_gate"][:, :], 1, GB), bc(pooled[l][:, :], 2, E), ALU.mult
                                                ).then_inc(gp_ready[l], 1)
                    for l in range(WIDE):
                        dve.wait_ge(lg_ps[l], u1)
                        nc.vector.tensor_scalar(lg[l][:, :, :].rearrange("p b e -> p (b e)"), ps[:, 4 * l + 1, 0:GB * E], 1.0 / S, None,
                                                ALU.mult).then_inc(route[l], 1)
                    each(2, lambda l: nc.vector.tensor_reduce(top[l][:, :], lg[l][:, :, :], AX.X, ALU.max))
                    each(3, lambda l: nc.vector.tensor_tensor(lg2[l][:, :, :], lg[l][:, :, :], bc(top[l][:, :], 2, E), ALU.subtract))
                    for l in range(WIDE):
                        dve.wait_ge(exp_ready[l], u1)
                        nc.vector.tensor_reduce(tot[l][:, :], lg2[l][:, :, :], AX.X, ALU.add).then_inc(route[l], 1)
                    each(5, lambda l: nc.vector.reciprocal(rtot[l][:, :], tot[l][:, :]))
                    each(6, lambda l: nc.vector.tensor_tensor(gate[l][:, :, :], lg2[l][:, :, :], bc(rtot[l][:, :], 2, E), ALU.mult))
                    each(7, lambda l: nc.vector.tensor_tensor(above[l][:, :, :, :], bc(gate[l][:, :, :], 2, E), bc(gate[l][:, :, :], 3, E), ALU.is_gt))
                    each(7, lambda l: nc.vector.tensor_tensor(same[l][:, :, :, :], bc(gate[l][:, :, :], 2, E), bc(gate[l][:, :, :], 3, E), ALU.is_equal))
                    each(9, lambda l: nc.vector.tensor_tensor(same[l][:, :, :, :], same[l][:, :, :, :], bc(k["lower"][:, :, :], 1, GB), ALU.mult))
                    each(10, lambda l: nc.vector.tensor_tensor(above[l][:, :, :, :], above[l][:, :, :, :], same[l][:, :, :, :], ALU.add))
                    each(11, lambda l: nc.vector.tensor_reduce(rank[l][:, :, :], above[l][:, :, :, :], AX.X, ALU.add))
                    each(12, lambda l: nc.vector.scalar_tensor_tensor(out=kept[l][:, :, :], in0=rank[l][:, :, :], scalar=1.5,
                                                                      in1=gate[l][:, :, :], op0=ALU.is_lt, op1=ALU.mult))
                    each(13, lambda l: nc.vector.tensor_reduce(tot[l][:, :], kept[l][:, :, :], AX.X, ALU.add))
                    each(14, lambda l: nc.vector.tensor_scalar(tot[l][:, :], tot[l][:, :], 1e-8, None, ALU.add))
                    each(15, lambda l: nc.vector.reciprocal(rtot[l][:, :], tot[l][:, :]))
                    for l in range(WIDE):
                        dve.wait_ge(route[l], r[16])
                        nc.vector.tensor_tensor(tw[l][:, :, :], kept[l][:, :, :], bc(rtot[l][:, :], 2, E), ALU.mult).then_inc(tw_ready[l], 1)
                    for l in range(WIDE):
                        dve.wait_ge(tw_ready[l], i * 2 + 1)
                        for half in range(2):
                            v = tw[l][64 * half:64 * half + 64, :, :].rearrange("p b (c e) -> p c b e", e=2)[:, :, :, half]
                            last = nc.vector.tensor_copy(twcol[l][64 * half:64 * half + 64, :, :], v)
                        last.then_inc(tw_ready[l], 1)
                    for c in range(NC):
                        for l in range(WIDE):
                            if c == 0:
                                dve.wait_ge(tw_ready[l], i * 2 + 2)
                            dve.wait_ge(h_ready[l], i * NC + (c + 1))
                            nc.vector.tensor_tensor(hs[l][c][:, :].rearrange("p (b s) -> p b s", b=GB), h[l][c][:, :].rearrange("p (b s) -> p b s", b=GB),
                                                    bc(twcol[l][:, c, :], 2, 128), ALU.mult).then_inc(hs_ready[l], 1)
                    for l in range(WIDE):
                        dve.wait_ge(y_ps[l], u1)
                        xb = cols(k["x"], (i * WIDE + l) * GB, GB)
                        nc.vector.tensor_tensor(xb, xb, ps[:, 4 * l + 2, :], ALU.add).then_inc(x_done[l], 1)

            @block.gpsimd
            def _(pool):
                with pool.Fori(0, ROUNDS) as i:
                    norm_pool(nc, pool, k, f, i)

            @block.tensor
            def _(pe):
                with pe.Fori(0, ROUNDS) as i:
                    u1 = pe.snap(i + 1)
                    for l in range(WIDE):
                        pe.wait_ge(x_done[l], u1)
                        pe.wait_ge(f["xn_ready"][l], u1)
                        for b in range(GB):
                            last = nc.tensor.transpose(ps[:, 4 * l, b * 128:(b + 1) * 128], xn[l][:, b, :], k["ident"][:, :])
                        last.then_inc(xT_ps[l], 1)
                    for c in range(NC):
                        for l in range(WIDE):
                            pe.wait_ge(xT_ready[l], u1)
                            if c >= 2:
                                pe.wait_ge(h_ready[l], i * NC + (c - 1))
                            nc.tensor.matmul(ps[:, 4 * l + 3 * (c % 2), :], k["T_down"][:, c, :], xT[l][:, :, :].rearrange("p b s -> p (b s)"),
                                             start=True, stop=True).then_inc(h_ps[l], 1)
                    for l in range(WIDE):
                        pe.wait_ge(gp_ready[l], u1)
                        nc.tensor.matmul(ps[:, 4 * l + 1, 0:GB * E], k["ones"][:, :], gp[l][:, :, :].rearrange("p b e -> p (b e)"),
                                         start=True, stop=True).then_inc(lg_ps[l], 1)
                    for l in range(WIDE):
                        pe.wait_ge(tw_ready[l], i * 2 + 1)
                        nc.tensor.transpose(ps[0:GB * E, 4 * l + 1, 0:128], tw[l][:, :, :].rearrange("p b e -> p (b e)"), k["ident"][:, :]
                                            ).then_inc(twT_ps[l], 1)
                    for l in range(WIDE):
                        pe.wait_ge(twT_ready[l], u1)
                        pe.wait_ge(hs_ready[l], i * NC + NC)
                        nc.tensor.matmul(ps[:, 4 * l + 2, :], twT[l][:, :], k["up_b"][:, :, :].rearrange("p b d -> p (b d)"), start=True, stop=False)
                        for b in range(GB):
                            for c in range(NC):
                                last = nc.tensor.matmul(ps[:, 4 * l + 2, b * 128:(b + 1) * 128], hs[l][c][:, b * 128:(b + 1) * 128],
                                                        k["T_up"][:, c, :], start=False, stop=(b == GB - 1 and c == NC - 1))
                        last.then_inc(y_ps[l], 1)

            @block.scalar
            def _(act):
                with act.Fori(0, ROUNDS) as i:
                    u1 = act.snap(i + 1)
                    for l in range(WIDE):
                        act.wait_ge(xT_ps[l], u1)
                        nc.scalar.copy(xT[l][:, :, :].rearrange("p b s -> p (b s)"), ps[:, 4 * l, :]).then_inc(xT_ready[l], 1)
                    for c in range(NC):
                        for l in range(WIDE):
                            act.wait_ge(h_ps[l], i * NC + (c + 1))
                            nc.scalar.activation(h[l][c][:, :], ps[:, 4 * l + 3 * (c % 2), :], ACT.Gelu, bias=k["c_down_b"][:, c:c + 1]
                                                 ).then_inc(h_ready[l], 1)
                    for l in range(WIDE):
                        act.wait_ge(route[l], i * N_ROUTE + 4)
                        v = lg2[l][:, :, :].rearrange("p b e -> p (b e)")
                        nc.scalar.activation(v, v, ACT.Exp).then_inc(exp_ready[l], 1)
                    for l in range(WIDE):
                        act.wait_ge(twT_ps[l], u1)
                        nc.scalar.copy(twT[l][:, :], ps[0:GB * E, 4 * l + 1, 0:128]).then_inc(twT_ready[l], 1)



def build(nc, a, out):
    with ExitStack() as ctx:
        m = Buffers(nc, ctx, "k")
        k = {}
        for n, shape in (("x", [128, B, D]), ("ctxT", [128, B, S2]), ("negm", [128, B, S2]), ("ident", [128, 128]),
                         ("shift", [128, 128]), ("headmask", [128, XH]), ("ones", [128, 128]), ("minus_half", [128, 16]), ("eps", [128, 16]), ("huge", [128, 16]), ("eight", [128, DH]),
                         ("wpad", [128, 63]), ("up_b", [GB * E, GB, D]), ("b2blk", [128, GB, D]), ("T_b1", [128, E * DFF // 128]), ("gateW", [128, E]), ("lower", [128, E, E]),
                         ("iota", [128, S2]), ("pos", [128, 1]), ("Wcw", [128, 128]), ("Wcb", [128, 128]),
                         ("boffpos", [128, XH * NK]), ("span", [128, B]), ("rspan", [128, B]), ("sgn", [128, B]),
                         ("sscale", [128, 1]), ("T_Woff", [128, XH * NK]), ("T_gate", [128, E]), ("T_down", [128, 4, 128]),
                         ("T_up", [128, 4, 128]), ("T_Wk", [128, 128]), ("T_Wv", [128, 128]), ("T_Wq", [128, 128]),
                         ("T_Wo", [128, 128]), ("L0_W", [128, 128]), ("L0_Ws", [128, 128]), ("L1_Wq", [128, 128]),
                         ("L1_Wk", [128, 128]), ("L1_Wv", [128, 128]), ("L1_We", [128, 128]), ("L2_Wq", [128, 128]),
                         ("L2_Wk", [128, 128]), ("L2_Wv", [128, 128]), ("L2_Wo", [128, 128]),
                         ("c_L1_bq", [128, 1]), ("c_L1_bk", [128, 1]), ("c_L2_bq", [128, 1]), ("c_L2_bk", [128, 1]),
                         ("c_L3_bq", [128, 1]), ("c_L3_bk", [128, 1]), ("c_L0_b", [128, 1]), ("c_down_b", [128, 4]),
                         ("r_L1_bv", [128, D]), ("r_L1_bo", [128, D]), ("r_L2_bv", [128, D]), ("r_L2_bo", [128, D]),
                         ("r_L3_bv", [128, D]), ("r_L3_bo", [128, D]), ("r_L3_boff", [128, XH * NK]), ("r_bcw", [128, 1]),
                         ("r_bcb", [128, 1]), ("r_gateb", [128, E]), ("r_sin", [128, 1]), ("r_sk", [128, 1]),
                         ("cosS", [128, 2, DH]), ("sinS", [128, 2, DH])):
            k[n] = m.sb(n, shape)
        k["identb"] = m.sb("identb", [128, 128], BF16)
        k["band"] = m.sb("band", [128, 4, 128], BF16)
        k["fkernel"] = m.sb("fkernel", [128, 128], BF16)
        k["r_fbias"] = m.sb("r_fbias", [128, 128], BF16)
        ps = ctx.enter_context(nc.psum_tensor("ps", [128, 8, 512], F32))
        setup_phase(nc, a, k, ps)
        if 1 in PHASES:
            additive_attention(nc, a, k, ps)
        if 2 in PHASES:
            with ExitStack() as p2:
                k["z"] = p2.enter_context(nc.sbuf_tensor("k_z", [128, B, D], F32))
                normalise_all(nc, k, ps)
                local_transformer(nc, a, k, ps)
        if 3 in PHASES:
            cross_attention(nc, a, k, ps, "dense", {"phase": "p3", "Wq": k["L1_Wq"], "Wk": k["L1_Wk"], "Wv": k["L1_Wv"], "Wo": k["L1_We"],
                                                    "bq": k["c_L1_bq"], "bk": k["c_L1_bk"], "bv": k["r_L1_bv"], "bo": k["r_L1_bo"]})
        with ExitStack() as moe:
            k["moe_w1"] = moe.enter_context(nc.sbuf_tensor("k_moe_w1", [128, E, DFF], F32))
            k["moe_w2"] = moe.enter_context(nc.sbuf_tensor("k_moe_w2", [128, E, DFF // 128, D], F32))
            k["moe_loaded"] = m.sem("moe_loaded")
            if 6 in PHASES:
                with nc.Block() as block:
                    @block.sync
                    def _(sp):
                        sp.dma_start(k["moe_w1"][:, :, :], a["L2_ffn_W1"].rearrange("e d n -> d e n")).then_inc(k["moe_loaded"], 16)
                        sp.dma_start(k["moe_w2"][:, :, :, :].rearrange("p e c n -> p (e c) n"),
                                     a["L2_ffn_W2"].rearrange("e (c p) n -> p (e c) n", p=128)).then_inc(k["moe_loaded"], 16)
            if 4 in PHASES:
                quantised_dense(nc, a, k, ps)
            if 5 in PHASES:
                cross_attention(nc, a, k, ps, "dense", {"phase": "p5", "Wq": k["L2_Wq"], "Wk": k["L2_Wk"], "Wv": k["L2_Wv"],
                                                        "Wo": k["L2_Wo"], "bq": k["c_L2_bq"], "bk": k["c_L2_bk"],
                                                        "bv": k["r_L2_bv"], "bo": k["r_L2_bo"]})
            if 6 in PHASES:
                mixture_top1(nc, a, k, ps)
        if 7 in PHASES:
            cross_attention(nc, a, k, ps, "sampled", {"phase": "p7", "Wq": k["T_Wq"], "Wk": k["T_Wk"], "Wv": k["T_Wv"], "Wo": k["T_Wo"],
                                                      "bq": k["c_L3_bq"], "bk": k["c_L3_bk"], "bv": k["r_L3_bv"], "bo": k["r_L3_bo"]})
        if 8 in PHASES:
            adapters_top2(nc, a, k, ps)
        stored = m.sem("stored")
        with nc.Block() as block:
            @block.sync
            def _(sp):
                sp.dma_start(out.rearrange("b s d -> s b d"), k["x"][:, :, :]).then_inc(stored, 16)
                sp.wait_ge(stored, 16)


def rope_tables(np):
    half = np.arange(0, DH, 2, dtype=np.float32)
    inv_freq = (np.float32(1.0) / np.float32(10000.0) ** (half / np.float32(DH))).astype(np.float32)
    t = np.arange(S, dtype=np.float32)
    freqs = (t[:, None] * inv_freq[None, :]).astype(np.float32)
    base = ((half + np.float32(0.4 * DH)) / np.float32(1.4 * DH)).astype(np.float32)
    scale = base[None, :] ** ((t - S // 2) / np.float32(WINDOW // 2))[:, None]
    cos, sin = np.cos(freqs), np.sin(freqs)
    c = np.stack([np.concatenate([cos * f, cos * f], -1) for f in (scale, 1.0 / scale)], 1)
    s = np.stack([np.concatenate([-sin * f, sin * f], -1) for f in (scale, 1.0 / scale)], 1)
    return c.astype(np.float32), s.astype(np.float32)


_OUTS = [((B, S, D), 'float32')]


def kernel(**inputs):
    import numpy as _np
    import concourse.bacc as _bacc
    from concourse import mybir as _mybir
    from concourse.bass_utils import run_bass_kernel_spmd as _run

    nc = _bacc.Bacc("TRN2", target_bir_lowering=False, num_devices=1)
    arrays, args = {}, {}
    cos, sin = rope_tables(_np)
    named = dict(inputs)
    del named["mask_BxS_ff1"]
    named["rope_cos"] = cos
    named["rope_sin"] = sin
    for name, value in named.items():
        v = _np.ascontiguousarray(value)
        arrays[f"in_{name}_dram"] = v
        args[name] = nc.dram_tensor(f"in_{name}_dram", v.shape, _mybir.dt.from_np(v.dtype), kind="ExternalInput").ap()
    shape, dtype = _OUTS[0]
    out = nc.dram_tensor("out_0_dram", shape, _mybir.dt.from_np(_np.dtype(dtype)), kind="ExternalOutput").ap()
    build(nc, args, out)
    r = _run(nc, [arrays], core_ids=[0])
    return r.results[0]["out_0_dram"]
```

```python
from contextlib import ExitStack

import concourse.bass as bass
from concourse import mybir

ALU = mybir.AluOpType
ACT = mybir.ActivationFunctionType
AX = mybir.AxisListType
F32 = mybir.dt.float32
BF16 = mybir.dt.bfloat16
FP8 = mybir.dt.float8e4
I32 = mybir.dt.int32

B, S, D, S2 = 32, 128, 128, 77
LANES = 4
ITERS = B // LANES
WIDE = 2
GB = 4
ROUNDS = B // GB // WIDE
DEPTH, HEADS, DH = 6, 16, 64
INNER = HEADS * DH
HG = 8
WINDOW = 32
FF = int(D * 4 * 2 / 3)
FFC = [(0, 128), (128, 128), (256, FF - 256)]
XH, XD = 16, 8
NK = 5
DFF, E = 512, 8
BN = 64
NEG = -1e30
EPS = 1e-5
MAGIC = 1.5 * 2.0 ** 23
PHASES = (1, 2, 3, 4, 5, 6, 7, 8)


class Buffers:

    def __init__(self, nc, ctx, phase):
        self.nc, self.ctx, self.phase, self.held = nc, ctx, phase, []
        ctx.callback(self.free_sems)

    def free_sems(self):
        if self.held:
            self.nc.all_engine_barrier()
            self.nc.clear_and_free_semaphores(self.held)
            self.nc.all_engine_barrier()

    def sb(self, name, shape, dt=F32):
        return self.ctx.enter_context(self.nc.sbuf_tensor(f"{self.phase}_{name}", list(shape), dt))

    def lanes(self, name, shape, dt=F32, n=LANES):
        return [self.sb(f"{name}{i}", shape, dt) for i in range(n)]

    def sem(self, name):
        self.held.append(self.nc.alloc_semaphore(f"{self.phase}_{name}"))
        return self.held[-1]

    def sems(self, name, n=LANES):
        return [self.sem(f"{name}{i}") for i in range(n)]


def bc(ap, axis, n):
    shape = list(ap.shape)
    shape.insert(axis, n)
    return ap.unsqueeze(axis).to_broadcast(shape)


def cols(t, b, n=1):
    return t[:, bass.ds(b, n), :].rearrange("p b d -> p (b d)")


def setup_phase(nc, a, k, ps):
    with ExitStack() as ctx:
        m = Buffers(nc, ctx, "setup")
        s_load, s_zero, s_shape = m.sem("loaded"), m.sem("zeroed"), m.sem("shaped")
        s_turn, s_evac, s_int, s_col = m.sem("turned"), m.sem("turn_copied"), m.sem("mask_float"), m.sem("wide_column")
        raw = {n: m.sb(f"raw_{n}", [128, 128]) for n in ("Wk", "Wv", "Wq", "Wo", "Woff", "gate")}
        raw_b1 = m.sb("raw_b1", [E * DFF // 128, 128])
        raw_down = m.sb("raw_down", [128, 4, 128])
        raw_up = m.sb("raw_up", [128, E, BN])
        qmask = m.sb("qmask", [128, B * S2], I32)
        fmask = m.sb("fmask", [128, B * S2], I32)
        fmaskf = m.sb("fmaskf", [128, B, S2])
        iota_i = m.sb("iota_i", [128, S2], I32)
        pos_i = m.sb("pos_i", [128, 1], I32)
        col = m.sb("col", [128, 3])
        turns = [(raw[n][:, :], k[f"T_{n}"][:, :], 128) for n in ("Wk", "Wv", "Wq", "Wo")]
        turns += [(raw["Woff"][0:XH * NK, :], k["T_Woff"][:, :], XH * NK), (raw["gate"][0:E, :], k["T_gate"][:, :], E)]
        turns.append((raw_b1[:, :], k["T_b1"][:, :], E * DFF // 128))
        turns += [(raw_down[:, c, :], k["T_down"][:, c, :], 128) for c in range(4)]
        turns += [(raw_up[:, 2 * c:2 * c + 2, :].rearrange("p e n -> p (e n)"), k["T_up"][:, c, :], 128) for c in range(4)]

        loads = [(k["x"][:, :, :], a["x"].rearrange("b s d -> s b d"))]
        for n in ("Wk", "Wv", "Wq", "Wo"):
            loads.append((raw[n][:, :], a[f"L3_xattn_{n}"]))
        loads.append((raw["Woff"][0:XH * NK, :], a["L3_xattn_Woff"]))
        loads.append((raw["gate"][0:E, :], a["L3_ffn_gate_w"]))
        loads.append((raw_b1[:, :], a["L2_ffn_b1"].rearrange("e (c n) -> (e c) n", n=128)))
        loads.append((k["gateW"][:, :], a["L2_ffn_gate_W"]))
        loads.append((raw_down[:, :, :], a["L3_ffn_down_w"].rearrange("(c e) n d -> (e n) c d", c=4)))
        loads.append((raw_up[:, :, :], a["L3_ffn_up_w"].rearrange("e d n -> d e n")))
        loads.append((qmask[:, :], a["mask_BxS2_ik0"].rearrange("b s -> (b s)").partition_broadcast(128)))
        loads.append((fmask[:, :], a["mask_BxS2_if0"].rearrange("b s -> (b s)").partition_broadcast(128)))
        loads += [(col[:, 0:1], a["L0_xattn_w"]),
                  (col[:, 1:2], a["L0_xattn_Wcw"].rearrange("o d -> d o")),
                  (col[:, 2:3], a["L0_xattn_Wcb"].rearrange("o d -> d o"))]
        for n, src in (("L0_W", "L0_xattn_W"), ("L0_Ws", "L0_xattn_Ws"), ("L1_Wq", "L1_xattn_Wq"), ("L1_Wk", "L1_xattn_Wk"),
                       ("L1_Wv", "L1_xattn_Wv"), ("L1_We", "L1_xattn_We"), ("L2_Wq", "L2_xattn_Wq"), ("L2_Wo", "L2_xattn_Wo")):
            loads.append((k[n][:, :], a[src]))
        for n in ("Wk", "Wv"):
            loads.append((k[f"L2_{n}"][:, :].rearrange("p (h d) -> p h d", d=XD), bc(a[f"L2_xattn_{n}"], 1, XH)))
        loads.append((k["r_L2_bv"][:, :].rearrange("p (h d) -> p h d", d=XD), bc(a["L2_xattn_bv"].partition_broadcast(128), 1, XH)))
        for h in range(XH):
            loads.append((k["c_L2_bk"][h * XD:(h + 1) * XD, :], a["L2_xattn_bk"].rearrange("(d o) -> d o", o=1)))
        for n, src in (("c_L1_bq", "L1_xattn_bq"), ("c_L1_bk", "L1_xattn_bk"), ("c_L2_bq", "L2_xattn_bq"),
                       ("c_L3_bq", "L3_xattn_bq"), ("c_L3_bk", "L3_xattn_bk")):
            loads.append((k[n][:, :], a[src].rearrange("(d o) -> d o", o=1)))
        loads.append((k["c_L0_b"][:, :], a["L0_xattn_b"].rearrange("o d -> d o")))
        for n, src in (("r_L1_bv", "L1_xattn_bv"), ("r_L1_bo", "L1_xattn_be"), ("r_L2_bo", "L2_xattn_bo"),
                       ("r_L3_bv", "L3_xattn_bv"), ("r_L3_bo", "L3_xattn_bo"), ("r_L3_boff", "L3_xattn_boff"),
                       ("r_bcw", "L0_xattn_bcw"), ("r_bcb", "L0_xattn_bcb"), ("r_gateb", "L2_ffn_gate_b"),
                       ("r_sin", "L1_ffn_input_scale"), ("r_sk", "L1_ffn_kernel_scale"), ("r_fbias", "L1_ffn_bias")):
            loads.append((k[n][:, :], a[src].partition_broadcast(128)))
        loads.append((k["fkernel"][:, :], a["L1_ffn_kernel"]))
        loads.append((k["cosS"][:, :, :], a["rope_cos"]))
        loads.append((k["sinS"][:, :, :], a["rope_sin"]))
        for c in range(4):
            loads.append((k["c_down_b"][:, c:c + 1], a["L3_ffn_down_b"][2 * c:2 * c + 2, :].rearrange("e (n o) -> (e n) o", o=1)))

        with nc.Block() as block:
            @block.sync
            def _(sp):
                sp.wait_ge(s_zero, 16)
                for b in range(GB):
                    sp.dma_start(k["up_b"][E * b:E * b + E, b, :], a["L3_ffn_up_b"]).then_inc(s_load, 16)
                    sp.dma_start(k["b2blk"][32 * b:32 * b + E, b, :], a["L2_ffn_b2"]).then_inc(s_load, 16)
                for dst, src in loads:
                    sp.dma_start(dst, src).then_inc(s_load, 16)
                sp.wait_ge(s_load, 16 * (len(loads) + 2 * GB))

            n_loads = 16 * (len(loads) + 2 * GB)

            @block.gpsimd
            def _(pool):
                pool.memset(k["ident"][:, :], 0.0).then_inc(s_zero, 1)
                pool.memset(k["identb"][:, :], 0.0).then_inc(s_zero, 1)
                pool.memset(k["shift"][:, :], 0.0).then_inc(s_zero, 1)
                pool.memset(k["band"][:, :, :], 0.0).then_inc(s_zero, 1)
                pool.memset(k["headmask"][:, :], 1.0).then_inc(s_zero, 1)
                pool.memset(k["ones"][:, :], 1.0).then_inc(s_zero, 1)
                pool.memset(k["minus_half"][:, :], -0.5).then_inc(s_zero, 1)
                pool.memset(k["eps"][:, :], EPS).then_inc(s_zero, 1)
                pool.memset(k["huge"][:, :], 1e12).then_inc(s_zero, 1)
                pool.memset(k["eight"][:, :], 8.0).then_inc(s_zero, 1)
                pool.memset(k["wpad"][:, :], 0.0).then_inc(s_zero, 1)
                pool.memset(k["up_b"][:, :, :], 0.0).then_inc(s_zero, 1)
                pool.memset(k["b2blk"][:, :, :], 0.0).then_inc(s_zero, 1)
                pool.memset(k["lower"][:, :, :], 1.0).then_inc(s_zero, 1)
                pool.iota(iota_i[:, :], pattern=[[1, S2]], base=0, channel_multiplier=0).then_inc(s_zero, 1)
                pool.iota(pos_i[:, :], pattern=[[0, 1]], base=0, channel_multiplier=1).then_inc(s_zero, 1)
                pool.wait_ge(s_zero, 16)
                for n in ("ident", "identb"):
                    pool.affine_select(out=k[n][:, :], in_=k[n][:, :], compare_op=ALU.not_equal, fill=1.0, base=0,
                                       pattern=[[-1, 128]], channel_multiplier=1).then_inc(s_shape, 1)
                pool.affine_select(out=k["shift"][:, :], in_=k["shift"][:, :], compare_op=ALU.not_equal, fill=1.0,
                                   base=-1, pattern=[[1, 128]], channel_multiplier=-1).then_inc(s_shape, 1)
                pool.affine_select(out=k["band"][:, :, :], in_=k["band"][:, :, :], compare_op=ALU.is_ge, fill=NEG,
                                   base=0, pattern=[[0, 4], [-1, 128]], channel_multiplier=1).then_inc(s_shape, 1)
                pool.affine_select(out=k["headmask"][:, :], in_=k["headmask"][:, :], compare_op=ALU.is_ge, fill=0.0,
                                   base=0, pattern=[[-XD, XH]], channel_multiplier=1).then_inc(s_shape, 1)
                pool.affine_select(out=k["lower"][:, :, :], in_=k["lower"][:, :, :], compare_op=ALU.is_gt, fill=0.0,
                                   base=0, pattern=[[1, E], [-1, E]], channel_multiplier=0).then_inc(s_shape, 1)
                pool.wait_ge(s_shape, 6)
                pool.affine_select(out=k["band"][:, :, :], in_=k["band"][:, :, :], compare_op=ALU.is_ge, fill=NEG,
                                   base=WINDOW, pattern=[[0, 4], [1, 128]], channel_multiplier=-1).then_inc(s_shape, 1)
                pool.affine_select(out=k["headmask"][:, :], in_=k["headmask"][:, :], compare_op=ALU.is_ge, fill=0.0,
                                   base=XD - 1, pattern=[[XD, XH]], channel_multiplier=-1).then_inc(s_shape, 1)

            @block.tensor
            def _(pe):
                pe.wait_ge(s_load, n_loads)
                pe.wait_ge(s_shape, 8)
                for j, (src, _, n) in enumerate(turns):
                    if j >= 8:
                        pe.wait_ge(s_evac, j - 7)
                    nc.tensor.transpose(ps[:, j % 8, 0:n], src, k["ident"][0:n, 0:n]).then_inc(s_turn, 1)

            @block.scalar
            def _(act):
                for j, (_, dst, n) in enumerate(turns):
                    act.wait_ge(s_turn, j + 1)
                    nc.scalar.copy(dst, ps[:, j % 8, 0:n]).then_inc(s_evac, 1)

            @block.vector
            def _(dve):
                dve.wait_ge(s_load, n_loads)
                dve.wait_ge(s_zero, 16)
                nc.vector.tensor_copy(k["iota"][:, :], iota_i[:, :])
                nc.vector.tensor_copy(k["pos"][:, :], pos_i[:, :])
                nc.vector.tensor_copy(k["wpad"][:, 31:32], col[:, 0:1])
                nc.vector.tensor_scalar(k["Wcw"][:, :], k["ones"][:, :], col[:, 1:2], None, ALU.mult)
                nc.vector.tensor_scalar(k["Wcb"][:, :], k["ones"][:, :], col[:, 2:3], None, ALU.mult)
                nc.vector.tensor_scalar(k["negm"][:, :, :].rearrange("p b s -> p (b s)"), qmask[:, :], -1.0, 1.0,
                                        ALU.mult, ALU.add).then_inc(s_int, 1)
                nc.vector.tensor_scalar(fmaskf[:, :, :].rearrange("p b s -> p (b s)"), fmask[:, :], -1.0, 1.0,
                                        ALU.mult, ALU.add).then_inc(s_int, 1)
                for n in range(NK):
                    nc.vector.tensor_scalar(k["boffpos"][:, :].rearrange("p (h n) -> p h n", n=NK)[:, :, n],
                                            k["r_L3_boff"][:, :].rearrange("p (h n) -> p h n", n=NK)[:, :, n],
                                            float(-NK // 2 + n), None, ALU.add).then_inc(s_col, 1)
                dve.wait_ge(s_int, 2)
                nc.vector.tensor_scalar(k["negm"][:, :, :], k["negm"][:, :, :], NEG, None, ALU.mult)
                nc.vector.tensor_reduce(k["span"][:, :], fmaskf[:, :, :], AX.X, ALU.add).then_inc(s_int, 1)
                dve.wait_ge(s_col, NK)
                dve.wait_ge(s_int, 3)
                nc.vector.tensor_scalar(k["span"][:, :], k["span"][:, :], -1.0, None, ALU.add).then_inc(s_int, 1)
                nc.vector.tensor_tensor(k["sscale"][:, :], k["r_sin"][:, :], k["r_sk"][:, :], ALU.mult)
                dve.wait_ge(s_int, 4)
                nc.vector.tensor_scalar(k["sgn"][:, :], k["span"][:, :], 0.0, 2.0, ALU.is_ge, ALU.mult).then_inc(s_int, 1)
                dve.wait_ge(s_int, 5)
                nc.vector.tensor_scalar(k["sgn"][:, :], k["sgn"][:, :], -1.0, None, ALU.add).then_inc(s_int, 1)
                dve.wait_ge(s_int, 6)
                nc.vector.tensor_tensor(k["span"][:, :], k["span"][:, :], k["sgn"][:, :], ALU.mult).then_inc(s_int, 1)
                dve.wait_ge(s_int, 7)
                nc.vector.reciprocal(k["rspan"][:, :], k["span"][:, :])


def additive_attention(nc, a, k, ps):
    CF = 16
    NCH = S // CF
    Q = 4
    POOL_Q = 2
    RING = 4
    with ExitStack() as ctx:
        m = Buffers(nc, ctx, "p1")
        stat, mv, ve, rstd = m.lanes("stat", [128, 6]), m.lanes("mv", [128, 2]), m.lanes("ve", [128, 1]), m.lanes("rstd", [128, 1])
        xn, xnT = m.lanes("xn", [128, 128]), m.lanes("xnT", [128, 128])
        ctl, ctxT = m.lanes("ctl", [S2, 128]), m.lanes("ctxT", [128, S2])
        featT, proj = m.lanes("featT", [128, 128]), m.lanes("proj", [128, 3, S2])
        ring = m.lanes("ring", [128, 4, 4, S2], n=RING)
        sc, pr, tw = m.lanes("sc", [128, Q, S2]), m.lanes("pr", [128, Q, S2]), m.lanes("tw", [128, 2, Q, S2])
        nm, den, rd = m.lanes("nm", [128, Q]), m.lanes("den", [128, Q]), m.lanes("rd", [128, Q])
        z, g, gt = m.lanes("z", [128, 2, Q]), m.lanes("g", [128, 2, Q]), m.lanes("gt", [128, 2])
        spread = m.sb("spread", [128, Q, 128])
        upd = m.lanes("upd", [128, 128])
        passed = m.sem("passed")
        ctx_loaded, ctx_free = m.sems("ctx_loaded"), m.sems("ctx_free")
        stats, moments, var_eps, rstd_ready, xn_ready = (m.sems(n) for n in ("stats", "moments", "var_eps", "rstd", "xn"))
        turned, turn_copied, projected, proj_copied = (m.sems(n) for n in ("turned", "turn_copied", "projected", "proj_copied"))
        summed, pool_summed, tanhed, dotted = m.sem("summed"), m.sem("pool_summed"), m.sem("tanhed"), m.sem("dotted")
        rho_ready = m.sems("rho_ready")
        masked, maxed, lessened, expd, weighted, gathered, scaled, gates, spread_ps, spread_copied, updated, x_done = (
            m.sems(n) for n in ("masked", "maxed", "lessened", "expd", "weighted", "gathered", "scaled", "gates", "spread_ps",
                                "spread_copied", "updated", "x_done"))
        spread_zeroed, spread_ready = m.sem("spread_zeroed"), m.sem("spread_ready")
        ctxT_kept = m.sem("ctxT_kept")

        def steps(chunk_of, ends):
            for t in range(LANES * NCH + 1 + max(step for step, _ in ends)):
                if t < LANES * NCH:
                    chunk_of(*divmod(t, NCH))
                for step, stage in ends:
                    l, rest = divmod(t - NCH - step, NCH)
                    if rest == 0 and 0 <= l < LANES:
                        stage(l)

        with nc.Block() as block:
            @block.sync
            def _(sp):
                with sp.Fori(0, ITERS) as i:
                    u1 = sp.snap(i + 1)
                    for l in range(LANES):
                        sp.wait_ge(ctx_free[l], u1)
                        sp.dma_start(ctl[l][:, :], a["ctx_1024"][bass.ds(i * LANES + l, 1), :, :].rearrange("b s d -> (b s) d")
                                     ).then_inc(ctx_loaded[l], 16)

            @block.tensor
            def _(pe):
                pe.wait_ge(spread_ready, 4)
                pe.sem_inc(passed, 1)
                with pe.Fori(0, ITERS) as i:
                    u1 = pe.snap(i + 1)
                    u16 = pe.snap(i * 16 + 16)
                    for l in range(LANES):
                        pe.wait_ge(spread_copied[l], u1)
                        pe.wait_ge(xn_ready[l], u1)
                        pe.wait_ge(ctx_loaded[l], u16)
                        nc.tensor.transpose(ps[:, 2 * l, 0:128], xn[l][:, :], k["ident"][:, :])
                        nc.tensor.transpose(ps[:, 2 * l, 128:128 + S2], ctl[l][:, :], k["ident"][0:S2, 0:S2]
                                            ).then_inc(turned[l], 1)
                    for l in range(LANES):
                        pe.wait_ge(turn_copied[l], u1)
                        nc.tensor.matmul(ps[:, 2 * l, 0:128], k["L0_W"][:, :], xnT[l][:, :], start=True, stop=True)
                        for j, w in enumerate(("L0_Ws", "Wcw", "Wcb")):
                            last = nc.tensor.matmul(ps[:, 2 * l, 128 + j * S2:128 + (j + 1) * S2], k[w][:, :], ctxT[l][:, :],
                                                    start=True, stop=True)
                        last.then_inc(projected[l], 1)
                    def dots(l, c):
                        pe.wait_ge(tanhed, i * (LANES * NCH) + (l * NCH + c + 1))
                        for kk in range(4):
                            last = nc.tensor.matmul(ps[32 * kk:32 * kk + 32, 2 * l + 1, 0:Q * S2], k["wpad"][:, 31 - c:63 - c],
                                                    ring[c % RING][:, :, kk, :], start=(c == 0), stop=(c == NCH - 1))
                        if c == NCH - 1:
                            last.then_inc(rho_ready[l], 1)
                            pe.wait_ge(rho_ready[l], u1)
                            pe.sem_inc(dotted, 1)
                        else:
                            last.then_inc(dotted, 1)

                    def spread_gates(l):
                        pe.wait_ge(gates[l], u1)
                        for q in range(Q):
                            last = nc.tensor.matmul(ps[:, 2 * l, 0:2], spread[:, q, :], g[l][:, :, q], start=(q == 0), stop=(q == Q - 1))
                        last.then_inc(spread_ps[l], 1)

                    steps(dots, ((8, spread_gates),))

            @block.vector
            def _(dve):
                for l in range(LANES):
                    dve.sem_inc(spread_copied[l], 1)
                    dve.sem_inc(ctx_free[l], 1)
                dve.sem_inc(dotted, RING)
                with dve.Fori(0, ITERS) as i:
                    u1, u2 = dve.snap(i + 1), dve.snap(i + 2)
                    for l in range(LANES):
                        nc.vector.bn_stats(stat[l][:, :], cols(k["x"], i * LANES + l)).then_inc(stats[l], 1)
                    dve.wait_ge(stats[LANES - 1], u1)
                    dve.sem_inc(passed, 1)
                    for l in range(LANES):
                        nc.vector.bn_aggr(mv[l][:, :], stat[l][:, :]).then_inc(moments[l], 1)
                    for l in range(LANES):
                        dve.wait_ge(rstd_ready[l], u1)
                        nc.vector.tensor_scalar(xn[l][:, :], cols(k["x"], i * LANES + l), mv[l][:, 0:1], rstd[l][:, 0:1],
                                                ALU.subtract, ALU.mult).then_inc(xn_ready[l], 1)
                    w2 = dve.snap(i * 2 + 2)

                    def sums(l, c):
                        if c == 0:
                            dve.wait_ge(proj_copied[l], u1)
                        dve.wait_ge(dotted, i * (LANES * NCH) + (l * NCH + c + 1))
                        feats = featT[l][:, :].rearrange("p (q k c) -> p q k c", q=Q, c=NCH)[:, :, :, c]
                        for q in range(POOL_Q):
                            last = nc.vector.tensor_tensor(ring[c % RING][:, q, :, :], bc(feats[:, q, :], 2, S2),
                                                           bc(proj[l][:, 0, :], 1, 4), ALU.add)
                        last.then_inc(summed, 1)

                    def mask(l):
                        dve.wait_ge(rho_ready[l], u1)
                        nc.vector.tensor_tensor(sc[l][:, :, :], ps[:, 2 * l + 1, 0:Q * S2].rearrange("p (q s) -> p q s", q=Q),
                                                bc(cols(k["negm"], i * LANES + l), 1, Q), ALU.add).then_inc(masked[l], 1)

                    def largest(l):
                        dve.wait_ge(masked[l], u1)
                        nc.vector.tensor_reduce(nm[l][:, :], sc[l][:, :, :], AX.X, ALU.max).then_inc(maxed[l], 1)

                    def less_largest(l):
                        dve.wait_ge(maxed[l], u1)
                        nc.vector.tensor_tensor(sc[l][:, :, :], sc[l][:, :, :], bc(nm[l][:, :], 2, S2), ALU.subtract).then_inc(lessened[l], 1)

                    def weight(l):
                        dve.wait_ge(expd[l], u1)
                        nc.vector.tensor_reduce(den[l][:, :], pr[l][:, :, :], AX.X, ALU.add).then_inc(weighted[l], 1)
                        for j in range(2):
                            last = nc.vector.tensor_tensor(tw[l][:, j, :, :], pr[l][:, :, :], bc(proj[l][:, 1 + j, :], 1, Q), ALU.mult)
                        last.then_inc(weighted[l], 1)

                    def gather(l):
                        dve.wait_ge(weighted[l], w2)
                        nc.vector.reciprocal(rd[l][:, :], den[l][:, :]).then_inc(gathered[l], 1)
                        nc.vector.tensor_reduce(z[l][:, :, :], tw[l][:, :, :, :], AX.X, ALU.add).then_inc(gathered[l], 1)

                    def divide(l):
                        dve.wait_ge(gathered[l], w2)
                        nc.vector.tensor_tensor(z[l][:, :, :], z[l][:, :, :], bc(rd[l][:, :], 1, 2), ALU.mult).then_inc(scaled[l], 1)

                    def copy_gates(l):
                        dve.wait_ge(spread_ps[l], u1)
                        nc.vector.tensor_copy(gt[l][:, :], ps[:, 2 * l, 0:2]).then_inc(spread_copied[l], 1)

                    def update(l):
                        dve.wait_ge(spread_copied[l], u2)
                        nc.vector.tensor_scalar(upd[l][:, :], xn[l][:, :], gt[l][:, 0:1], gt[l][:, 1:2], ALU.mult, ALU.add
                                                ).then_inc(updated[l], 1)

                    def add_to_stream(l):
                        dve.wait_ge(updated[l], u1)
                        nc.vector.tensor_tensor(cols(k["x"], i * LANES + l), cols(k["x"], i * LANES + l), upd[l][:, :],
                                                ALU.add).then_inc(x_done[l], 1)

                    steps(sums, ((3, mask), (3, largest), (4, less_largest), (6, weight), (7, gather), (7, divide),
                                 (12, copy_gates), (12, update), (13, add_to_stream)))

            @block.scalar
            def _(act):
                with act.Fori(0, ITERS) as i:
                    u1 = act.snap(i + 1)
                    for l in range(LANES):
                        act.wait_ge(turned[l], u1)
                        nc.scalar.copy(xnT[l][:, :], ps[:, 2 * l, 0:128])
                        nc.scalar.copy(cols(k["ctxT"], i * LANES + l), ps[:, 2 * l, 128:128 + S2])
                        nc.scalar.copy(ctxT[l][:, :], ps[:, 2 * l, 128:128 + S2]).then_inc(turn_copied[l], 1)
                        act.sem_inc(ctx_free[l], 1)
                    for l in range(LANES):
                        act.wait_ge(projected[l], u1)
                        nc.scalar.activation(featT[l][:, :], ps[:, 2 * l, 0:128], ACT.Identity, bias=k["c_L0_b"][:, 0:1])
                        nc.scalar.copy(proj[l][:, :, :].rearrange("p j s -> p (j s)"), ps[:, 2 * l, 128:128 + 3 * S2]
                                       ).then_inc(proj_copied[l], 1)
                    def tanhs(l, c):
                        act.wait_ge(summed, i * (LANES * NCH) + (l * NCH + c + 1))
                        act.wait_ge(pool_summed, i * (LANES * NCH) + (l * NCH + c + 1))
                        h = ring[c % RING][:, :, :, :].rearrange("p q k s -> p (q k s)")
                        nc.scalar.activation(h, h, ACT.Tanh).then_inc(tanhed, 1)

                    def exponent(l):
                        act.wait_ge(lessened[l], u1)
                        nc.scalar.activation(pr[l][:, :, :].rearrange("p q s -> p (q s)"), sc[l][:, :, :].rearrange("p q s -> p (q s)"),
                                             ACT.Exp).then_inc(expd[l], 1)

                    def gate(l):
                        act.wait_ge(scaled[l], u1)
                        nc.scalar.activation(g[l][:, 0, :], z[l][:, 0, :], ACT.Tanh, bias=k["r_bcw"][:, 0:1])
                        nc.scalar.activation(g[l][:, 1, :], z[l][:, 1, :], ACT.Tanh, bias=k["r_bcb"][:, 0:1]).then_inc(gates[l], 1)

                    steps(tanhs, ((4, exponent), (7, gate)))

            @block.gpsimd
            def _(pool):
                nc.gpsimd.memset(spread[:, :, :], 0.0).then_inc(spread_zeroed, 1)
                pool.wait_ge(spread_zeroed, 1)
                for j in range(4):
                    rows = spread[32 * j:32 * j + NCH, :, :]
                    nc.gpsimd.affine_select(out=rows, in_=rows, compare_op=ALU.not_equal, fill=1.0, base=NCH * j,
                                            pattern=[[32, Q], [-1, 128]], channel_multiplier=1).then_inc(spread_ready, 1)
                pool.wait_ge(spread_ready, 4)
                pool.sem_inc(passed, 1)
                with pool.Fori(0, ITERS) as i:
                    u1 = pool.snap(i + 1)
                    for l in range(LANES):
                        pool.wait_ge(moments[l], u1)
                        nc.gpsimd.tensor_tensor(ve[l][:, :], mv[l][:, 1:2], k["eps"][:, 0:1], ALU.add).then_inc(var_eps[l], 1)
                        pool.wait_ge(var_eps[l], u1)
                        nc.gpsimd.tensor_tensor(rstd[l][:, :], ve[l][:, :], k["minus_half"][:, 0:1], ALU.pow
                                                ).then_inc(rstd_ready[l], 1)
                    for l in range(LANES):
                        pool.wait_ge(proj_copied[l], u1)
                        for c in range(NCH):
                            pool.wait_ge(dotted, i * (LANES * NCH) + (l * NCH + c + 1))
                            feats = featT[l][:, :].rearrange("p (q k c) -> p q k c", q=Q, c=NCH)[:, :, :, c]
                            for q in range(POOL_Q, Q):
                                last = nc.gpsimd.tensor_tensor(ring[c % RING][:, q, :, :], bc(feats[:, q, :], 2, S2),
                                                               bc(proj[l][:, 0, :], 1, 4), ALU.add)
                            last.then_inc(pool_summed, 1)


def normalise_all(nc, k, ps):
    with ExitStack() as ctx:
        m = Buffers(nc, ctx, "p2n")
        stat, mv, ve, rstd = m.sb("stat", [128, B, 6]), m.sb("mv", [128, B, 2]), m.sb("ve", [128, B]), m.sb("rstd", [128, B])
        passed = m.sem("passed")
        stats, moments, var_eps, rstd_ready = (m.sem(n) for n in ("stats", "moments", "var_eps", "rstd"))
        with nc.Block() as block:
            @block.vector
            def _(dve):
                for b in range(B):
                    nc.vector.bn_stats(stat[:, b, :], k["x"][:, b, :]).then_inc(stats, 1)
                dve.wait_ge(stats, B)
                dve.sem_inc(passed, 1)
                for b in range(B):
                    nc.vector.bn_aggr(mv[:, b, :], stat[:, b, :]).then_inc(moments, 1)
                dve.wait_ge(rstd_ready, 1)
                for b in range(B):
                    nc.vector.tensor_scalar(k["z"][:, b, :], k["x"][:, b, :], mv[:, b, 0:1], rstd[:, b:b + 1],
                                            ALU.subtract, ALU.mult)

            @block.gpsimd
            def _(pool):
                pool.wait_ge(moments, B)
                nc.gpsimd.tensor_tensor(ve[:, :], mv[:, :, 1], k["eps"][:, 0:1].to_broadcast([128, B]), ALU.add).then_inc(var_eps, 1)
                pool.wait_ge(var_eps, 1)
                nc.gpsimd.tensor_tensor(rstd[:, :], ve[:, :], k["minus_half"][:, 0:1].to_broadcast([128, B]), ALU.pow
                                        ).then_inc(rstd_ready, 1)


AGES = 5


def attention_layer(eng, layer, begin, slot):
    def numbers(i):
        it = layer * ITERS + i
        return i, eng.snap(it + 1), (eng.snap(it * 2 + 1), eng.snap(it * 2 + 2))

    def turn(before, now, after, slots=2 * LANES):
        for s in range(slots):
            age = []
            for j in range(AGES):
                n, following = (now, after) if s >= j else (before, now)
                q = (s - j) % (2 * LANES)
                age.append((q % LANES, q // LANES, n, following) if n else None)
            slot(age)

    first, last = numbers(0), ITERS - 1
    begin(first)
    turn(None, first, numbers(1))
    with eng.Fori(1, last) as i:
        turn(numbers(i - 1), numbers(i), numbers(i + 1))
    turn(numbers(last - 1), numbers(last), None)
    turn(numbers(last), None, None, AGES - 1)


def ffn_layer(eng, layer, slot):
    def numbers(i):
        it = layer * ROUNDS + i
        return i, eng.snap(it + 1), (eng.snap(it * 3 + 1), eng.snap(it * 3 + 2), eng.snap(it * 3 + 3)), eng.snap(it * 4 + 4)

    first = numbers(0)
    slot((0, first), None)
    slot((1, first), (0, first))
    with eng.Fori(1, ROUNDS) as i:
        n, before = numbers(i), numbers(i - 1)
        slot((0, n), (1, before))
        slot((1, n), (0, n))
    slot(None, (1, numbers(ROUNDS - 1)))


def local_transformer(nc, a, k, ps):
    QK = 2 * HG
    with ExitStack() as ctx:
        m = Buffers(nc, ctx, "p2")
        wqkv, wo = m.sb("wqkv", [128, 3, 2, HG * DH]), m.sb("wo", [128, HG, D])
        w1, w2 = m.sb("w1", [128, 2 * FF]), m.sb("w2", [128, 3, D])
        b1, gcol, bcol, b2 = m.sb("b1", [128, 2, 3]), m.sb("gcol", [128, 1]), m.sb("bcol", [128, 1]), m.sb("b2", [128, D])
        qks, tabA, tabB = m.sb("qks", [128, 2, DH]), m.sb("tabA", [128, 2, DH]), m.sb("tabB", [128, 2, DH])
        zl, zT = m.lanes("zl", [128, 128]), m.lanes("zT", [128, 128])
        sq = m.lanes("sq", [128, QK, DH])
        ropeB = sq
        qn = m.lanes("qn", [128, 2, HG, DH])
        probs = [t[:, :, :, :].rearrange("p a h d -> p (a h d)").rearrange("p (r j n) -> p r j n", r=2, j=4) for t in qn]
        rope = m.lanes("rope", [128, 2, HG, DH])
        oh = [t[:, 0, :, :] for t in rope]
        qkT = m.lanes("qkT", [128, 2, 4, 128])
        vx = m.lanes("vx", [128, HEADS, DH + 1])
        oT = m.lanes("oT", [128, HG, 128])
        ss, rn, rn1 = m.lanes("ss", [128, QK]), m.lanes("rn", [128, QK]), m.lanes("rn1", [128, QK])
        nm, rd = m.lanes("nm", [128, HG]), m.lanes("rd", [128, HG])

        attn_loaded, attn_free, ffn_loaded, ffn_free = (m.sem(n) for n in ("attn_loaded", "attn_free", "ffn_loaded", "ffn_free"))
        passed = m.sem("passed")
        tabs_half, tabs_ready = m.sem("tabs_half"), m.sem("tabs_ready")
        (zl_ready, zT_ps, zT_ready, v_ps, v_ready, qk_ps, sq_ready, ss_ready, ss_floored, rn_ready, qn_ready, ropeB_ready,
         ropeA_ready, rope_ready, qkT_ps, qkT_ready, s_ps, max_ready, sub_ready, p_ready, pT_ps, pT_ready, pv_ps, rd_ready,
         o_ready, oT_ps, oT_ready, y_ps, z_done) = (
            m.sems(n) for n in ("zl", "zT_ps", "zT", "v_ps", "v", "qk_ps", "sq", "ss", "ss_floored", "rn", "qn", "ropeB", "ropeA",
                                "rope", "qkT_ps", "qkT", "s_ps", "max", "sub", "p", "pT_ps", "pT", "pv_ps", "rd", "o",
                                "oT_ps", "oT", "y_ps", "z_done"))
        fz = [t[:, :, :, :].rearrange("p a h d -> p (a h d)")[:, 0:512].rearrange("p (b d) -> p b d", b=GB) for t in qn[0:WIDE]]
        fxn = [t[:, :, :, :].rearrange("p a h d -> p (a h d)")[:, 512:1024].rearrange("p (b d) -> p b d", b=GB) for t in qn[0:WIDE]]
        fsecond = [t[:, :, :].rearrange("p a d -> p (a d)")[:, 0:256].rearrange("p (b d) -> p b d", b=GB) for t in sq[0:WIDE]]
        fxT = [t[:, :, :, :].rearrange("p a h d -> p (a h d)")[:, 0:512] for t in qkT[0:WIDE]]
        fg = [[t[:, :, :, :].rearrange("p a h d -> p (a h d)")[:, c:c + 512] for t, c in ((rope[l], 0), (qn[l], 512))] for l in range(WIDE)]
        fh = [[t[:, :, :].rearrange("p a d -> p (a d)")[:, 0:512] for t in (oT[l], oT[l + 2], sq[l + 2])] for l in range(WIDE)]
        fzb = [t[:, :, :, :].rearrange("p a h d -> p (a h d)")[:, 512:1024].rearrange("p (b d) -> p b d", b=GB) for t in rope[0:WIDE]]
        fst, fmv, fve, frs = (m.lanes(n, s, n=WIDE) for n, s in (("fst", [128, GB, 6]), ("fmv", [128, GB, 2]), ("fve", [128, GB]),
                                                                 ("frs", [128, GB])))
        (f_split, f_shift_ps, f_shifted, f_stats, f_moments, f_eps, f_rs, f_xn, f_xT_ps, f_xT, f_y_ps, f_zb, f_done) = (
            m.sems(n, WIDE) for n in ("f_split", "f_shift_ps", "f_shifted", "f_stats", "f_moments", "f_eps", "f_rs", "f_xn",
                                      "f_xT_ps", "f_xT", "f_y_ps", "f_zb", "f_done"))
        f_ag_ps, f_gelu, f_h = m.sems("f_ag_ps", WIDE), m.sems("f_gelu", WIDE), m.sems("f_h", WIDE)

        N_ATTN, N_FFN_LOADS = 6, 12
        z = k["z"]

        with nc.Block() as block:
            @block.sync
            def _(sp):
                with sp.Fori(0, DEPTH) as layer:
                    n1 = sp.snap(layer + 1)
                    row = lambda t: a[f"L0_ffn_{t}"][bass.ds(layer, 1)]
                    sp.wait_ge(attn_free, n1)
                    for j in range(3):
                        sp.dma_start(wqkv[:, j, :, :], row("Wqkv").rearrange("o d (j h n) -> (o d) j h n", j=3, h=2)[:, j, :, :]
                                     ).then_inc(attn_loaded, 16)
                    sp.dma_start(wo[:, :, :], row("Wo").rearrange("o (c p) n -> p (o c) n", p=128)).then_inc(attn_loaded, 16)
                    sp.dma_start(qks[:, 0, :], row("q_scale").rearrange("o d -> (o d)").partition_broadcast(128)).then_inc(attn_loaded, 16)
                    sp.dma_start(qks[:, 1, :], row("k_scale").rearrange("o d -> (o d)").partition_broadcast(128)).then_inc(attn_loaded, 16)
                    sp.wait_ge(ffn_free, n1)
                    sp.dma_start(w1[:, :], row("W1").rearrange("o d n -> (o d) n")).then_inc(ffn_loaded, 16)
                    sp.dma_start(w2[:, 0:2, :], row("W2")[:, 0:256, :].rearrange("o (c p) n -> p (o c) n", p=128)).then_inc(ffn_loaded, 16)
                    sp.dma_start(w2[0:FF - 256, 2, :], row("W2")[:, 256:FF, :].rearrange("o p n -> (o p) n")).then_inc(ffn_loaded, 16)
                    for c, (f0, fn) in enumerate(FFC):
                        for half in range(2):
                            sp.dma_start(b1[0:fn, half, c:c + 1],
                                         row("b1")[:, half * FF + f0:half * FF + f0 + fn].rearrange("o d -> d o")).then_inc(ffn_loaded, 16)
                    sp.dma_start(gcol[:, :], row("ln_g").rearrange("o d -> d o")).then_inc(ffn_loaded, 16)
                    sp.dma_start(bcol[:, :], row("ln_b").rearrange("o d -> d o")).then_inc(ffn_loaded, 16)
                    sp.dma_start(b2[:, :], row("b2").rearrange("o d -> (o d)").partition_broadcast(128)).then_inc(ffn_loaded, 16)

            @block.tensor
            def _(pe):
                def rows_turn(l, n):
                    pe.wait_ge(zl_ready[l], n[1])
                    nc.tensor.transpose(ps[:, 2 * l + 1, 0:128], zl[l][:, :], k["ident"][:, :]).then_inc(zT_ps[l], 1)

                def next_rows_turn(l, h, n, following):
                    if h == 1 and following:
                        pe.wait_ge(o_ready[l], n[2][1])
                        rows_turn(l, following)

                def queries_keys(l, h, n, following):
                    if h == 0:
                        pe.wait_ge(z_done[l], n[1])
                        pe.wait_ge(zT_ready[l], n[1])
                    else:
                        pe.wait_ge(oT_ready[l], n[2][0])
                    for j in range(2):
                        last = nc.tensor.matmul(ps[:, 2 * l + j, :], zT[l][:, :], wqkv[:, j, h, :], start=True, stop=True)
                    last.then_inc(qk_ps[l], 1)

                def values(l, h, n, following, j):
                    if h == 0:
                        pe.wait_ge(qn_ready[l], n[2][0])
                        nc.tensor.matmul(ps[:, 2 * l + j, :], zT[l][:, :], wqkv[:, 2, j, :], start=True, stop=True).then_inc(v_ps[l], 1)

                def qkT_turn(l, h, n, following):
                    if h == 0:
                        pe.wait_ge(v_ready[l], n[2][1])
                    pe.wait_ge(rope_ready[l], n[2][h])
                    for j in range(2):
                        for c in range(4):
                            last = nc.tensor.transpose(ps[:, 2 * l + j, c * 128:(c + 1) * 128],
                                                       rope[l][:, j, 2 * c:2 * c + 2, :].rearrange("p h d -> p (h d)"), k["ident"][:, :])
                    last.then_inc(qkT_ps[l], 1)

                def scores(l, h, n, following):
                    pe.wait_ge(qkT_ready[l], n[2][h])
                    for r in range(2):
                        nc.tensor.matmul(ps[:, 2 * l + r, :], k["identb"][:, :], k["band"][:, :, :].rearrange("p j n -> p (j n)"),
                                         start=True, stop=False)
                    for c in range(4):
                        for r in range(2):
                            last = nc.tensor.matmul(ps[:, 2 * l + r, c * 128:(c + 1) * 128],
                                                    qkT[l][DH * r:DH * r + DH, 0, c, :], qkT[l][DH * r:DH * r + DH, 1, c, :],
                                                    start=False, stop=(c == 3))
                    last.then_inc(s_ps[l], 1)

                def probs_turn(l, h, n, following):
                    pe.wait_ge(p_ready[l], n[2][h])
                    for r in range(2):
                        for c in range(4):
                            last = nc.tensor.transpose(ps[:, 2 * l + r, c * 128:(c + 1) * 128], probs[l][:, r, c, :], k["ident"][:, :])
                    last.then_inc(pT_ps[l], 1)

                def values_sum(l, h, n, following):
                    pe.wait_ge(pT_ready[l], n[2][h])
                    for r in range(2):
                        for c in range(4):
                            last = nc.tensor.matmul(ps[:, 2 * l + r, c * (DH + 1):(c + 1) * (DH + 1)], qkT[l][:, r, c, :],
                                                    vx[l][:, h * HG + 2 * c + r, :], start=True, stop=True)
                    last.then_inc(pv_ps[l], 1)

                def out_turn(l, h, n, following):
                    pe.wait_ge(o_ready[l], n[2][h])
                    for c in range(4):
                        last = nc.tensor.transpose(ps[:, 2 * l, c * 128:(c + 1) * 128],
                                                   oh[l][:, 2 * c:2 * c + 2, :].rearrange("p h d -> p (h d)"), k["ident"][:, :])
                    last.then_inc(oT_ps[l], 1)

                def out_project(l, h, n, following):
                    if h == 1:
                        pe.wait_ge(oT_ready[l], n[2][1])
                        for c in range(HG):
                            last = nc.tensor.matmul(ps[:, 2 * l, 0:128], oT[l][:, c, :], wo[:, c, :], start=(c == 0), stop=(c == HG - 1))
                        last.then_inc(y_ps[l], 1)

                def begin(n):
                    for l in range(LANES):
                        rows_turn(l, n)

                def slot(age):
                    if age[0]:
                        queries_keys(*age[0])
                    if age[1]:
                        values(*age[1], 1)
                    if age[3]:
                        values_sum(*age[3])
                    if age[1]:
                        qkT_turn(*age[1])
                    if age[2]:
                        probs_turn(*age[2])
                    if age[3]:
                        next_rows_turn(*age[3])
                        out_turn(*age[3])
                    if age[1]:
                        scores(*age[1])
                    if age[3]:
                        out_project(*age[3])
                    if age[0]:
                        values(*age[0], 0)

                def shift(l, n):
                    pe.wait_ge(f_split[l], n[1])
                    pe.wait_ge(f_done[l], n[1])
                    nc.tensor.matmul(ps[:, 4 * l, 0:256], k["shift"][:, :], fsecond[l], start=True, stop=True).then_inc(f_shift_ps[l], 1)

                def x_turn(l, n):
                    pe.wait_ge(f_xn[l], n[1])
                    for b in range(GB):
                        last = nc.tensor.transpose(ps[:, 4 * l + 1, b * 128:(b + 1) * 128], fxn[l][:, b, :], k["ident"][:, :])
                    last.then_inc(f_xT_ps[l], 1)

                def gate_up(l, c, n):
                    if c == 0:
                        pe.wait_ge(f_xT[l], n[1])
                    if c == 2:
                        pe.wait_ge(f_h[l], n[2][0])
                    (f0, fn), o = FFC[c], 4 * l + 2 * (c % 2)
                    nc.tensor.matmul(ps[0:fn, o, :], w1[:, f0:f0 + fn], fxT[l], start=True, stop=True)
                    nc.tensor.matmul(ps[0:fn, o + 1, :], w1[:, FF + f0:FF + f0 + fn], fxT[l], start=True, stop=True
                                     ).then_inc(f_ag_ps[l], 1)

                def down(l, n):
                    pe.wait_ge(f_h[l], n[2][2])
                    for b in range(GB):
                        for c, (f0, fn) in enumerate(FFC):
                            last = nc.tensor.matmul(ps[:, 4 * l + 2, b * 128:(b + 1) * 128], fh[l][c][0:fn, b * 128:(b + 1) * 128],
                                                    w2[0:fn, c, :], start=(c == 0), stop=(c == 2))
                    last.then_inc(f_y_ps[l], 1)

                def ffn_slot(F, R):
                    f, fn = F or (0, None)
                    r, rn = R or (0, None)
                    if F:
                        shift(f, fn)
                    if R:
                        gate_up(r, 1, rn)
                        gate_up(r, 2, rn)
                    if F:
                        x_turn(f, fn)
                    if R:
                        down(r, rn)
                    if F:
                        gate_up(f, 0, fn)

                with pe.Fori(0, DEPTH) as layer:
                    pe.wait_ge(attn_loaded, layer * (16 * N_ATTN) + 16 * N_ATTN)
                    pe.sem_inc(passed, 1)
                    attention_layer(pe, layer, begin, slot)
                    for l in range(LANES):
                        pe.wait_ge(y_ps[l], layer * ITERS + ITERS)
                    pe.sem_inc(attn_free, 1)
                    pe.wait_ge(ffn_loaded, layer * (16 * N_FFN_LOADS) + 16 * N_FFN_LOADS)
                    pe.sem_inc(passed, 1)
                    ffn_layer(pe, layer, ffn_slot)

            @block.vector
            def _(dve):
                for l in range(LANES):
                    nc.vector.memset(vx[l][:, :, DH:DH + 1], 1.0)
                    nc.vector.memset(zT[l][64:128, 0:1], 0.0).then_inc(z_done[l], 1)
                for l in range(WIDE):
                    dve.sem_inc(f_done[l], 1)

                def norms(l, h, n, following):
                    dve.wait_ge(sq_ready[l], n[2][h])
                    nc.vector.tensor_reduce(ss[l][:, :], sq[l][:, :, :], AX.X, ALU.add).then_inc(ss_ready[l], 1)

                def normalise(l, h, n, following):
                    dve.wait_ge(rn_ready[l], n[2][h])
                    nc.vector.tensor_tensor(qn[l][:, :, :, :].rearrange("p a h d -> p (a h) d"),
                                            ps[:, 2 * l:2 * l + 2, :].rearrange("p a (h d) -> p (a h) d", d=DH),
                                            bc(rn[l][:, :], 2, DH), ALU.mult).then_inc(qn_ready[l], 1)

                def rotate(l, h, n, following):
                    dve.wait_ge(qn_ready[l], n[2][h])
                    nc.vector.tensor_tensor(rope[l][:, :, :, :], qn[l][:, :, :, :], bc(tabA[:, :, :], 2, HG), ALU.mult
                                            ).then_inc(ropeA_ready[l], 1)

                def rotate_sum(l, h, n, following):
                    dve.wait_ge(ropeA_ready[l], n[2][h])
                    dve.wait_ge(ropeB_ready[l], n[2][h])
                    flat = rope[l][:, :, :, :].rearrange("p a h d -> p (a h d)")
                    nc.vector.tensor_tensor(flat, flat, ropeB[l][:, :, :].rearrange("p h d -> p (h d)"), ALU.add
                                            ).then_inc(rope_ready[l], 1)

                def largest(l, h, n, following):
                    dve.wait_ge(s_ps[l], n[2][h])
                    nc.vector.tensor_reduce(nm[l][:, :], ps[:, 2 * l:2 * l + 2, :].rearrange("p r (j n) -> p (r j) n", n=128),
                                            AX.X, ALU.max).then_inc(max_ready[l], 1)

                def less_largest(l, h, n, following):
                    dve.wait_ge(max_ready[l], n[2][h])
                    nc.vector.tensor_tensor(probs[l].rearrange("p r j n -> p (r j) n"),
                                            ps[:, 2 * l:2 * l + 2, :].rearrange("p r (j n) -> p (r j) n", n=128),
                                            bc(nm[l][:, :], 2, 128), ALU.subtract).then_inc(sub_ready[l], 1)

                def inverse_sums(l, h, n, following):
                    dve.wait_ge(pv_ps[l], n[2][h])
                    pv = ps[:, 2 * l:2 * l + 2, 0:4 * (DH + 1)].rearrange("p r (j d) -> p r j d", d=DH + 1)
                    nc.vector.reciprocal(rd[l][:, :].rearrange("p (r j) -> p r j", r=2), pv[:, :, :, DH]).then_inc(rd_ready[l], 1)

                def outputs(l, h, n, following):
                    dve.wait_ge(rd_ready[l], n[2][h])
                    pv = ps[:, 2 * l:2 * l + 2, 0:4 * (DH + 1)].rearrange("p r (j d) -> p r j d", d=DH + 1)
                    nc.vector.tensor_tensor(oh[l].rearrange("p (j r) d -> p r j d", r=2), pv[:, :, :, 0:DH],
                                            bc(rd[l][:, :].rearrange("p (r j) -> p r j", r=2), 3, DH), ALU.mult
                                            ).then_inc(o_ready[l], 1)

                def add_to_stream(l, h, n, following):
                    if h == 1:
                        dve.wait_ge(y_ps[l], n[1])
                        zb = cols(z, n[0] * LANES + l)
                        nc.vector.tensor_tensor(zb, zb, ps[:, 2 * l, 0:128], ALU.add).then_inc(z_done[l], 1)

                def begin(n):
                    pass

                def slot(age):
                    if age[4]:
                        outputs(*age[4])
                    if age[1]:
                        normalise(*age[1])
                    if age[2]:
                        largest(*age[2])
                    if age[4]:
                        add_to_stream(*age[4])
                    if age[1]:
                        rotate(*age[1])
                    if age[2]:
                        less_largest(*age[2])
                    if age[1]:
                        rotate_sum(*age[1])
                    if age[0]:
                        norms(*age[0])
                    if age[3]:
                        inverse_sums(*age[3])

                def statistics(l, n):
                    dve.wait_ge(f_shifted[l], n[1])
                    for b in range(GB):
                        nc.vector.bn_stats(fst[l][:, b, :], fz[l][:, b, :]).then_inc(f_stats[l], 1)

                def moments_of(l, n):
                    dve.wait_ge(f_stats[l], n[3])
                    dve.sem_inc(passed, 1)
                    for b in range(GB):
                        last = nc.vector.bn_aggr(fmv[l][:, b, :], fst[l][:, b, :])
                    last.then_inc(f_moments[l], 1)

                def normalise_rows(l, n):
                    dve.wait_ge(f_rs[l], n[1])
                    for b in range(GB):
                        last = nc.vector.tensor_scalar(fxn[l][:, b, :], fz[l][:, b, :], fmv[l][:, b, 0:1], frs[l][:, b:b + 1],
                                                       ALU.subtract, ALU.mult)
                    last.then_inc(f_xn[l], 1)

                def product(l, c, n):
                    dve.wait_ge(f_gelu[l], n[2][c])
                    fn = FFC[c][1]
                    nc.vector.scalar_tensor_tensor(out=fh[l][c][0:fn, :], in0=ps[0:fn, 4 * l + 2 * (c % 2), :],
                                                   scalar=b1[0:fn, 0, c:c + 1], in1=fg[l][c % 2][0:fn, :], op0=ALU.add, op1=ALU.mult
                                                   ).then_inc(f_h[l], 1)

                def add_group(l, n):
                    dve.wait_ge(f_y_ps[l], n[1])
                    dve.wait_ge(f_zb[l], n[1])
                    nc.vector.tensor_tensor(cols(z, (n[0] * WIDE + l) * GB, GB), fzb[l].rearrange("p b d -> p (b d)"),
                                            ps[:, 4 * l + 2, :], ALU.add).then_inc(f_done[l], 1)

                def ffn_slot(F, R):
                    f, fn = F or (0, None)
                    r, rn = R or (0, None)
                    if R:
                        product(r, 0, rn)
                    if F:
                        statistics(f, fn)
                        moments_of(f, fn)
                    if R:
                        product(r, 1, rn)
                    if F:
                        normalise_rows(f, fn)
                    if R:
                        product(r, 2, rn)
                        add_group(r, rn)

                with dve.Fori(0, DEPTH) as layer:
                    dve.wait_ge(tabs_ready, layer * 2 + 2)
                    for l in range(WIDE):
                        dve.wait_ge(f_done[l], layer * ROUNDS + 1)
                    dve.sem_inc(passed, 1)
                    attention_layer(dve, layer, begin, slot)
                    for l in range(LANES):
                        dve.wait_ge(z_done[l], layer * ITERS + (ITERS + 1))
                    dve.wait_ge(ffn_loaded, layer * (16 * N_FFN_LOADS) + 16 * N_FFN_LOADS)
                    dve.sem_inc(passed, 1)
                    ffn_layer(dve, layer, ffn_slot)
                    for l in range(WIDE):
                        dve.wait_ge(f_done[l], layer * ROUNDS + (ROUNDS + 1))
                    dve.sem_inc(ffn_free, 1)
                for b in range(0, B, GB):
                    nc.vector.tensor_tensor(k["x"][:, b:b + GB, :], k["x"][:, b:b + GB, :], z[:, b:b + GB, :], ALU.add)

            @block.scalar
            def _(act):
                def rows_copy(l, n):
                    nc.scalar.copy(zl[l][:, :], cols(z, n[0] * LANES + l)).then_inc(zl_ready[l], 1)

                def next_rows_copy(l, h, n, following):
                    if h == 1 and following:
                        rows_copy(l, following)

                def zT_copy(l, n):
                    act.wait_ge(zT_ps[l], n[1])
                    nc.scalar.copy(zT[l][0:64, :], ps[0:64, 2 * l + 1, 0:128])
                    nc.scalar.copy(zT[l][64:128, 1:128], ps[64:128, 2 * l + 1, 0:127]).then_inc(zT_ready[l], 1)

                def next_zT_copy(l, h, n, following):
                    if h == 1 and following:
                        zT_copy(l, following)

                def values_copy(l, h, n, following, j):
                    if h == 0:
                        act.wait_ge(v_ps[l], n[2][j])
                        nc.scalar.copy(vx[l][:, HG * j:HG * j + HG, 0:DH], ps[:, 2 * l + j, :].rearrange("p (h d) -> p h d", d=DH)
                                       ).then_inc(v_ready[l], 1)

                def squares(l, h, n, following):
                    act.wait_ge(qk_ps[l], n[2][h])
                    nc.scalar.activation(sq[l][:, :, :].rearrange("p h d -> p (h d)"),
                                         ps[:, 2 * l:2 * l + 2, :].rearrange("p a n -> p (a n)"), ACT.Square).then_inc(sq_ready[l], 1)

                def qkT_copy(l, h, n, following):
                    act.wait_ge(qkT_ps[l], n[2][h])
                    nc.scalar.copy(qkT[l][:, :, :, :].rearrange("p a c n -> p (a c n)"),
                                   ps[:, 2 * l:2 * l + 2, :].rearrange("p a n -> p (a n)")).then_inc(qkT_ready[l], 1)

                def exponent(l, h, n, following):
                    act.wait_ge(sub_ready[l], n[2][h])
                    pf = probs[l].rearrange("p r j n -> p (r j n)")
                    nc.scalar.activation(pf, pf, ACT.Exp).then_inc(p_ready[l], 1)

                def pT_copy(l, h, n, following):
                    act.wait_ge(pT_ps[l], n[2][h])
                    nc.scalar.copy(qkT[l][:, :, :, :].rearrange("p a c n -> p (a c n)"),
                                   ps[:, 2 * l:2 * l + 2, :].rearrange("p a n -> p (a n)")).then_inc(pT_ready[l], 1)

                def oT_copy(l, h, n, following):
                    act.wait_ge(oT_ps[l], n[2][h])
                    nc.scalar.copy(oT[l][:, 4 * h:4 * h + 4, :].rearrange("p c n -> p (c n)"), ps[:, 2 * l, :]).then_inc(oT_ready[l], 1)

                def begin(n):
                    for l in range(LANES):
                        rows_copy(l, n)
                    for l in range(LANES):
                        zT_copy(l, n)

                def slot(age):
                    if age[1]:
                        values_copy(*age[1], 0)
                    if age[0]:
                        squares(*age[0])
                    if age[1]:
                        values_copy(*age[1], 1)
                    if age[2]:
                        exponent(*age[2])
                    if age[1]:
                        qkT_copy(*age[1])
                        next_rows_copy(*age[1])
                    if age[2]:
                        pT_copy(*age[2])
                    if age[3]:
                        next_zT_copy(*age[3])
                        oT_copy(*age[3])

                def split(l, n):
                    act.wait_ge(f_done[l], n[1])
                    zb = z[:, bass.ds((n[0] * WIDE + l) * GB, GB), :]
                    nc.scalar.copy(fz[l][:, :, 0:64], zb[:, :, 0:64])
                    nc.scalar.copy(fsecond[l], zb[:, :, 64:128]).then_inc(f_split[l], 1)

                def shift_copy(l, n):
                    act.wait_ge(f_shift_ps[l], n[1])
                    nc.scalar.copy(fz[l][:, :, 64:128], ps[:, 4 * l, 0:256].rearrange("p (b d) -> p b d", b=GB)).then_inc(f_shifted[l], 1)

                def scale_shift(l, n):
                    act.wait_ge(f_xT_ps[l], n[1])
                    nc.scalar.activation(fxT[l], ps[:, 4 * l + 1, :], ACT.Identity, scale=gcol[:, 0:1], bias=bcol[:, 0:1]
                                         ).then_inc(f_xT[l], 1)

                def gate(l, c, n):
                    act.wait_ge(f_ag_ps[l], n[2][c])
                    if c == 2:
                        act.wait_ge(f_h[l], n[2][0])
                    fn = FFC[c][1]
                    nc.scalar.activation(fg[l][c % 2][0:fn, :], ps[0:fn, 4 * l + 2 * (c % 2) + 1, :], ACT.Gelu,
                                         bias=b1[0:fn, 1, c:c + 1]).then_inc(f_gelu[l], 1)

                def ffn_slot(F, R):
                    f, fn = F or (0, None)
                    r, rn = R or (0, None)
                    if F:
                        split(f, fn)
                    if R:
                        gate(r, 0, rn)
                    if F:
                        shift_copy(f, fn)
                    if R:
                        gate(r, 1, rn)
                        gate(r, 2, rn)
                    if F:
                        scale_shift(f, fn)

                with act.Fori(0, DEPTH) as layer:
                    for l in range(LANES):
                        act.wait_ge(z_done[l], layer * ITERS + 1)
                    for l in range(WIDE):
                        act.wait_ge(f_done[l], layer * ROUNDS + 1)
                    attention_layer(act, layer, begin, slot)
                    for l in range(LANES):
                        act.wait_ge(z_done[l], layer * ITERS + (ITERS + 1))
                    act.wait_ge(ffn_loaded, layer * (16 * N_FFN_LOADS) + 16 * N_FFN_LOADS)
                    ffn_layer(act, layer, ffn_slot)

            @block.gpsimd
            def _(pool):
                pool.sem_inc(attn_free, 1)
                pool.sem_inc(ffn_free, 1)
                H2 = DH // 2

                def inverse_norms(l, h, n, following):
                    pool.wait_ge(ss_ready[l], n[2][h])
                    pool.sem_inc(passed, 1)
                    nc.gpsimd.tensor_scalar(rn1[l][:, :], ss[l][:, :], 1e-24, None, ALU.max).then_inc(ss_floored[l], 1)
                    pool.wait_ge(ss_floored[l], n[2][h])
                    nc.gpsimd.tensor_tensor(rn[l][:, :], rn1[l][:, :], k["minus_half"][:, :], ALU.pow).then_inc(rn_ready[l], 1)

                def rotate_partner(l, h, n, following):
                    pool.wait_ge(qn_ready[l], n[2][h])
                    out = ropeB[l][:, :, :].rearrange("p (a h) d -> p a h d", a=2)
                    for half in range(2):
                        last = nc.gpsimd.tensor_tensor(out[:, :, :, half * H2:(half + 1) * H2],
                                                       qn[l][:, :, :, (1 - half) * H2:(2 - half) * H2],
                                                       bc(tabB[:, :, half * H2:(half + 1) * H2], 2, HG), ALU.mult)
                    last.then_inc(ropeB_ready[l], 1)

                def begin(n):
                    pass

                def slot(age):
                    if age[0]:
                        inverse_norms(*age[0])
                        rotate_partner(*age[0])

                def variance_eps(l, n):
                    pool.wait_ge(f_moments[l], n[1])
                    nc.gpsimd.tensor_tensor(fve[l][:, :], fmv[l][:, :, 1], k["eps"][:, 0:GB], ALU.add).then_inc(f_eps[l], 1)

                def inverse_deviation(l, n):
                    pool.wait_ge(f_eps[l], n[1])
                    nc.gpsimd.tensor_tensor(frs[l][:, :], fve[l][:, :], k["minus_half"][:, 0:GB], ALU.pow).then_inc(f_rs[l], 1)

                def add_out_bias(l, n):
                    pool.wait_ge(f_xT[l], n[1])
                    nc.gpsimd.tensor_tensor(fzb[l], z[:, bass.ds((n[0] * WIDE + l) * GB, GB), :], bc(b2[:, :], 1, GB), ALU.add
                                            ).then_inc(f_zb[l], 1)

                def ffn_slot(F, R):
                    f, fn = F or (0, None)
                    r, rn = R or (0, None)
                    if F:
                        variance_eps(f, fn)
                        inverse_deviation(f, fn)
                        add_out_bias(f, fn)

                with pool.Fori(0, DEPTH) as layer:
                    pool.wait_ge(attn_loaded, layer * (16 * N_ATTN) + 16 * N_ATTN)
                    for l in range(LANES):
                        pool.wait_ge(z_done[l], layer * ITERS + 1)
                    for l in range(WIDE):
                        pool.wait_ge(f_done[l], layer * ROUNDS + 1)
                    nc.gpsimd.tensor_tensor(qks[:, 0, :], qks[:, 0, :], k["eight"][:, :], ALU.mult).then_inc(tabs_half, 1)
                    pool.wait_ge(tabs_half, layer + 1)
                    nc.gpsimd.tensor_tensor(tabA[:, :, :], qks[:, :, :], k["cosS"][:, :, :], ALU.mult).then_inc(tabs_ready, 1)
                    for half in range(2):
                        last = nc.gpsimd.tensor_tensor(tabB[:, :, half * H2:(half + 1) * H2], qks[:, :, (1 - half) * H2:(2 - half) * H2],
                                                       k["sinS"][:, :, half * H2:(half + 1) * H2], ALU.mult)
                    last.then_inc(tabs_ready, 1)
                    pool.wait_ge(tabs_ready, layer * 2 + 2)
                    pool.sem_inc(passed, 1)
                    attention_layer(pool, layer, begin, slot)
                    pool.wait_ge(ffn_loaded, layer * (16 * N_FFN_LOADS) + 16 * N_FFN_LOADS)
                    for l in range(LANES):
                        pool.wait_ge(z_done[l], layer * ITERS + (ITERS + 1))
                    pool.sem_inc(passed, 1)
                    ffn_layer(pool, layer, ffn_slot)


def cross_attention(nc, a, k, ps, kind, w):
    C2 = 4
    scale = float(XD) ** -0.5 * (0.5 if kind == "sampled" else 1.0)
    with ExitStack() as ctx:
        m = Buffers(nc, ctx, w["phase"])
        passed = m.sem("passed")
        stat, mv, ve, rstd = m.lanes("stat", [128, 6]), m.lanes("mv", [128, 2]), m.lanes("ve", [128, 1]), m.lanes("rstd", [128, 1])
        xn, xnT, ctxT = m.lanes("xn", [128, 128]), m.lanes("xnT", [128, 128]), m.lanes("ctxT", [128, S2])
        qT, kT = m.lanes("qT", [128, 128]), m.lanes("kT", [128, S2])
        vx = m.lanes("vx", [S2, XH, XD + 1])
        kbd = m.lanes("kbd", [128, XH, S2])
        probs, pT = m.lanes("probs", [128, HG, S2]), m.lanes("pT", [S2, HG, 128])
        nm, rd = m.lanes("nm", [128, HG]), m.lanes("rd", [128, HG])
        o, oT, yb = m.lanes("o", [128, XH, XD]), m.lanes("oT", [128, 128]), m.lanes("yb", [128, 128])
        (stats, moments, var_eps, rstd_ready, xn_ready, xT_ps, xT_ready, qkv_ps, q_ready, kbd_ready, v_ready, s_ps,
         p_ready, pT_ps, pT_ready, pv_ps, o_ready, oT_ps, oT_ready, y_ps, yb_ready, x_done,
         k_ready) = (
            m.sems(n) for n in ("stats", "moments", "var_eps", "rstd", "xn", "xT_ps", "xT", "qkv_ps", "q", "kbd", "v", "s_ps",
                                "p", "pT_ps", "pT", "pv_ps", "o", "oT_ps", "oT", "y_ps", "yb", "x_done", "k"))
        sampled = kind == "sampled"
        if not sampled:
            max_ready, sub_ready, rd_ready = m.sems("max"), m.sems("sub"), m.sems("rd")
        if sampled:
            HN = XH * NK
            loc, quo, rnd, rem, low, high, ix = (m.lanes(n, [128, HN]) for n in ("loc", "quo", "rnd", "rem", "low", "high", "ix"))
            hats = [m.lanes(f"hat{c}_", [128, C2 * NK, S2]) for c in range(2)]
            hat = lambda l, c: hats[c % 2][l]
            prod = m.lanes("prod", [128, C2 * NK, S2])
            sc, sc2, at = (m.lanes(n, [128, C2, NK]) for n in ("sc", "sc2", "at"))
            smx, ssum, srd = (m.lanes(n, [128, C2]) for n in ("smx", "ssum", "srd"))
            sp_l, rsp_l, sgn_l = (m.lanes(n, [128, 1]) for n in ("sp_l", "rsp_l", "sgn_l"))
            (off_ps, span_ready, chain, dist, bumped, hat_ready, prod_ready, sc_ready, soft, weighted, summed) = (
                m.sems(n) for n in ("off_ps", "span", "chain", "dist", "bumped", "hat", "prod", "sc", "soft", "weighted", "summed"))

        def numbers(eng, i):
            return i, eng.snap(i + 1), (eng.snap(i * 2 + 1), eng.snap(i * 2 + 2))

        def chunk(n, c):
            return n[0] * 4 + (c + 1)

        def small(n, c, j):
            return n[0] * 24 + (6 * c + j + 1)

        def pipeline(eng, slot):
            G = ((0, 1), (2, 3))
            first = numbers(eng, 0)
            slot((G[0], first), None)
            slot((G[1], first), (G[0], first))
            with eng.Fori(1, ITERS) as i:
                n, before = numbers(eng, i), numbers(eng, i - 1)
                slot((G[0], n), (G[1], before))
                slot((G[1], n), (G[0], n))
            slot(None, (G[1], numbers(eng, ITERS - 1)))

        with nc.Block() as block:
            @block.tensor
            def _(pe):
                def x_turn(l, n):
                    pe.wait_ge(x_done[l], n[1])
                    pe.wait_ge(xn_ready[l], n[1])
                    nc.tensor.transpose(ps[:, 2 * l, 0:128], xn[l][:, :], k["ident"][:, :]).then_inc(xT_ps[l], 1)

                def project(l, n):
                    pe.wait_ge(xT_ready[l], n[1])
                    nc.tensor.matmul(ps[:, 2 * l, 0:128], w["Wq"][:, :], xnT[l][:, :], start=True, stop=True)
                    nc.tensor.matmul(ps[:, 2 * l, 128:128 + S2], w["Wk"][:, :], ctxT[l][:, :], start=True, stop=True)
                    nc.tensor.matmul(ps[0:S2, 2 * l + 1, 0:128], ctxT[l][:, :], w["Wv"][:, :], start=True, stop=True
                                     ).then_inc(qkv_ps[l], 1)

                def offsets(l, n):
                    pe.wait_ge(q_ready[l], n[1])
                    pe.wait_ge(k_ready[l], n[1])
                    nc.tensor.matmul(ps[:, 2 * l, 0:XH * NK], qT[l][:, :], k["T_Woff"][:, :], start=True, stop=True
                                     ).then_inc(off_ps[l], 1)

                def scores(l, h, n):
                    if h == 0:
                        pe.wait_ge(q_ready[l], n[1])
                        pe.wait_ge(v_ready[l], n[1])
                        pe.wait_ge(kbd_ready[l], n[1])
                        if sampled:
                            pe.wait_ge(span_ready[l], n[1])
                    else:
                        pe.wait_ge(o_ready[l], n[2][0])
                    for j in range(2):
                        h0 = h * HG + j * C2
                        last = nc.tensor.matmul(ps[:, 2 * l + j, 0:C2 * S2], qT[l][:, :],
                                                kbd[l][:, h0:h0 + C2, :].rearrange("p h s -> p (h s)"), start=True, stop=True)
                    last.then_inc(s_ps[l], 1)

                def sum_samples(l, c, n):
                    pe.wait_ge(weighted[l], chunk(n, c))
                    for j in range(NK):
                        last = nc.tensor.matmul(ps[:, 2 * l + c % 2, 0:C2 * S2], k["ident"][:, :],
                                                prod[l][:, :, :].rearrange("p (h j) s -> p j h s", j=NK)[:, j, :, :],
                                                start=(j == 0), stop=(j == NK - 1))
                    last.then_inc(summed[l], 1)

                def probs_turn(l, c, n):
                    if sampled:
                        pe.wait_ge(p_ready[l], chunk(n, c))
                    else:
                        pe.wait_ge(p_ready[l], n[2][c])
                    for j in range(c % 2 * C2, c % 2 * C2 + C2) if sampled else range(HG):
                        last = nc.tensor.transpose(ps[0:S2, 2 * l + j // C2, (j % C2) * 128:(j % C2 + 1) * 128], probs[l][:, j, :],
                                                   k["ident"][:, :])
                    last.then_inc(pT_ps[l], 1)

                def values_sum(l, h, n):
                    if sampled:
                        pe.wait_ge(pT_ready[l], chunk(n, 2 * h + 1))
                    else:
                        pe.wait_ge(pT_ready[l], n[2][h])
                    for j in range(HG):
                        last = nc.tensor.matmul(ps[:, 2 * l, j * (XD + 1):(j + 1) * (XD + 1)], pT[l][:, j, :],
                                                vx[l][:, h * HG + j, :], start=True, stop=True)
                    last.then_inc(pv_ps[l], 1)

                def out_turn(l, n):
                    pe.wait_ge(o_ready[l], n[2][1])
                    nc.tensor.transpose(ps[:, 2 * l, 0:128], o[l][:, :, :].rearrange("p h d -> p (h d)"), k["ident"][:, :]
                                        ).then_inc(oT_ps[l], 1)

                def out_project(l, n):
                    pe.wait_ge(oT_ready[l], n[1])
                    nc.tensor.matmul(ps[:, 2 * l, 0:128], oT[l][:, :], w["Wo"][:, :], start=True, stop=True).then_inc(y_ps[l], 1)

                def slot(F, R):
                    (f0, f1), fn = F or ((0, 0), None)
                    (r0, r1), rn = R or ((0, 0), None)
                    if sampled:
                        if R:
                            scores(r0, 1, rn)
                            scores(r1, 1, rn)
                        if F:
                            x_turn(f1, fn)
                            x_turn(f0, fn)
                            project(f1, fn)
                            project(f0, fn)
                            offsets(f1, fn)
                            offsets(f0, fn)
                            scores(f1, 0, fn)
                            scores(f0, 0, fn)
                        if R:
                            sum_samples(r0, 2, rn)
                            sum_samples(r1, 2, rn)
                            probs_turn(r1, 2, rn)
                        if F:
                            sum_samples(f0, 0, fn)
                        if R:
                            probs_turn(r0, 2, rn)
                        if F:
                            probs_turn(f0, 0, fn)
                            sum_samples(f1, 0, fn)
                        if R:
                            sum_samples(r0, 3, rn)
                        if F:
                            probs_turn(f1, 0, fn)
                        if R:
                            probs_turn(r0, 3, rn)
                            sum_samples(r1, 3, rn)
                            values_sum(r0, 1, rn)
                        if F:
                            sum_samples(f0, 1, fn)
                        if R:
                            out_turn(r0, rn)
                            probs_turn(r1, 3, rn)
                        if F:
                            sum_samples(f1, 1, fn)
                            probs_turn(f0, 1, fn)
                        if R:
                            values_sum(r1, 1, rn)
                        if F:
                            probs_turn(f1, 1, fn)
                        if R:
                            out_project(r0, rn)
                            out_turn(r1, rn)
                        if F:
                            values_sum(f0, 0, fn)
                        if R:
                            out_project(r1, rn)
                        if F:
                            values_sum(f1, 0, fn)
                    else:
                        if R:
                            scores(r0, 1, rn)
                            scores(r1, 1, rn)
                        if F:
                            x_turn(f0, fn)
                            x_turn(f1, fn)
                        if R:
                            probs_turn(r0, 1, rn)
                        if F:
                            project(f0, fn)
                            project(f1, fn)
                        if R:
                            values_sum(r0, 1, rn)
                            probs_turn(r1, 1, rn)
                        if F:
                            scores(f0, 0, fn)
                        if R:
                            out_turn(r0, rn)
                        if F:
                            scores(f1, 0, fn)
                        if R:
                            values_sum(r1, 1, rn)
                        if F:
                            probs_turn(f0, 0, fn)
                        if R:
                            out_turn(r1, rn)
                        if F:
                            probs_turn(f1, 0, fn)
                        if R:
                            out_project(r0, rn)
                        if F:
                            values_sum(f0, 0, fn)
                        if R:
                            out_project(r1, rn)
                        if F:
                            values_sum(f1, 0, fn)

                pipeline(pe, slot)

            @block.vector
            def _(dve):
                for l in range(LANES):
                    nc.vector.memset(vx[l][:, :, XD:XD + 1], 1.0).then_inc(x_done[l], 1)

                def statistics(l, n):
                    nc.vector.bn_stats(stat[l][:, :], cols(k["x"], n[0] * LANES + l)).then_inc(stats[l], 1)

                def moments_of(l, n):
                    dve.wait_ge(stats[l], n[1])
                    dve.sem_inc(passed, 1)
                    nc.vector.bn_aggr(mv[l][:, :], stat[l][:, :]).then_inc(moments[l], 1)

                def normalise(l, n):
                    dve.wait_ge(rstd_ready[l], n[1])
                    nc.vector.tensor_scalar(xn[l][:, :], cols(k["x"], n[0] * LANES + l), mv[l][:, 0:1], rstd[l][:, 0:1],
                                            ALU.subtract, ALU.mult).then_inc(xn_ready[l], 1)

                def add_biases(l, n):
                    dve.wait_ge(qkv_ps[l], n[1])
                    nc.vector.tensor_scalar(kT[l][:, :], ps[:, 2 * l, 128:128 + S2], w["bk"][:, 0:1], scale, ALU.add, ALU.mult
                                            ).then_inc(k_ready[l], 1)
                    nc.vector.tensor_scalar(qT[l][:, :], ps[:, 2 * l, 0:128], w["bq"][:, 0:1], None, ALU.add).then_inc(q_ready[l], 1)
                    nc.vector.tensor_tensor(vx[l][:, :, 0:XD], ps[0:S2, 2 * l + 1, 0:128].rearrange("p (h d) -> p h d", d=XD),
                                            w["bv"][0:S2, :].rearrange("p (h d) -> p h d", d=XD), ALU.add).then_inc(v_ready[l], 1)

                def locate(l, n):
                    nc.vector.tensor_copy(sp_l[l][:, :], k["span"][:, bass.ds(n[0] * LANES + l, 1)])
                    nc.vector.tensor_copy(rsp_l[l][:, :], k["rspan"][:, bass.ds(n[0] * LANES + l, 1)])
                    nc.vector.tensor_copy(sgn_l[l][:, :], k["sgn"][:, bass.ds(n[0] * LANES + l, 1)])
                    dve.wait_ge(off_ps[l], n[1])
                    nc.vector.tensor_tensor(loc[l][:, :], ps[:, 2 * l, 0:HN], k["boffpos"][:, :], ALU.add).then_inc(span_ready[l], 1)

                def remainders(lanes, n):
                    c = [n[0] * 11 + (j + 1) for j in range(11)]
                    for l in lanes:
                        dve.wait_ge(span_ready[l], n[1])
                        nc.vector.tensor_scalar(loc[l][:, :], loc[l][:, :], k["pos"][:, 0:1], sgn_l[l][:, 0:1], ALU.add, ALU.mult
                                                ).then_inc(chain[l], 1)
                    for l in lanes:
                        dve.wait_ge(chain[l], c[0])
                        nc.vector.tensor_scalar(quo[l][:, :], loc[l][:, :], rsp_l[l][:, 0:1], None, ALU.mult).then_inc(chain[l], 1)
                    for l in lanes:
                        dve.wait_ge(chain[l], c[1])
                        nc.vector.tensor_scalar(rnd[l][:, :], quo[l][:, :], MAGIC, MAGIC, ALU.add, ALU.subtract).then_inc(chain[l], 1)
                    for l in lanes:
                        dve.wait_ge(chain[l], c[2])
                        nc.vector.tensor_scalar(rnd[l][:, :], rnd[l][:, :], sp_l[l][:, 0:1], None, ALU.mult).then_inc(chain[l], 1)
                    for l in lanes:
                        dve.wait_ge(chain[l], c[3])
                        nc.vector.tensor_tensor(rem[l][:, :], loc[l][:, :], rnd[l][:, :], ALU.subtract).then_inc(chain[l], 1)
                    for l in lanes:
                        dve.wait_ge(chain[l], c[4])
                        nc.vector.tensor_scalar(low[l][:, :], rem[l][:, :], 0.0, sp_l[l][:, 0:1], ALU.is_lt, ALU.mult).then_inc(chain[l], 1)
                    for l in lanes:
                        dve.wait_ge(chain[l], c[5])
                        nc.vector.tensor_tensor(rem[l][:, :], rem[l][:, :], low[l][:, :], ALU.add).then_inc(chain[l], 1)
                    for l in lanes:
                        dve.wait_ge(chain[l], c[6])
                        nc.vector.tensor_scalar(low[l][:, :], rem[l][:, :], sp_l[l][:, 0:1], sp_l[l][:, 0:1], ALU.is_ge, ALU.mult
                                                ).then_inc(chain[l], 1)
                    for l in lanes:
                        dve.wait_ge(chain[l], c[7])
                        nc.vector.tensor_tensor(rem[l][:, :], rem[l][:, :], low[l][:, :], ALU.subtract).then_inc(chain[l], 1)
                    for l in lanes:
                        dve.wait_ge(chain[l], c[8])
                        nc.vector.tensor_scalar(high[l][:, :], rem[l][:, :], sgn_l[l][:, 0:1], S2 / (S2 - 1.0), ALU.mult, ALU.mult
                                                ).then_inc(chain[l], 1)
                    for l in lanes:
                        dve.wait_ge(chain[l], c[9])
                        nc.vector.tensor_scalar(ix[l][:, :], high[l][:, :], -0.5, None, ALU.add).then_inc(chain[l], 1)

                if sampled:
                    def less_largest(l, c, n):
                        dve.wait_ge(sc_ready[l], chunk(n, c))
                        nc.vector.tensor_reduce(smx[l][:, :], sc[l][:, :, :], AX.X, ALU.max).then_inc(soft[l], 1)
                        dve.wait_ge(soft[l], small(n, c, 0))
                        nc.vector.tensor_tensor(sc2[l][:, :, :], sc[l][:, :, :], bc(smx[l][:, :], 2, NK), ALU.subtract
                                                ).then_inc(soft[l], 1)

                    def outputs(l, h, n):
                        dve.wait_ge(pv_ps[l], n[2][h])
                        pv = ps[:, 2 * l, 0:HG * (XD + 1)].rearrange("p (h d) -> p h d", d=XD + 1)
                        nc.vector.tensor_scalar(o[l][:, h * HG:(h + 1) * HG, :], pv[:, :, 0:XD], 0.5, None, ALU.mult
                                                ).then_inc(o_ready[l], 1)
                else:
                    def less_largest(l, h, n):
                        dve.wait_ge(max_ready[l], n[2][h])
                        s = ps[:, 2 * l:2 * l + 2, 0:C2 * S2].rearrange("p j (h s) -> p j h s", s=S2)
                        nc.vector.tensor_tensor(probs[l][:, :, :].rearrange("p (j h) s -> p j h s", j=2), s,
                                                bc(nm[l][:, :].rearrange("p (j h) -> p j h", j=2), 3, S2), ALU.subtract
                                                ).then_inc(sub_ready[l], 1)

                    def outputs(l, h, n):
                        dve.wait_ge(rd_ready[l], n[2][h])
                        pv = ps[:, 2 * l, 0:HG * (XD + 1)].rearrange("p (h d) -> p h d", d=XD + 1)
                        nc.vector.tensor_tensor(o[l][:, h * HG:(h + 1) * HG, :], pv[:, :, 0:XD], bc(rd[l][:, :], 2, XD), ALU.mult
                                                ).then_inc(o_ready[l], 1)

                def largest(l, h, n):
                    dve.wait_ge(s_ps[l], n[2][h])
                    s = ps[:, 2 * l:2 * l + 2, 0:C2 * S2].rearrange("p j (h s) -> p j h s", s=S2)
                    nc.vector.tensor_reduce(nm[l][:, :].rearrange("p (j h) -> p j h", j=2), s, AX.X, ALU.max).then_inc(max_ready[l], 1)

                def inverse_sums(l, h, n):
                    dve.wait_ge(pv_ps[l], n[2][h])
                    pv = ps[:, 2 * l, 0:HG * (XD + 1)].rearrange("p (h d) -> p h d", d=XD + 1)
                    nc.vector.reciprocal(rd[l][:, :], pv[:, :, XD]).then_inc(rd_ready[l], 1)

                def distances(l, c, n):
                    if c < 2:
                        dve.wait_ge(chain[l], n[0] * 11 + 11)
                    else:
                        dve.wait_ge(weighted[l], chunk(n, c - 2))
                    h0 = c * C2 * NK
                    nc.vector.tensor_tensor(hat(l, c)[:, :, :], bc(ix[l][:, h0:h0 + C2 * NK], 2, S2),
                                            bc(k["iota"][:, :], 1, C2 * NK), ALU.subtract).then_inc(dist[l], 1)

                def hat_scores(l, c, n):
                    if c % 2 == 0:
                        dve.wait_ge(s_ps[l], n[2][c // 2])
                    if c > 0:
                        dve.wait_ge(summed[l], chunk(n, c - 1))
                    dve.wait_ge(hat_ready[l], chunk(n, c))
                    nc.vector.tensor_tensor(prod[l][:, :, :].rearrange("p (h n) s -> p h n s", n=NK),
                                            hat(l, c)[:, :, :].rearrange("p (h n) s -> p h n s", n=NK),
                                            bc(ps[:, 2 * l + c % 2, 0:C2 * S2].rearrange("p (h s) -> p h s", s=S2), 2, NK),
                                            ALU.mult).then_inc(prod_ready[l], 1)

                def sample_scores(l, c, n):
                    dve.wait_ge(prod_ready[l], chunk(n, c))
                    nc.vector.tensor_reduce(sc[l][:, :, :].rearrange("p h n -> p (h n)"), prod[l][:, :, :], AX.X, ALU.add
                                            ).then_inc(sc_ready[l], 1)

                def sample_weights(l, c, n):
                    dve.wait_ge(soft[l], small(n, c, 2))
                    nc.vector.tensor_reduce(ssum[l][:, :], sc2[l][:, :, :], AX.X, ALU.add).then_inc(soft[l], 1)
                    dve.wait_ge(soft[l], small(n, c, 3))
                    nc.vector.reciprocal(srd[l][:, :], ssum[l][:, :]).then_inc(soft[l], 1)
                    dve.wait_ge(soft[l], small(n, c, 4))
                    nc.vector.tensor_tensor(at[l][:, :, :], sc2[l][:, :, :], bc(srd[l][:, :], 2, NK), ALU.mult).then_inc(soft[l], 1)

                def add_out_bias(l, n):
                    dve.wait_ge(y_ps[l], n[1])
                    nc.vector.tensor_tensor(yb[l][:, :], ps[:, 2 * l, 0:128], w["bo"][:, :], ALU.add).then_inc(yb_ready[l], 1)

                def add_to_stream(l, n):
                    dve.wait_ge(yb_ready[l], n[1])
                    xb = cols(k["x"], n[0] * LANES + l)
                    nc.vector.tensor_tensor(xb, xb, yb[l][:, :], ALU.add).then_inc(x_done[l], 1)

                def slot(F, R):
                    (f0, f1), fn = F or ((0, 0), None)
                    (r0, r1), rn = R or ((0, 0), None)
                    if sampled:
                        if F:
                            statistics(f0, fn)
                            statistics(f1, fn)
                            moments_of(f0, fn)
                            moments_of(f1, fn)
                            normalise(f1, fn)
                            normalise(f0, fn)
                        if R:
                            hat_scores(r0, 2, rn)
                        if F:
                            add_biases(f1, fn)
                            add_biases(f0, fn)
                            locate(f1, fn)
                            locate(f0, fn)
                            remainders((f0, f1), fn)
                        if R:
                            sample_scores(r0, 2, rn)
                            less_largest(r0, 2, rn)
                            hat_scores(r1, 2, rn)
                            sample_weights(r0, 2, rn)
                            sample_scores(r1, 2, rn)
                        if F:
                            hat_scores(f0, 0, fn)
                        if R:
                            less_largest(r1, 2, rn)
                        if F:
                            sample_scores(f0, 0, fn)
                        if R:
                            sample_weights(r1, 2, rn)
                        if F:
                            less_largest(f0, 0, fn)
                            hat_scores(f1, 0, fn)
                            sample_weights(f0, 0, fn)
                            sample_scores(f1, 0, fn)
                        if R:
                            hat_scores(r0, 3, rn)
                        if F:
                            less_largest(f1, 0, fn)
                        if R:
                            sample_scores(r0, 3, rn)
                        if F:
                            sample_weights(f1, 0, fn)
                        if R:
                            less_largest(r0, 3, rn)
                            hat_scores(r1, 3, rn)
                            sample_weights(r0, 3, rn)
                            sample_scores(r1, 3, rn)
                            less_largest(r1, 3, rn)
                        if F:
                            hat_scores(f0, 1, fn)
                        if R:
                            sample_weights(r1, 3, rn)
                        if F:
                            sample_scores(f0, 1, fn)
                            less_largest(f0, 1, fn)
                            hat_scores(f1, 1, fn)
                            sample_weights(f0, 1, fn)
                            sample_scores(f1, 1, fn)
                            less_largest(f1, 1, fn)
                            sample_weights(f1, 1, fn)
                        if R:
                            outputs(r0, 1, rn)
                            outputs(r1, 1, rn)
                            add_out_bias(r0, rn)
                            add_out_bias(r1, rn)
                            add_to_stream(r0, rn)
                        if F:
                            outputs(f0, 0, fn)
                        if R:
                            add_to_stream(r1, rn)
                        if F:
                            outputs(f1, 0, fn)
                    else:
                        if F:
                            statistics(f1, fn)
                            statistics(f0, fn)
                            moments_of(f1, fn)
                        if R:
                            largest(r0, 1, rn)
                        if F:
                            moments_of(f0, fn)
                        if R:
                            less_largest(r0, 1, rn)
                        if F:
                            normalise(f1, fn)
                            normalise(f0, fn)
                        if R:
                            largest(r1, 1, rn)
                        if F:
                            add_biases(f0, fn)
                        if R:
                            less_largest(r1, 1, rn)
                        if F:
                            add_biases(f1, fn)
                        if R:
                            inverse_sums(r0, 1, rn)
                            outputs(r0, 1, rn)
                        if F:
                            largest(f0, 0, fn)
                            less_largest(f0, 0, fn)
                            largest(f1, 0, fn)
                            less_largest(f1, 0, fn)
                        if R:
                            inverse_sums(r1, 1, rn)
                            outputs(r1, 1, rn)
                            add_out_bias(r0, rn)
                        if F:
                            inverse_sums(f0, 0, fn)
                        if R:
                            add_out_bias(r1, rn)
                        if F:
                            outputs(f0, 0, fn)
                        if R:
                            add_to_stream(r0, rn)
                        if F:
                            inverse_sums(f1, 0, fn)
                        if R:
                            add_to_stream(r1, rn)
                        if F:
                            outputs(f1, 0, fn)

                pipeline(dve, slot)

            @block.scalar
            def _(act):
                def xT_copy(l, n):
                    act.wait_ge(xT_ps[l], n[1])
                    nc.scalar.copy(xnT[l][:, :], ps[:, 2 * l, 0:128])
                    nc.scalar.copy(ctxT[l][:, :], cols(k["ctxT"], n[0] * LANES + l)).then_inc(xT_ready[l], 1)

                def absolute(l, c, n):
                    act.wait_ge(dist[l], chunk(n, c))
                    f = hat(l, c)[:, :, :].rearrange("p n s -> p (n s)")
                    nc.scalar.activation(f, f, ACT.Abs).then_inc(bumped[l], 1)

                def hats_of(l, c, n):
                    act.wait_ge(bumped[l], chunk(n, c))
                    f = hat(l, c)[:, :, :].rearrange("p n s -> p (n s)")
                    nc.scalar.activation(f, f, ACT.Relu, bias=1.0, scale=-1.0).then_inc(hat_ready[l], 1)

                def exponent(l, c, n):
                    if sampled:
                        act.wait_ge(soft[l], small(n, c, 1))
                        f = sc2[l][:, :, :].rearrange("p h n -> p (h n)")
                        nc.scalar.activation(f, f, ACT.Exp).then_inc(soft[l], 1)
                    else:
                        act.wait_ge(sub_ready[l], n[2][c])
                        f = probs[l][:, :, :].rearrange("p h s -> p (h s)")
                        nc.scalar.activation(f, f, ACT.Exp).then_inc(p_ready[l], 1)

                def probs_copy(l, c, n):
                    act.wait_ge(summed[l], chunk(n, c))
                    j = c % 2
                    nc.scalar.copy(probs[l][:, j * C2:(j + 1) * C2, :].rearrange("p h s -> p (h s)"), ps[:, 2 * l + j, 0:C2 * S2]
                                   ).then_inc(p_ready[l], 1)

                def pT_copy(l, c, n):
                    if sampled:
                        act.wait_ge(pT_ps[l], chunk(n, c))
                        j = c % 2
                        nc.scalar.copy(pT[l][:, j * C2:(j + 1) * C2, :].rearrange("p h n -> p (h n)"), ps[0:S2, 2 * l + j, :]
                                       ).then_inc(pT_ready[l], 1)
                    else:
                        act.wait_ge(pT_ps[l], n[2][c])
                        nc.scalar.copy(pT[l][:, :, :].rearrange("p h n -> p (h n)"),
                                       ps[0:S2, 2 * l:2 * l + 2, :].rearrange("p a n -> p (a n)")).then_inc(pT_ready[l], 1)

                def oT_copy(l, n):
                    act.wait_ge(oT_ps[l], n[1])
                    nc.scalar.copy(oT[l][:, :], ps[:, 2 * l, 0:128]).then_inc(oT_ready[l], 1)

                def slot(F, R):
                    (f0, f1), fn = F or ((0, 0), None)
                    (r0, r1), rn = R or ((0, 0), None)
                    if sampled:
                        if R:
                            absolute(r0, 2, rn)
                            hats_of(r0, 2, rn)
                        if F:
                            xT_copy(f1, fn)
                            xT_copy(f0, fn)
                        if R:
                            absolute(r1, 2, rn)
                            absolute(r1, 3, rn)
                            hats_of(r1, 2, rn)
                            absolute(r0, 3, rn)
                            exponent(r0, 2, rn)
                        if F:
                            absolute(f0, 0, fn)
                            hats_of(f0, 0, fn)
                            absolute(f1, 0, fn)
                        if R:
                            exponent(r1, 2, rn)
                        if F:
                            hats_of(f1, 0, fn)
                        if R:
                            hats_of(r0, 3, rn)
                        if F:
                            exponent(f0, 0, fn)
                        if R:
                            probs_copy(r0, 2, rn)
                            probs_copy(r1, 2, rn)
                        if F:
                            exponent(f1, 0, fn)
                        if R:
                            hats_of(r1, 3, rn)
                            exponent(r0, 3, rn)
                        if F:
                            absolute(f0, 1, fn)
                            probs_copy(f0, 0, fn)
                            hats_of(f0, 1, fn)
                            absolute(f1, 1, fn)
                        if R:
                            pT_copy(r0, 2, rn)
                            exponent(r1, 3, rn)
                        if F:
                            probs_copy(f1, 0, fn)
                            hats_of(f1, 1, fn)
                            exponent(f0, 1, fn)
                        if R:
                            probs_copy(r0, 3, rn)
                            pT_copy(r0, 3, rn)
                            pT_copy(r1, 2, rn)
                        if F:
                            pT_copy(f0, 0, fn)
                            exponent(f1, 1, fn)
                        if R:
                            probs_copy(r1, 3, rn)
                        if F:
                            probs_copy(f0, 1, fn)
                        if R:
                            pT_copy(r1, 3, rn)
                            oT_copy(r0, rn)
                        if F:
                            pT_copy(f1, 0, fn)
                            probs_copy(f1, 1, fn)
                            pT_copy(f0, 1, fn)
                        if R:
                            oT_copy(r1, rn)
                        if F:
                            pT_copy(f1, 1, fn)
                    else:
                        if R:
                            exponent(r0, 1, rn)
                        if F:
                            xT_copy(f0, fn)
                            xT_copy(f1, fn)
                        if R:
                            pT_copy(r0, 1, rn)
                            exponent(r1, 1, rn)
                            oT_copy(r0, rn)
                            pT_copy(r1, 1, rn)
                        if F:
                            exponent(f0, 0, fn)
                            exponent(f1, 0, fn)
                            pT_copy(f0, 0, fn)
                        if R:
                            oT_copy(r1, rn)
                        if F:
                            pT_copy(f1, 0, fn)

                pipeline(act, slot)

            @block.gpsimd
            def _(pool):
                def variance_eps(l, n):
                    pool.wait_ge(moments[l], n[1])
                    nc.gpsimd.tensor_tensor(ve[l][:, :], mv[l][:, 1:2], k["eps"][:, 0:1], ALU.add).then_inc(var_eps[l], 1)

                def inverse_deviation(l, n):
                    pool.wait_ge(var_eps[l], n[1])
                    nc.gpsimd.tensor_tensor(rstd[l][:, :], ve[l][:, :], k["minus_half"][:, 0:1], ALU.pow).then_inc(rstd_ready[l], 1)

                def spread_keys(l, n):
                    pool.wait_ge(k_ready[l], n[1])
                    nc.gpsimd.tensor_tensor(kbd[l][:, :, :], bc(kT[l][:, :], 1, XH), bc(k["headmask"][:, :], 2, S2), ALU.mult
                                            ).then_inc(kbd_ready[l], 1)

                def distances(l, c, n):
                    if c < 2:
                        pool.wait_ge(chain[l], n[0] * 11 + 11)
                    else:
                        pool.wait_ge(weighted[l], chunk(n, c - 2))
                    h0 = c * C2 * NK
                    nc.gpsimd.tensor_tensor(hat(l, c)[:, :, :], bc(ix[l][:, h0:h0 + C2 * NK], 2, S2),
                                            bc(k["iota"][:, :], 1, C2 * NK), ALU.subtract).then_inc(dist[l], 1)

                def weighted_hats(l, c, n):
                    pool.wait_ge(soft[l], small(n, c, 5))
                    nc.gpsimd.tensor_tensor(prod[l][:, :, :], hat(l, c)[:, :, :],
                                            bc(at[l][:, :, :].rearrange("p h n -> p (h n)"), 2, S2), ALU.mult).then_inc(weighted[l], 1)

                def slot(F, R):
                    (f0, f1), fn = F or ((0, 0), None)
                    (r0, r1), rn = R or ((0, 0), None)
                    if sampled:
                        if R:
                            distances(r0, 2, rn)
                            distances(r1, 2, rn)
                            distances(r0, 3, rn)
                        if F:
                            variance_eps(f1, fn)
                            variance_eps(f0, fn)
                            inverse_deviation(f1, fn)
                            inverse_deviation(f0, fn)
                        if R:
                            distances(r1, 3, rn)
                        if F:
                            spread_keys(f1, fn)
                            spread_keys(f0, fn)
                            distances(f0, 0, fn)
                            distances(f1, 0, fn)
                        if R:
                            weighted_hats(r0, 2, rn)
                        if F:
                            distances(f1, 1, fn)
                        if R:
                            weighted_hats(r1, 2, rn)
                        if F:
                            weighted_hats(f0, 0, fn)
                            distances(f0, 1, fn)
                            weighted_hats(f1, 0, fn)
                        if R:
                            weighted_hats(r0, 3, rn)
                            weighted_hats(r1, 3, rn)
                        if F:
                            weighted_hats(f0, 1, fn)
                            weighted_hats(f1, 1, fn)
                    else:
                        if F:
                            variance_eps(f1, fn)
                            inverse_deviation(f1, fn)
                            variance_eps(f0, fn)
                            inverse_deviation(f0, fn)
                            spread_keys(f0, fn)
                            spread_keys(f1, fn)

                pipeline(pool, slot)


def norm_front(nc, m, k):
    f = {"stat": m.lanes("stat", [128, GB, 6], n=WIDE), "mv": m.lanes("mv", [128, GB, 2], n=WIDE),
         "ve": m.lanes("ve", [128, GB], n=WIDE), "rs": m.lanes("rs", [128, GB], n=WIDE)}
    for n in ("stats", "moments", "eps", "rstd", "xn_ready"):
        f[n] = m.sems(n, WIDE)
    return f


def norm_vector(nc, dve, k, f, xn, i, passed):
    u1, u4 = dve.snap(i + 1), dve.snap(i * GB + GB)
    for l in range(WIDE):
        for b in range(GB):
            nc.vector.bn_stats(f["stat"][l][:, b, :], cols(k["x"], (i * WIDE + l) * GB + b)).then_inc(f["stats"][l], 1)
    for l in range(WIDE):
        dve.wait_ge(f["stats"][l], u4)
        dve.sem_inc(passed, 1)
        for b in range(GB):
            last = nc.vector.bn_aggr(f["mv"][l][:, b, :], f["stat"][l][:, b, :])
        last.then_inc(f["moments"][l], 1)
    for l in range(WIDE):
        dve.wait_ge(f["rstd"][l], u1)
        for b in range(GB):
            last = nc.vector.tensor_scalar(xn[l][:, b, :], cols(k["x"], (i * WIDE + l) * GB + b), f["mv"][l][:, b, 0:1],
                                           f["rs"][l][:, b:b + 1], ALU.subtract, ALU.mult)
        last.then_inc(f["xn_ready"][l], 1)


def norm_pool(nc, pool, k, f, i):
    u1 = pool.snap(i + 1)
    for l in range(WIDE):
        pool.wait_ge(f["moments"][l], u1)
        nc.gpsimd.tensor_tensor(f["ve"][l][:, :], f["mv"][l][:, :, 1], k["eps"][:, 0:GB], ALU.add).then_inc(f["eps"][l], 1)
    for l in range(WIDE):
        pool.wait_ge(f["eps"][l], u1)
        nc.gpsimd.tensor_tensor(f["rs"][l][:, :], f["ve"][l][:, :], k["minus_half"][:, 0:GB], ALU.pow).then_inc(f["rstd"][l], 1)


Q_STEPS = 10


def quantise(nc, dve, src, rscale, t, step, count, passed):
    u, v, lo, hi, big, ok, sq = t
    nc.vector.tensor_scalar(u, src, rscale, None, ALU.mult).then_inc(step, 1)
    dve.wait_ge(step, count(1))
    dve.sem_inc(passed, 1)
    nc.vector.tensor_scalar(lo, u, 240.0, -240.0, ALU.min, ALU.max, saturate=False)
    nc.vector.tensor_scalar(v, u, 0.5, 240.0, ALU.mult, ALU.min).then_inc(step, 1)
    nc.vector.tensor_tensor(sq, u, u, ALU.mult).then_inc(step, 1)
    dve.wait_ge(step, count(3))
    nc.vector.tensor_scalar(big, sq, 240.0 ** 2, None, ALU.is_gt)
    nc.vector.tensor_scalar(ok, sq, 464.0 ** 2, None, ALU.is_le).then_inc(step, 1)
    nc.vector.tensor_scalar(hi, v, -240.0, None, ALU.max, saturate=False).then_inc(step, 1)
    dve.wait_ge(step, count(5))
    dve.sem_inc(passed, 1)
    nc.vector.scalar_tensor_tensor(out=v, in0=hi, scalar=2.0, in1=lo, op0=ALU.mult, op1=ALU.subtract).then_inc(step, 1)
    nc.vector.reciprocal(sq, ok).then_inc(step, 1)
    dve.wait_ge(step, count(7))
    nc.vector.tensor_tensor(v, v, big, ALU.mult).then_inc(step, 1)
    nc.vector.tensor_tensor(ok, ok, sq, ALU.mult).then_inc(step, 1)
    dve.wait_ge(step, count(9))
    dve.sem_inc(passed, 1)
    nc.vector.tensor_tensor(u, v, lo, ALU.add).then_inc(step, 1)
    dve.wait_ge(step, count(10))


def quantised_dense(nc, a, k, ps):
    with ExitStack() as ctx:
        m = Buffers(nc, ctx, "p4")
        passed = m.sem("passed")
        f = norm_front(nc, m, k)
        xn = m.lanes("xn", [128, GB, D], BF16, n=WIDE)
        tmp = [(m.sb(f"u{l}", [128, 512]), m.sb(f"v{l}", [128, 512]), m.sb(f"lo{l}", [128, 512], FP8), m.sb(f"hi{l}", [128, 512], FP8),
                m.sb(f"big{l}", [128, 512]), m.sb(f"ok{l}", [128, 512]), m.sb(f"sq{l}", [128, 512])) for l in range(WIDE)]
        xq = m.lanes("xq", [128, 512], BF16, n=WIDE)
        xqT = m.lanes("xqT", [128, 512], BF16, n=WIDE)
        kq = m.sb("kq", [128, 128], BF16)
        rin, rk = m.sb("rin", [128, 1]), m.sb("rk", [128, 1])
        y, y2 = m.lanes("y", [128, 512], BF16, n=WIDE), m.lanes("y2", [128, 512], BF16, n=WIDE)
        kstep, k_ready = m.sem("kstep"), m.sem("k_ready")
        step, q_ready, qT_ps, qT_ready, y_ps, y_ready, yb_ready, x_done = (
            m.sems(n, WIDE) for n in ("step", "q", "qT_ps", "qT", "y_ps", "y", "yb", "x_done"))
        turned = [ps[:, 4 * l, 0:256].bitcast(BF16) for l in range(WIDE)]

        with nc.Block() as block:
            @block.vector
            def _(dve):
                for l in range(WIDE):
                    dve.sem_inc(x_done[l], 1)
                nc.vector.reciprocal(rin[:, :], k["r_sin"][:, :])
                nc.vector.reciprocal(rk[:, :], k["r_sk"][:, :]).then_inc(k_ready, 1)
                dve.wait_ge(k_ready, 1)
                quantise(nc, dve, k["fkernel"][:, :], rk[:, 0:1], [t[:, 0:128] for t in tmp[0]], kstep, lambda n: n, passed)
                nc.vector.tensor_tensor(kq[:, :], tmp[0][0][:, 0:128], tmp[0][5][:, 0:128], ALU.mult).then_inc(k_ready, 1)
                dve.wait_ge(k_ready, 2)
                with dve.Fori(0, ROUNDS) as i:
                    u1 = dve.snap(i + 1)
                    norm_vector(nc, dve, k, f, xn, i, passed)
                    for l in range(WIDE):
                        dve.wait_ge(f["xn_ready"][l], u1)
                        quantise(nc, dve, xn[l][:, :, :].rearrange("p b d -> p (b d)"), rin[:, 0:1], [t[:, :] for t in tmp[l]],
                                 step[l], lambda n: i * Q_STEPS + n, passed)
                        nc.vector.tensor_tensor(xq[l][:, :], tmp[l][0][:, :], tmp[l][5][:, :], ALU.mult).then_inc(q_ready[l], 1)
                    for l in range(WIDE):
                        dve.wait_ge(y_ps[l], u1)
                        nc.vector.tensor_scalar(y[l][:, :], ps[:, 4 * l + 1, :], k["sscale"][:, 0:1], None, ALU.mult).then_inc(y_ready[l], 1)
                    for l in range(WIDE):
                        dve.wait_ge(y_ready[l], u1)
                        nc.vector.tensor_tensor(y2[l][:, :].rearrange("p (b d) -> p b d", b=GB),
                                                y[l][:, :].rearrange("p (b d) -> p b d", b=GB), bc(k["r_fbias"][:, :], 1, GB), ALU.add
                                                ).then_inc(yb_ready[l], 1)
                    for l in range(WIDE):
                        dve.wait_ge(yb_ready[l], u1)
                        xb = cols(k["x"], (i * WIDE + l) * GB, GB)
                        nc.vector.tensor_tensor(xb, xb, y2[l][:, :], ALU.add).then_inc(x_done[l], 1)

            @block.gpsimd
            def _(pool):
                with pool.Fori(0, ROUNDS) as i:
                    norm_pool(nc, pool, k, f, i)

            @block.tensor
            def _(pe):
                pe.wait_ge(k_ready, 2)
                pe.sem_inc(passed, 1)
                with pe.Fori(0, ROUNDS) as i:
                    u1 = pe.snap(i + 1)
                    for l in range(WIDE):
                        pe.wait_ge(x_done[l], u1)
                        pe.wait_ge(q_ready[l], u1)
                        for b in range(GB):
                            last = nc.tensor.transpose(turned[l][:, b * 128:(b + 1) * 128], xq[l][:, b * 128:(b + 1) * 128], k["identb"][:, :])
                        last.then_inc(qT_ps[l], 1)
                    for l in range(WIDE):
                        pe.wait_ge(qT_ready[l], u1)
                        for b in range(GB):
                            last = nc.tensor.matmul(ps[:, 4 * l + 1, b * 128:(b + 1) * 128], xqT[l][:, b * 128:(b + 1) * 128], kq[:, :],
                                                    start=True, stop=True)
                        last.then_inc(y_ps[l], 1)

            @block.scalar
            def _(act):
                with act.Fori(0, ROUNDS) as i:
                    u1 = act.snap(i + 1)
                    for l in range(WIDE):
                        act.wait_ge(qT_ps[l], u1)
                        nc.scalar.copy(xqT[l][:, :], turned[l]).then_inc(qT_ready[l], 1)


def mixture_top1(nc, a, k, ps):
    NC = DFF // 128
    with ExitStack() as ctx:
        m = Buffers(nc, ctx, "p6")
        passed = m.sem("passed")
        f = norm_front(nc, m, k)
        xn, xT = m.lanes("xn", [128, GB, D], n=WIDE), m.lanes("xT", [128, 512], n=WIDE)
        lg, top, hit, before = (m.lanes(n, s, n=WIDE) for n, s in (("lg", [128, GB, E]), ("top", [128, GB]), ("hit", [128, GB, E]),
                                                                   ("before", [128, GB, E])))
        prior = m.lanes("prior", [128, GB, E, E], n=WIDE)
        sel, selT = m.lanes("sel", [128, GB, 32], n=WIDE), m.lanes("selT", [128, 128], n=WIDE)
        acc, pick = m.lanes("acc", [128, GB, D], n=WIDE), m.lanes("pick", [128, GB, D], n=WIDE)
        hT = [[m.sb(f"hT{l}_{c}", [128, 512]) for c in range(NC)] for l in range(WIDE)]
        (xT_ps, xT_ready, lg_ps, route, sel_ready, selT_ps, selT_ready, b_ps, acc_ready, h_ps, gelu_ready, y_ps, picked, x_done) = (
            m.sems(n, WIDE) for n in ("xT_ps", "xT", "lg_ps", "route", "sel", "selT_ps", "selT", "b_ps", "acc", "h_ps", "gelu",
                                      "y_ps", "picked", "x_done"))

        with nc.Block() as block:
            @block.vector
            def _(dve):
                for l in range(WIDE):
                    nc.vector.memset(sel[l][:, :, :], 0.0).then_inc(x_done[l], 1)
                    dve.sem_inc(picked[l], 2)
                    dve.wait_ge(x_done[l], 1)
                with dve.Fori(0, ROUNDS) as i:
                    u1 = dve.snap(i + 1)
                    norm_vector(nc, dve, k, f, xn, i, passed)
                    r = [dve.snap(i * 5 + j + 1) for j in range(5)]
                    for l in range(WIDE):
                        dve.wait_ge(lg_ps[l], u1)
                        nc.vector.tensor_tensor(lg[l][:, :, :], ps[:, 4 * l + 1, 0:GB * E].rearrange("p (b e) -> p b e", b=GB),
                                                bc(k["r_gateb"][:, :], 1, GB), ALU.add).then_inc(route[l], 1)
                    for l in range(WIDE):
                        dve.wait_ge(route[l], r[0])
                        nc.vector.tensor_reduce(top[l][:, :], lg[l][:, :, :], AX.X, ALU.max).then_inc(route[l], 1)
                    for l in range(WIDE):
                        dve.wait_ge(route[l], r[1])
                        nc.vector.tensor_tensor(hit[l][:, :, :], lg[l][:, :, :], bc(top[l][:, :], 2, E), ALU.is_equal).then_inc(route[l], 1)
                    for l in range(WIDE):
                        dve.wait_ge(route[l], r[2])
                        nc.vector.tensor_tensor(prior[l][:, :, :, :], bc(hit[l][:, :, :], 2, E), bc(k["lower"][:, :, :], 1, GB), ALU.mult
                                                ).then_inc(route[l], 1)
                    for l in range(WIDE):
                        dve.wait_ge(route[l], r[3])
                        nc.vector.tensor_reduce(before[l][:, :, :], prior[l][:, :, :, :], AX.X, ALU.add).then_inc(route[l], 1)
                    for l in range(WIDE):
                        dve.wait_ge(route[l], r[4])
                        nc.vector.scalar_tensor_tensor(out=sel[l][:, :, 0:E], in0=before[l][:, :, :], scalar=0.5, in1=hit[l][:, :, :],
                                                       op0=ALU.is_lt, op1=ALU.mult).then_inc(sel_ready[l], 1)
                    for l in range(WIDE):
                        dve.wait_ge(b_ps[l], u1)
                        dve.wait_ge(sel_ready[l], u1)
                        nc.vector.tensor_tensor(acc[l][:, :, :].rearrange("p b d -> p (b d)"), ps[:, 4 * l + 2, :],
                                                cols(k["x"], (i * WIDE + l) * GB, GB), ALU.add).then_inc(acc_ready[l], 1)
                    for e in range(E):
                        w = dve.snap(i * E + (e + 1))
                        w3 = dve.snap(i * E + (e + 3))
                        for l in range(WIDE):
                            dve.wait_ge(acc_ready[l], w)
                            dve.wait_ge(y_ps[l], w)
                            nc.vector.tensor_tensor(pick[l][:, :, :], ps[:, 4 * l + 2 + e % 2, :].rearrange("p (b d) -> p b d", b=GB),
                                                    bc(sel[l][:, :, e], 2, D), ALU.mult).then_inc(picked[l], 1)
                        for l in range(WIDE):
                            dve.wait_ge(picked[l], w3)
                            if e < E - 1:
                                nc.vector.tensor_tensor(acc[l][:, :, :], acc[l][:, :, :], pick[l][:, :, :], ALU.add).then_inc(acc_ready[l], 1)
                            else:
                                nc.vector.tensor_tensor(cols(k["x"], (i * WIDE + l) * GB, GB), acc[l][:, :, :].rearrange("p b d -> p (b d)"),
                                                        pick[l][:, :, :].rearrange("p b d -> p (b d)"), ALU.add).then_inc(x_done[l], 1)

            @block.gpsimd
            def _(pool):
                with pool.Fori(0, ROUNDS) as i:
                    norm_pool(nc, pool, k, f, i)

            @block.tensor
            def _(pe):
                pe.wait_ge(k["moe_loaded"], 32)
                pe.sem_inc(passed, 1)
                with pe.Fori(0, ROUNDS) as i:
                    u1 = pe.snap(i + 1)
                    for l in range(WIDE):
                        pe.wait_ge(x_done[l], u1)
                        pe.wait_ge(f["xn_ready"][l], u1)
                        for b in range(GB):
                            last = nc.tensor.transpose(ps[:, 4 * l, b * 128:(b + 1) * 128], xn[l][:, b, :], k["ident"][:, :])
                        last.then_inc(xT_ps[l], 1)
                    for l in range(WIDE):
                        pe.wait_ge(xT_ready[l], u1)
                        for b in range(GB):
                            last = nc.tensor.matmul(ps[:, 4 * l + 1, b * E:(b + 1) * E], xT[l][:, b * 128:(b + 1) * 128], k["gateW"][:, :],
                                                    start=True, stop=True)
                        last.then_inc(lg_ps[l], 1)
                    for l in range(WIDE):
                        pe.wait_ge(sel_ready[l], u1)
                        nc.tensor.transpose(ps[:, 4 * l + 1, 0:128], sel[l][:, :, :].rearrange("p b e -> p (b e)"), k["ident"][:, :]
                                            ).then_inc(selT_ps[l], 1)
                    for l in range(WIDE):
                        pe.wait_ge(selT_ready[l], u1)
                        nc.tensor.matmul(ps[:, 4 * l + 2, :], selT[l][:, :], k["b2blk"][:, :, :].rearrange("p b d -> p (b d)"),
                                         start=True, stop=True).then_inc(b_ps[l], 1)

                    def outputs(e):
                        g4 = pe.snap(i * (E * NC) + (e * NC + NC))
                        w = pe.snap(i * E + (e + 1))
                        for l in range(WIDE):
                            pe.wait_ge(gelu_ready[l], g4)
                            pe.wait_ge(picked[l], w)
                            if e == 0:
                                pe.wait_ge(acc_ready[l], w)
                            for b in range(GB):
                                for c in range(NC):
                                    last = nc.tensor.matmul(ps[:, 4 * l + 2 + e % 2, b * 128:(b + 1) * 128],
                                                            hT[l][c][:, b * 128:(b + 1) * 128], k["moe_w2"][:, e, c, :],
                                                            start=(c == 0), stop=(c == NC - 1))
                            last.then_inc(y_ps[l], 1)

                    for e in range(E):
                        for c in range(NC):
                            for l in range(WIDE):
                                if e * NC + c >= 2:
                                    pe.wait_ge(gelu_ready[l], i * (E * NC) + (e * NC + c - 1))
                                elif c == 1:
                                    pe.wait_ge(selT_ready[l], u1)
                                nc.tensor.matmul(ps[:, 4 * l + c % 2, :], k["moe_w1"][:, e, c * 128:(c + 1) * 128], xT[l][:, :],
                                                 start=True, stop=True).then_inc(h_ps[l], 1)
                        outputs(e)

            @block.scalar
            def _(act):
                with act.Fori(0, ROUNDS) as i:
                    u1 = act.snap(i + 1)
                    for l in range(WIDE):
                        act.wait_ge(xT_ps[l], u1)
                        nc.scalar.copy(xT[l][:, :], ps[:, 4 * l, :]).then_inc(xT_ready[l], 1)
                    for l in range(WIDE):
                        act.wait_ge(selT_ps[l], u1)
                        nc.scalar.copy(selT[l][:, :], ps[:, 4 * l + 1, 0:128]).then_inc(selT_ready[l], 1)
                    for e in range(E):
                        for c in range(NC):
                            for l in range(WIDE):
                                if e and c == 0:
                                    act.wait_ge(y_ps[l], i * E + e)
                                act.wait_ge(h_ps[l], i * (E * NC) + (e * NC + c + 1))
                                nc.scalar.activation(hT[l][c][:, :], ps[:, 4 * l + c % 2, :], ACT.Gelu,
                                                     bias=k["T_b1"][:, e * NC + c:e * NC + c + 1]).then_inc(gelu_ready[l], 1)


def adapters_top2(nc, a, k, ps):
    NC = E * BN // 128
    with ExitStack() as ctx:
        m = Buffers(nc, ctx, "p8")
        passed = m.sem("passed")
        f = norm_front(nc, m, k)
        L = lambda n, s: m.lanes(n, s, n=WIDE)
        xn, xT, pooled, gp = L("xn", [128, GB, D]), L("xT", [128, GB, 128]), L("pooled", [128, GB]), L("gp", [128, GB, E])
        lg, lg2, top, gate, tot, rtot = L("lg", [128, GB, E]), L("lg2", [128, GB, E]), L("top", [128, GB]), L("gate", [128, GB, E]), L("tot", [128, GB]), L("rtot", [128, GB])
        above, same, rank, kept = L("above", [128, GB, E, E]), L("same", [128, GB, E, E]), L("rank", [128, GB, E]), L("kept", [128, GB, E])
        tw, twT, twcol = L("tw", [128, GB, E]), L("twT", [GB * E, 128]), L("twcol", [128, NC, GB])
        h = [[m.sb(f"h{l}_{c}", [128, 512]) for c in range(NC)] for l in range(WIDE)]
        hs = [[m.sb(f"hs{l}_{c}", [128, 512]) for c in range(NC)] for l in range(WIDE)]
        xT_ps, xT_ready, gp_ready, lg_ps, route, exp_ready, tw_ready, twT_ps, twT_ready, h_ps, h_ready, hs_ready, y_ps, x_done = (
            m.sems(n, WIDE) for n in ("xT_ps", "xT", "gp", "lg_ps", "route", "exp", "tw", "twT_ps", "twT", "h_ps", "h", "hs", "y_ps",
                                      "x_done"))
        N_ROUTE = 16

        with nc.Block() as block:
            @block.vector
            def _(dve):
                for l in range(WIDE):
                    dve.sem_inc(x_done[l], 1)
                with dve.Fori(0, ROUNDS) as i:
                    u1 = dve.snap(i + 1)
                    norm_vector(nc, dve, k, f, xn, i, passed)
                    r = [dve.snap(i * N_ROUTE + j) if j else None for j in range(N_ROUTE + 1)]

                    def each(after, emit):
                        for l in range(WIDE):
                            dve.wait_ge(route[l], r[after])
                            emit(l).then_inc(route[l], 1)

                    for l in range(WIDE):
                        dve.wait_ge(xT_ready[l], u1)
                        nc.vector.tensor_reduce(pooled[l][:, :], xT[l][:, :, :], AX.X, ALU.add).then_inc(route[l], 1)
                    for l in range(WIDE):
                        dve.wait_ge(route[l], r[1])
                        nc.vector.tensor_tensor(gp[l][:, :, :], bc(k["T_gate"][:, :], 1, GB), bc(pooled[l][:, :], 2, E), ALU.mult
                                                ).then_inc(gp_ready[l], 1)
                    for l in range(WIDE):
                        dve.wait_ge(lg_ps[l], u1)
                        nc.vector.tensor_scalar(lg[l][:, :, :].rearrange("p b e -> p (b e)"), ps[:, 4 * l + 1, 0:GB * E], 1.0 / S, None,
                                                ALU.mult).then_inc(route[l], 1)
                    each(2, lambda l: nc.vector.tensor_reduce(top[l][:, :], lg[l][:, :, :], AX.X, ALU.max))
                    each(3, lambda l: nc.vector.tensor_tensor(lg2[l][:, :, :], lg[l][:, :, :], bc(top[l][:, :], 2, E), ALU.subtract))
                    for l in range(WIDE):
                        dve.wait_ge(exp_ready[l], u1)
                        nc.vector.tensor_reduce(tot[l][:, :], lg2[l][:, :, :], AX.X, ALU.add).then_inc(route[l], 1)
                    each(5, lambda l: nc.vector.reciprocal(rtot[l][:, :], tot[l][:, :]))
                    each(6, lambda l: nc.vector.tensor_tensor(gate[l][:, :, :], lg2[l][:, :, :], bc(rtot[l][:, :], 2, E), ALU.mult))
                    each(7, lambda l: nc.vector.tensor_tensor(above[l][:, :, :, :], bc(gate[l][:, :, :], 2, E), bc(gate[l][:, :, :], 3, E), ALU.is_gt))
                    each(7, lambda l: nc.vector.tensor_tensor(same[l][:, :, :, :], bc(gate[l][:, :, :], 2, E), bc(gate[l][:, :, :], 3, E), ALU.is_equal))
                    each(9, lambda l: nc.vector.tensor_tensor(same[l][:, :, :, :], same[l][:, :, :, :], bc(k["lower"][:, :, :], 1, GB), ALU.mult))
                    each(10, lambda l: nc.vector.tensor_tensor(above[l][:, :, :, :], above[l][:, :, :, :], same[l][:, :, :, :], ALU.add))
                    each(11, lambda l: nc.vector.tensor_reduce(rank[l][:, :, :], above[l][:, :, :, :], AX.X, ALU.add))
                    each(12, lambda l: nc.vector.scalar_tensor_tensor(out=kept[l][:, :, :], in0=rank[l][:, :, :], scalar=1.5,
                                                                      in1=gate[l][:, :, :], op0=ALU.is_lt, op1=ALU.mult))
                    each(13, lambda l: nc.vector.tensor_reduce(tot[l][:, :], kept[l][:, :, :], AX.X, ALU.add))
                    each(14, lambda l: nc.vector.tensor_scalar(tot[l][:, :], tot[l][:, :], 1e-8, None, ALU.add))
                    each(15, lambda l: nc.vector.reciprocal(rtot[l][:, :], tot[l][:, :]))
                    for l in range(WIDE):
                        dve.wait_ge(route[l], r[16])
                        nc.vector.tensor_tensor(tw[l][:, :, :], kept[l][:, :, :], bc(rtot[l][:, :], 2, E), ALU.mult).then_inc(tw_ready[l], 1)
                    for l in range(WIDE):
                        dve.wait_ge(tw_ready[l], i * 2 + 1)
                        for half in range(2):
                            v = tw[l][64 * half:64 * half + 64, :, :].rearrange("p b (c e) -> p c b e", e=2)[:, :, :, half]
                            last = nc.vector.tensor_copy(twcol[l][64 * half:64 * half + 64, :, :], v)
                        last.then_inc(tw_ready[l], 1)
                    for c in range(NC):
                        for l in range(WIDE):
                            if c == 0:
                                dve.wait_ge(tw_ready[l], i * 2 + 2)
                            dve.wait_ge(h_ready[l], i * NC + (c + 1))
                            nc.vector.tensor_tensor(hs[l][c][:, :].rearrange("p (b s) -> p b s", b=GB), h[l][c][:, :].rearrange("p (b s) -> p b s", b=GB),
                                                    bc(twcol[l][:, c, :], 2, 128), ALU.mult).then_inc(hs_ready[l], 1)
                    for l in range(WIDE):
                        dve.wait_ge(y_ps[l], u1)
                        xb = cols(k["x"], (i * WIDE + l) * GB, GB)
                        nc.vector.tensor_tensor(xb, xb, ps[:, 4 * l + 2, :], ALU.add).then_inc(x_done[l], 1)

            @block.gpsimd
            def _(pool):
                with pool.Fori(0, ROUNDS) as i:
                    norm_pool(nc, pool, k, f, i)

            @block.tensor
            def _(pe):
                with pe.Fori(0, ROUNDS) as i:
                    u1 = pe.snap(i + 1)
                    for l in range(WIDE):
                        pe.wait_ge(x_done[l], u1)
                        pe.wait_ge(f["xn_ready"][l], u1)
                        for b in range(GB):
                            last = nc.tensor.transpose(ps[:, 4 * l, b * 128:(b + 1) * 128], xn[l][:, b, :], k["ident"][:, :])
                        last.then_inc(xT_ps[l], 1)
                    for c in range(NC):
                        for l in range(WIDE):
                            pe.wait_ge(xT_ready[l], u1)
                            if c >= 2:
                                pe.wait_ge(h_ready[l], i * NC + (c - 1))
                            nc.tensor.matmul(ps[:, 4 * l + 3 * (c % 2), :], k["T_down"][:, c, :], xT[l][:, :, :].rearrange("p b s -> p (b s)"),
                                             start=True, stop=True).then_inc(h_ps[l], 1)
                    for l in range(WIDE):
                        pe.wait_ge(gp_ready[l], u1)
                        nc.tensor.matmul(ps[:, 4 * l + 1, 0:GB * E], k["ones"][:, :], gp[l][:, :, :].rearrange("p b e -> p (b e)"),
                                         start=True, stop=True).then_inc(lg_ps[l], 1)
                    for l in range(WIDE):
                        pe.wait_ge(tw_ready[l], i * 2 + 1)
                        nc.tensor.transpose(ps[0:GB * E, 4 * l + 1, 0:128], tw[l][:, :, :].rearrange("p b e -> p (b e)"), k["ident"][:, :]
                                            ).then_inc(twT_ps[l], 1)
                    for l in range(WIDE):
                        pe.wait_ge(twT_ready[l], u1)
                        pe.wait_ge(hs_ready[l], i * NC + NC)
                        nc.tensor.matmul(ps[:, 4 * l + 2, :], twT[l][:, :], k["up_b"][:, :, :].rearrange("p b d -> p (b d)"), start=True, stop=False)
                        for b in range(GB):
                            for c in range(NC):
                                last = nc.tensor.matmul(ps[:, 4 * l + 2, b * 128:(b + 1) * 128], hs[l][c][:, b * 128:(b + 1) * 128],
                                                        k["T_up"][:, c, :], start=False, stop=(b == GB - 1 and c == NC - 1))
                        last.then_inc(y_ps[l], 1)

            @block.scalar
            def _(act):
                with act.Fori(0, ROUNDS) as i:
                    u1 = act.snap(i + 1)
                    for l in range(WIDE):
                        act.wait_ge(xT_ps[l], u1)
                        nc.scalar.copy(xT[l][:, :, :].rearrange("p b s -> p (b s)"), ps[:, 4 * l, :]).then_inc(xT_ready[l], 1)
                    for c in range(NC):
                        for l in range(WIDE):
                            act.wait_ge(h_ps[l], i * NC + (c + 1))
                            nc.scalar.activation(h[l][c][:, :], ps[:, 4 * l + 3 * (c % 2), :], ACT.Gelu, bias=k["c_down_b"][:, c:c + 1]
                                                 ).then_inc(h_ready[l], 1)
                    for l in range(WIDE):
                        act.wait_ge(route[l], i * N_ROUTE + 4)
                        v = lg2[l][:, :, :].rearrange("p b e -> p (b e)")
                        nc.scalar.activation(v, v, ACT.Exp).then_inc(exp_ready[l], 1)
                    for l in range(WIDE):
                        act.wait_ge(twT_ps[l], u1)
                        nc.scalar.copy(twT[l][:, :], ps[0:GB * E, 4 * l + 1, 0:128]).then_inc(twT_ready[l], 1)



def build(nc, a, out):
    with ExitStack() as ctx:
        m = Buffers(nc, ctx, "k")
        k = {}
        for n, shape in (("x", [128, B, D]), ("ctxT", [128, B, S2]), ("negm", [128, B, S2]), ("ident", [128, 128]),
                         ("shift", [128, 128]), ("headmask", [128, XH]), ("ones", [128, 128]), ("minus_half", [128, 16]), ("eps", [128, 16]), ("huge", [128, 16]), ("eight", [128, DH]),
                         ("wpad", [128, 63]), ("up_b", [GB * E, GB, D]), ("b2blk", [128, GB, D]), ("T_b1", [128, E * DFF // 128]), ("gateW", [128, E]), ("lower", [128, E, E]),
                         ("iota", [128, S2]), ("pos", [128, 1]), ("Wcw", [128, 128]), ("Wcb", [128, 128]),
                         ("boffpos", [128, XH * NK]), ("span", [128, B]), ("rspan", [128, B]), ("sgn", [128, B]),
                         ("sscale", [128, 1]), ("T_Woff", [128, XH * NK]), ("T_gate", [128, E]), ("T_down", [128, 4, 128]),
                         ("T_up", [128, 4, 128]), ("T_Wk", [128, 128]), ("T_Wv", [128, 128]), ("T_Wq", [128, 128]),
                         ("T_Wo", [128, 128]), ("L0_W", [128, 128]), ("L0_Ws", [128, 128]), ("L1_Wq", [128, 128]),
                         ("L1_Wk", [128, 128]), ("L1_Wv", [128, 128]), ("L1_We", [128, 128]), ("L2_Wq", [128, 128]),
                         ("L2_Wk", [128, 128]), ("L2_Wv", [128, 128]), ("L2_Wo", [128, 128]),
                         ("c_L1_bq", [128, 1]), ("c_L1_bk", [128, 1]), ("c_L2_bq", [128, 1]), ("c_L2_bk", [128, 1]),
                         ("c_L3_bq", [128, 1]), ("c_L3_bk", [128, 1]), ("c_L0_b", [128, 1]), ("c_down_b", [128, 4]),
                         ("r_L1_bv", [128, D]), ("r_L1_bo", [128, D]), ("r_L2_bv", [128, D]), ("r_L2_bo", [128, D]),
                         ("r_L3_bv", [128, D]), ("r_L3_bo", [128, D]), ("r_L3_boff", [128, XH * NK]), ("r_bcw", [128, 1]),
                         ("r_bcb", [128, 1]), ("r_gateb", [128, E]), ("r_sin", [128, 1]), ("r_sk", [128, 1]),
                         ("cosS", [128, 2, DH]), ("sinS", [128, 2, DH])):
            k[n] = m.sb(n, shape)
        k["identb"] = m.sb("identb", [128, 128], BF16)
        k["band"] = m.sb("band", [128, 4, 128], BF16)
        k["fkernel"] = m.sb("fkernel", [128, 128], BF16)
        k["r_fbias"] = m.sb("r_fbias", [128, 128], BF16)
        ps = ctx.enter_context(nc.psum_tensor("ps", [128, 8, 512], F32))
        setup_phase(nc, a, k, ps)
        if 1 in PHASES:
            additive_attention(nc, a, k, ps)
        if 2 in PHASES:
            with ExitStack() as p2:
                k["z"] = p2.enter_context(nc.sbuf_tensor("k_z", [128, B, D], F32))
                normalise_all(nc, k, ps)
                local_transformer(nc, a, k, ps)
        if 3 in PHASES:
            cross_attention(nc, a, k, ps, "dense", {"phase": "p3", "Wq": k["L1_Wq"], "Wk": k["L1_Wk"], "Wv": k["L1_Wv"], "Wo": k["L1_We"],
                                                    "bq": k["c_L1_bq"], "bk": k["c_L1_bk"], "bv": k["r_L1_bv"], "bo": k["r_L1_bo"]})
        with ExitStack() as moe:
            k["moe_w1"] = moe.enter_context(nc.sbuf_tensor("k_moe_w1", [128, E, DFF], F32))
            k["moe_w2"] = moe.enter_context(nc.sbuf_tensor("k_moe_w2", [128, E, DFF // 128, D], F32))
            k["moe_loaded"] = m.sem("moe_loaded")
            if 6 in PHASES:
                with nc.Block() as block:
                    @block.sync
                    def _(sp):
                        sp.dma_start(k["moe_w1"][:, :, :], a["L2_ffn_W1"].rearrange("e d n -> d e n")).then_inc(k["moe_loaded"], 16)
                        sp.dma_start(k["moe_w2"][:, :, :, :].rearrange("p e c n -> p (e c) n"),
                                     a["L2_ffn_W2"].rearrange("e (c p) n -> p (e c) n", p=128)).then_inc(k["moe_loaded"], 16)
            if 4 in PHASES:
                quantised_dense(nc, a, k, ps)
            if 5 in PHASES:
                cross_attention(nc, a, k, ps, "dense", {"phase": "p5", "Wq": k["L2_Wq"], "Wk": k["L2_Wk"], "Wv": k["L2_Wv"],
                                                        "Wo": k["L2_Wo"], "bq": k["c_L2_bq"], "bk": k["c_L2_bk"],
                                                        "bv": k["r_L2_bv"], "bo": k["r_L2_bo"]})
            if 6 in PHASES:
                mixture_top1(nc, a, k, ps)
        if 7 in PHASES:
            cross_attention(nc, a, k, ps, "sampled", {"phase": "p7", "Wq": k["T_Wq"], "Wk": k["T_Wk"], "Wv": k["T_Wv"], "Wo": k["T_Wo"],
                                                      "bq": k["c_L3_bq"], "bk": k["c_L3_bk"], "bv": k["r_L3_bv"], "bo": k["r_L3_bo"]})
        if 8 in PHASES:
            adapters_top2(nc, a, k, ps)
        stored = m.sem("stored")
        with nc.Block() as block:
            @block.sync
            def _(sp):
                sp.dma_start(out.rearrange("b s d -> s b d"), k["x"][:, :, :]).then_inc(stored, 16)
                sp.wait_ge(stored, 16)


def rope_tables(np):
    half = np.arange(0, DH, 2, dtype=np.float32)
    inv_freq = (np.float32(1.0) / np.float32(10000.0) ** (half / np.float32(DH))).astype(np.float32)
    t = np.arange(S, dtype=np.float32)
    freqs = (t[:, None] * inv_freq[None, :]).astype(np.float32)
    base = ((half + np.float32(0.4 * DH)) / np.float32(1.4 * DH)).astype(np.float32)
    scale = base[None, :] ** ((t - S // 2) / np.float32(WINDOW // 2))[:, None]
    cos, sin = np.cos(freqs), np.sin(freqs)
    c = np.stack([np.concatenate([cos * f, cos * f], -1) for f in (scale, 1.0 / scale)], 1)
    s = np.stack([np.concatenate([-sin * f, sin * f], -1) for f in (scale, 1.0 / scale)], 1)
    return c.astype(np.float32), s.astype(np.float32)


_OUTS = [((B, S, D), 'float32')]


def kernel(**inputs):
    import numpy as _np
    import concourse.bacc as _bacc
    from concourse import mybir as _mybir
    from concourse.bass_utils import run_bass_kernel_spmd as _run

    nc = _bacc.Bacc("TRN2", target_bir_lowering=False, num_devices=1)
    arrays, args = {}, {}
    cos, sin = rope_tables(_np)
    named = dict(inputs)
    del named["mask_BxS_ff1"]
    named["rope_cos"] = cos
    named["rope_sin"] = sin
    for name, value in named.items():
        v = _np.ascontiguousarray(value)
        arrays[f"in_{name}_dram"] = v
        args[name] = nc.dram_tensor(f"in_{name}_dram", v.shape, _mybir.dt.from_np(v.dtype), kind="ExternalInput").ap()
    shape, dtype = _OUTS[0]
    out = nc.dram_tensor("out_0_dram", shape, _mybir.dt.from_np(_np.dtype(dtype)), kind="ExternalOutput").ap()
    build(nc, args, out)
    r = _run(nc, [arrays], core_ids=[0])
    return r.results[0]["out_0_dram"]
```
